# Optimizing a Trainium2 kernel written in Bass

```python
import numpy as np
import jax
import jax.numpy as jnp

def _softmax(x, axis=-1):
    return jax.nn.softmax(x, axis=axis)

def _gelu(x):
    return jax.nn.gelu(x, approximate=True)

def _silu(x):
    return jax.nn.silu(x)

def _sigmoid(x):
    return jax.nn.sigmoid(x)

def _layernorm(x, axis=-1, eps=1e-05):
    m = jnp.mean(x, axis=axis, keepdims=True)
    v = jnp.var(x, axis=axis, keepdims=True)
    return (x - m) / jnp.sqrt(v + eps)

def _scatter_add(tgt, idx, src, axis=0):
    return tgt.at[idx].add(src)

def _segment_sum(src, seg, n):
    return jax.ops.segment_sum(src, seg, n)
kernel_name = 'mk_perceiver_d2_seqx_r8_8fbaf5'

def setup_inputs(seed: int=0):
    np.random.seed(seed)
    _w = jnp.asarray

    def _rec_inputs():
        import jax
        import jax.numpy as jnp
        _rk = jax.random.key(seed)
        x = -0.0003929 + 0.9999 * jax.random.normal(jax.random.fold_in(_rk, 1), (64, 32, 256), jnp.float32)
        _lenS = 32 - jax.random.randint(jax.random.fold_in(_rk, 7), (64,), 0, max(1, 32 // 4) + 1, jnp.int32)
        _lenS2 = 257 - jax.random.randint(jax.random.fold_in(_rk, 8), (64,), 0, max(1, 257 // 4) + 1, jnp.int32)
        _ctx_1024P = jax.random.normal(jax.random.fold_in(_rk, 11), (64, 16, 128), jnp.float32)
        _ctx_1024c = jax.random.dirichlet(jax.random.fold_in(_rk, 511), 0.3 * jnp.ones((16,), jnp.float32), (64, 257))
        _ctx_1024t = jnp.einsum('bsk,bkd->bsd', _ctx_1024c, _ctx_1024P)
        _ctx_1024t = _ctx_1024t * jax.lax.rsqrt(jnp.mean(jnp.square(_ctx_1024t)) + 1e-12) * 0.953939
        ctx_1024 = -0.000494167 + 1.00018 * (_ctx_1024t + 0.3 * jax.random.normal(jax.random.fold_in(_rk, 611), (64, 257, 128), jnp.float32))
        _validS = jnp.arange(32)[None, :] < _lenS[:, None]
        _validS2 = jnp.arange(257)[None, :] < _lenS2[:, None]
        _causal = jnp.tril(jnp.ones((32, 32), dtype=bool))
        mask_BxS2_bf1 = jnp.ones((64, 257), dtype=bool)
        return (x, ctx_1024, mask_BxS2_bf1)
    x, ctx_1024, mask_BxS2_bf1 = _rec_inputs()

    def _L0_xattn_setup():
        import jax, jax.numpy as jnp
        import numpy as np
        N_HEADS = 16
        N_KV_HEADS = 8
        HEAD_DIM = 128
        D_TEXT = 256
        D_VISION = 128
        GROUPS = N_HEADS // N_KV_HEADS
        key = jax.random.key(seed)
        ks = jax.random.split(key, 6)
        B, T_text, T_vis = (4, 256, 72)
        text_hidden = jax.random.normal(ks[0], (B, T_text, D_TEXT), dtype=jnp.float32)
        vision_tokens = jax.random.normal(ks[1], (B, T_vis, D_VISION), dtype=jnp.float32)
        vision_mask = jnp.ones((B, T_vis), dtype=bool)
        s = 0.02
        Wq = jax.random.normal(ks[2], (D_TEXT, N_HEADS * HEAD_DIM), dtype=jnp.float32) * s
        Wk = jax.random.normal(ks[3], (D_VISION, N_KV_HEADS * HEAD_DIM), dtype=jnp.float32) * s
        Wv = jax.random.normal(ks[4], (D_VISION, N_KV_HEADS * HEAD_DIM), dtype=jnp.float32) * s
        Wo = jax.random.normal(ks[5], (N_HEADS * HEAD_DIM, D_TEXT), dtype=jnp.float32) * s
        return {'text_hidden': text_hidden, 'vision_tokens': vision_tokens, 'vision_mask': vision_mask, 'Wq': Wq, 'Wk': Wk, 'Wv': Wv, 'Wo': Wo}
    _L0_xattn_all = _L0_xattn_setup()
    _L0_xattn_in = {k: v for k, v in _L0_xattn_all.items() if k in ('Wq', 'Wk', 'Wv', 'Wo')}
    del _L0_xattn_all

    def _L0_attn_setup():
        import jax, jax.numpy as jnp
        import numpy as np
        HIDDEN = 256
        HQ = 32
        HKV = 4
        D = 64
        THETA = 10000.0
        SEQ = 256

        def _rope(x, pos):
            d = x.shape[-1]
            inv = 1.0 / THETA ** (jnp.arange(0, d, 2, dtype=jnp.float32) / d)
            ang = pos[:, None] * inv
            cos = jnp.cos(ang)[None, :, None, :]
            sin = jnp.sin(ang)[None, :, None, :]
            x1, x2 = jnp.split(x, 2, axis=-1)
            return jnp.concatenate([x1 * cos - x2 * sin, x2 * cos + x1 * sin], axis=-1)
        key = jax.random.key(seed)
        k1, k2, k3 = jax.random.split(key, 3)
        hidden_states = jax.random.normal(k1, (1, SEQ, HIDDEN), jnp.float32)
        w_qkv = jax.random.normal(k2, ((HQ + 2 * HKV) * D, HIDDEN), jnp.float32) * 0.02
        w_o = jax.random.normal(k3, (HIDDEN, HQ * D), jnp.float32) * 0.02
        return {'hidden_states': hidden_states, 'w_qkv': w_qkv, 'w_o': w_o}
    _L0_attn_all = _L0_attn_setup()
    _L0_attn_in = {k: v for k, v in _L0_attn_all.items() if k in ('w_qkv', 'w_o')}
    del _L0_attn_all

    def _L0_ffn_setup():
        import jax, jax.numpy as jnp
        import numpy as np
        NUM_EXPERTS = 32
        TOP_K = 4
        HIDDEN = 256
        INTER = 96
        key = jax.random.key(seed)
        k1, k2, k3, k4 = jax.random.split(key, 4)
        hidden_states = jax.random.normal(k1, (4, 64, HIDDEN), dtype=jnp.float32)
        gate = jax.random.normal(k2, (HIDDEN, NUM_EXPERTS), dtype=jnp.float32) * 0.02
        gate_up_proj = jax.random.normal(k3, (NUM_EXPERTS, HIDDEN, 2 * INTER), dtype=jnp.float32) * 0.02
        down_proj = jax.random.normal(k4, (NUM_EXPERTS, INTER, HIDDEN), dtype=jnp.float32) * 0.02
        return {'hidden_states': hidden_states, 'gate': gate, 'gate_up_proj': gate_up_proj, 'down_proj': down_proj}
    _L0_ffn_all = _L0_ffn_setup()
    _L0_ffn_in = {k: v for k, v in _L0_ffn_all.items() if k in ('gate', 'gate_up_proj', 'down_proj')}
    del _L0_ffn_all

    def _L1_xattn_setup():
        import jax, jax.numpy as jnp
        import numpy as np
        EPS = 1e-05

        def rmsnorm(x, g, eps=EPS):
            var = jnp.mean(jnp.square(x), axis=-1, keepdims=True)
            return x * jax.lax.rsqrt(var + eps) * g
        key = jax.random.key(seed)
        ks = jax.random.split(key, 8)
        B, Sq, Skv = (2, 512, 64)
        dim, cdim, H, D = (256, 128, 16, 128)
        inner = H * D
        s = lambda f: 1.0 / np.sqrt(f)
        return {'hidden_states': jax.random.normal(ks[0], (B, Sq, dim), jnp.float32), 'encoder_hidden_states': jax.random.normal(ks[1], (B, Skv, cdim), jnp.float32), 'Wq': jax.random.normal(ks[2], (dim, inner), jnp.float32) * s(dim), 'Wk': jax.random.normal(ks[3], (cdim, inner), jnp.float32) * s(cdim), 'Wv': jax.random.normal(ks[4], (cdim, inner), jnp.float32) * s(cdim), 'Wo': jax.random.normal(ks[5], (inner, dim), jnp.float32) * s(inner), 'gq': jnp.ones((D,), jnp.float32), 'gk': jnp.ones((D,), jnp.float32)}
    _L1_xattn_all = _L1_xattn_setup()
    _L1_xattn_in = {k: v for k, v in _L1_xattn_all.items() if k in ('Wq', 'Wk', 'Wv', 'Wo', 'gq', 'gk')}
    del _L1_xattn_all

    def _L1_attn_setup():
        import jax, jax.numpy as jnp
        import numpy as np
        H = 256
        NH = 16
        HD = H // NH
        NB = 8
        INTER = 2 * H
        EPS = 1e-05
        THETA = 10000.0

        def rmsnorm(x, w):
            return x * jax.lax.rsqrt(jnp.mean(x * x, axis=-1, keepdims=True) + EPS) * w

        def _act_quant(x):
            scale = 127.0 / jnp.maximum(jnp.max(jnp.abs(x), axis=-1, keepdims=True), 1e-05)
            return jnp.clip(jnp.round(x * scale), -128, 127) / scale

        def _weight_quant(w):
            scale = 1.0 / jnp.maximum(jnp.mean(jnp.abs(w)), 1e-05)
            return jnp.clip(jnp.round(w * scale), -1, 1) / scale

        def bitlinear(x, w):
            xq = x + jax.lax.stop_gradient(_act_quant(x) - x)
            wq = w + jax.lax.stop_gradient(_weight_quant(w) - w)
            return xq @ wq.T

        def rope_cache(seq_len, dim, theta):
            inv_freq = 1.0 / theta ** (jnp.arange(0, dim, 2, dtype=jnp.float32) / dim)
            t = jnp.arange(seq_len, dtype=jnp.float32)
            freqs = jnp.outer(t, inv_freq)
            return (jnp.cos(freqs), jnp.sin(freqs))

        def apply_rope(x, cos, sin):
            half = x.shape[-1] // 2
            x1, x2 = (x[..., :half], x[..., half:])
            return jnp.concatenate([x1 * cos - x2 * sin, x2 * cos + x1 * sin], axis=-1)
        key = jax.random.key(seed)
        ks = jax.random.split(key, 7)
        B, S = (2, 512)
        w = lambda k, shp: jax.random.normal(k, shp, dtype=jnp.float32) * 0.02
        return {'x': jax.random.normal(ks[0], (B, S, H), dtype=jnp.float32), 'attn_norm_w': jnp.ones((H,), jnp.float32), 'ffn_norm_w': jnp.ones((H,), jnp.float32), 'qkv_w': w(ks[1], (3 * H, H)), 'o_w': w(ks[2], (H, H)), 'ffn_up_w': w(ks[3], (2 * INTER, H)), 'ffn_down_w': w(ks[4], (H, INTER))}
    _L1_attn_all = _L1_attn_setup()
    _L1_attn_in = {k: v for k, v in _L1_attn_all.items() if k in ('attn_norm_w', 'ffn_norm_w', 'qkv_w', 'o_w', 'ffn_up_w', 'ffn_down_w')}
    del _L1_attn_all

    def _L1_ffn_setup():
        import jax, jax.numpy as jnp
        import numpy as np
        HIDDEN = 256
        INTER = 688
        LUT_SIZE = 16

        def _ghost_linear(x, idx, lut):
            w = lut[idx]
            return jnp.einsum('bsh,oh->bso', x, w)
        key = jax.random.key(seed)
        k_x, k_lut, k_g, k_u, k_d = jax.random.split(key, 5)
        x = jax.random.normal(k_x, (2, 512, HIDDEN), dtype=jnp.float32)
        lut = jax.random.normal(k_lut, (LUT_SIZE,), dtype=jnp.float32) * 0.02
        gate_idx = jax.random.randint(k_g, (INTER, HIDDEN), 0, LUT_SIZE, dtype=jnp.int32)
        up_idx = jax.random.randint(k_u, (INTER, HIDDEN), 0, LUT_SIZE, dtype=jnp.int32)
        down_idx = jax.random.randint(k_d, (HIDDEN, INTER), 0, LUT_SIZE, dtype=jnp.int32)
        return {'x': x, 'lut': lut, 'gate_idx': gate_idx, 'up_idx': up_idx, 'down_idx': down_idx}
    _L1_ffn_all = _L1_ffn_setup()
    _L1_ffn_in = {k: v for k, v in _L1_ffn_all.items() if k in ('lut', 'gate_idx', 'up_idx', 'down_idx')}
    del _L1_ffn_all
    return {'x': x, 'ctx_1024': ctx_1024, 'mask_BxS2_bf1': mask_BxS2_bf1, 'L0_xattn_Wq': _L0_xattn_in['Wq'], 'L0_xattn_Wk': _L0_xattn_in['Wk'], 'L0_xattn_Wv': _L0_xattn_in['Wv'], 'L0_xattn_Wo': _L0_xattn_in['Wo'], 'L0_attn_w_qkv': _L0_attn_in['w_qkv'], 'L0_attn_w_o': _L0_attn_in['w_o'], 'L0_ffn_gate': _L0_ffn_in['gate'], 'L0_ffn_gate_up_proj': _L0_ffn_in['gate_up_proj'], 'L0_ffn_down_proj': _L0_ffn_in['down_proj'], 'L1_xattn_Wq': _L1_xattn_in['Wq'], 'L1_xattn_Wk': _L1_xattn_in['Wk'], 'L1_xattn_Wv': _L1_xattn_in['Wv'], 'L1_xattn_Wo': _L1_xattn_in['Wo'], 'L1_xattn_gq': _L1_xattn_in['gq'], 'L1_xattn_gk': _L1_xattn_in['gk'], 'L1_attn_attn_norm_w': _L1_attn_in['attn_norm_w'], 'L1_attn_ffn_norm_w': _L1_attn_in['ffn_norm_w'], 'L1_attn_qkv_w': _L1_attn_in['qkv_w'], 'L1_attn_o_w': _L1_attn_in['o_w'], 'L1_attn_ffn_up_w': _L1_attn_in['ffn_up_w'], 'L1_attn_ffn_down_w': _L1_attn_in['ffn_down_w'], 'L1_ffn_lut': _L1_ffn_in['lut'], 'L1_ffn_gate_idx': _L1_ffn_in['gate_idx'], 'L1_ffn_up_idx': _L1_ffn_in['up_idx'], 'L1_ffn_down_idx': _L1_ffn_in['down_idx']}

def reference(x, ctx_1024, mask_BxS2_bf1, L0_xattn_Wq, L0_xattn_Wk, L0_xattn_Wv, L0_xattn_Wo, L0_attn_w_qkv, L0_attn_w_o, L0_ffn_gate, L0_ffn_gate_up_proj, L0_ffn_down_proj, L1_xattn_Wq, L1_xattn_Wk, L1_xattn_Wv, L1_xattn_Wo, L1_xattn_gq, L1_xattn_gk, L1_attn_attn_norm_w, L1_attn_ffn_norm_w, L1_attn_qkv_w, L1_attn_o_w, L1_attn_ffn_up_w, L1_attn_ffn_down_w, L1_ffn_lut, L1_ffn_gate_idx, L1_ffn_up_idx, L1_ffn_down_idx):
    import jax
    import jax.numpy as jnp

    def _L0_xattn_ref(text_hidden, vision_tokens, vision_mask, Wq, Wk, Wv, Wo):
        import jax, jax.numpy as jnp
        import numpy as np
        N_HEADS = 16
        N_KV_HEADS = 8
        HEAD_DIM = 128
        D_TEXT = 256
        D_VISION = 128
        GROUPS = N_HEADS // N_KV_HEADS
        B, T_text, _ = text_hidden.shape
        T_vis = vision_tokens.shape[1]
        scale = jnp.float32(np.sqrt(HEAD_DIM))
        q = (text_hidden @ Wq).reshape(B, T_text, N_HEADS, HEAD_DIM).transpose(0, 2, 1, 3)
        k = (vision_tokens @ Wk).reshape(B, T_vis, N_KV_HEADS, HEAD_DIM).transpose(0, 2, 1, 3)
        v = (vision_tokens @ Wv).reshape(B, T_vis, N_KV_HEADS, HEAD_DIM).transpose(0, 2, 1, 3)
        k = jnp.repeat(k, GROUPS, axis=1)
        v = jnp.repeat(v, GROUPS, axis=1)
        scores = jnp.einsum('bhtd,bhsd->bhts', q, k) / scale
        mask = vision_mask[:, None, None, :]
        scores = jnp.where(mask, scores, -jnp.inf)
        attn = jax.nn.softmax(scores, axis=-1)
        attn = jnp.nan_to_num(attn, nan=0.0)
        out = jnp.einsum('bhts,bhsd->bhtd', attn, v)
        out = out.transpose(0, 2, 1, 3).reshape(B, T_text, N_HEADS * HEAD_DIM)
        return out @ Wo

    def _L0_attn_ref(hidden_states, w_qkv, w_o):
        import jax, jax.numpy as jnp
        import numpy as np
        HIDDEN = 256
        HQ = 32
        HKV = 4
        D = 64
        THETA = 10000.0
        SEQ = 256

        def _rope(x, pos):
            d = x.shape[-1]
            inv = 1.0 / THETA ** (jnp.arange(0, d, 2, dtype=jnp.float32) / d)
            ang = pos[:, None] * inv
            cos = jnp.cos(ang)[None, :, None, :]
            sin = jnp.sin(ang)[None, :, None, :]
            x1, x2 = jnp.split(x, 2, axis=-1)
            return jnp.concatenate([x1 * cos - x2 * sin, x2 * cos + x1 * sin], axis=-1)
        b, s, _ = hidden_states.shape
        qkv = jnp.einsum('bsh,oh->bso', hidden_states, w_qkv).reshape(b, s, HQ + 2 * HKV, D)
        q = qkv[:, :, :HQ]
        k = qkv[:, :, HQ:HQ + HKV]
        v = qkv[:, :, HQ + HKV:]
        pos = jnp.arange(s, dtype=jnp.float32)
        q = _rope(q, pos)
        k = _rope(k, pos)
        rep = HQ // HKV
        k = jnp.repeat(k, rep, axis=2)
        v = jnp.repeat(v, rep, axis=2)
        scores = jnp.einsum('bqhd,bkhd->bhqk', q, k) * D ** (-0.5)
        causal = jnp.tril(jnp.ones((s, s), dtype=bool))
        scores = jnp.where(causal[None, None], scores, jnp.finfo(scores.dtype).min)
        attn = jax.nn.softmax(scores, axis=-1)
        out = jnp.einsum('bhqk,bkhd->bqhd', attn, v).reshape(b, s, HQ * D)
        return jnp.einsum('bso,ho->bsh', out, w_o)

    def _L0_ffn_ref(hidden_states, gate, gate_up_proj, down_proj):
        import jax, jax.numpy as jnp
        import numpy as np
        NUM_EXPERTS = 32
        TOP_K = 4
        HIDDEN = 256
        INTER = 96
        batch_size = hidden_states.shape[0]
        x = hidden_states.reshape(-1, HIDDEN)
        num_tokens = x.shape[0]
        router_logits = jnp.einsum('TD,DE->TE', x, gate)
        routing_weights = jax.nn.softmax(router_logits.astype(jnp.float32), axis=-1)
        top_k_weights, top_k_indices = jax.lax.top_k(routing_weights, TOP_K)
        top_k_weights = top_k_weights / top_k_weights.sum(axis=-1, keepdims=True)
        top_k_weights = top_k_weights.astype(x.dtype)
        router_weights = jnp.zeros((num_tokens, NUM_EXPERTS), dtype=x.dtype)
        token_indices = jnp.broadcast_to(jnp.arange(num_tokens)[:, None], top_k_indices.shape)
        router_weights = router_weights.at[token_indices, top_k_indices].set(top_k_weights)
        gate_up = jnp.einsum('TD,EDF->TEF', x, gate_up_proj)
        g, u = jnp.split(gate_up, 2, axis=-1)
        gated = u * jax.nn.silu(g)
        next_states = jnp.einsum('TEF,EFD->TED', gated, down_proj)
        next_states = (next_states * router_weights[..., None]).sum(axis=1)
        return next_states.reshape(batch_size, -1, HIDDEN)

    def _L1_xattn_ref(hidden_states, encoder_hidden_states, Wq, Wk, Wv, Wo, gq, gk):
        import jax, jax.numpy as jnp
        import numpy as np
        EPS = 1e-05

        def rmsnorm(x, g, eps=EPS):
            var = jnp.mean(jnp.square(x), axis=-1, keepdims=True)
            return x * jax.lax.rsqrt(var + eps) * g
        B, Sq, _ = hidden_states.shape
        Skv = encoder_hidden_states.shape[1]
        D = gq.shape[0]
        H = Wq.shape[1] // D
        scale = 1.0 / np.sqrt(D)
        q = (hidden_states @ Wq).reshape(B, Sq, H, D)
        k = (encoder_hidden_states @ Wk).reshape(B, Skv, H, D)
        v = (encoder_hidden_states @ Wv).reshape(B, Skv, H, D)
        q = rmsnorm(q, gq)
        k = rmsnorm(k, gk)
        scores = jnp.einsum('bqhd,bkhd->bhqk', q, k) * scale
        attn = jax.nn.softmax(scores, axis=-1)
        out = jnp.einsum('bhqk,bkhd->bqhd', attn, v)
        out = out.reshape(B, Sq, H * D)
        return out @ Wo

    def _L1_attn_ref(x, attn_norm_w, ffn_norm_w, qkv_w, o_w, ffn_up_w, ffn_down_w):
        import jax, jax.numpy as jnp
        import numpy as np
        H = 256
        NH = 16
        HD = H // NH
        NB = 8
        INTER = 2 * H
        EPS = 1e-05
        THETA = 10000.0

        def rmsnorm(x, w):
            return x * jax.lax.rsqrt(jnp.mean(x * x, axis=-1, keepdims=True) + EPS) * w

        def _act_quant(x):
            scale = 127.0 / jnp.maximum(jnp.max(jnp.abs(x), axis=-1, keepdims=True), 1e-05)
            return jnp.clip(jnp.round(x * scale), -128, 127) / scale

        def _weight_quant(w):
            scale = 1.0 / jnp.maximum(jnp.mean(jnp.abs(w)), 1e-05)
            return jnp.clip(jnp.round(w * scale), -1, 1) / scale

        def bitlinear(x, w):
            xq = x + jax.lax.stop_gradient(_act_quant(x) - x)
            wq = w + jax.lax.stop_gradient(_weight_quant(w) - w)
            return xq @ wq.T

        def rope_cache(seq_len, dim, theta):
            inv_freq = 1.0 / theta ** (jnp.arange(0, dim, 2, dtype=jnp.float32) / dim)
            t = jnp.arange(seq_len, dtype=jnp.float32)
            freqs = jnp.outer(t, inv_freq)
            return (jnp.cos(freqs), jnp.sin(freqs))

        def apply_rope(x, cos, sin):
            half = x.shape[-1] // 2
            x1, x2 = (x[..., :half], x[..., half:])
            return jnp.concatenate([x1 * cos - x2 * sin, x2 * cos + x1 * sin], axis=-1)
        B, S, _ = x.shape
        bt = S // NB
        h = rmsnorm(x, attn_norm_w)
        qkv = bitlinear(h, qkv_w).reshape(B, S, 3, NH, HD)
        q = jnp.transpose(qkv[:, :, 0], (0, 2, 1, 3))
        k = jnp.transpose(qkv[:, :, 1], (0, 2, 1, 3))
        v = jnp.transpose(qkv[:, :, 2], (0, 2, 1, 3))
        cos, sin = rope_cache(S, HD, THETA)
        q = apply_rope(q, cos, sin)
        k = apply_rope(k, cos, sin)
        blk = lambda t: jnp.transpose(t.reshape(B, NH, NB, bt, HD), (0, 2, 1, 3, 4))
        qb, kb, vb = (blk(q), blk(k), blk(v))
        scale = HD ** (-0.5)
        scores = jnp.einsum('bnhqd,bnhkd->bnhqk', qb, kb) * scale
        causal = jnp.triu(jnp.ones((bt, bt), bool), 1)
        scores = jnp.where(causal, jnp.finfo(scores.dtype).min, scores)
        attn = jax.nn.softmax(scores, axis=-1)
        ctx = jnp.einsum('bnhqk,bnhkd->bnhqd', attn, vb)
        ctx = jnp.transpose(ctx, (0, 2, 1, 3, 4)).reshape(B, NH, S, HD)
        ctx = jnp.transpose(ctx, (0, 2, 1, 3)).reshape(B, S, H)
        x1 = x + bitlinear(ctx, o_w)
        hn = rmsnorm(x1, ffn_norm_w)
        gv = hn @ ffn_up_w.T
        gate, val = jnp.split(gv, 2, axis=-1)
        return x1 + bitlinear(jax.nn.silu(gate) * val, ffn_down_w)

    def _L1_ffn_ref(x, lut, gate_idx, up_idx, down_idx):
        import jax, jax.numpy as jnp
        import numpy as np
        HIDDEN = 256
        INTER = 688
        LUT_SIZE = 16

        def _ghost_linear(x, idx, lut):
            w = lut[idx]
            return jnp.einsum('bsh,oh->bso', x, w)
        gate = _ghost_linear(x, gate_idx, lut)
        up = _ghost_linear(x, up_idx, lut)
        h = jax.nn.silu(gate) * up
        return _ghost_linear(h, down_idx, lut)
    x = x + _L0_xattn_ref(_layernorm(x, axis=-1), ctx_1024, mask_BxS2_bf1, L0_xattn_Wq, L0_xattn_Wk, L0_xattn_Wv, L0_xattn_Wo)
    x = x + _L0_attn_ref(_layernorm(x, axis=-1), L0_attn_w_qkv, L0_attn_w_o)
    x = x + _L0_ffn_ref(_layernorm(x, axis=-1), L0_ffn_gate, L0_ffn_gate_up_proj, L0_ffn_down_proj)
    x = x + _L1_xattn_ref(_layernorm(x, axis=-1), ctx_1024, L1_xattn_Wq, L1_xattn_Wk, L1_xattn_Wv, L1_xattn_Wo, L1_xattn_gq, L1_xattn_gk)
    x = x + _L1_attn_ref(_layernorm(x, axis=-1), L1_attn_attn_norm_w, L1_attn_ffn_norm_w, L1_attn_qkv_w, L1_attn_o_w, L1_attn_ffn_up_w, L1_attn_ffn_down_w)
    x = x + _L1_ffn_ref(_layernorm(x, axis=-1), L1_ffn_lut, L1_ffn_gate_idx, L1_ffn_up_idx, L1_ffn_down_idx)
    return x

_drawn_inputs = setup_inputs


def setup_inputs(seed=0):
    import zlib

    import numpy as np

    out = dict(_drawn_inputs(seed))
    spreads = {'L1_xattn_gq': (1.0, 0.6),
     'L1_xattn_gk': (1.0, 0.6),
     'L1_attn_attn_norm_w': (1.0, 0.6),
     'L1_attn_ffn_norm_w': (1.0, 0.6)}
    factors = {'L0_xattn_Wq': 8.0,
     'L0_xattn_Wk': 8.0,
     'L0_ffn_gate': 8.0,
     'L0_ffn_gate_up_proj': 8.0,
     'L0_ffn_down_proj': 8.0,
     'L1_attn_qkv_w': 3.228,
     'L1_attn_o_w': 3.206,
     'L1_attn_ffn_up_w': 7.257,
     'L1_attn_ffn_down_w': 7.279,
     'L1_ffn_lut': 2.924}
    for name, (base, spread) in spreads.items():
        noise = np.random.default_rng([zlib.crc32(name.encode()), seed]).standard_normal(out[name].shape)
        drawn = base * np.exp(spread * noise) if base else spread * noise
        out[name] = jnp.asarray(drawn.astype(out[name].dtype))
    for name, factor in factors.items():
        out[name] = (out[name] * factor).astype(out[name].dtype)
    return out
```

```python
from contextlib import ExitStack

import numpy as np
import concourse.bass as bass
from concourse import mybir
from concourse.alu_op_type import AluOpType as ALU

F32 = mybir.dt.float32
BF16 = mybir.dt.bfloat16
U8 = mybir.dt.uint8
I32 = mybir.dt.int32
ACT = mybir.ActivationFunctionType
AX = mybir.AxisListType

P = 128
B, S, D = 64, 32, 256
TOK = B * S
NT = TOK // P
KC = D // P
SUP = 4
ST = TOK // SUP
CD, CS = 128, 257
NH, HD = 16, 128
GQ = 4
EPS = 1e-5
NEG = -1e30

SB0 = 16512
X_OFF = SB0
C_OFF = X_OFF + NT * D * 4
L_OFF = C_OFF + 8192
TOP = 229344
QO_OFF = TOP - NH * TOK * 4

CONSTS = {"cos64": 64, "sin64": 64, "causal": S, "diag": S}


def tables():
    pos = np.arange(P) % S
    out = {}
    for d in (64, 16):
        inv = (1.0 / np.float32(10000.0) ** (np.arange(0, d, 2, dtype=np.float32) / np.float32(d))).astype(np.float32)
        ang = pos.astype(np.float32)[:, None] * inv
        co, si = np.cos(ang).astype(np.float32), np.sin(ang).astype(np.float32)
        out[f"cos{d}"] = np.concatenate([co, co], 1)
        out[f"sin{d}"] = np.concatenate([-si, si], 1)
    out["causal"] = np.where(np.arange(S)[None, :] <= pos[:, None], 0.0, NEG).astype(np.float32)
    out["diag"] = (np.arange(S)[None, :] == pos[:, None]).astype(np.float32)
    out["shift"] = (np.arange(P)[:, None, None] == np.arange(P)[None, None] - np.arange(1, 4)[None, :, None]).astype(np.float32)
    out["bmask"] = np.where(np.arange(4)[None, :] <= (np.arange(P) % 4)[:, None], 0.0, NEG).astype(np.float32)
    row_head = np.arange(4)[:, None] * 4 + (np.arange(P) // S)[None, :]
    pick = (np.arange(3 * NH)[:, None, None] % NH == row_head[None]).astype(np.float32)
    out["pick"] = pick
    return out


class Plan:

    def __init__(self, nc, ctx, ap):
        self.nc, self.ctx, self.ap = nc, ctx, ap
        self.layer_sems = []

    def at(self, name, shape, dt, off):
        t = self.nc.alloc_sbuf_tensor_at(name, shape, dt, offset=off)
        size = {F32: 4, I32: 4, BF16: 2, U8: 1}[dt]
        for n in shape[1:]:
            size *= n
        assert off + size <= TOP, (name, off + size - TOP)
        self.end = -(-(off + size) // 32) * 32
        return t

    def sem(self, name):
        s = self.nc.alloc_semaphore(name)
        self.layer_sems.append(s)
        return s

    def clear_layer(self):
        self.nc.clear_and_free_semaphores(self.layer_sems)
        self.layer_sems = []
        self.nc.all_engine_barrier()


def common(pl):
    nc = pl.nc
    pl.x = pl.at("x_sb", [P, NT, D], F32, X_OFF)
    pl.ident = pl.at("ident", [P, P], F32, C_OFF)
    pl.identb = pl.at("identb", [P, P], BF16, pl.end)
    pl.mv = pl.at("mv_all", [P, NT, 2], F32, pl.end)
    pl.rstd = pl.at("rstd_all", [P, NT], F32, pl.end)
    pl.veps = pl.at("veps_all", [P, NT], F32, pl.end)
    pl.bn = pl.at("bn_out", [P, 6], F32, pl.end)
    pl.mv1 = pl.at("mv_one", [P, 2], F32, pl.end)
    pl.mhalf = pl.at("minus_half", [P, NT], F32, pl.end)
    pl.maskb = pl.at("mask_bias", [B, CS], BF16, pl.end)
    pl.flag = pl.at("any_valid", [P, B], F32, pl.end)
    pl.cst = {n: pl.at(n, [P, w], F32, pl.end) for n, w in CONSTS.items()}
    pl.const_end = pl.end
    assert pl.end <= L_OFF
    pl.ps = pl.ctx.enter_context(nc.psum_tensor("ps", [P, 8, 512], F32))
    pl.x_loaded = nc.alloc_semaphore("x_loaded")
    pl.stats = nc.alloc_semaphore("stats_step")
    pl.stats_n = 0


def apart(pl, eng):
    eng.nop(nofuse=True)


def token_stats(pl, eng, t):
    n = t * 3 + pl.stats_n
    apart(pl, eng)
    eng.bn_stats(pl.bn[:, :], pl.x[:, t, :]).then_inc(pl.stats, 1)
    eng.wait_ge(pl.stats, n + 1)
    apart(pl, eng)
    eng.bn_aggr(pl.mv1[:, :], pl.bn[:, :]).then_inc(pl.stats, 1)
    eng.wait_ge(pl.stats, n + 2)
    apart(pl, eng)
    eng.tensor_copy(pl.mv[:, t, :], pl.mv1[:, :]).then_inc(pl.stats, 1)


def setup(pl):
    nc, ap = pl.nc, pl.ap
    pl.Aw = pl.at("Aw", [P, KC, NH, CD], F32, L_OFF)
    pl.Bw = pl.at("Bw", [P, NH, D], F32, pl.end)
    pl.tmp_off = pl.end
    wq = pl.at("s_wqT", [P, NH, D], F32, QO_OFF)
    wk = pl.at("s_wkT", [P, 8, CD], F32, pl.end)
    wv = pl.at("s_wvT", [P, 8, CD], F32, pl.end)
    wo = pl.at("s_wo", [P, NH, D], F32, pl.end)
    mask8 = pl.at("s_mask8", [B, CS], U8, pl.end)
    maskf = pl.at("s_maskf", [B, CS], F32, pl.end)
    vflag = pl.at("s_vflag", [B, 1], F32, pl.end)
    dflag = pl.at("s_dflag", [B, B], F32, pl.end)
    ones = pl.at("s_ones", [B, P], F32, pl.end)
    w_loaded, mask_loaded = pl.sem("set_w_loaded"), pl.sem("set_mask_loaded")
    ones_set, filled = pl.sem("set_ones"), pl.sem("set_filled")
    evac = [pl.sem("set_evac_vector"), pl.sem("set_evac_scalar")]
    ident_set, ident_zero, mstep = pl.sem("ident_set"), pl.sem("ident_zero"), pl.sem("set_mask_step")
    fl_done = pl.sem("set_flag_product")
    pl.ident_set = ident_set
    ps = pl.ps
    NA, NBK = KC * NH // 4, NH // 2

    consts_in = pl.sem("consts_loaded")
    with nc.Block() as block:
        @block.sync
        def _(eng):
            eng.dma_start(wq[:, :, :], ap["L0_WqT"]).then_inc(w_loaded, 16)
            eng.dma_start(wk[:, :, :], ap["L0_WkT"]).then_inc(w_loaded, 16)
            eng.dma_start(mask8[:, :], ap["mask"]).then_inc(mask_loaded, 16)
            eng.dma_start(wv[:, :, :], ap["L0_WvT"]).then_inc(w_loaded, 16)
            eng.dma_start(wo[:, :, :], ap["L0_Wo"]).then_inc(w_loaded, 16)

        @block.scalar
        def _(eng):
            eng.dma_start(pl.x[:, :, :], ap["x"]).then_inc(pl.x_loaded, 16)
            for name in CONSTS:
                eng.dma_start(pl.cst[name][:, :], ap[name]).then_inc(consts_in, 16)
            for k in range(1, NA + NBK, 2):
                eng.wait_ge(filled, k + 1)
                dst = pl.Aw[:, k * 4 // NH, k * 4 % NH:k * 4 % NH + 4, :] if k < NA else pl.Bw[:, 2 * (k - NA):2 * (k - NA) + 2, :]
                src = ps[:, k % 8, :].rearrange("p (h c) -> p h c", h=4 if k < NA else 2)
                eng.activation(dst, src, ACT.Copy).then_inc(evac[1], 1)

        @block.gpsimd
        def _(eng):
            eng.memset(pl.ident[:, :], 0.0).then_inc(ident_zero, 1)
            eng.memset(pl.identb[:, :], 0.0).then_inc(ident_zero, 1)
            eng.wait_ge(ident_zero, 2)
            for m in (pl.ident, pl.identb):
                eng.affine_select(out=m[:, :], in_=m[:, :], compare_op=ALU.not_equal, fill=1.0, base=0,
                                  pattern=[[-1, P]], channel_multiplier=1).then_inc(ident_set, 1)
            eng.memset(ones[:, :], 1.0).then_inc(ones_set, 1)
            eng.memset(pl.mhalf[:, :], -0.5).then_inc(ones_set, 1)

        @block.vector
        def _(eng):
            eng.wait_ge(mask_loaded, 16)
            eng.tensor_copy(maskf[:, :], mask8[:, :]).then_inc(mstep, 1)
            eng.wait_ge(mstep, 1)
            eng.tensor_scalar(pl.maskb[:, :], maskf[:, :], -1.0, -NEG, ALU.add, ALU.mult).then_inc(mstep, 1)
            eng.tensor_reduce(vflag[:, :], maskf[:, :], AX.X, ALU.max).then_inc(mstep, 1)
            eng.wait_ge(mstep, 3)
            eng.wait_ge(ident_set, 2)
            eng.tensor_scalar(dflag[:, :], pl.ident[0:B, 0:B], vflag[:, 0:1], None, ALU.mult).then_inc(mstep, 1)
            eng.wait_ge(fl_done, 1)
            eng.tensor_copy(pl.flag[:, :], ps[:, 7, 0:B]).then_inc(mstep, 1)
            for k in range(0, NA + NBK, 2):
                eng.wait_ge(filled, k + 1)
                dst = pl.Aw[:, k * 4 // NH, k * 4 % NH:k * 4 % NH + 4, :] if k < NA else pl.Bw[:, 2 * (k - NA):2 * (k - NA) + 2, :]
                src = ps[:, k % 8, :].rearrange("p (h c) -> p h c", h=4 if k < NA else 2)
                eng.tensor_copy(dst, src).then_inc(evac[0], 1)
            eng.wait_ge(pl.x_loaded, 16)
            for t in range(NT):
                token_stats(pl, eng, t)
            pl.stats_n += 3 * NT
            eng.wait_ge(consts_in, 16 * len(CONSTS))

        @block.tensor
        def _(eng):
            eng.wait_ge(mstep, 4)
            eng.wait_ge(ones_set, 1)
            eng.matmul(ps[:, 7, 0:B], ones[:, :], dflag[:, :], start=True, stop=True).then_inc(fl_done, 1)
            eng.wait_ge(mstep, 5)
            eng.wait_ge(w_loaded, 32)
            for k in range(NA):
                if k >= 8:
                    eng.wait_ge(evac[k % 2], (k - 8) // 2 + 1)
                for j in range(4):
                    c, h = divmod(4 * k + j, NH)
                    mm = eng.matmul(ps[:, k % 8, j * CD:(j + 1) * CD], wq[:, h, c * P:(c + 1) * P], wk[:, h // 2, :],
                                    start=True, stop=True)
                mm.then_inc(filled, 1)
            eng.wait_ge(w_loaded, 64)
            for k in range(NA, NA + NBK):
                eng.wait_ge(evac[k % 2], (k - 8) // 2 + 1)
                for j in range(2):
                    h = 2 * (k - NA) + j
                    mm = eng.matmul(ps[:, k % 8, j * D:(j + 1) * D], wv[:, h // 2, :], wo[:, h, :], start=True, stop=True)
                mm.then_inc(filled, 1)


def layer_norm_steps(pl, name):
    return {k: pl.sem(f"{name}_{k}") for k in ("rs_in", "rstd", "xn", "turned", "xT")}


def rstd_of_all(pl, eng, s):
    eng.wait_ge(pl.stats, pl.stats_n)
    eng.tensor_scalar(pl.veps[:, :], pl.mv[:, :, 1], EPS, None, ALU.add).then_inc(s["rs_in"], 1)
    eng.wait_ge(s["rstd"], 1)


def pow_of_all(pl, eng, s):
    eng.wait_ge(s["rs_in"], 1)
    eng.tensor_tensor(pl.rstd[:, :], pl.veps[:, :], pl.mhalf[:, :], ALU.pow).then_inc(s["rstd"], 1)


def norm_supertile(pl, eng, s, xn, xT, i):
    for j in range(4):
        if j == 0:
            eng.wait_ge(s["turned"], i * 2)
        eng.tensor_scalar(xn[:, j, :], pl.x[:, i * 4 + j, :], pl.mv[:, i * 4 + j, 0:1], pl.rstd[:, bass.ds(i * 4 + j, 1)],
                          ALU.subtract, ALU.mult).then_inc(s["xn"], 1)
    for m in range(2):
        eng.wait_ge(s["turned"], i * 2 + m + 1)
        eng.tensor_copy(xT[:, :, bass.ds(i * ST + m * 256, 256)],
                        pl.ps[:, 6 + m, :].rearrange("p (k n) -> p k n", k=KC)).then_inc(s["xT"], 1)


def turn_supertile(pl, eng, s, xn, i):
    for m in range(2):
        eng.wait_ge(s["xn"], i * 4 + 2 * m + 2)
        eng.wait_ge(s["xT"], i * 2)
        for j in range(2):
            for k in range(KC):
                mm = eng.transpose(pl.ps[:, 6 + m, k * 256 + j * P:k * 256 + j * P + P],
                                   xn[:, 2 * m + j, k * P:(k + 1) * P], pl.ident[:, :])
        mm.then_inc(s["turned"], 1)


def l0x_queries(pl):
    nc = pl.nc
    pl.QO = pl.at("QO", [P, NH, TOK], F32, QO_OFF)
    xT = pl.at("l0x_xT", [P, KC, TOK], F32, pl.tmp_off)
    xn = pl.at("l0x_xn", [P, 4, D], F32, pl.end)
    assert pl.end <= QO_OFF
    s = layer_norm_steps(pl, "l0xq")
    filled, evac = pl.sem("l0xq_filled"), pl.sem("l0xq_bank_free")

    with nc.Block() as block:
        @block.gpsimd
        def _(eng):
            pow_of_all(pl, eng, s)

        @block.vector
        def _(eng):
            rstd_of_all(pl, eng, s)
            with eng.Fori(0, SUP) as i:
                norm_supertile(pl, eng, s, xn, xT, i)

        @block.scalar
        def _(eng):
            eng.sem_inc(evac, 4)
            with eng.Fori(0, SUP) as i:
                for h in range(NH):
                    eng.wait_ge(filled, i * NH + h + 1)
                    eng.activation(pl.QO[:, h, bass.ds(i * ST, ST)], pl.ps[:, h % 4, :], ACT.Copy).then_inc(evac, 1)

        @block.tensor
        def _(eng):
            def heads(i, lo, hi):
                for h in range(lo, hi):
                    eng.wait_ge(evac, i * NH + h + 1)
                    for k in range(KC):
                        mm = eng.matmul(pl.ps[:, h % 4, :], pl.Aw[:, k, h, :], xT[:, k, bass.ds(i * ST, ST)],
                                        start=(k == 0), stop=(k == KC - 1))
                    mm.then_inc(filled, 1)

            turn_supertile(pl, eng, s, xn, 0)
            with eng.Fori(0, SUP - 1) as i:
                eng.wait_ge(s["xT"], i * 2 + 2)
                heads(i, 0, NH // 2)
                turn_supertile(pl, eng, s, xn, i + 1)
                heads(i, NH // 2, NH)
            eng.wait_ge(s["xT"], SUP * 2)
            heads(SUP - 1, 0, NH)


UB = 4


def xattn_batches(pl, name, low, high, masked, normed=False):
    nc, ps, QO = pl.nc, pl.ps, pl.QO
    SC = float(HD) ** -0.5
    sm = {}
    qb = [pl.at(f"{name}_qb{j}", [P, NH, S], F32, low if j == 0 else pl.end) for j in range(2)]
    ctxT = [pl.at(f"{name}_ctxT{j}", [P, CS], F32, pl.end) for j in range(UB)]
    ctxn = [pl.at(f"{name}_ctx{j}", [P, 2, CD], F32, pl.end) for j in range(UB)]
    ctxl = [pl.at(f"{name}_ctxl{j}", [1, CD], F32, pl.end) for j in range(UB)]
    if normed:
        rk = [pl.at(f"{name}_rk{j}", [3 * NH, CS], BF16, pl.end) for j in range(UB)]
        rkr = [pl.at(f"{name}_rkr{j}", [P, CS], F32, pl.end) for j in range(2)]
    assert high is None or pl.end <= high, pl.end
    prob = [pl.at(f"{name}_prob{j}", [P, GQ, CS], F32, high if high and j == 0 else pl.end) for j in range(2)]
    pT = pl.at(f"{name}_pT", [P, 2, 512], F32, pl.end)
    pTl = pl.at(f"{name}_pTl", [1, 512], F32, pl.end)
    mx = [pl.at(f"{name}_mx{j}", [P, GQ], F32, pl.end) for j in range(2)]
    nb = [pl.at(f"{name}_nb{j}", [P, GQ], F32, pl.end) for j in range(2)]
    sums = [pl.at(f"{name}_sum{j}", [P, GQ], F32, pl.end) for j in range(2)]
    rinv = [pl.at(f"{name}_rinv{j}", [P, GQ], F32, pl.end) for j in range(2)]
    rfl = [pl.at(f"{name}_rfl{j}", [P, GQ], F32, pl.end) for j in range(2)]
    mx_end = pl.end
    if normed:
        bw = pl.Bw1 = pl.at("Bw1", [P, NH, D], F32, QO_OFF - NH * D * 4)
        bw_in = pl.bw1_in = pl.sem(f"{name}_bw_loaded")
        assert pl.end >= QO_OFF - 32
        assert mx_end <= QO_OFF - NH * D * 4, mx_end
        pl.end = mx_end
    assert pl.end <= QO_OFF, pl.end - QO_OFF
    T0, T1, TL, O = 4, 5, 6, 7
    ctxT_in = [pl.sem(f"{name}_ctxT_loaded{j}") for j in range(UB)]
    ctxn_in = [pl.sem(f"{name}_ctx_loaded{j}") for j in range(UB)]
    rk_in = [pl.sem(f"{name}_rk_loaded{j}") for j in range(UB)] if normed else None
    for k in ("qb", "rep", "rep_out", "scaled", "scored", "mx", "nb", "exp", "rinv", "rfl", "norm", "turned",
              "pT_scalar", "pT_vector", "attended", "out_read"):
        sm[k] = pl.sem(f"{name}_{k}")
    NI = B // UB

    with nc.Block() as block:
        @block.sync
        def _(eng):
            def load(i, p):
                b = i * UB + p
                eng.wait_ge(sm["scored"], (i - 1) * UB * GQ + (p + 1) * GQ) if not isinstance(i, int) else None
                eng.dma_start(ctxT[p][:, :], pl.ap["ctxT"][:, bass.ds(b * CS, CS)]).then_inc(ctxT_in[p], 16)
                if normed:
                    eng.dma_start(rk[p][:, :], pl.rk_dram[:, bass.ds(b * CS, CS)]).then_inc(rk_in[p], 16)
                eng.wait_ge(sm["attended"], (i - 1) * UB + p + 1) if not isinstance(i, int) else None
                eng.dma_start(ctxn[p][:, :, :], pl.ap["ctx"][b, 0:2 * P, :].rearrange("(c p) d -> p c d", p=P) if isinstance(b, int)
                              else pl.ap["ctx"][bass.ds(b, 1), 0:2 * P, :].rearrange("b (c p) d -> p (b c) d", p=P)).then_inc(ctxn_in[p], 16)
                eng.dma_start(ctxl[p][:, :], pl.ap["ctx"][bass.ds(b, 1), 2 * P, :]).then_inc(ctxn_in[p], 16)
            for p in range(UB):
                load(0, p)
            if normed:
                eng.dma_start(bw[:, :, :], pl.bw1_dram).then_inc(bw_in, 16)
            with eng.Fori(1, NI) as i:
                for p in range(UB):
                    load(i, p)

        def each_batch(eng, first, step):
            first()
            with eng.Fori(0, NI - 1) as i:
                for p in range(UB):
                    step(i, p, True)
            for p in range(UB):
                step(NI - 1, p, p < UB - 1)

        @block.gpsimd
        def _(eng):
            def copy_q(i, p):
                b = i * UB + p
                if not (isinstance(i, int) and i * UB + p < 2):
                    eng.wait_ge(sm["scored"], b * GQ - GQ)
                eng.tensor_copy(qb[p % 2][:, :, :], QO[:, :, bass.ds(b * S, S)]).then_inc(sm["qb"], 1)

            def first():
                copy_q(0, 0)
                copy_q(0, 1)

            def step(i, p, more):
                if not (isinstance(i, int) and i == NI - 1 and p >= UB - 2):
                    b = i * UB + p + 2
                    eng.wait_ge(sm["scored"], b * GQ - GQ)
                    eng.tensor_copy(qb[p % 2][:, :, :], QO[:, :, bass.ds(b * S, S)]).then_inc(sm["qb"], 1)
            each_batch(eng, first, step)

        @block.vector
        def _(eng):
            def scaled_maxima(i, p, m):
                b = i * UB + p
                for g in (2 * m, 2 * m + 1):
                    eng.wait_ge(sm["rep_out"], b * GQ + g + 1)
                    eng.wait_ge(sm["scored"], b * GQ + g + 1)
                    if g == 0 and not (isinstance(i, int) and b < 2):
                        eng.wait_ge(sm["turned"], b - 1)
                    apart(pl, eng)
                    eng.tensor_tensor_reduce(out=prob[p % 2][:, g, :], in0=ps[:, g % 2, 0:CS], in1=rkr[g % 2][:, :], scale=1.0,
                                             scalar=-3.0e38, op0=ALU.mult, op1=ALU.max, accum_out=mx[p % 2][:, g:g + 1]).then_inc(sm["scaled"], 1)
                if m == 0:
                    return
                eng.wait_ge(sm["scaled"], (b + 1) * GQ)
                eng.scalar_tensor_tensor(out=nb[p % 2][:, :], in0=mx[p % 2][:, :], scalar=-1.0,
                                         in1=pl.rq[:, bass.ds(b, 1), :].rearrange("p a g -> p (a g)"), op0=ALU.mult, op1=ALU.mult).then_inc(sm["nb"], 1)

            def maxima(i, p, m):
                b = i * UB + p
                if normed:
                    return scaled_maxima(i, p, m)
                eng.wait_ge(sm["scored"], b * GQ + 2 * m + 2)
                eng.tensor_reduce(mx[p % 2][:, 2 * m:2 * m + 2], ps[:, 2 * m:2 * m + 2, 0:CS], AX.X, ALU.max).then_inc(sm["mx"], 1)
                eng.wait_ge(sm["mx"], b * 2 + m + 1)
                eng.tensor_scalar(nb[p % 2][:, 2 * m:2 * m + 2], mx[p % 2][:, 2 * m:2 * m + 2], -SC, None,
                                  ALU.mult).then_inc(sm["nb"], 1)

            def inverse(i, p):
                b = i * UB + p
                eng.wait_ge(sm["exp"], (b + 1) * GQ)
                eng.reciprocal(rinv[p % 2][:, :], sums[p % 2][:, :]).then_inc(sm["rinv"], 1)
                eng.wait_ge(sm["rinv"], b + 1)
                if masked:
                    eng.tensor_scalar(rfl[p % 2][:, :], rinv[p % 2][:, :], pl.flag[:, bass.ds(b, 1)], None, ALU.mult).then_inc(sm["rfl"], 1)
                    eng.wait_ge(sm["rfl"], b + 1)
                factor = rfl if masked else rinv
                for g in range(GQ):
                    eng.tensor_scalar(prob[p % 2][:, g, :], prob[p % 2][:, g, :], factor[p % 2][:, g:g + 1], None,
                                      ALU.mult).then_inc(sm["norm"], 1)

            def first():
                maxima(0, 0, 0)
                maxima(0, 0, 1)
                inverse(0, 0)

            def step(i, p, more):
                b = i * UB + p
                if more:
                    maxima(i + (p + 1) // UB, (p + 1) % UB, 0)
                eng.wait_ge(sm["turned"], b + 1)
                eng.wait_ge(sm["attended"], b)
                eng.tensor_copy(pT[:, 1, :], ps[:, T1, :]).then_inc(sm["pT_vector"], 1)
                eng.tensor_copy(pTl[:, :], ps[0:1, TL, :]).then_inc(sm["pT_vector"], 1)
                if more:
                    maxima(i + (p + 1) // UB, (p + 1) % UB, 1)
                    inverse(i + (p + 1) // UB, (p + 1) % UB)
                eng.wait_ge(sm["attended"], b + 1)
                eng.tensor_copy(QO[:, :, bass.ds(b * S, S)], ps[:, O, :].rearrange("p (h s) -> p h s", s=S)).then_inc(sm["out_read"], 1)
            each_batch(eng, first, step)

        @block.scalar
        def _(eng):
            eng.preload_act_table(ACT.Exp)

            def exps(i, p, groups):
                b = i * UB + p
                if normed:
                    for g in groups:
                        eng.wait_ge(sm["rep"], b * GQ + g + 1)
                        if g >= 2 or not (isinstance(i, int) and b == 0):
                            eng.wait_ge(sm["scaled"], b * GQ + g - 1)
                        eng.activation(rkr[g % 2][:, :], ps[:, 2 + g % 2, 0:CS], ACT.Copy).then_inc(sm["rep_out"], 1)
                    if groups[-1] < GQ - 1:
                        return
                    eng.wait_ge(sm["nb"], b + 1)
                    for g in range(GQ):
                        eng.activation(prob[p % 2][:, g, :], prob[p % 2][:, g, :], ACT.Exp, bias=nb[p % 2][:, g:g + 1],
                                       scale=pl.rq[:, b, g:g + 1], accum_out=sums[p % 2][:, g:g + 1]).then_inc(sm["exp"], 1)
                    return
                for g in groups:
                    if g % 2 == 0:
                        eng.wait_ge(sm["nb"], b * 2 + g // 2 + 1)
                    if g == 0 and not (isinstance(i, int) and b < 2):
                        eng.wait_ge(sm["turned"], b - 1)
                    eng.activation(prob[p % 2][:, g, :], ps[:, g, 0:CS], ACT.Exp, bias=nb[p % 2][:, g:g + 1], scale=SC,
                                   accum_out=sums[p % 2][:, g:g + 1]).then_inc(sm["exp"], 1)

            def step(i, p, more):
                b = i * UB + p
                if more:
                    exps(i + (p + 1) // UB, (p + 1) % UB, (0, 1))
                eng.wait_ge(sm["turned"], b + 1)
                eng.wait_ge(sm["attended"], b)
                eng.activation(pT[:, 0, :], ps[:, T0, :], ACT.Copy).then_inc(sm["pT_scalar"], 1)
                if more:
                    exps(i + (p + 1) // UB, (p + 1) % UB, (2, 3))
            each_batch(eng, lambda: exps(0, 0, range(GQ)), step)

        @block.tensor
        def _(eng):
            def scores(i, p, groups):
                b = i * UB + p
                if groups[0] == 0:
                    eng.wait_ge(ctxT_in[p], i * 16 + 16)
                    eng.wait_ge(sm["qb"], b + 1)
                    if normed:
                        eng.wait_ge(rk_in[p], i * 16 + 16)
                for g in groups:
                    if normed:
                        if g >= 2 or not (isinstance(i, int) and b == 0):
                            eng.wait_ge(sm["rep_out"], b * GQ + g - 1)
                        eng.matmul(ps[:, 2 + g % 2, 0:CS], pl.pick[:, g, :], rk[p][:, :], start=True, stop=True).then_inc(sm["rep"], 1)
                        if g >= 2 or not (isinstance(i, int) and b == 0):
                            eng.wait_ge(sm["scaled"], b * GQ + g - 1)
                        eng.matmul(ps[:, g % 2, 0:CS], qb[p % 2][:, 4 * g:4 * g + 4, :], ctxT[p][:, :], start=True, stop=True).then_inc(sm["scored"], 1)
                        continue
                    if not (isinstance(i, int) and b == 0):
                        eng.wait_ge(sm["exp"], b * GQ - GQ + g + 1)
                    mm = eng.matmul(ps[:, g, 0:CS], qb[p % 2][:, 4 * g:4 * g + 4, :], ctxT[p][:, :], start=True, stop=not masked)
                    if masked:
                        mm = eng.matmul(ps[:, g, 0:CS], pl.identb[0:B, bass.ds(b, 1)].to_broadcast([B, P]), pl.maskb[:, :],
                                        start=False, stop=True)
                    mm.then_inc(sm["scored"], 1)

            def step(i, p, more):
                b = i * UB + p
                if more:
                    scores(i + (p + 1) // UB, (p + 1) % UB, (0, 1))
                eng.wait_ge(sm["pT_scalar"], b)
                eng.wait_ge(sm["pT_vector"], 2 * b)
                for g in range(GQ):
                    eng.wait_ge(sm["norm"], b * GQ + g + 1)
                    for c, (bank, n) in enumerate(((T0, P), (T1, P), (TL, 1))):
                        mm = eng.transpose(ps[0:n, bank, g * P:(g + 1) * P], prob[p % 2][:, g, c * P:c * P + n], pl.ident[:, :])
                mm.then_inc(sm["turned"], 1)
                if more:
                    scores(i + (p + 1) // UB, (p + 1) % UB, (2, 3))
                eng.wait_ge(ctxn_in[p], i * 32 + 32)
                eng.wait_ge(sm["out_read"], b)
                eng.wait_ge(sm["pT_scalar"], b + 1)
                eng.matmul(ps[:, O, :], ctxn[p][:, 0, :], pT[:, 0, :], start=True, stop=False)
                eng.wait_ge(sm["pT_vector"], 2 * b + 2)
                eng.matmul(ps[:, O, :], ctxn[p][:, 1, :], pT[:, 1, :], start=False, stop=False)
                eng.matmul(ps[:, O, :], ctxl[p][:, :], pTl[:, :], start=False, stop=True).then_inc(sm["attended"], 1)
            each_batch(eng, lambda: scores(0, 0, range(GQ)), step)


def xattn_project(pl, name, Bw, low, bw_in=None):
    nc, ps, QO = pl.nc, pl.ps, pl.QO
    yT = [pl.at(f"{name}_yT{j}", [P, KC, 512], F32, low if j == 0 else pl.end) for j in range(2)]
    assert pl.end <= QO_OFF - (NH * D * 4 if bw_in is not None else 0)
    made, y0, y1, turned, added = (pl.sem(f"{name}_{k}") for k in ("made", "y_scalar", "y_vector", "turned", "added"))

    with nc.Block() as block:
        @block.tensor
        def _(eng):
            def products(s):
                for k in range(KC):
                    if s >= 2:
                        eng.wait_ge((y0, y1)[k], s - 1)
                    for h in range(NH):
                        mm = eng.matmul(ps[:, 2 * (s % 2) + k, :], Bw[:, h, k * P:(k + 1) * P], QO[:, h, s * ST:(s + 1) * ST],
                                        start=(h == 0), stop=(h == NH - 1))
                    mm.then_inc(made, 1)

            def turn(s):
                eng.wait_ge(y0, s + 1)
                eng.wait_ge(y1, s + 1)
                if s >= 1:
                    eng.wait_ge(added, 2 * s)
                for m in range(2):
                    for j in range(2):
                        for k in range(KC):
                            mm = eng.transpose(ps[:, 4 + m, j * D + k * P:j * D + (k + 1) * P],
                                               yT[s % 2][:, k, (2 * m + j) * P:(2 * m + j + 1) * P], pl.ident[:, :])
                    mm.then_inc(turned, 1)

            if bw_in is not None:
                eng.wait_ge(bw_in, 16)
            products(0)
            for s in range(SUP):
                if s + 1 < SUP:
                    products(s + 1)
                turn(s)

        @block.scalar
        def _(eng):
            for s in range(SUP):
                eng.wait_ge(made, 2 * s + 1)
                if s >= 2:
                    eng.wait_ge(turned, 2 * (s - 1))
                eng.activation(yT[s % 2][:, 0, :], ps[:, 2 * (s % 2), :], ACT.Copy).then_inc(y0, 1)

        @block.vector
        def _(eng):
            def take(s):
                eng.wait_ge(made, 2 * s + 2)
                if s >= 2:
                    eng.wait_ge(turned, 2 * (s - 1))
                eng.tensor_copy(yT[s % 2][:, 1, :], ps[:, 2 * (s % 2) + 1, :]).then_inc(y1, 1)

            def add(s):
                for m in range(2):
                    t = 4 * s + 2 * m
                    eng.wait_ge(turned, 2 * s + m + 1)
                    eng.tensor_tensor(pl.x[:, t:t + 2, :], ps[:, 4 + m, :].rearrange("p (t d) -> p t d", t=2),
                                      pl.x[:, t:t + 2, :], ALU.add).then_inc(added, 1)
                for t in range(4 * s, 4 * s + 4):
                    eng.wait_ge(added, 2 * s + (t - 4 * s) // 2 + 1)
                    token_stats(pl, eng, t)

            take(0)
            for s in range(SUP):
                if s + 1 < SUP:
                    take(s + 1)
                add(s)
            pl.stats_n += 3 * NT


def self_attention(pl):
    nc, ps = pl.nc, pl.ps
    HQ, HKV, E = 32, 4, 64
    NQ, NKV = HQ * E, HKV * E
    NB = P // S
    SC = float(E) ** -0.5
    w = pl.at("sa_wqkv", [P, KC, NQ + 2 * NKV], F32, L_OFF)
    wo = pl.at("sa_wo", [P, NQ // P, D], F32, pl.end)
    xn = pl.at("sa_xn", [P, D], F32, pl.end)
    xT = pl.at("sa_xT", [P, KC, P], F32, pl.end)
    qk = pl.at("sa_qk", [P, HQ + HKV, 2, E // 2], F32, pl.end)
    v = [pl.at(f"sa_v{j}", [P, NKV], F32, pl.end) for j in range(2)]
    rot = pl.at("sa_rot", [P, HQ + HKV, 2, E // 2], F32, pl.end)
    rsin = pl.at("sa_rsin", [P, HQ + HKV, 2, E // 2], F32, pl.end)
    kd = pl.at("sa_kd", [P, HKV, 2, E], F32, pl.end)
    qT = pl.at("sa_qT", [P, NQ // P, P], F32, pl.end)
    kT = pl.at("sa_kT", [P, HKV, P], F32, pl.end)
    sc = pl.at("sa_sc", [P, HQ, S], F32, pl.end)
    pT = pl.at("sa_pT", [P, HQ, S], F32, pl.end)
    mx = pl.at("sa_mx", [P, HQ], F32, pl.end)
    sums = pl.at("sa_sums", [P, HQ], F32, pl.end)
    rinv = pl.at("sa_rinv", [P, HQ], F32, pl.end)
    oT = pl.at("sa_oT", [P, NQ // P, P], F32, pl.end)
    s = {k: pl.sem(f"sa_{k}") for k in (
        "w_in", "wo_in", "rs_in", "rstd", "xn", "xturned", "xT", "projected", "qkv", "cos", "sin", "rotated", "turned",
        "turned_scalar", "turned_vector", "scored", "soft", "exp", "pT", "valued", "oT", "output", "added")}
    NW = 5

    def each_tile(eng, first, step):
        first()
        with eng.Fori(0, NT // 2 - 1) as u:
            for p in range(2):
                step(u * 2 + p, p, True)
        for p in range(2):
            step(NT - 2 + p, p, p == 0)

    with nc.Block() as block:
        @block.sync
        def _(eng):
            eng.dma_start(w[:, :, :], pl.ap["L0_wqkvT"]).then_inc(s["w_in"], 16)
            eng.dma_start(wo[:, :, :], pl.ap["L0_woT"]).then_inc(s["wo_in"], 16)

        @block.gpsimd
        def _(eng):
            pow_of_all(pl, eng, s)

            def sine(t):
                eng.wait_ge(s["qkv"], t * 6 + 5)
                eng.wait_ge(s["rotated"], t * 3)
                for a in range(2):
                    eng.tensor_tensor(rsin[:, :, a, :], qk[:, :, 1 - a, :],
                                      pl.cst["sin64"][:, None, a * 32:a * 32 + 32].to_broadcast([P, HQ + HKV, 32]),
                                      ALU.mult).then_inc(s["sin"], 1)
            each_tile(eng, lambda: sine(0), lambda t, p, more: sine(t + 1) if more else None)

        @block.vector
        def _(eng):
            rstd_of_all(pl, eng, s)

            def norm(t):
                eng.wait_ge(s["xturned"], t)
                eng.tensor_scalar(xn[:, :], pl.x[:, t, :] if isinstance(t, int) else pl.x[:, bass.ds(t, 1), :].rearrange("p a d -> p (a d)"),
                                  pl.mv[:, t, 0:1], pl.rstd[:, bass.ds(t, 1)], ALU.subtract, ALU.mult).then_inc(s["xn"], 1)

            def rotate(t):
                eng.wait_ge(s["qkv"], t * 6 + 5)
                eng.wait_ge(s["turned"], t * 5)
                eng.tensor_tensor(rot[:, :, :, :].rearrange("p h a e -> p h (a e)"), qk[:, :, :, :].rearrange("p h a e -> p h (a e)"),
                                  pl.cst["cos64"][:, None, :].to_broadcast([P, HQ + HKV, E]), ALU.mult).then_inc(s["cos"], 1)
                eng.wait_ge(s["cos"], t + 1)
                eng.wait_ge(s["sin"], t * 2 + 2)
                f = lambda a: a.rearrange("p h a e -> p h (a e)")
                eng.tensor_tensor(f(rot[:, 0:HQ]), f(rot[:, 0:HQ]), f(rsin[:, 0:HQ]), ALU.add).then_inc(s["rotated"], 1)
                for a in range(2):
                    eng.tensor_tensor(kd[:, :, a, :], f(rot[:, HQ:]), f(rsin[:, HQ:]), ALU.add).then_inc(s["rotated"], 1)

            def take_turned(t):
                for k in (1, 3):
                    eng.wait_ge(s["turned"], t * 5 + k + 1)
                    eng.wait_ge(s["scored"], t)
                    eng.tensor_copy(qT[:, 4 * k:4 * k + 4, :], ps[:, 6 + (7 + k) % 2, :].rearrange("p (c n) -> p c n", c=4)).then_inc(s["turned_vector"], 1)

            def softmax(t):
                n = t * 6
                eng.wait_ge(s["scored"], t + 1)
                eng.tensor_tensor(sc[:, :, :], ps[:, 0:2, :].rearrange("p a (h k) -> p (a h) k", k=S),
                                  pl.cst["causal"][:, None, :].to_broadcast([P, HQ, S]), ALU.add).then_inc(s["soft"], 1)
                eng.wait_ge(s["soft"], n + 1)
                eng.tensor_reduce(mx[:, :], sc[:, :, :], AX.X, ALU.max).then_inc(s["soft"], 1)
                eng.wait_ge(s["soft"], n + 2)
                eng.tensor_tensor(sc[:, :, :], sc[:, :, :], mx[:, :, None].to_broadcast([P, HQ, S]), ALU.subtract).then_inc(s["soft"], 1)
                eng.wait_ge(s["exp"], t + 1)
                eng.tensor_reduce(sums[:, :], sc[:, :, :], AX.X, ALU.add).then_inc(s["soft"], 1)
                eng.wait_ge(s["soft"], n + 4)
                eng.reciprocal(rinv[:, :], sums[:, :]).then_inc(s["soft"], 1)
                eng.wait_ge(s["soft"], n + 5)
                eng.tensor_tensor(sc[:, :, :], sc[:, :, :], rinv[:, :, None].to_broadcast([P, HQ, S]), ALU.mult).then_inc(s["soft"], 1)
                eng.wait_ge(s["soft"], n + 6)
                eng.wait_ge(s["valued"], t * 4)
                eng.transpose(pT[:, :, :].rearrange("p h q -> p (h q)"), sc[:, :, :].rearrange("p h k -> p (h k)")).then_inc(s["pT"], 1)

            def add(t):
                eng.wait_ge(s["output"], t + 1)
                xt = pl.x[:, t, :]
                eng.tensor_tensor(xt, ps[:, 6, 0:D], xt, ALU.add).then_inc(s["added"], 1)
                eng.wait_ge(s["added"], t + 1)
                token_stats(pl, eng, t)

            def first():
                norm(0)
                rotate(0)
                take_turned(0)

            def step(t, p, more):
                if more:
                    norm(t + 1)
                softmax(t)
                if more:
                    rotate(t + 1)
                add(t)
                if more:
                    take_turned(t + 1)
            each_tile(eng, first, step)
            pl.stats_n += 3 * NT

        @block.scalar
        def _(eng):
            eng.preload_act_table(ACT.Exp)

            def take_xT(t):
                eng.wait_ge(s["xturned"], t + 1)
                eng.wait_ge(s["projected"], t * NW)
                eng.activation(xT[:, :, :], ps[:, 6, 0:KC * P].rearrange("p (k n) -> p k n", k=KC), ACT.Copy).then_inc(s["xT"], 1)

            def take_qkv(t, p, lo, hi):
                for k in range(lo, hi):
                    eng.wait_ge(s["projected"], t * NW + k + 1)
                    eng.wait_ge(s["cos"], t)
                    eng.wait_ge(s["sin"], 2 * t)
                    bank = ps[:, 6 + (1 + k) % 2, :]
                    if k < NW - 1:
                        eng.activation(qk[:, 8 * k:8 * k + 8, :, :].rearrange("p h a e -> p (h a e)"), bank, ACT.Copy).then_inc(s["qkv"], 1)
                    else:
                        eng.activation(qk[:, HQ:, :, :].rearrange("p h a e -> p (h a e)"), bank[:, 0:NKV], ACT.Copy).then_inc(s["qkv"], 1)
                        eng.activation(v[p][:, :], bank[:, NKV:2 * NKV], ACT.Copy).then_inc(s["qkv"], 1)

            def take_turned(t):
                for k in (0, 2, 4):
                    eng.wait_ge(s["turned"], t * 5 + k + 1)
                    eng.wait_ge(s["scored"], t)
                    dst = qT[:, 4 * k:4 * k + 4, :] if k < 4 else kT[:, :, :]
                    eng.activation(dst, ps[:, 6 + (7 + k) % 2, :].rearrange("p (c n) -> p c n", c=4), ACT.Copy).then_inc(s["turned_scalar"], 1)

            def first():
                take_xT(0)
                take_qkv(0, 0, 0, NW)
                take_turned(0)

            def step(t, p, more):
                if more:
                    take_xT(t + 1)
                    take_qkv(t + 1, 1 - p, 0, 2)
                eng.wait_ge(s["soft"], t * 6 + 3)
                eng.activation(sc[:, :, :], sc[:, :, :], ACT.Exp, scale=SC).then_inc(s["exp"], 1)
                if more:
                    take_qkv(t + 1, 1 - p, 2, NW)
                for b in range(NB):
                    eng.wait_ge(s["valued"], t * 4 + b + 1)
                    eng.wait_ge(s["output"], t)
                    eng.activation(oT[:, :, b * S:(b + 1) * S], ps[:, 2 + b, :].rearrange("p (c q) -> p c q", q=S),
                                   ACT.Copy).then_inc(s["oT"], 1)
                if more:
                    take_turned(t + 1)
            each_tile(eng, first, step)

        @block.tensor
        def _(eng):
            def project(t):
                eng.wait_ge(s["xn"], t + 1)
                eng.wait_ge(s["turned_vector"], 2 * t)
                for k in range(KC):
                    mm = eng.transpose(ps[:, 6, k * P:(k + 1) * P], xn[:, k * P:(k + 1) * P], pl.ident[:, :])
                mm.then_inc(s["xturned"], 1)
                eng.wait_ge(s["xT"], t + 1)
                eng.wait_ge(s["turned_scalar"], 3 * t)
                for n in range(NW):
                    if n >= 2:
                        eng.wait_ge(s["qkv"], t * 6 + n - 1)
                    for k in range(KC):
                        mm = eng.matmul(ps[:, 6 + (1 + n) % 2, :], xT[:, k, :], w[:, k, n * 512:(n + 1) * 512], start=(k == 0), stop=(k == KC - 1))
                    mm.then_inc(s["projected"], 1)

            def turn(t):
                eng.wait_ge(s["rotated"], t * 3 + 3)
                for n in range(5):
                    if n == 0:
                        eng.wait_ge(s["qkv"], t * 6 + 6)
                    elif n == 1:
                        eng.wait_ge(s["added"], t)
                    elif n % 2 == 0:
                        eng.wait_ge(s["turned_scalar"], t * 3 + n // 2)
                    else:
                        eng.wait_ge(s["turned_vector"], t * 2 + 1)
                    for j in range(4):
                        src = rot[:, 8 * n + 2 * j:8 * n + 2 * j + 2, :, :].rearrange("p h a e -> p (h a e)") if n < 4 else \
                            kd[:, j, :, :].rearrange("p a e -> p (a e)")
                        mm = eng.transpose(ps[:, 6 + (7 + n) % 2, j * P:(j + 1) * P], src, pl.ident[:, :])
                    mm.then_inc(s["turned"], 1)

            def first():
                eng.wait_ge(s["w_in"], 16)
                project(0)
                turn(0)
                eng.wait_ge(s["wo_in"], 16)

            def step(t, p, more):
                eng.wait_ge(s["turned_scalar"], 3 * t + 3)
                eng.wait_ge(s["turned_vector"], 2 * t + 2)
                eng.wait_ge(s["soft"], 6 * t)
                apart(pl, eng)
                for h in range(HQ):
                    a = (h % 2) * E
                    for b in range(NB):
                        mm = eng.matmul(ps[b * S:(b + 1) * S, h % 2, (h // 2) * S:(h // 2 + 1) * S],
                                        qT[a:a + E, h // 2, b * S:(b + 1) * S], kT[a:a + E, h // 8, b * S:(b + 1) * S],
                                        start=True, stop=True)
                mm.then_inc(s["scored"], 1)
                if more:
                    project(t + 1)
                eng.wait_ge(s["pT"], t + 1)
                eng.wait_ge(s["oT"], 4 * t)
                for b in range(NB):
                    for k in range(HKV):
                        for a in range(2):
                            mm = eng.matmul(ps[a * E:(a + 1) * E, 2 + b, k * P:(k + 1) * P], v[p][b * S:(b + 1) * S, k * E:(k + 1) * E],
                                            pT[b * S:(b + 1) * S, NQ // P * a + 4 * k:NQ // P * a + 4 * k + 4, :], start=True, stop=True)
                    mm.then_inc(s["valued"], 1)
                eng.wait_ge(s["oT"], 4 * t + 4)
                if more:
                    eng.wait_ge(s["qkv"], t * 6 + 6 + 4)
                for c in range(NQ // P):
                    mm = eng.matmul(ps[:, 6, 0:D], oT[:, c, :], wo[:, c, :], start=(c == 0), stop=(c == NQ // P - 1))
                mm.then_inc(s["output"], 1)
                if more:
                    turn(t + 1)
            each_tile(eng, first, step)


def experts(pl):
    nc, ps = pl.nc, pl.ps
    NE, F, TOPK, EB = 32, 96, 4, 4
    W = EB * F
    NS = NE // EB
    CB = W // P
    wg = pl.at("ex_wg", [P, KC, NE * F], F32, L_OFF)
    wu = pl.at("ex_wu", [P, KC, NE * F], F32, pl.end)
    wd = pl.at("ex_wd", [P, NE * F // P, D], F32, pl.end)
    gate = pl.at("ex_gate", [P, KC, NE], F32, pl.end)
    xn = pl.at("ex_xn", [P, D], F32, pl.end)
    xT = [pl.at(f"ex_xT{j}", [P, KC, P], F32, pl.end) for j in range(2)]
    sg = [pl.at(f"ex_sg{j}", [P, W], F32, pl.end) for j in range(2)]
    h = [pl.at(f"ex_h{j}", [P, W], F32, pl.end) for j in range(2)]
    hT = [pl.at(f"ex_hT{j}", [P, CB, P], F32, pl.end) for j in range(2)]
    route = pl.at("ex_route", [P, NT, NE], F32, pl.end)
    e, gt, eq, cum, le, one = (pl.at(f"ex_{k}", [P, NE], F32, pl.end) for k in ("e", "gt", "eq", "cum", "le", "one"))
    m8 = pl.at("ex_m8", [P, 8], F32, pl.end)
    nm, cnt, tot, inv = (pl.at(f"ex_{k}", [P, 1], F32, pl.end) for k in ("nm", "cnt", "tot", "inv"))
    s = {k: pl.sem(f"ex_{k}") for k in (
        "w_in", "wd_in", "rs_in", "rstd", "xn", "xturned", "xT", "logits", "routed", "exp", "one", "gates", "ups", "silu",
        "gated", "turned", "hT", "summed", "added")}
    LC = (KC * 688, KC * 688, 6 * D)
    idx = pl.at("lu_idx", [P, sum(LC)], I32, pl.end)
    acc = pl.at("lu_acc", [P, sum(LC)], F32, pl.end)
    hit = pl.at("lu_hit", [P, max(LC)], F32, pl.end)
    lut = pl.at("lu_lut", [P, NT], F32, pl.end)
    kv = pl.at("lu_entry", [P, NT], F32, pl.end)
    pl.lut_dram = nc.dram_tensor("lut_scratch", (P, sum(LC)), F32, kind="Internal").ap()
    l_in, l_step, l_stored = pl.sem("lu_in"), pl.sem("lu_step"), pl.sem("lu_stored")
    NR = 11

    def each_tile(eng, first, step):
        first()
        with eng.Fori(0, NT // 2 - 1) as u:
            for p in range(2):
                step(u * 2 + p, p, True)
        for p in range(2):
            step(NT - 2 + p, p, p == 0)

    with nc.Block() as block:
        @block.sync
        def _(eng):
            eng.dma_start(gate[:, :, :], pl.ap["L0_gate"]).then_inc(s["w_in"], 16)
            eng.dma_start(wg[:, :, :], pl.ap["L0_wg"]).then_inc(s["w_in"], 16)
            eng.dma_start(wu[:, :, :], pl.ap["L0_wu"]).then_inc(s["w_in"], 16)
            eng.dma_start(wd[:, :, :], pl.ap["L0_wd"]).then_inc(s["wd_in"], 16)
            eng.dma_start(idx[:, :], pl.ap["L1_idx"]).then_inc(l_in, 16)
            eng.dma_start(lut[:, :], pl.ap["L1_lut"].to_broadcast([P, NT])).then_inc(l_in, 16)
            eng.dma_start(kv[:, :], pl.ap["entries"]).then_inc(l_in, 16)
            eng.wait_ge(l_step, 1 + 2 * len(LC) * NT)
            eng.dma_start(pl.lut_dram, acc[:, :]).then_inc(l_stored, 16)
            eng.wait_ge(l_stored, 16)

        @block.gpsimd
        def _(eng):
            pow_of_all(pl, eng, s)

        @block.vector
        def _(eng):
            eng.memset(one[:, :], 1.0).then_inc(s["one"], 1)
            rstd_of_all(pl, eng, s)

            def norm(t):
                eng.wait_ge(s["xturned"], t)
                eng.tensor_scalar(xn[:, :], pl.x[:, t, :], pl.mv[:, t, 0:1], pl.rstd[:, bass.ds(t, 1)],
                                  ALU.subtract, ALU.mult).then_inc(s["xn"], 1)

            def routing(t):
                n = t * NR
                r = s["routed"]
                lg = ps[:, 7, KC * P:KC * P + NE]
                eng.wait_ge(s["logits"], t + 1)
                eng.tensor_reduce(nm[:, :], lg, AX.X, ALU.max, negate=True).then_inc(r, 1)
                eng.wait_ge(s["exp"], t + 1)
                apart(pl, eng)
                eng.max(m8[:, :], e[:, :]).then_inc(r, 1)
                eng.wait_ge(r, n + 2)
                kth = m8[:, TOPK - 1:TOPK]
                eng.tensor_scalar(gt[:, :], e[:, :], kth, None, ALU.is_gt).then_inc(r, 1)
                eng.tensor_scalar(eq[:, :], e[:, :], kth, None, ALU.is_equal).then_inc(r, 1)
                eng.wait_ge(r, n + 4)
                eng.tensor_reduce(cnt[:, :], gt[:, :], AX.X, ALU.add).then_inc(r, 1)
                eng.tensor_tensor_scan(cum[:, :], one[:, :], eq[:, :], 0.0, ALU.mult, ALU.add).then_inc(r, 1)
                eng.wait_ge(r, n + 6)
                eng.tensor_scalar(le[:, :], cum[:, :], cnt[:, 0:1], float(TOPK), ALU.add, ALU.is_le).then_inc(r, 1)
                eng.wait_ge(r, n + 7)
                eng.tensor_tensor(le[:, :], le[:, :], eq[:, :], ALU.mult).then_inc(r, 1)
                eng.wait_ge(r, n + 8)
                eng.tensor_tensor(le[:, :], le[:, :], gt[:, :], ALU.add).then_inc(r, 1)
                eng.wait_ge(r, n + 9)
                eng.tensor_tensor_reduce(out=le[:, :], in0=le[:, :], in1=e[:, :], scale=1.0, scalar=0.0,
                                         op0=ALU.mult, op1=ALU.add, accum_out=tot[:, :]).then_inc(r, 1)
                eng.wait_ge(r, n + 10)
                eng.reciprocal(inv[:, :], tot[:, :]).then_inc(r, 1)
                eng.wait_ge(r, n + 11)
                eng.tensor_scalar(route[:, t, :], le[:, :], inv[:, 0:1], None, ALU.mult).then_inc(s["one"], 1)

            def look_up(t, c):
                a, b = sum(LC[:c]), sum(LC[:c + 1])
                n = 1 + (t * len(LC) + c) * 2
                eng.wait_ge(l_step, n)
                eng.tensor_scalar(hit[:, 0:b - a], idx[:, a:b], kv[:, bass.ds(t, 1)], lut[:, bass.ds(t, 1)], ALU.is_equal, ALU.mult).then_inc(l_step, 1)
                eng.wait_ge(l_step, n + 1)
                eng.tensor_tensor(acc[:, a:b], acc[:, a:b], hit[:, 0:b - a], ALU.add).then_inc(l_step, 1)

            def first():
                norm(0)
                routing(0)
                eng.memset(acc[:, :], 0.0).then_inc(l_step, 1)
                eng.wait_ge(l_in, 48)

            def step(t, p, more):
                for j in range(NS):
                    k = t * NS + j
                    if j == 0:
                        eng.wait_ge(s["one"], t + 2)
                    eng.wait_ge(s["silu"], k + 1)
                    eng.wait_ge(s["ups"], k + 1)
                    for i in range(EB):
                        ex = j * EB + i
                        st = eng.scalar_tensor_tensor(out=h[j % 2][:, i * F:(i + 1) * F], in0=ps[:, 2 + j % 2, i * F:(i + 1) * F],
                                                      scalar=route[:, t, ex:ex + 1], in1=sg[j % 2][:, i * F:(i + 1) * F],
                                                      op0=ALU.mult, op1=ALU.mult)
                    st.then_inc(s["gated"], 1)
                    if more and j == 0:
                        norm(t + 1)
                    if more and j == 4:
                        routing(t + 1)
                    if j in (2, 5, 7):
                        look_up(t, (2, 5, 7).index(j))
                eng.wait_ge(s["summed"], t + 1)
                eng.tensor_tensor(pl.x[:, t, :], ps[:, 6, 0:D], pl.x[:, t, :], ALU.add).then_inc(s["added"], 1)
                eng.wait_ge(s["added"], t + 1)
                token_stats(pl, eng, t)
            each_tile(eng, first, step)
            pl.stats_n += 3 * NT

        @block.scalar
        def _(eng):
            def take_xT(t, p):
                eng.wait_ge(s["xturned"], t + 1)
                eng.activation(xT[p][:, :, :], ps[:, 7, 0:KC * P].rearrange("p (k n) -> p k n", k=KC), ACT.Copy).then_inc(s["xT"], 1)

            def exp_logits(t):
                eng.wait_ge(s["routed"], t * NR + 1)
                eng.activation(e[:, :], ps[:, 7, KC * P:KC * P + NE], ACT.Exp, bias=nm[:, 0:1]).then_inc(s["exp"], 1)

            def first():
                take_xT(0, 0)
                exp_logits(0)

            def step(t, p, more):
                for j in range(NS):
                    k = t * NS + j
                    eng.wait_ge(s["gates"], k + 1)
                    eng.activation(sg[j % 2][:, :], ps[:, j % 2, 0:W], ACT.Silu).then_inc(s["silu"], 1)
                    eng.wait_ge(s["turned"], k + 1)
                    eng.activation(hT[j % 2][:, :, :], ps[:, 4 + j % 2, 0:W].rearrange("p (c n) -> p c n", c=CB), ACT.Copy).then_inc(s["hT"], 1)
                    if more and j == 2:
                        take_xT(t + 1, 1 - p)
                    if more and j == 4:
                        exp_logits(t + 1)
            each_tile(eng, first, step)

        @block.tensor
        def _(eng):
            def turn_x(t):
                eng.wait_ge(s["xn"], t + 1)
                for k in range(KC):
                    mm = eng.transpose(ps[:, 7, k * P:(k + 1) * P], xn[:, k * P:(k + 1) * P], pl.ident[:, :])
                mm.then_inc(s["xturned"], 1)

            def logits(t, p):
                eng.wait_ge(s["xT"], t + 1)
                for k in range(KC):
                    mm = eng.matmul(ps[:, 7, KC * P:KC * P + NE], xT[p][:, k, :], gate[:, k, :], start=(k == 0), stop=(k == KC - 1))
                mm.then_inc(s["logits"], 1)

            def product(w, bank, p, j, sem):
                for k in range(KC):
                    mm = eng.matmul(ps[:, bank, 0:W], xT[p][:, k, :], w[:, k, j * W:(j + 1) * W], start=(k == 0), stop=(k == KC - 1))
                mm.then_inc(sem, 1)

            def first():
                turn_x(0)
                eng.wait_ge(s["w_in"], 48)
                logits(0, 0)
                product(wg, 0, 0, 0, s["gates"])
                product(wu, 2, 0, 0, s["ups"])
                eng.wait_ge(s["wd_in"], 16)

            def step(t, p, more):
                for j in range(NS):
                    k = t * NS + j
                    nxt = j + 1 < NS or more
                    np_, nj = (p, j + 1) if j + 1 < NS else (1 - p, 0)
                    if nxt:
                        eng.wait_ge(s["gated"], k)
                        product(wg, nj % 2, np_, nj, s["gates"])
                    eng.wait_ge(s["gated"], k + 1)
                    for c in range(CB):
                        mm = eng.transpose(ps[:, 4 + j % 2, c * P:(c + 1) * P], h[j % 2][:, c * P:(c + 1) * P], pl.ident[:, :])
                    mm.then_inc(s["turned"], 1)
                    if nxt:
                        product(wu, 2 + nj % 2, np_, nj, s["ups"])
                    if j == 0:
                        eng.wait_ge(s["added"], t)
                    eng.wait_ge(s["hT"], k + 1)
                    for c in range(CB):
                        n = j * CB + c
                        mm = eng.matmul(ps[:, 6, 0:D], hT[j % 2][:, c, :], wd[:, n, :], start=(n == 0), stop=(n == NS * CB - 1))
                    if j == NS - 1:
                        mm.then_inc(s["summed"], 1)
                    if more and j == 2:
                        turn_x(t + 1)
                    if more and j == 4:
                        logits(t + 1, 1 - p)
            each_tile(eng, first, step)


def inverse_root(pl, eng, x, y, t, sem, n, root):
    eng.wait_ge(root, 1)
    eng.reciprocal(y, y).then_inc(sem, 1)
    eng.wait_ge(sem, n + 1)
    eng.tensor_tensor(t, y, y, ALU.mult).then_inc(sem, 1)
    eng.wait_ge(sem, n + 2)
    eng.tensor_tensor(t, t, x, ALU.mult).then_inc(sem, 1)
    eng.wait_ge(sem, n + 3)
    eng.tensor_scalar(t, t, -0.5, 1.5, ALU.mult, ALU.add).then_inc(sem, 1)
    eng.wait_ge(sem, n + 4)
    eng.tensor_tensor(y, y, t, ALU.mult).then_inc(sem, 1)
    eng.wait_ge(sem, n + 5)


def key_norms(pl):
    nc, ps = pl.nc, pl.ps
    R = B * CS
    NC = -(-R // P)
    LAST = R - (NC - 1) * P
    G = 4
    pl.rq = pl.at("rq", [P, B, GQ], F32, L_OFF)
    pl.pick = pl.at("pick", [3 * NH, GQ, P], BF16, pl.end)
    pl.low1_off = pl.end
    pl.WkTg = pl.at("WkTg", [P, NH, CD], F32, pl.end)
    pl.tmp1_off = pl.end
    pickf = pl.at("kn_pickf", [3 * NH, GQ, P], F32, QO_OFF)
    wk = pl.at("kn_wk", [P, NH * HD], F32, pl.end)
    wv = pl.at("kn_wv", [P, NH, CD], F32, pl.end)
    wo = pl.at("kn_wo", [P, NH, D], F32, pl.end)
    bw = pl.at("kn_bw", [P, NH, D], F32, pl.end)
    g2 = pl.at("kn_g", [P, 2], F32, pl.end)
    gg = pl.at("kn_gg", [P, 1], F32, pl.end)
    ct = [pl.at(f"kn_ctx{j}", [P, G * P], F32, pl.end) for j in range(2)]
    sq = [pl.at(f"kn_sq{j}", [P, 512], F32, pl.end) for j in range(2)]
    ss = pl.at("kn_ss", [P, NC, NH], F32, pl.end)
    rs, nt = (pl.at(f"kn_{k}", [P, NC, NH], F32, pl.end) for k in ("rs", "newton"))
    parts = pl.at("kn_parts", [P, NC, 3, NH], BF16, pl.end)
    rkT = pl.at("kn_rkT", [3 * NH, NC * P], BF16, pl.end)
    pl.rk_dram = nc.dram_tensor("rk_scratch", (3 * NH, R), BF16, kind="Internal").ap()
    s = {k: pl.sem(f"kn_{k}") for k in (
        "w_in", "k", "sq", "ss", "made", "made_v", "made_s", "fin", "root", "newton", "turned", "rk_s", "rk_v", "stored", "mh", "gain")}
    c_in = [pl.sem(f"kn_ctx_loaded{j}") for j in range(2)]
    pl.bw1_dram = nc.dram_tensor("bw1_scratch", (P, NH, D), F32, kind="Internal").ap()
    NG = (NC - 1) // G
    NB2 = NH // 2
    assert (NC - 1) % G == 0 and NG % 2 == 0

    with nc.Block() as block:
        @block.sync
        def _(eng):
            eng.dma_start(wk[:, :], pl.ap["L1_Wk"]).then_inc(s["w_in"], 16)

            def load(u, p):
                if not isinstance(u, int):
                    eng.wait_ge(s["k"], u * 8 * G + p * 4 * G - 4 * G)
                eng.dma_start(ct[p][:, :], pl.ap["ctxT"][:, bass.ds((u * 2 + p) * G * P, G * P)]).then_inc(c_in[p], 16)
            load(0, 0)
            load(0, 1)
            for d, n in ((wv, "L1_WvT"), (wo, "L1_Wo"), (pl.WkTg, "L1_WkT"), (pickf, "pick")):
                eng.dma_start(d[:, :, :], pl.ap[n]).then_inc(s["w_in"], 16)
            eng.dma_start(g2[:, :], pl.ap["L1_g"]).then_inc(s["w_in"], 16)
            with eng.Fori(1, NG // 2) as u:
                for p in range(2):
                    load(u, p)
            eng.wait_ge(s["k"], 4 * G * (NG - 1))
            eng.dma_start(ct[0][:, 0:LAST], pl.ap["ctxT"][:, NG * G * P:R]).then_inc(c_in[0], 16)
            eng.wait_ge(s["made_s"], NB2 // 2)
            eng.wait_ge(s["made_v"], NB2 // 2)
            eng.dma_start(pl.bw1_dram, bw[:, :, :]).then_inc(s["stored"], 16)
            eng.wait_ge(s["rk_s"], (NC - 1) // 8)
            eng.wait_ge(s["rk_v"], (NC - 1) // 8 + 1)
            eng.dma_start(pl.rk_dram, rkT[:, 0:R]).then_inc(s["stored"], 16)
            eng.wait_ge(s["stored"], 32)

        @block.gpsimd
        def _(eng):
            eng.memset(ss[:, NC - 1, :], 1.0).then_inc(s["mh"], 1)

        @block.scalar
        def _(eng):
            eng.preload_act_table(ACT.Square)

            def squares(c, m):
                for n in range(4):
                    k = c * 4 + n
                    eng.wait_ge(s["k"], k + 1)
                    if not (isinstance(c, int) and c == 0 and n < 2):
                        eng.wait_ge(s["ss"], k - 1)
                    eng.activation(sq[n % 2][0:m, :], ps[0:m, n, :], ACT.Square).then_inc(s["sq"], 1)
            squares(0, P)
            with eng.Fori(1, NC - 1) as c:
                squares(c, P)
            squares(NC - 1, LAST)
            eng.wait_ge(s["fin"], 1)
            eng.activation(rs[:, :, :], ss[:, :, :], ACT.Sqrt).then_inc(s["root"], 1)
            for k in range(1, NB2, 2):
                eng.wait_ge(s["made"], k + 1)
                eng.activation(bw[:, 2 * k:2 * k + 2, :], ps[:, 4 + k % 4, :].rearrange("p (h c) -> p h c", h=2), ACT.Copy).then_inc(s["made_s"], 1)
            for k in range(0, (NC - 1) // 8, 1):
                eng.wait_ge(s["turned"], 2 * k + 1)
                eng.activation(rkT[:, 8 * k * P:(8 * k + 4) * P], ps[0:3 * NH, 0, 0:256].bitcast(BF16), ACT.Copy).then_inc(s["rk_s"], 1)

        @block.vector
        def _(eng):
            eng.wait_ge(s["w_in"], 96)
            eng.tensor_copy(pl.pick[:, :, :], pickf[:, :, :]).then_inc(s["gain"], 1)
            eng.tensor_tensor(gg[:, :], g2[:, 0:1], g2[:, 1:2], ALU.mult).then_inc(s["gain"], 1)
            eng.wait_ge(s["gain"], 2)
            eng.tensor_scalar(pl.WkTg[:, :, :], pl.WkTg[:, :, :], gg[:, 0:1], None, ALU.mult).then_inc(s["gain"], 1)

            def sums(c, m):
                for n in range(4):
                    eng.wait_ge(s["sq"], c * 4 + n + 1)
                    eng.tensor_reduce(ss[0:m, c, 4 * n:4 * n + 4], sq[n % 2][0:m, :].rearrange("p (h d) -> p h d", h=4), AX.X, ALU.add).then_inc(s["ss"], 1)
            with eng.Fori(0, NC - 1) as c:
                sums(c, P)
            eng.wait_ge(s["mh"], 1)
            sums(NC - 1, LAST)
            eng.wait_ge(s["ss"], 4 * NC)
            eng.tensor_scalar(ss[:, :, :], ss[:, :, :], 1.0 / HD, EPS, ALU.mult, ALU.add).then_inc(s["fin"], 1)
            for k in range(0, NB2, 2):
                eng.wait_ge(s["made"], k + 1)
                eng.tensor_copy(bw[:, 2 * k:2 * k + 2, :], ps[:, 4 + k % 4, :].rearrange("p (h c) -> p h c", h=2)).then_inc(s["made_v"], 1)
            inverse_root(pl, eng, ss[:, :, :], rs[:, :, :], nt[:, :, :], s["newton"], 0, s["root"])
            for j in range(3):
                eng.tensor_copy(parts[:, :, j, :], rs[:, :, :]).then_inc(s["fin"], 1)
                if j < 2:
                    eng.wait_ge(s["fin"], 2 * j + 2)
                    eng.tensor_tensor(rs[:, :, :], rs[:, :, :], parts[:, :, j, :], ALU.subtract).then_inc(s["fin"], 1)
                    eng.wait_ge(s["fin"], 2 * j + 3)
            for k in range((NC - 1) // 8):
                eng.wait_ge(s["turned"], 2 * k + 2)
                eng.tensor_copy(rkT[:, (8 * k + 4) * P:(8 * k + 8) * P], ps[0:3 * NH, 1, 0:256].bitcast(BF16)).then_inc(s["rk_v"], 1)
            eng.wait_ge(s["turned"], 2 * ((NC - 1) // 8) + 1)
            eng.tensor_copy(rkT[:, (NC - 1) * P:R], ps[0:3 * NH, 2, 0:LAST // 2].bitcast(BF16)).then_inc(s["rk_v"], 1)

        @block.tensor
        def _(eng):
            def keys(c, p, j, m):
                for n in range(4):
                    if not (isinstance(c, int) and c == 0):
                        eng.wait_ge(s["sq"], c * 4 + n - 3)
                    eng.matmul(ps[0:m, n, :], ct[p][:, j * P:j * P + m], wk[:, n * 512:(n + 1) * 512], start=True, stop=True).then_inc(s["k"], 1)

            eng.wait_ge(s["w_in"], 16)
            for p in range(2):
                eng.wait_ge(c_in[p], 16)
                for j in range(G):
                    keys(p * G + j, p, j, P)
            with eng.Fori(1, NG // 2) as u:
                for p in range(2):
                    eng.wait_ge(c_in[p], u * 16 + 16)
                    for j in range(G):
                        keys(u * 2 * G + p * G + j, p, j, P)
            eng.wait_ge(c_in[0], (NG // 2 + 1) * 16)
            keys(NC - 1, 0, 0, LAST)
            eng.wait_ge(s["w_in"], 96)
            for k in range(NB2):
                if k >= 4:
                    eng.wait_ge((s["made_v"], s["made_s"])[k % 2], (k - 4) // 2 + 1)
                for j in range(2):
                    h = 2 * k + j
                    mm = eng.matmul(ps[:, 4 + k % 4, j * D:(j + 1) * D], wv[:, h, :], wo[:, h, :], start=True, stop=True)
                mm.then_inc(s["made"], 1)
            eng.wait_ge(s["fin"], 6)
            eng.wait_ge(s["sq"], 4 * NC)
            for k in range(2 * ((NC - 1) // 8)):
                if k >= 2:
                    eng.wait_ge((s["rk_s"], s["rk_v"])[k % 2], k // 2)
                for j in range(4):
                    mm = eng.transpose(ps[0:3 * NH, k % 2, j * P // 2:(j + 1) * P // 2].bitcast(BF16),
                                       parts[:, 4 * k + j, :, :].rearrange("p a h -> p (a h)"), pl.identb[:, :])
                mm.then_inc(s["turned"], 1)
            eng.transpose(ps[0:3 * NH, 2, 0:LAST // 2].bitcast(BF16), parts[0:LAST, NC - 1, :, :].rearrange("p a h -> p (a h)"),
                          pl.identb[0:LAST, 0:LAST]).then_inc(s["turned"], 1)


def l1x_queries(pl):
    nc, ps = pl.nc, pl.ps
    QO = pl.QO = pl.at("QO1", [P, NH, TOK], F32, QO_OFF)
    xT = pl.at("l1q_xT", [P, KC, ST], F32, pl.tmp1_off)
    xn = pl.at("l1q_xn", [P, 4, D], F32, pl.end)
    wq = pl.at("l1q_wq", [P, KC, NH * HD], F32, pl.end)
    qT = [pl.at(f"l1q_qT{j}", [P, ST], F32, pl.end) for j in range(2)]
    sq = pl.at("l1q_sq", [P, 4, ST], F32, pl.end)
    ones = pl.at("l1q_ones", [P, S], F32, pl.end)
    qs, nt = (pl.at(f"l1q_{k}", [P, B, GQ], F32, pl.end) for k in ("qs", "newton"))
    assert pl.end <= QO_OFF, pl.end - QO_OFF
    s = layer_norm_steps(pl, "l1q")
    for k in ("w_in", "ones", "q", "sq", "qT", "made", "out", "sums", "diag", "fin", "root", "newton"):
        s[k] = pl.sem(f"l1q_{k}")
    NBS = ST // S

    def supertiles(eng, step):
        step(0, True)
        with eng.Fori(1, SUP - 1) as i:
            step(i, True)
        step(SUP - 1, False)

    def first(i, h, lim):
        return isinstance(i, int) and i * NH + h < lim

    with nc.Block() as block:
        @block.sync
        def _(eng):
            eng.dma_start(wq[:, :, :], pl.ap["L1_WqT"]).then_inc(s["w_in"], 16)

        @block.gpsimd
        def _(eng):
            pow_of_all(pl, eng, s)
            eng.memset(ones[:, :], 1.0).then_inc(s["ones"], 1)

        @block.vector
        def _(eng):
            rstd_of_all(pl, eng, s)

            def norm(i):
                eng.wait_ge(s["turned"], i * 2)
                for j in range(4):
                    eng.tensor_scalar(xn[:, j, :], pl.x[:, i * 4 + j, :], pl.mv[:, i * 4 + j, 0:1], pl.rstd[:, bass.ds(i * 4 + j, 1)],
                                      ALU.subtract, ALU.mult).then_inc(s["xn"], 1)

            def take_xT(i):
                eng.wait_ge(s["q"], i * NH)
                for m in range(2):
                    eng.wait_ge(s["turned"], i * 2 + m + 1)
                    eng.tensor_copy(xT[:, :, m * 256:(m + 1) * 256], ps[:, 6 + m, :].rearrange("p (k n) -> p k n", k=KC)).then_inc(s["xT"], 1)

            def step(i, more):
                for h in range(NH):
                    k = i * NH + h
                    eng.wait_ge(s["q"], k + 1)
                    if not first(i, h, 2):
                        eng.wait_ge(s["made"], k - 1)
                        eng.wait_ge(s["sq"], k - 1)
                    eng.tensor_copy(qT[h % 2][:, :], ps[:, h % 2, :]).then_inc(s["qT"], 1)
                    if more and h == 5:
                        norm(i + 1)
                    if h % 4 == 3:
                        m = i * 4 + h // 4
                        eng.wait_ge(s["sums"], m + 1)
                        v = ps[:, 4, :].rearrange("p (b s) -> p b s", s=S)
                        eng.tensor_tensor(v, v, pl.cst["diag"][:, None, :].to_broadcast([P, NBS, S]), ALU.mult).then_inc(s["diag"], 1)
                        eng.wait_ge(s["diag"], m * 2 + 1)
                        apart(pl, eng)
                        eng.tensor_reduce(qs[:, bass.ds(i * NBS, NBS), h // 4], v, AX.X, ALU.add).then_inc(s["diag"], 1)
                if more:
                    take_xT(i + 1)

            norm(0)
            take_xT(0)
            supertiles(eng, step)
            eng.wait_ge(s["diag"], 2 * 4 * SUP)
            eng.tensor_scalar(qs[:, :, :], qs[:, :, :], 1.0 / HD, EPS, ALU.mult, ALU.add).then_inc(s["fin"], 1)
            inverse_root(pl, eng, qs[:, :, :], pl.rq[:, :, :], nt[:, :, :], s["newton"], 0, s["root"])
            eng.tensor_scalar(pl.rq[:, :, :], pl.rq[:, :, :], float(HD) ** -0.5, None, ALU.mult).then_inc(s["fin"], 1)

        @block.scalar
        def _(eng):
            eng.preload_act_table(ACT.Square)

            def out(i, h):
                eng.wait_ge(s["made"], i * NH + h + 1)
                eng.activation(QO[:, h, bass.ds(i * ST, ST)], ps[:, 2 + h % 2, :], ACT.Copy).then_inc(s["out"], 1)

            def step(i, more):
                for h in range(NH):
                    eng.wait_ge(s["qT"], i * NH + h + 1)
                    if not first(i, h, 4):
                        eng.wait_ge(s["sums"], i * 4 + h // 4)
                    eng.activation(sq[:, h % 4, :], qT[h % 2][:, :], ACT.Square).then_inc(s["sq"], 1)
                    if h >= 1:
                        out(i, h - 1)
                out(i, NH - 1)
            supertiles(eng, step)
            eng.wait_ge(s["fin"], 1)
            eng.activation(pl.rq[:, :, :], qs[:, :, :], ACT.Sqrt).then_inc(s["root"], 1)

        @block.tensor
        def _(eng):
            def through_wk(i, h):
                k = i * NH + h
                eng.wait_ge(s["qT"], k + 1)
                if not first(i, h, 2):
                    eng.wait_ge(s["out"], k - 1)
                eng.matmul(ps[:, 2 + h % 2, :], pl.WkTg[:, h, :], qT[h % 2][:, :], start=True, stop=True).then_inc(s["made"], 1)

            def step(i, more):
                eng.wait_ge(s["xT"], i * 2 + 2)
                for h in range(NH):
                    k = i * NH + h
                    if not first(i, h, 2):
                        eng.wait_ge(s["qT"], k - 1)
                    for c in range(KC):
                        mm = eng.matmul(ps[:, h % 2, :], wq[:, c, h * HD:(h + 1) * HD], xT[:, c, :], start=(c == 0), stop=(c == KC - 1))
                    mm.then_inc(s["q"], 1)
                    if more and h == 8:
                        turn_supertile(pl, eng, s, xn, i + 1)
                    if h >= 1:
                        through_wk(i, h - 1)
                    if h % 4 == 3:
                        m = i * 4 + h // 4
                        eng.wait_ge(s["sq"], k + 1)
                        eng.wait_ge(s["diag"], 2 * m)
                        apart(pl, eng)
                        for j in range(4):
                            mm = eng.matmul(ps[j * S:(j + 1) * S, 4, :], ones[:, :], sq[:, j, :], start=True, stop=True)
                        mm.then_inc(s["sums"], 1)
                through_wk(i, NH - 1)

            turn_supertile(pl, eng, s, xn, 0)
            eng.wait_ge(s["w_in"], 16)
            eng.wait_ge(s["ones"], 1)
            supertiles(eng, step)


MAGIC = 12582912.0


def staggered(eng, pieces):
    top = max(lag for lag, _ in pieces)

    def turn(n, slot):
        for lag, piece in pieces:
            t = n - lag
            if isinstance(t, int) and not 0 <= t < NT:
                continue
            piece(t, (slot - lag) % 2)
    lo = -(-(top + 2) // 2) * 2
    hi = NT // 2 * 2
    for n in range(lo):
        turn(n, n % 2)
    with eng.Fori(lo // 2, hi // 2) as u:
        for p in range(2):
            turn(u * 2 + p, p)
    for n in range(hi, NT + top):
        turn(n, n % 2)


def early(t):
    return isinstance(t, int) and t < 2


def quantise(eng, src, rounded, out, st, sem, n, ready):
    eng.tensor_reduce(st[:, 3:4], src, AX.X, ALU.max, apply_absolute_value=True).then_inc(sem, 1)
    eng.wait_ge(sem, n + 1)
    eng.tensor_scalar(st[:, 0:1], st[:, 3:4], 1e-5, None, ALU.max).then_inc(sem, 1)
    eng.wait_ge(sem, n + 2)
    eng.reciprocal(st[:, 1:2], st[:, 0:1]).then_inc(sem, 1)
    eng.wait_ge(sem, n + 3)
    eng.tensor_scalar(st[:, 2:3], st[:, 1:2], 127.0, None, ALU.mult).then_inc(sem, 1)
    eng.wait_ge(sem, n + 4)
    eng.tensor_scalar(rounded, src, st[:, 2:3], MAGIC, ALU.mult, ALU.add).then_inc(sem, 1)
    eng.wait_ge(sem, n + 5)
    eng.tensor_scalar(out, rounded, -MAGIC, None, ALU.add).then_inc(ready, 1)


NQS = 5


def block_attention(pl):
    nc, ps = pl.nc, pl.ps
    H, E, BT = 16, 16, 4
    pl.x1 = pl.at("x1", [P, NT, D], F32, L_OFF)
    pl.wd = pl.at("bl_wd", [P, 4, D], BF16, pl.end)
    pl.deq = pl.at("bl_deq", [P, 3], F32, pl.end)
    pl.ms = pl.at("bl_ms", [P, NT], F32, pl.end)
    pl.rs2 = pl.at("bl_rs2", [P, NT], F32, pl.end)
    pl.blk_low = pl.end
    sizes = {"qkv": KC * 3 * D, "o": KC * D, "down": 4 * D}
    wf = {k: pl.at(f"bl_{k}_f", [P, n], F32, pl.end) for k, n in sizes.items()}
    wqkv = pl.at("bl_wqkv", [P, KC, 3 * D], BF16, pl.end)
    wo = pl.at("bl_wo", [P, KC, D], BF16, pl.end)
    wn = pl.at("bl_wn", [P, D], F32, pl.end)
    sh = pl.at("bl_shift", [P, 3, P], F32, pl.end)
    bm = pl.at("bl_mask", [P, BT], F32, pl.end)
    cos = pl.at("bl_cos", [P, E], F32, pl.end)
    sin = pl.at("bl_sin", [P, E], F32, pl.end)
    ones = pl.at("bl_ones", [P, P], F32, pl.end)
    wsum = pl.at("bl_wsum", [P, 3], F32, pl.end)
    wmean = pl.at("bl_wmean", [P, 3], F32, pl.end)
    wscale = pl.at("bl_wscale", [P, 3], F32, pl.end)
    two = lambda name, shape, dt=F32: [pl.at(f"bl_{name}{j}", shape, dt, pl.end) for j in range(2)]
    h, hr, hq = two("h", [P, D]), two("hr", [P, D]), two("hq", [P, D], BF16)
    hqT = two("hqT", [P, KC, P], BF16)
    st, fac = two("st", [P, 4]), two("fac", [P, 1])
    R = two("R", [P, 3, H, 2, E // 2])
    rc, rsn = two("rc", [P, 2 * H, 2, E // 2]), two("rs", [P, 2 * H, 2, E // 2])
    prod = two("prod", [P, BT, H, E])
    sc, sx = two("sc", [P, BT, H]), two("sx", [P, BT, H])
    mx, sm_, inv = two("mx", [P, H]), two("sum", [P, H]), two("inv", [P, H])
    cx, cr, cq = two("cx", [P, D]), two("cr", [P, D]), two("cq", [P, D], BF16)
    cqT = two("cqT", [P, KC, P], BF16)
    st2, fac2 = two("st2", [P, 4]), two("fac2", [P, 1])
    s = {k: pl.sem(f"bl_{k}") for k in (
        "w_in", "wq", "wabs", "ones", "wsummed", "rs_in", "rstd", "pow2", "ln", "q1", "hq", "fac", "hturned", "hqT", "qkv",
        "R", "cos", "sin", "rot", "shifted", "att", "exp", "ctx", "q2", "cq", "cturned", "cqT", "proj", "x1", "ms", "wst", "sqs")}
    sqj = pl.at("bl_sqj", [P, D], F32, pl.end)
    ms1 = pl.at("bl_ms1", [P, 1], F32, pl.end)
    names = ("qkv", "o", "down")

    with nc.Block() as block:
        @block.sync
        def _(eng):
            for k in names:
                eng.dma_start(wf[k][:, :], pl.ap[f"L1_{k}T"]).then_inc(s["w_in"], 16)
            eng.dma_start(wn[:, :], pl.ap["L1_attn_norm"].to_broadcast([P, D])).then_inc(s["w_in"], 16)
            for d, n in ((sh, "shift"),):
                eng.dma_start(d[:, :, :], pl.ap[n]).then_inc(s["w_in"], 16)
            for d, n in ((bm, "bmask"), (cos, "cos16"), (sin, "sin16")):
                eng.dma_start(d[:, :], pl.ap[n]).then_inc(s["w_in"], 16)

        @block.gpsimd
        def _(eng):
            eng.memset(ones[:, :], 1.0).then_inc(s["ones"], 1)
            pow_of_all(pl, eng, s)
            eng.wait_ge(s["pow2"], 2)
            eng.tensor_tensor(pl.rs2[:, :], pl.rs2[:, :], pl.mhalf[:, :], ALU.pow).then_inc(s["pow2"], 1)

            def sine(t, p):
                eng.wait_ge(s["R"], 2 * t + 2)
                eng.wait_ge(s["w_in"], 128)
                if not early(t):
                    eng.wait_ge(s["rot"], t - 1)
                qk = R[p][:, 0:2].rearrange("p n h a e -> p (n h) a e")
                for a in range(2):
                    eng.tensor_tensor(rsn[p][:, :, a, :], qk[:, :, 1 - a, :],
                                      sin[:, None, a * 8:a * 8 + 8].to_broadcast([P, 2 * H, 8]), ALU.mult).then_inc(s["sin"], 1)
            staggered(eng, [(0, sine)])

        @block.vector
        def _(eng):
            eng.wait_ge(s["w_in"], 128)
            for j, k in enumerate(names):
                eng.tensor_reduce(wsum[:, j:j + 1], wf[k][:, :], AX.X, ALU.add, apply_absolute_value=True).then_inc(s["wabs"], 1)
            eng.wait_ge(s["wsummed"], 1)
            for j, k in enumerate(names):
                eng.tensor_scalar(wmean[:, j:j + 1], ps[:, 0, j:j + 1], 1.0 / (P * sizes[k]), 1e-5, ALU.mult, ALU.max).then_inc(s["wq"], 1)
            eng.wait_ge(s["wq"], 3)
            eng.reciprocal(wscale[:, :], wmean[:, :]).then_inc(s["wq"], 1)
            eng.tensor_scalar(pl.deq[:, :], wmean[:, :], 1.0 / 127.0, None, ALU.mult).then_inc(s["wq"], 1)
            eng.wait_ge(s["wq"], 5)
            for j, (k, d) in enumerate(zip(names, (wqkv, wo, pl.wd))):
                eng.tensor_scalar(wf[k][:, :], wf[k][:, :], wscale[:, j:j + 1], MAGIC, ALU.mult, ALU.add).then_inc(s["wq"], 1)
                eng.wait_ge(s["wq"], 6 + 3 * j)
                eng.tensor_scalar(wf[k][:, :], wf[k][:, :], -MAGIC, -1.0, ALU.add, ALU.max).then_inc(s["wq"], 1)
                eng.wait_ge(s["wq"], 7 + 3 * j)
                eng.tensor_scalar(d[:, :, :].rearrange("p a b -> p (a b)"), wf[k][:, :], 1.0, None, ALU.min).then_inc(s["wq"], 1)
            rstd_of_all(pl, eng, s)
            eng.tensor_tensor(pl.rs2[:, :], pl.rstd[:, :], pl.rstd[:, :], ALU.mult).then_inc(s["ms"], 1)
            eng.wait_ge(s["ms"], 1)
            eng.tensor_tensor(pl.rs2[:, :], pl.rs2[:, :], pl.mv[:, :, 1], ALU.mult).then_inc(s["pow2"], 1)
            eng.wait_ge(s["pow2"], 1)
            eng.tensor_scalar(pl.rs2[:, :], pl.rs2[:, :], EPS, None, ALU.add).then_inc(s["pow2"], 1)
            eng.wait_ge(s["pow2"], 3)

            def norm_quantise(t, p):
                eng.tensor_scalar(pl.x1[:, t, :], pl.x[:, t, :], pl.mv[:, t, 0:1], pl.rstd[:, bass.ds(t, 1)],
                                  ALU.subtract, ALU.mult).then_inc(s["ln"], 1)
                eng.wait_ge(s["ln"], 2 * t + 1)
                eng.scalar_tensor_tensor(out=h[p][:, :], in0=pl.x1[:, t, :], scalar=pl.rs2[:, bass.ds(t, 1)], in1=wn[:, :],
                                         op0=ALU.mult, op1=ALU.mult).then_inc(s["ln"], 1)
                eng.wait_ge(s["ln"], 2 * t + 2)
                if not early(t):
                    eng.wait_ge(s["hturned"], t - 1)
                    eng.wait_ge(s["R"], 2 * t - 2)
                quantise(eng, h[p][:, :], hr[p][:, :], hq[p][:, :], st[p], s["q1"], t * NQS, s["hq"])
                eng.tensor_tensor(fac[p][:, :], st[p][:, 0:1], pl.deq[:, 0:1], ALU.mult).then_inc(s["fac"], 1)

            def rotate(t, p):
                eng.wait_ge(s["R"], 2 * t + 2)
                qk = R[p][:, 0:2].rearrange("p n h a e -> p (n h) (a e)")
                f = lambda a: a[:, :, :, :].rearrange("p h a e -> p h (a e)")
                eng.tensor_tensor(f(rc[p]), qk, cos[:, None, :].to_broadcast([P, 2 * H, E]), ALU.mult).then_inc(s["cos"], 1)
                eng.wait_ge(s["cos"], t + 1)
                eng.wait_ge(s["sin"], 2 * t + 2)
                eng.tensor_tensor(qk, f(rc[p]), f(rsn[p]), ALU.add).then_inc(s["rot"], 1)

            def scores(t, p):
                a = s["att"]
                n = t * 8
                q = R[p][:, 0].rearrange("p h a e -> p h (a e)")
                eng.wait_ge(s["rot"], t + 1)
                for j in range(BT):
                    if j == 1:
                        eng.wait_ge(s["shifted"], t + 1)
                    k = R[p][:, 1].rearrange("p h a e -> p h (a e)") if j == 0 else ps[:, 3 + j, 0:D].rearrange("p (h e) -> p h e", h=H)
                    eng.tensor_tensor(prod[p][:, j, :, :], k, q, ALU.mult).then_inc(a, 1)
                eng.wait_ge(a, n + 4)
                eng.tensor_reduce(sc[p][:, :, :], prod[p][:, :, :, :], AX.X, ALU.add).then_inc(a, 1)
                eng.wait_ge(a, n + 5)
                eng.tensor_tensor(sc[p][:, :, :], sc[p][:, :, :], bm[:, :, None].to_broadcast([P, BT, H]), ALU.add).then_inc(a, 1)
                eng.wait_ge(a, n + 6)
                eng.tensor_reduce(mx[p][:, :], sc[p][:, :, :].rearrange("p j h -> p h j"), AX.X, ALU.max).then_inc(a, 1)
                eng.wait_ge(a, n + 7)
                if not early(t):
                    eng.wait_ge(s["ctx"], t - 1)
                eng.tensor_tensor(sx[p][:, :, :], sc[p][:, :, :], mx[p][:, None, :].to_broadcast([P, BT, H]), ALU.subtract).then_inc(a, 1)

            def weigh(t, p):
                base = s["wst"]
                m = t * 8
                eng.wait_ge(s["exp"], t + 1)
                eng.tensor_reduce(sm_[p][:, :], sx[p][:, :, :].rearrange("p j h -> p h j"), AX.X, ALU.add).then_inc(base, 1)
                eng.wait_ge(base, m + 1)
                eng.reciprocal(inv[p][:, :], sm_[p][:, :]).then_inc(base, 1)
                eng.wait_ge(base, m + 2)
                eng.tensor_tensor(sx[p][:, :, :], sx[p][:, :, :], inv[p][:, None, :].to_broadcast([P, BT, H]), ALU.mult).then_inc(base, 1)
                eng.wait_ge(base, m + 3)
                for j in range(BT):
                    v = R[p][:, 2].rearrange("p h a e -> p h (a e)") if j == 0 else ps[:, 3 + j, D:2 * D].rearrange("p (h e) -> p h e", h=H)
                    eng.tensor_tensor(prod[p][:, j, :, :], v, sx[p][:, j, :, None].to_broadcast([P, H, E]), ALU.mult).then_inc(base, 1)
                eng.wait_ge(base, m + 7)
                eng.tensor_reduce(cx[p][:, :], prod[p][:, :, :, :].rearrange("p j h e -> p (h e) j"), AX.X, ALU.add).then_inc(base, 1)
                eng.wait_ge(base, m + 8)
                if not early(t):
                    eng.wait_ge(s["cturned"], t - 1)
                quantise(eng, cx[p][:, :], cr[p][:, :], cq[p][:, :], st2[p], s["q2"], t * NQS, s["cq"])
                eng.tensor_tensor(fac2[p][:, :], st2[p][:, 0:1], pl.deq[:, 1:2], ALU.mult).then_inc(s["ctx"], 1)

            def residual(t, p):
                eng.wait_ge(s["proj"], t + 1)
                eng.wait_ge(s["ctx"], t + 1)
                eng.scalar_tensor_tensor(out=pl.x1[:, t, :], in0=ps[:, 7, 0:D], scalar=fac2[p][:, 0:1], in1=pl.x1[:, t, :],
                                         op0=ALU.mult, op1=ALU.add).then_inc(s["x1"], 1)

            staggered(eng, [(0, norm_quantise), (2, scores), (2, weigh), (1, rotate), (3, residual)])

        @block.scalar
        def _(eng):
            eng.preload_act_table(ACT.Exp)

            def take_hq(t, p):
                eng.wait_ge(s["hturned"], t + 1)
                if not early(t):
                    eng.wait_ge(s["qkv"], 2 * t - 2)
                eng.activation(hqT[p][:, :, :], ps[:, 0, 0:P].bitcast(BF16).rearrange("p (k n) -> p k n", k=KC), ACT.Copy).then_inc(s["hqT"], 1)

            def take_qkv(t, p):
                eng.wait_ge(s["fac"], t + 1)
                if not early(t):
                    eng.wait_ge(s["shifted"], t - 1)
                    eng.wait_ge(s["ctx"], t - 1)
                f = R[p][:, :, :, :, :].rearrange("p n h a e -> p (n h a e)")
                eng.wait_ge(s["qkv"], 2 * t + 1)
                eng.activation(f[:, 0:2 * D], ps[:, 2, :], ACT.Copy, scale=fac[p][:, 0:1]).then_inc(s["R"], 1)
                eng.wait_ge(s["qkv"], 2 * t + 2)
                eng.activation(f[:, 2 * D:3 * D], ps[:, 3, 0:D], ACT.Copy, scale=fac[p][:, 0:1]).then_inc(s["R"], 1)

            def exponential(t, p):
                eng.wait_ge(s["att"], t * 8 + 8)
                eng.activation(sx[p][:, :, :], sx[p][:, :, :], ACT.Exp, scale=float(E) ** -0.5).then_inc(s["exp"], 1)

            def take_cq(t, p):
                eng.wait_ge(s["cturned"], t + 1)
                if not early(t):
                    eng.wait_ge(s["proj"], t - 1)
                eng.activation(cqT[p][:, :, :], ps[:, 1, 0:P].bitcast(BF16).rearrange("p (k n) -> p k n", k=KC), ACT.Copy).then_inc(s["cqT"], 1)

            def square(t, p):
                eng.wait_ge(s["sqs"], 2 * t)
                eng.wait_ge(s["x1"], t + 1)
                eng.activation(sqj[:, :], pl.x1[:, t, :], ACT.Square, accum_out=ms1[:, :]).then_inc(s["sqs"], 1)
                eng.wait_ge(s["sqs"], 2 * t + 1)
                eng.activation(pl.ms[:, bass.ds(t, 1)], ms1[:, :], ACT.Copy).then_inc(s["sqs"], 1)

            staggered(eng, [(0, take_hq), (2, exponential), (2, take_cq), (0, take_qkv), (3, square)])

        @block.tensor
        def _(eng):
            eng.wait_ge(s["ones"], 1)
            eng.wait_ge(s["wabs"], 3)
            eng.matmul(ps[:, 0, 0:3], ones[:, :], wsum[:, :], start=True, stop=True).then_inc(s["wsummed"], 1)
            eng.wait_ge(s["wq"], 14)

            def turn_h(t, p):
                eng.wait_ge(s["hq"], t + 1)
                eng.wait_ge(s["hqT"], t)
                for k in range(KC):
                    mm = eng.transpose(ps[:, 0, k * P // 2:(k + 1) * P // 2].bitcast(BF16), hq[p][:, k * P:(k + 1) * P], pl.identb[:, :])
                mm.then_inc(s["hturned"], 1)

            def project(t, p):
                eng.wait_ge(s["hqT"], t + 1)
                eng.wait_ge(s["R"], 2 * t)
                for n, w in ((0, 2 * D), (1, D)):
                    for k in range(KC):
                        mm = eng.matmul(ps[:, 2 + n, 0:w], hqT[p][:, k, :], wqkv[:, k, n * 512:n * 512 + w], start=(k == 0), stop=(k == KC - 1))
                    mm.then_inc(s["qkv"], 1)

            def shift(t, p):
                eng.wait_ge(s["rot"], t + 1)
                eng.wait_ge(s["wst"], 8 * t)
                kv = R[p][:, 1:3].rearrange("p n h a e -> p (n h a e)")
                for j in range(3):
                    mm = eng.matmul(ps[:, 4 + j, :], sh[:, j, :], kv, start=True, stop=True)
                mm.then_inc(s["shifted"], 1)

            def turn_c(t, p):
                eng.wait_ge(s["cq"], t + 1)
                eng.wait_ge(s["cqT"], t)
                for k in range(KC):
                    mm = eng.transpose(ps[:, 1, k * P // 2:(k + 1) * P // 2].bitcast(BF16), cq[p][:, k * P:(k + 1) * P], pl.identb[:, :])
                mm.then_inc(s["cturned"], 1)

            def output(t, p):
                eng.wait_ge(s["cqT"], t + 1)
                eng.wait_ge(s["x1"], t)
                for k in range(KC):
                    mm = eng.matmul(ps[:, 7, 0:D], cqT[p][:, k, :], wo[:, k, :], start=(k == 0), stop=(k == KC - 1))
                mm.then_inc(s["proj"], 1)

            staggered(eng, [(0, turn_h), (0, project), (2, turn_c), (2, output), (1, shift)])


def block_ffn(pl):
    nc, ps = pl.nc, pl.ps
    I = 2 * D
    up = pl.at("bf_up", [P, KC, 2 * I], F32, pl.blk_low)
    wn = pl.at("bf_wn", [P, D], F32, pl.end)
    two = lambda name, shape, dt=F32: [pl.at(f"bf_{name}{j}", shape, dt, pl.end) for j in range(2)]
    hn = two("hn", [P, D])
    hT = two("hT", [P, KC, P])
    sg, g, gr = two("sg", [P, I]), two("g", [P, I]), two("gr", [P, I])
    gq = two("gq", [P, I], BF16)
    gT = two("gT", [P, 4, P], BF16)
    st, fac = two("st", [P, 4]), two("fac", [P, 1])
    s = {k: pl.sem(f"bf_{k}") for k in (
        "w_in", "ms", "rs", "hn", "hturned", "hT", "gate", "val", "silu", "g", "q", "gq", "fac", "gturned", "gT", "down", "res", "added")}

    with nc.Block() as block:
        @block.sync
        def _(eng):
            eng.dma_start(up[:, :, :], pl.ap["L1_upT"]).then_inc(s["w_in"], 16)
            eng.dma_start(wn[:, :], pl.ap["L1_ffn_norm"].to_broadcast([P, D])).then_inc(s["w_in"], 16)

        @block.gpsimd
        def _(eng):
            eng.wait_ge(s["ms"], 1)
            eng.tensor_tensor(pl.rs2[:, :], pl.rs2[:, :], pl.mhalf[:, :], ALU.pow).then_inc(s["rs"], 1)

        @block.vector
        def _(eng):
            eng.tensor_scalar(pl.rs2[:, :], pl.ms[:, :], 1.0 / D, EPS, ALU.mult, ALU.add).then_inc(s["ms"], 1)
            eng.wait_ge(s["rs"], 1)
            eng.wait_ge(s["w_in"], 32)

            def norm(t, p):
                if not early(t):
                    eng.wait_ge(s["hturned"], t - 1)
                eng.scalar_tensor_tensor(out=hn[p][:, :], in0=pl.x1[:, t, :], scalar=pl.rs2[:, bass.ds(t, 1)], in1=wn[:, :],
                                         op0=ALU.mult, op1=ALU.mult).then_inc(s["hn"], 1)

            def gated(t, p):
                eng.wait_ge(s["silu"], t + 1)
                eng.wait_ge(s["val"], t + 1)
                eng.tensor_tensor(g[p][:, :], ps[:, 2, :], sg[p][:, :], ALU.mult).then_inc(s["g"], 1)
                eng.wait_ge(s["g"], t + 1)
                if not early(t):
                    eng.wait_ge(s["gturned"], t - 1)
                quantise(eng, g[p][:, :], gr[p][:, :], gq[p][:, :], st[p], s["q"], t * NQS, s["gq"])
                eng.tensor_tensor(fac[p][:, :], st[p][:, 0:1], pl.deq[:, 2:3], ALU.mult).then_inc(s["fac"], 1)

            def residual(t, p):
                eng.wait_ge(s["down"], t + 1)
                eng.wait_ge(s["fac"], t + 1)
                eng.scalar_tensor_tensor(out=pl.x1[:, t, :], in0=ps[:, 6, 0:D], scalar=fac[p][:, 0:1], in1=pl.x1[:, t, :],
                                         op0=ALU.mult, op1=ALU.add).then_inc(s["res"], 1)
                eng.wait_ge(s["res"], t + 1)
                eng.tensor_tensor(pl.x[:, t, :], pl.x[:, t, :], pl.x1[:, t, :], ALU.add).then_inc(s["added"], 1)
                eng.wait_ge(s["added"], t + 1)
                token_stats(pl, eng, t)

            staggered(eng, [(0, norm), (1, gated), (2, residual)])
            pl.stats_n += 3 * NT

        @block.scalar
        def _(eng):
            eng.preload_act_table(ACT.Silu)

            def take_h(t, p):
                eng.wait_ge(s["hturned"], t + 1)
                if not early(t):
                    eng.wait_ge(s["val"], t - 1)
                eng.activation(hT[p][:, :, :], ps[:, 0, 0:KC * P].rearrange("p (k n) -> p k n", k=KC), ACT.Copy).then_inc(s["hT"], 1)

            def silu(t, p):
                eng.wait_ge(s["gate"], t + 1)
                if not early(t):
                    eng.wait_ge(s["g"], t - 1)
                eng.activation(sg[p][:, :], ps[:, 1, :], ACT.Silu).then_inc(s["silu"], 1)

            def take_g(t, p):
                eng.wait_ge(s["gturned"], t + 1)
                if not early(t):
                    eng.wait_ge(s["down"], t - 1)
                eng.activation(gT[p][:, :, :], ps[:, 3, 0:2 * P].bitcast(BF16).rearrange("p (k n) -> p k n", k=4), ACT.Copy).then_inc(s["gT"], 1)

            staggered(eng, [(0, take_h), (0, silu), (1, take_g)])

        @block.tensor
        def _(eng):
            eng.wait_ge(s["w_in"], 32)

            def turn_h(t, p):
                eng.wait_ge(s["hn"], t + 1)
                eng.wait_ge(s["hT"], t)
                for k in range(KC):
                    mm = eng.transpose(ps[:, 0, k * P:(k + 1) * P], hn[p][:, k * P:(k + 1) * P], pl.ident[:, :])
                mm.then_inc(s["hturned"], 1)

            def ups(t, p):
                eng.wait_ge(s["hT"], t + 1)
                for n, (bank, sem, free) in enumerate(((1, s["gate"], s["silu"]), (2, s["val"], s["g"]))):
                    eng.wait_ge(free, t)
                    for k in range(KC):
                        mm = eng.matmul(ps[:, bank, :], hT[p][:, k, :], up[:, k, n * I:(n + 1) * I], start=(k == 0), stop=(k == KC - 1))
                    mm.then_inc(sem, 1)

            def turn_g(t, p):
                eng.wait_ge(s["gq"], t + 1)
                eng.wait_ge(s["gT"], t)
                for k in range(4):
                    mm = eng.transpose(ps[:, 3, k * P // 2:(k + 1) * P // 2].bitcast(BF16), gq[p][:, k * P:(k + 1) * P], pl.identb[:, :])
                mm.then_inc(s["gturned"], 1)

            def down(t, p):
                eng.wait_ge(s["gT"], t + 1)
                eng.wait_ge(s["res"], t)
                for k in range(4):
                    mm = eng.matmul(ps[:, 6, 0:D], gT[p][:, k, :], pl.wd[:, k, :], start=(k == 0), stop=(k == 3))
                mm.then_inc(s["down"], 1)

            staggered(eng, [(0, turn_h), (0, ups), (1, turn_g), (1, down)])


def lut_ffn(pl):
    nc, ps = pl.nc, pl.ps
    I = 688
    half = I // 2
    NC = -(-I // P)
    LAST = I - (NC - 1) * P
    wgu = pl.at("lf_wgu", [P, KC, 2, I], F32, L_OFF)
    wdn = pl.at("lf_wdn", [P, NC, D], F32, pl.end)
    two = lambda name, shape, dt=F32: [pl.at(f"lf_{name}{j}", shape, dt, pl.end) for j in range(2)]
    xn, xT = two("xn", [P, D]), two("xT", [P, KC, P])
    sg, h = two("sg", [P, I]), two("h", [P, I])
    hT = two("hT", [P, NC, P])
    s = {k: pl.sem(f"lf_{k}") for k in (
        "w_in", "rs_in", "rstd", "xn", "xturned", "xT", "gate", "up", "silu", "h", "hturned", "hT", "down", "added", "stored")}

    with nc.Block() as block:
        @block.sync
        def _(eng):
            n = KC * 2 * I
            eng.dma_start(wgu[:, :, :, :].rearrange("p k a n -> p (k a n)"), pl.lut_dram[:, 0:n]).then_inc(s["w_in"], 16)
            eng.dma_start(wdn[:, :, :].rearrange("p k n -> p (k n)"), pl.lut_dram[:, n:]).then_inc(s["w_in"], 16)

            def store(t, p):
                eng.wait_ge(s["added"], t + 1)
                eng.dma_start(pl.out[:, t, :], pl.x[:, t, :]).then_inc(s["stored"], 16)
            staggered(eng, [(0, store)])
            eng.wait_ge(s["stored"], 16 * NT)

        @block.gpsimd
        def _(eng):
            pow_of_all(pl, eng, s)

        @block.vector
        def _(eng):
            rstd_of_all(pl, eng, s)

            def norm(t, p):
                if not early(t):
                    eng.wait_ge(s["xturned"], t - 1)
                eng.tensor_scalar(xn[p][:, :], pl.x[:, t, :], pl.mv[:, t, 0:1], pl.rstd[:, bass.ds(t, 1)],
                                  ALU.subtract, ALU.mult).then_inc(s["xn"], 1)

            def gated(t, p):
                eng.wait_ge(s["silu"], t + 1)
                eng.wait_ge(s["up"], t + 1)
                if not early(t):
                    eng.wait_ge(s["hturned"], 2 * t - 2)
                eng.tensor_tensor(h[p][:, :].rearrange("p (a n) -> p a n", a=2), ps[:, 2:4, 0:half],
                                  sg[p][:, :].rearrange("p (a n) -> p a n", a=2), ALU.mult).then_inc(s["h"], 1)

            def add(t, p):
                eng.wait_ge(s["down"], t + 1)
                eng.tensor_tensor(pl.x[:, t, :], ps[:, 6, 0:D], pl.x[:, t, :], ALU.add).then_inc(s["added"], 1)

            staggered(eng, [(0, norm), (1, gated), (2, add)])

        @block.scalar
        def _(eng):
            eng.preload_act_table(ACT.Silu)

            def take_x(t, p):
                eng.wait_ge(s["xturned"], t + 1)
                if not early(t):
                    eng.wait_ge(s["up"], t - 1)
                eng.activation(xT[p][:, :, :], ps[:, 7, 0:KC * P].rearrange("p (k n) -> p k n", k=KC), ACT.Copy).then_inc(s["xT"], 1)

            def silu(t, p):
                eng.wait_ge(s["gate"], t + 1)
                if not early(t):
                    eng.wait_ge(s["h"], t - 1)
                eng.activation(sg[p][:, :].rearrange("p (a n) -> p a n", a=2), ps[:, 0:2, 0:half], ACT.Silu).then_inc(s["silu"], 1)

            def take_h(t, p):
                eng.wait_ge(s["hturned"], 2 * t + 2)
                if not early(t):
                    eng.wait_ge(s["down"], t - 1)
                eng.activation(hT[p][:, 0:4, :], ps[:, 4, :].rearrange("p (c n) -> p c n", c=4), ACT.Copy).then_inc(s["hT"], 1)
                eng.activation(hT[p][:, 4, :], ps[:, 5, 0:P], ACT.Copy).then_inc(s["hT"], 1)
                eng.activation(hT[p][0:LAST, 5, :], ps[0:LAST, 5, P:2 * P], ACT.Copy).then_inc(s["hT"], 1)

            staggered(eng, [(0, take_x), (0, silu), (1, take_h)])

        @block.tensor
        def _(eng):
            eng.wait_ge(s["w_in"], 32)

            def turn_x(t, p):
                eng.wait_ge(s["xn"], t + 1)
                eng.wait_ge(s["xT"], t)
                for k in range(KC):
                    mm = eng.transpose(ps[:, 7, k * P:(k + 1) * P], xn[p][:, k * P:(k + 1) * P], pl.ident[:, :])
                mm.then_inc(s["xturned"], 1)

            def ups(t, p):
                eng.wait_ge(s["xT"], t + 1)
                for a, (sem, free) in enumerate(((s["gate"], s["silu"]), (s["up"], s["h"]))):
                    eng.wait_ge(free, t)
                    for m in range(2):
                        for k in range(KC):
                            mm = eng.matmul(ps[:, 2 * a + m, 0:half], xT[p][:, k, :], wgu[:, k, a, m * half:(m + 1) * half],
                                            start=(k == 0), stop=(k == KC - 1))
                    mm.then_inc(sem, 1)

            def turn_h(t, p):
                eng.wait_ge(s["h"], t + 1)
                eng.wait_ge(s["hT"], 3 * t)
                for c in range(NC):
                    m = P if c < NC - 1 else LAST
                    mm = eng.transpose(ps[0:m, 4 + c // 4, c % 4 * P:c % 4 * P + P], h[p][:, c * P:c * P + m], pl.ident[:, :])
                    if c in (3, NC - 1):
                        mm.then_inc(s["hturned"], 1)

            def down(t, p):
                eng.wait_ge(s["hT"], 3 * t + 3)
                eng.wait_ge(s["added"], t)
                for c in range(NC):
                    m = P if c < NC - 1 else LAST
                    mm = eng.matmul(ps[:, 6, 0:D], hT[p][0:m, c, :], wdn[0:m, c, :], start=(c == 0), stop=(c == NC - 1))
                mm.then_inc(s["down"], 1)

            staggered(eng, [(0, turn_x), (0, ups), (1, turn_h), (1, down)])


def store(pl, out):
    done = pl.sem("stored")
    with pl.nc.Block() as block:
        @block.sync
        def _(eng):
            eng.dma_start(out.rearrange("(t p) d -> p t d", p=P), pl.x[:, :, :]).then_inc(done, 16)
            eng.wait_ge(done, 16)


def build(nc, ap, out, start=0, stop=6):
    with ExitStack() as ctx:
        pl = Plan(nc, ctx, ap)
        common(pl)
        setup(pl)
        if start < 1 <= stop:
            l0x_queries(pl)
            xattn_batches(pl, "l0x", L_OFF, pl.tmp_off, True)
            xattn_project(pl, "l0xo", pl.Bw, pl.tmp_off)
            pl.clear_layer()
        if start < 2 <= stop:
            self_attention(pl)
        if start < 3 <= stop:
            experts(pl)
            pl.clear_layer()
        if start < 4 <= stop:
            key_norms(pl)
            l1x_queries(pl)
            xattn_batches(pl, "l1x", pl.low1_off, None, False, normed=True)
            xattn_project(pl, "l1xo", pl.Bw1, pl.low1_off, pl.bw1_in)
            pl.clear_layer()
        if start < 5 <= stop:
            block_attention(pl)
            block_ffn(pl)
        pl.out = out.rearrange("(t p) d -> p t d", p=P)
        if stop >= 6:
            lut_ffn(pl)
        else:
            store(pl, out)


def layout(inputs):
    a = {k: np.asarray(v) for k, v in inputs.items()}
    c = np.ascontiguousarray
    heads = lambda w, n: w.reshape(w.shape[0], n, -1)
    turned = lambda w: w.T.reshape(-1, P, w.shape[0]).transpose(1, 0, 2).reshape(P, -1)
    gu = np.stack([a["L1_ffn_gate_idx"].T, a["L1_ffn_up_idx"].T], 1)
    gu = gu.reshape(KC, P, -1).transpose(1, 0, 2).reshape(P, -1)
    dn = a["L1_ffn_down_idx"].T
    dn = np.concatenate([dn, np.zeros((-dn.shape[0] % P, D), dn.dtype)])
    idx = np.concatenate([gu, dn.reshape(-1, P, D).transpose(1, 0, 2).reshape(P, -1)], 1)
    return {
        **tables(),
        "x": c(a["x"].reshape(NT, P, D).transpose(1, 0, 2)),
        "ctx": c(a["ctx_1024"]),
        "ctxT": c(a["ctx_1024"].reshape(B * CS, CD).T),
        "mask": c(a["mask_BxS2_bf1"]).view(np.uint8),
        "L0_WqT": c(heads(a["L0_xattn_Wq"], NH).transpose(2, 1, 0)),
        "L0_WkT": c(heads(a["L0_xattn_Wk"], 8).transpose(2, 1, 0)),
        "L0_WvT": c(heads(a["L0_xattn_Wv"], 8).transpose(2, 1, 0)),
        "L0_wqkvT": c(a["L0_attn_w_qkv"].T.reshape(KC, P, -1).transpose(1, 0, 2)),
        "L0_woT": c(a["L0_attn_w_o"].T.reshape(NT, P, D).transpose(1, 0, 2)),
        "L1_WqT": c(a["L1_xattn_Wq"].reshape(KC, P, -1).transpose(1, 0, 2)),
        "L1_Wk": c(a["L1_xattn_Wk"]),
        "L1_WkT": c(heads(a["L1_xattn_Wk"], NH).transpose(2, 1, 0)),
        "L1_WvT": c(heads(a["L1_xattn_Wv"], NH).transpose(2, 1, 0)),
        "L1_Wo": c(a["L1_xattn_Wo"].reshape(NH, HD, D).transpose(1, 0, 2)),
        "L1_g": c(np.stack([a["L1_xattn_gq"], a["L1_xattn_gk"]], 1)),
        "L1_qkvT": c(turned(a["L1_attn_qkv_w"])),
        "L1_oT": c(turned(a["L1_attn_o_w"])),
        "L1_downT": c(turned(a["L1_attn_ffn_down_w"])),
        "L1_upT": c(turned(a["L1_attn_ffn_up_w"]).reshape(P, KC, -1)),
        "L1_attn_norm": c(a["L1_attn_attn_norm_w"][None]),
        "L1_ffn_norm": c(a["L1_attn_ffn_norm_w"][None]),
        "L1_lut": c(a["L1_ffn_lut"][None]),
        "L1_idx": c(idx),
        "entries": np.ascontiguousarray(np.broadcast_to(np.arange(NT, dtype=np.float32), (P, NT))),
        "L0_gate": c(a["L0_ffn_gate"].reshape(KC, P, -1).transpose(1, 0, 2)),
        "L0_wg": c(a["L0_ffn_gate_up_proj"][:, :, :96].transpose(1, 0, 2).reshape(KC, P, -1).transpose(1, 0, 2)),
        "L0_wu": c(a["L0_ffn_gate_up_proj"][:, :, 96:].transpose(1, 0, 2).reshape(KC, P, -1).transpose(1, 0, 2)),
        "L0_wd": c(a["L0_ffn_down_proj"].reshape(-1, P, D).transpose(1, 0, 2)),
        "L0_Wo": c(a["L0_xattn_Wo"].reshape(NH, HD, D).transpose(1, 0, 2)),
    }


def kernel(**inputs):
    import concourse.bacc as _bacc
    from concourse import mybir as _mybir
    from concourse.bass_utils import run_bass_kernel_spmd as _run

    nc = _bacc.Bacc("TRN2", target_bir_lowering=False, num_devices=1)
    arrays = layout(inputs)
    ap = {k: nc.dram_tensor(k, a.shape, _mybir.dt.from_np(a.dtype), kind="ExternalInput").ap() for k, a in arrays.items()}
    out = nc.dram_tensor("out", (TOK, D), F32, kind="ExternalOutput").ap()
    build(nc, ap, out)
    r = _run(nc, [arrays], core_ids=[0])
    return r.results[0]["out"].reshape(B, S, D)
```

```python
from contextlib import ExitStack

import numpy as np
import concourse.bass as bass
from concourse import mybir
from concourse.alu_op_type import AluOpType as ALU

F32 = mybir.dt.float32
BF16 = mybir.dt.bfloat16
U8 = mybir.dt.uint8
I32 = mybir.dt.int32
F32R = mybir.dt.float32r
ACT = mybir.ActivationFunctionType
AX = mybir.AxisListType

P = 128
B, S, D = 64, 32, 256
TOK = B * S
NT = TOK // P
KC = D // P
SUP = 4
ST = TOK // SUP
CD, CS = 128, 257
NH, HD = 16, 128
GQ = 4
EPS = 1e-5
NEG = -1e30

SB0 = 16512
X_OFF = SB0
C_OFF = X_OFF + NT * D * 4
L_OFF = C_OFF + 8192
TOP = 229344
QO_OFF = TOP - NH * TOK * 4

CONSTS = {"cos64": 64, "sin64": 64, "causal": S, "diag": S}


def tables():
    pos = np.arange(P) % S
    out = {}
    for d in (64, 16):
        inv = (1.0 / np.float32(10000.0) ** (np.arange(0, d, 2, dtype=np.float32) / np.float32(d))).astype(np.float32)
        ang = pos.astype(np.float32)[:, None] * inv
        co, si = np.cos(ang).astype(np.float32), np.sin(ang).astype(np.float32)
        out[f"cos{d}"] = np.concatenate([co, co], 1)
        out[f"sin{d}"] = np.concatenate([-si, si], 1)
    out["causal"] = np.where(np.arange(S)[None, :] <= pos[:, None], 0.0, NEG).astype(np.float32)
    out["diag"] = (np.arange(S)[None, :] == pos[:, None]).astype(np.float32)
    out["shift"] = (np.arange(P)[:, None, None] == np.arange(P)[None, None] - np.arange(1, 4)[None, :, None]).astype(np.float32)
    out["bmask"] = np.where(np.arange(4)[None, :] <= (np.arange(P) % 4)[:, None], 0.0, NEG).astype(np.float32)
    row_head = np.arange(4)[:, None] * 4 + (np.arange(P) // S)[None, :]
    pick = (np.arange(3 * NH)[:, None, None] % NH == row_head[None]).astype(np.float32)
    out["pick"] = pick
    return out


class Plan:

    def __init__(self, nc, ctx, ap):
        self.nc, self.ctx, self.ap = nc, ctx, ap
        self.layer_sems = []

    def at(self, name, shape, dt, off):
        t = self.nc.alloc_sbuf_tensor_at(name, shape, dt, offset=off)
        size = {F32: 4, I32: 4, BF16: 2, U8: 1}[dt]
        for n in shape[1:]:
            size *= n
        assert off + size <= TOP, (name, off + size - TOP)
        self.end = -(-(off + size) // 32) * 32
        return t

    def sem(self, name):
        s = self.nc.alloc_semaphore(name)
        self.layer_sems.append(s)
        return s

    def clear_layer(self):
        self.nc.clear_and_free_semaphores(self.layer_sems)
        self.layer_sems = []
        self.nc.all_engine_barrier()


def common(pl):
    nc = pl.nc
    pl.x = pl.at("x_sb", [P, NT, D], F32, X_OFF)
    pl.ident = pl.at("ident", [P, P], F32, C_OFF)
    pl.identb = pl.at("identb", [P, P], BF16, pl.end)
    pl.mv = pl.at("mv_all", [P, NT, 2], F32, pl.end)
    pl.rstd = pl.at("rstd_all", [P, NT], F32, pl.end)
    pl.veps = pl.at("veps_all", [P, NT], F32, pl.end)
    pl.bn = pl.at("bn_out", [P, 6], F32, pl.end)
    pl.mv1 = pl.at("mv_one", [P, 2], F32, pl.end)
    pl.mhalf = pl.at("minus_half", [P, NT], F32, pl.end)
    pl.maskb = pl.at("mask_bias", [B, CS], BF16, pl.end)
    pl.flag = pl.at("any_valid", [P, B], F32, pl.end)
    pl.cst = {n: pl.at(n, [P, w], F32, pl.end) for n, w in CONSTS.items()}
    pl.const_end = pl.end
    assert pl.end <= L_OFF
    pl.ps = pl.ctx.enter_context(nc.psum_tensor("ps", [P, 8, 512], F32))
    pl.x_loaded = nc.alloc_semaphore("x_loaded")
    pl.stats = nc.alloc_semaphore("stats_step")
    pl.stats_n = 0


def apart(pl, eng):
    eng.nop(nofuse=True)




def leading_bits(eng, src, head):
    return eng.tensor_copy(head.bitcast(F32R), src)


def rest_of(eng, src, head, rest):
    return eng.tensor_tensor(rest.bitcast(F32R), src, head, ALU.subtract)


def split(eng, src, head, rest, sem, n):
    leading_bits(eng, src, head).then_inc(sem, 1)
    eng.wait_ge(sem, n + 1)
    rest_of(eng, src, head, rest).then_inc(sem, 1)


def bfloat_parts(eng, src, parts, rests, sem, n):
    left = [src, *rests]
    for j in range(3):
        if j > 0:
            eng.wait_ge(sem, n + 2 * j - 1)
            eng.tensor_tensor(left[j], left[j - 1], parts[j - 1], ALU.subtract).then_inc(sem, 1)
            eng.wait_ge(sem, n + 2 * j)
        eng.tensor_copy(parts[j], left[j]).then_inc(sem, 1)


def split_product(eng, out, a, b, start=True, stop=True):
    r = [[x.bitcast(F32R) for x in y] for y in (a, b)]
    eng.matmul(out, r[0][0], r[1][0], start=start, stop=False)
    eng.matmul(out, r[0][0], r[1][1], start=False, stop=False)
    return eng.matmul(out, r[0][1], r[1][0], start=False, stop=stop)


def token_stats(pl, eng, t):
    n = t * 3 + pl.stats_n
    apart(pl, eng)
    eng.bn_stats(pl.bn[:, :], pl.x[:, t, :]).then_inc(pl.stats, 1)
    eng.wait_ge(pl.stats, n + 1)
    apart(pl, eng)
    eng.bn_aggr(pl.mv1[:, :], pl.bn[:, :]).then_inc(pl.stats, 1)
    eng.wait_ge(pl.stats, n + 2)
    apart(pl, eng)
    eng.tensor_copy(pl.mv[:, t, :], pl.mv1[:, :]).then_inc(pl.stats, 1)


def setup(pl):
    nc, ap = pl.nc, pl.ap
    pl.Aw = pl.at("Aw", [P, KC, NH, CD], F32, L_OFF)
    pl.Bw = pl.at("Bw", [P, NH, D], F32, pl.end)
    pl.tmp_off = pl.end
    wq = pl.at("s_wqT", [P, NH, D], F32, QO_OFF)
    wk = pl.at("s_wkT", [P, 8, CD], F32, pl.end)
    wv = pl.at("s_wvT", [P, 8, CD], F32, pl.end)
    wo = pl.at("s_wo", [P, NH, D], F32, pl.end)
    mask8 = pl.at("s_mask8", [B, CS], U8, pl.end)
    maskf = pl.at("s_maskf", [B, CS], F32, pl.end)
    vflag = pl.at("s_vflag", [B, 1], F32, pl.end)
    dflag = pl.at("s_dflag", [B, B], F32, pl.end)
    ones = pl.at("s_ones", [B, P], F32, pl.end)
    last, lrest0, lrest1 = (pl.at(f"s_last{j}", [B, CD], F32, pl.end) for j in range(3))
    lparts = pl.at("s_last_parts", [B, 3, CD], BF16, pl.end)
    pl.last_dram = nc.dram_tensor("last_row_scratch", (B, 9, CD), BF16, kind="Internal").ap()
    last_in, last_step, last_stored = pl.sem("set_last_loaded"), pl.sem("set_last_step"), pl.sem("set_last_stored")
    w_loaded, mask_loaded = pl.sem("set_w_loaded"), pl.sem("set_mask_loaded")
    ones_set, filled = pl.sem("set_ones"), pl.sem("set_filled")
    evac = [pl.sem("set_evac_vector"), pl.sem("set_evac_scalar")]
    ident_set, ident_zero, mstep = pl.sem("ident_set"), pl.sem("ident_zero"), pl.sem("set_mask_step")
    fl_done = pl.sem("set_flag_product")
    pl.ident_set = ident_set
    ps = pl.ps
    NA, NBK = KC * NH // 4, NH // 2

    consts_in = pl.sem("consts_loaded")
    with nc.Block() as block:
        @block.sync
        def _(eng):
            eng.dma_start(wq[:, :, :], ap["L0_WqT"]).then_inc(w_loaded, 16)
            eng.dma_start(wk[:, :, :], ap["L0_WkT"]).then_inc(w_loaded, 16)
            eng.dma_start(mask8[:, :], ap["mask"]).then_inc(mask_loaded, 16)
            eng.dma_start(wv[:, :, :], ap["L0_WvT"]).then_inc(w_loaded, 16)
            eng.dma_start(wo[:, :, :], ap["L0_Wo"]).then_inc(w_loaded, 16)
            eng.dma_start(last[:, :], ap["ctx"][:, CS - 1, :]).then_inc(last_in, 16)
            eng.wait_ge(last_step, 5)
            for r in range(3):
                eng.dma_start(pl.last_dram[:, 3 * r:3 * r + 3, :], lparts[:, :, :]).then_inc(last_stored, 16)
            eng.wait_ge(last_stored, 48)

        @block.scalar
        def _(eng):
            eng.dma_start(pl.x[:, :, :], ap["x"]).then_inc(pl.x_loaded, 16)
            for name in CONSTS:
                eng.dma_start(pl.cst[name][:, :], ap[name]).then_inc(consts_in, 16)
            for k in range(1, NA + NBK, 2):
                eng.wait_ge(filled, k + 1)
                dst = pl.Aw[:, k * 4 // NH, k * 4 % NH:k * 4 % NH + 4, :] if k < NA else pl.Bw[:, 2 * (k - NA):2 * (k - NA) + 2, :]
                src = ps[:, k % 8, :].rearrange("p (h c) -> p h c", h=4 if k < NA else 2)
                eng.activation(dst, src, ACT.Copy).then_inc(evac[1], 1)

        @block.gpsimd
        def _(eng):
            eng.memset(pl.ident[:, :], 0.0).then_inc(ident_zero, 1)
            eng.memset(pl.identb[:, :], 0.0).then_inc(ident_zero, 1)
            eng.wait_ge(ident_zero, 2)
            for m in (pl.ident, pl.identb):
                eng.affine_select(out=m[:, :], in_=m[:, :], compare_op=ALU.not_equal, fill=1.0, base=0,
                                  pattern=[[-1, P]], channel_multiplier=1).then_inc(ident_set, 1)
            eng.memset(ones[:, :], 1.0).then_inc(ones_set, 1)
            eng.memset(pl.mhalf[:, :], -0.5).then_inc(ones_set, 1)

        @block.vector
        def _(eng):
            eng.wait_ge(mask_loaded, 16)
            eng.tensor_copy(maskf[:, :], mask8[:, :]).then_inc(mstep, 1)
            eng.wait_ge(mstep, 1)
            eng.tensor_scalar(pl.maskb[:, :], maskf[:, :], -1.0, -NEG, ALU.add, ALU.mult).then_inc(mstep, 1)
            eng.tensor_reduce(vflag[:, :], maskf[:, :], AX.X, ALU.max).then_inc(mstep, 1)
            eng.wait_ge(mstep, 3)
            eng.wait_ge(ident_set, 2)
            eng.tensor_scalar(dflag[:, :], pl.ident[0:B, 0:B], vflag[:, 0:1], None, ALU.mult).then_inc(mstep, 1)
            eng.wait_ge(fl_done, 1)
            eng.tensor_copy(pl.flag[:, :], ps[:, 7, 0:B]).then_inc(mstep, 1)
            for k in range(0, NA + NBK, 2):
                eng.wait_ge(filled, k + 1)
                dst = pl.Aw[:, k * 4 // NH, k * 4 % NH:k * 4 % NH + 4, :] if k < NA else pl.Bw[:, 2 * (k - NA):2 * (k - NA) + 2, :]
                src = ps[:, k % 8, :].rearrange("p (h c) -> p h c", h=4 if k < NA else 2)
                eng.tensor_copy(dst, src).then_inc(evac[0], 1)
            eng.wait_ge(last_in, 16)
            bfloat_parts(eng, last[:, :], [lparts[:, j, :] for j in range(3)], (lrest0[:, :], lrest1[:, :]), last_step, 0)
            eng.wait_ge(pl.x_loaded, 16)
            for t in range(NT):
                token_stats(pl, eng, t)
            pl.stats_n += 3 * NT
            eng.wait_ge(consts_in, 16 * len(CONSTS))

        @block.tensor
        def _(eng):
            eng.wait_ge(mstep, 4)
            eng.wait_ge(ones_set, 1)
            eng.matmul(ps[:, 7, 0:B], ones[:, :], dflag[:, :], start=True, stop=True).then_inc(fl_done, 1)
            eng.wait_ge(mstep, 5)
            eng.wait_ge(w_loaded, 32)
            for k in range(NA):
                if k >= 8:
                    eng.wait_ge(evac[k % 2], (k - 8) // 2 + 1)
                for j in range(4):
                    c, h = divmod(4 * k + j, NH)
                    mm = eng.matmul(ps[:, k % 8, j * CD:(j + 1) * CD], wq[:, h, c * P:(c + 1) * P], wk[:, h // 2, :],
                                    start=True, stop=True)
                mm.then_inc(filled, 1)
            eng.wait_ge(w_loaded, 64)
            for k in range(NA, NA + NBK):
                eng.wait_ge(evac[k % 2], (k - 8) // 2 + 1)
                for j in range(2):
                    h = 2 * (k - NA) + j
                    mm = eng.matmul(ps[:, k % 8, j * D:(j + 1) * D], wv[:, h // 2, :], wo[:, h, :], start=True, stop=True)
                mm.then_inc(filled, 1)


def layer_norm_steps(pl, name):
    return {k: pl.sem(f"{name}_{k}") for k in ("rs_in", "rstd", "xn", "turned", "xT")}


def rstd_of_all(pl, eng, s):
    eng.wait_ge(pl.stats, pl.stats_n)
    eng.tensor_scalar(pl.veps[:, :], pl.mv[:, :, 1], EPS, None, ALU.add).then_inc(s["rs_in"], 1)
    eng.wait_ge(s["rstd"], 1)


def pow_of_all(pl, eng, s):
    eng.wait_ge(s["rs_in"], 1)
    eng.tensor_tensor(pl.rstd[:, :], pl.veps[:, :], pl.mhalf[:, :], ALU.pow).then_inc(s["rstd"], 1)


def norm_supertile(pl, eng, s, xn, xT, i):
    for j in range(4):
        if j == 0:
            eng.wait_ge(s["turned"], i * 2)
        eng.tensor_scalar(xn[:, j, :], pl.x[:, i * 4 + j, :], pl.mv[:, i * 4 + j, 0:1], pl.rstd[:, bass.ds(i * 4 + j, 1)],
                          ALU.subtract, ALU.mult).then_inc(s["xn"], 1)
    for m in range(2):
        eng.wait_ge(s["turned"], i * 2 + m + 1)
        eng.tensor_copy(xT[:, :, bass.ds(i * ST + m * 256, 256)],
                        pl.ps[:, 6 + m, :].rearrange("p (k n) -> p k n", k=KC)).then_inc(s["xT"], 1)


def turn_supertile(pl, eng, s, xn, i):
    for m in range(2):
        eng.wait_ge(s["xn"], i * 4 + 2 * m + 2)
        eng.wait_ge(s["xT"], i * 2)
        for j in range(2):
            for k in range(KC):
                mm = eng.transpose(pl.ps[:, 6 + m, k * 256 + j * P:k * 256 + j * P + P],
                                   xn[:, 2 * m + j, k * P:(k + 1) * P], pl.ident[:, :])
        mm.then_inc(s["turned"], 1)


def l0x_queries(pl):
    nc = pl.nc
    pl.QO = pl.at("QO", [P, NH, TOK], F32, QO_OFF)
    xT = pl.at("l0x_xT", [P, KC, TOK], F32, pl.tmp_off)
    xn = pl.at("l0x_xn", [P, 4, D], F32, pl.end)
    assert pl.end <= QO_OFF
    s = layer_norm_steps(pl, "l0xq")
    filled, evac = pl.sem("l0xq_filled"), pl.sem("l0xq_bank_free")

    with nc.Block() as block:
        @block.gpsimd
        def _(eng):
            pow_of_all(pl, eng, s)

        @block.vector
        def _(eng):
            rstd_of_all(pl, eng, s)
            with eng.Fori(0, SUP) as i:
                norm_supertile(pl, eng, s, xn, xT, i)

        @block.scalar
        def _(eng):
            eng.sem_inc(evac, 4)
            with eng.Fori(0, SUP) as i:
                for h in range(NH):
                    eng.wait_ge(filled, i * NH + h + 1)
                    eng.activation(pl.QO[:, h, bass.ds(i * ST, ST)], pl.ps[:, h % 4, :], ACT.Copy).then_inc(evac, 1)

        @block.tensor
        def _(eng):
            def heads(i, lo, hi):
                for h in range(lo, hi):
                    eng.wait_ge(evac, i * NH + h + 1)
                    for k in range(KC):
                        mm = eng.matmul(pl.ps[:, h % 4, :], pl.Aw[:, k, h, :], xT[:, k, bass.ds(i * ST, ST)],
                                        start=(k == 0), stop=(k == KC - 1))
                    mm.then_inc(filled, 1)

            turn_supertile(pl, eng, s, xn, 0)
            with eng.Fori(0, SUP - 1) as i:
                eng.wait_ge(s["xT"], i * 2 + 2)
                heads(i, 0, NH // 2)
                turn_supertile(pl, eng, s, xn, i + 1)
                heads(i, NH // 2, NH)
            eng.wait_ge(s["xT"], SUP * 2)
            heads(SUP - 1, 0, NH)


UB = 4


def xattn_batches(pl, name, low, high, masked, normed=False):
    nc, ps, QO = pl.nc, pl.ps, pl.QO
    SC = float(HD) ** -0.5
    sm = {}
    qb = [pl.at(f"{name}_qb{j}", [P, NH, S], F32, low if j == 0 else pl.end) for j in range(2)]
    ctxT = [pl.at(f"{name}_ctxT{j}", [P, CS], F32, pl.end) for j in range(UB)]
    ctxn = [pl.at(f"{name}_ctx{j}", [P, 2, CD], F32, pl.end) for j in range(UB)]
    ctxl = [pl.at(f"{name}_ctxl{j}", [9, CD], BF16, pl.end) for j in range(UB)]
    if normed:
        rk = [pl.at(f"{name}_rk{j}", [3 * NH, CS], BF16, pl.end) for j in range(UB)]
        rkr = [pl.at(f"{name}_rkr{j}", [P, CS], F32, pl.end) for j in range(2)]
    assert high is None or pl.end <= high, pl.end
    prob = [pl.at(f"{name}_prob{j}", [P, GQ, CS], F32, high if high and j == 0 else pl.end) for j in range(2)]
    pT = pl.at(f"{name}_pT", [P, 2, 512], F32, pl.end)
    pTl = pl.at(f"{name}_pTl", [9, 512], BF16, pl.end)
    pl9 = [pl.at(f"{name}_last{j}", [P, GQ, 9], BF16, pl.end) for j in range(2)]
    lr = [pl.at(f"{name}_last_rest{j}", [P, GQ], F32, pl.end) for j in range(3)]
    mx = [pl.at(f"{name}_mx{j}", [P, GQ], F32, pl.end) for j in range(2)]
    nb = [pl.at(f"{name}_nb{j}", [P, GQ], F32, pl.end) for j in range(2)]
    sums = [pl.at(f"{name}_sum{j}", [P, GQ], F32, pl.end) for j in range(2)]
    rinv = [pl.at(f"{name}_rinv{j}", [P, GQ], F32, pl.end) for j in range(2)]
    rfl = [pl.at(f"{name}_rfl{j}", [P, GQ], F32, pl.end) for j in range(2)]
    mx_end = pl.end
    if normed:
        bw = pl.Bw1 = pl.at("Bw1", [P, NH, D], F32, QO_OFF - NH * D * 4)
        bw_in = pl.bw1_in = pl.sem(f"{name}_bw_loaded")
        assert pl.end >= QO_OFF - 32
        assert mx_end <= QO_OFF - NH * D * 4, mx_end
        pl.end = mx_end
    assert pl.end <= QO_OFF, pl.end - QO_OFF
    T0, T1, TL, O = 4, 5, 6, 7
    ctxT_in = [pl.sem(f"{name}_ctxT_loaded{j}") for j in range(UB)]
    ctxn_in = [pl.sem(f"{name}_ctx_loaded{j}") for j in range(UB)]
    rk_in = [pl.sem(f"{name}_rk_loaded{j}") for j in range(UB)] if normed else None
    for k in ("qb", "rep", "rep_out", "scaled", "scored", "mx", "nb", "exp", "rinv", "rfl", "norm", "turned",
              "pT_scalar", "pT_vector", "attended", "out_read", "last"):
        sm[k] = pl.sem(f"{name}_{k}")
    NI = B // UB

    with nc.Block() as block:
        @block.sync
        def _(eng):
            def load(i, p):
                b = i * UB + p
                eng.wait_ge(sm["scored"], (i - 1) * UB * GQ + (p + 1) * GQ) if not isinstance(i, int) else None
                eng.dma_start(ctxT[p][:, :], pl.ap["ctxT"][:, bass.ds(b * CS, CS)]).then_inc(ctxT_in[p], 16)
                if normed:
                    eng.dma_start(rk[p][:, :], pl.rk_dram[:, bass.ds(b * CS, CS)]).then_inc(rk_in[p], 16)
                eng.wait_ge(sm["attended"], (i - 1) * UB + p + 1) if not isinstance(i, int) else None
                eng.dma_start(ctxn[p][:, :, :], pl.ap["ctx"][b, 0:2 * P, :].rearrange("(c p) d -> p c d", p=P) if isinstance(b, int)
                              else pl.ap["ctx"][bass.ds(b, 1), 0:2 * P, :].rearrange("b (c p) d -> p (b c) d", p=P)).then_inc(ctxn_in[p], 16)
                eng.dma_start(ctxl[p][:, :], pl.last_dram[bass.ds(b, 1), :, :].rearrange("b r d -> (b r) d")).then_inc(ctxn_in[p], 16)
            for p in range(UB):
                load(0, p)
            if normed:
                eng.dma_start(bw[:, :, :], pl.bw1_dram).then_inc(bw_in, 16)
            with eng.Fori(1, NI) as i:
                for p in range(UB):
                    load(i, p)

        def each_batch(eng, first, step):
            first()
            for p in range(UB):
                step(0, p, True)
            with eng.Fori(1, NI - 1) as i:
                for p in range(UB):
                    step(i, p, True)
            for p in range(UB):
                step(NI - 1, p, p < UB - 1)

        @block.gpsimd
        def _(eng):
            def copy_q(i, p):
                b = i * UB + p
                if not (isinstance(i, int) and i * UB + p < 2):
                    eng.wait_ge(sm["scored"], b * GQ - GQ)
                eng.tensor_copy(qb[p % 2][:, :, :], QO[:, :, bass.ds(b * S, S)]).then_inc(sm["qb"], 1)

            def first():
                copy_q(0, 0)
                copy_q(0, 1)

            def step(i, p, more):
                if not (isinstance(i, int) and i == NI - 1 and p >= UB - 2):
                    b = i * UB + p + 2
                    eng.wait_ge(sm["scored"], b * GQ - GQ)
                    eng.tensor_copy(qb[p % 2][:, :, :], QO[:, :, bass.ds(b * S, S)]).then_inc(sm["qb"], 1)
            each_batch(eng, first, step)

        @block.vector
        def _(eng):
            def scaled_maxima(i, p, m):
                b = i * UB + p
                for g in (2 * m, 2 * m + 1):
                    eng.wait_ge(sm["rep_out"], b * GQ + g + 1)
                    eng.wait_ge(sm["scored"], b * GQ + g + 1)
                    if g == 0 and not (isinstance(i, int) and b < 2):
                        eng.wait_ge(sm["turned"], b - 1)
                    apart(pl, eng)
                    eng.tensor_tensor_reduce(out=prob[p % 2][:, g, :], in0=ps[:, g % 2, 0:CS], in1=rkr[g % 2][:, :], scale=1.0,
                                             scalar=-3.0e38, op0=ALU.mult, op1=ALU.max, accum_out=mx[p % 2][:, g:g + 1]).then_inc(sm["scaled"], 1)
                eng.wait_ge(sm["scaled"], b * GQ + 2 * m + 2)
                eng.scalar_tensor_tensor(out=nb[p % 2][:, 2 * m:2 * m + 2], in0=mx[p % 2][:, 2 * m:2 * m + 2], scalar=-1.0,
                                         in1=pl.rq[:, bass.ds(b, 1), 2 * m:2 * m + 2].rearrange("p a g -> p (a g)"),
                                         op0=ALU.mult, op1=ALU.mult).then_inc(sm["nb"], 1)

            def maxima(i, p, m):
                b = i * UB + p
                if normed:
                    return scaled_maxima(i, p, m)
                eng.wait_ge(sm["scored"], b * GQ + 2 * m + 2)
                eng.tensor_reduce(mx[p % 2][:, 2 * m:2 * m + 2], ps[:, 2 * m:2 * m + 2, 0:CS], AX.X, ALU.max).then_inc(sm["mx"], 1)
                eng.wait_ge(sm["mx"], b * 2 + m + 1)
                eng.tensor_scalar(nb[p % 2][:, 2 * m:2 * m + 2], mx[p % 2][:, 2 * m:2 * m + 2], -SC, None,
                                  ALU.mult).then_inc(sm["nb"], 1)

            def inverse(i, p):
                b = i * UB + p
                eng.wait_ge(sm["exp"], (b + 1) * GQ)
                eng.reciprocal(rinv[p % 2][:, :], sums[p % 2][:, :]).then_inc(sm["rinv"], 1)
                eng.wait_ge(sm["rinv"], b + 1)
                if masked:
                    eng.tensor_scalar(rfl[p % 2][:, :], rinv[p % 2][:, :], pl.flag[:, bass.ds(b, 1)], None, ALU.mult).then_inc(sm["rfl"], 1)
                    eng.wait_ge(sm["rfl"], b + 1)
                factor = rfl if masked else rinv
                if not (isinstance(i, int) and b < 2):
                    eng.wait_ge(sm["turned"], b - 1)
                q, n = p % 2, b * 6
                eng.tensor_tensor(lr[0][:, :], prob[q][:, :, CS - 1], factor[q][:, :], ALU.mult).then_inc(sm["last"], 1)
                for g in range(GQ):
                    eng.tensor_scalar(prob[q][:, g, 0:CS - 1], prob[q][:, g, 0:CS - 1], factor[q][:, g:g + 1], None,
                                      ALU.mult).then_inc(sm["norm"], 1)
                    eng.wait_ge(sm["last"], n + g + 1)
                    j = g // 2
                    if g % 2 == 0:
                        eng.tensor_copy(pl9[q][:, :, 3 * j:3 * j + 3], lr[j][:, :, None].to_broadcast([P, GQ, 3])).then_inc(sm["last"], 1)
                    else:
                        eng.tensor_tensor(lr[j + 1][:, :], lr[j][:, :], pl9[q][:, :, 3 * j], ALU.subtract).then_inc(sm["last"], 1)
                eng.wait_ge(sm["last"], n + 5)
                eng.tensor_copy(pl9[q][:, :, 6:9], lr[2][:, :, None].to_broadcast([P, GQ, 3])).then_inc(sm["last"], 1)

            def first():
                maxima(0, 0, 0)
                maxima(0, 0, 1)
                inverse(0, 0)

            def step(i, p, more):
                b = i * UB + p
                if more:
                    n = i + (p + 1) // UB, (p + 1) % UB
                    maxima(*n, 0)
                    maxima(*n, 1)
                    inverse(*n)
                eng.wait_ge(sm["turned"], b + 1)
                eng.wait_ge(sm["attended"], b)
                eng.tensor_copy(pTl[:, :], ps[0:9, TL, 0:256].bitcast(BF16)).then_inc(sm["pT_vector"], 1)
            each_batch(eng, first, step)

        @block.scalar
        def _(eng):
            eng.preload_act_table(ACT.Exp)

            def exps(i, p):
                b = i * UB + p
                if normed:
                    for g in range(GQ):
                        eng.wait_ge(sm["rep"], b * GQ + g + 1)
                        if g >= 2 or not (isinstance(i, int) and b == 0):
                            eng.wait_ge(sm["scaled"], b * GQ + g - 1)
                        eng.activation(rkr[g % 2][:, :], ps[:, 2 + g % 2, 0:CS], ACT.Copy).then_inc(sm["rep_out"], 1)
                for g in range(GQ):
                    if g % 2 == 0:
                        eng.wait_ge(sm["nb"], b * 2 + g // 2 + 1)
                    if g == 0 and not (isinstance(i, int) and b < 2):
                        eng.wait_ge(sm["turned"], b - 1)
                    src, scale = (prob[p % 2][:, g, :], pl.rq[:, b, g:g + 1]) if normed else (ps[:, g, 0:CS], SC)
                    eng.activation(prob[p % 2][:, g, :], src, ACT.Exp, bias=nb[p % 2][:, g:g + 1], scale=scale,
                                   accum_out=sums[p % 2][:, g:g + 1]).then_inc(sm["exp"], 1)

            def take_output(b):
                eng.wait_ge(sm["attended"], b + 1)
                eng.activation(QO[:, :, bass.ds(b * S, S)], ps[:, O, :].rearrange("p (h s) -> p h s", s=S), ACT.Copy).then_inc(sm["out_read"], 1)

            def step(i, p, more):
                b = i * UB + p
                if more:
                    exps(i + (p + 1) // UB, (p + 1) % UB)
                if not (isinstance(b, int) and b == 0):
                    take_output(b - 1)
                eng.wait_ge(sm["turned"], b + 1)
                eng.wait_ge(sm["attended"], b)
                for c, bank in enumerate((T0, T1)):
                    eng.activation(pT[:, c, :], ps[:, bank, :], ACT.Copy).then_inc(sm["pT_scalar"], 1)
                if not more:
                    take_output(b)
            each_batch(eng, lambda: exps(0, 0), step)

        @block.tensor
        def _(eng):
            def scores(i, p, groups):
                b = i * UB + p
                if groups[0] == 0:
                    eng.wait_ge(ctxT_in[p], i * 16 + 16)
                    eng.wait_ge(sm["qb"], b + 1)
                    if normed:
                        eng.wait_ge(rk_in[p], i * 16 + 16)
                for g in groups:
                    if normed:
                        if g >= 2 or not (isinstance(i, int) and b == 0):
                            eng.wait_ge(sm["rep_out"], b * GQ + g - 1)
                        eng.matmul(ps[:, 2 + g % 2, 0:CS], pl.pick[:, g, :], rk[p][:, :], start=True, stop=True).then_inc(sm["rep"], 1)
                        if g >= 2 or not (isinstance(i, int) and b == 0):
                            eng.wait_ge(sm["scaled"], b * GQ + g - 1)
                        eng.matmul(ps[:, g % 2, 0:CS], qb[p % 2][:, 4 * g:4 * g + 4, :], ctxT[p][:, :], start=True, stop=True).then_inc(sm["scored"], 1)
                        continue
                    if not (isinstance(i, int) and b == 0):
                        eng.wait_ge(sm["exp"], b * GQ - GQ + g + 1)
                    mm = eng.matmul(ps[:, g, 0:CS], qb[p % 2][:, 4 * g:4 * g + 4, :], ctxT[p][:, :], start=True, stop=not masked)
                    if masked:
                        mm = eng.matmul(ps[:, g, 0:CS], pl.identb[0:B, bass.ds(b, 1)].to_broadcast([B, P]), pl.maskb[:, :],
                                        start=False, stop=True)
                    mm.then_inc(sm["scored"], 1)

            def products(i, p):
                b = i * UB + p
                eng.wait_ge(ctxn_in[p], i * 32 + 32)
                eng.wait_ge(sm["out_read"], b)
                eng.wait_ge(sm["pT_scalar"], 2 * b + 1)
                eng.matmul(ps[:, O, :], ctxn[p][:, 0, :], pT[:, 0, :], start=True, stop=False)
                eng.wait_ge(sm["pT_scalar"], 2 * b + 2)
                eng.matmul(ps[:, O, :], ctxn[p][:, 1, :], pT[:, 1, :], start=False, stop=False)
                eng.wait_ge(sm["pT_vector"], b + 1)
                eng.matmul(ps[:, O, :], ctxl[p][:, :], pTl[:, :], start=False, stop=True).then_inc(sm["attended"], 1)

            def step(i, p, more):
                b = i * UB + p
                if more:
                    scores(i + (p + 1) // UB, (p + 1) % UB, range(GQ))
                if not (isinstance(b, int) and b == 0):
                    products(i - (p == 0), (p - 1) % UB)
                eng.wait_ge(sm["pT_scalar"], 2 * b)
                eng.wait_ge(sm["pT_vector"], b)
                for g in range(GQ):
                    eng.wait_ge(sm["norm"], b * GQ + g + 1)
                    for c, bank in enumerate((T0, T1)):
                        eng.transpose(ps[:, bank, g * P:(g + 1) * P], prob[p % 2][:, g, c * P:(c + 1) * P], pl.ident[:, :])
                eng.wait_ge(sm["last"], b * 6 + 6)
                for g in range(GQ):
                    mm = eng.transpose(ps[0:9, TL, g * P // 2:(g + 1) * P // 2].bitcast(BF16), pl9[p % 2][:, g, :], pl.identb[:, :])
                mm.then_inc(sm["turned"], 1)
                if not more:
                    products(i, p)
            each_batch(eng, lambda: scores(0, 0, range(GQ)), step)


def xattn_project(pl, name, Bw, low, bw_in=None):
    nc, ps, QO = pl.nc, pl.ps, pl.QO
    yT = [pl.at(f"{name}_yT{j}", [P, KC, 512], F32, low if j == 0 else pl.end) for j in range(2)]
    assert pl.end <= QO_OFF - (NH * D * 4 if bw_in is not None else 0)
    made, y0, y1, turned, added = (pl.sem(f"{name}_{k}") for k in ("made", "y_scalar", "y_vector", "turned", "added"))

    with nc.Block() as block:
        @block.tensor
        def _(eng):
            def products(s):
                for k in range(KC):
                    if s >= 2:
                        eng.wait_ge((y0, y1)[k], s - 1)
                    for h in range(NH):
                        mm = eng.matmul(ps[:, 2 * (s % 2) + k, :], Bw[:, h, k * P:(k + 1) * P], QO[:, h, s * ST:(s + 1) * ST],
                                        start=(h == 0), stop=(h == NH - 1))
                    mm.then_inc(made, 1)

            def turn(s):
                eng.wait_ge(y0, s + 1)
                eng.wait_ge(y1, s + 1)
                if s >= 1:
                    eng.wait_ge(added, 2 * s)
                for m in range(2):
                    for j in range(2):
                        for k in range(KC):
                            mm = eng.transpose(ps[:, 4 + m, j * D + k * P:j * D + (k + 1) * P],
                                               yT[s % 2][:, k, (2 * m + j) * P:(2 * m + j + 1) * P], pl.ident[:, :])
                    mm.then_inc(turned, 1)

            if bw_in is not None:
                eng.wait_ge(bw_in, 16)
            products(0)
            for s in range(SUP):
                if s + 1 < SUP:
                    products(s + 1)
                turn(s)

        @block.scalar
        def _(eng):
            for s in range(SUP):
                eng.wait_ge(made, 2 * s + 1)
                if s >= 2:
                    eng.wait_ge(turned, 2 * (s - 1))
                eng.activation(yT[s % 2][:, 0, :], ps[:, 2 * (s % 2), :], ACT.Copy).then_inc(y0, 1)

        @block.vector
        def _(eng):
            def take(s):
                eng.wait_ge(made, 2 * s + 2)
                if s >= 2:
                    eng.wait_ge(turned, 2 * (s - 1))
                eng.tensor_copy(yT[s % 2][:, 1, :], ps[:, 2 * (s % 2) + 1, :]).then_inc(y1, 1)

            def add(s):
                for m in range(2):
                    t = 4 * s + 2 * m
                    eng.wait_ge(turned, 2 * s + m + 1)
                    eng.tensor_tensor(pl.x[:, t:t + 2, :], ps[:, 4 + m, :].rearrange("p (t d) -> p t d", t=2),
                                      pl.x[:, t:t + 2, :], ALU.add).then_inc(added, 1)
                for t in range(4 * s, 4 * s + 4):
                    eng.wait_ge(added, 2 * s + (t - 4 * s) // 2 + 1)
                    token_stats(pl, eng, t)

            take(0)
            for s in range(SUP):
                if s + 1 < SUP:
                    take(s + 1)
                add(s)
            pl.stats_n += 3 * NT


def self_attention(pl):
    nc, ps = pl.nc, pl.ps
    HQ, HKV, E = 32, 4, 64
    NQ, NKV = HQ * E, HKV * E
    NB = P // S
    SC = float(E) ** -0.5
    w = pl.at("sa_wqkv", [P, KC, NQ + 2 * NKV], F32, L_OFF)
    wo = pl.at("sa_wo", [P, NQ // P, D], F32, pl.end)
    wp = [pl.at(f"sa_wqkv_{k}", [P, KC, NQ + 2 * NKV], F32, pl.end) for k in ("head", "rest")]
    wop = [pl.at(f"sa_wo_{k}", [P, NQ // P, D], F32, pl.end) for k in ("head", "rest")]
    xn = pl.at("sa_xn", [P, D], F32, pl.end)
    xT = [pl.at(f"sa_xT_{k}", [P, KC, P], F32, pl.end) for k in ("head", "rest")]
    qk = pl.at("sa_qk", [P, HQ + HKV, 2, E // 2], F32, pl.end)
    v = [pl.at(f"sa_v{j}", [P, NKV], F32, pl.end) for j in range(2)]
    rot = pl.at("sa_rot", [P, HQ + HKV, 2, E // 2], F32, pl.end)
    rsin = pl.at("sa_rsin", [P, HQ + HKV, 2, E // 2], F32, pl.end)
    kd = pl.at("sa_kd", [P, HKV, 2, E], F32, pl.end)
    qT = pl.at("sa_qT", [P, NQ // P, P], F32, pl.end)
    kT = pl.at("sa_kT", [P, HKV, P], F32, pl.end)
    sc = pl.at("sa_sc", [P, HQ, S], F32, pl.end)
    pT = pl.at("sa_pT", [P, HQ, S], F32, pl.end)
    mx = pl.at("sa_mx", [P, HQ], F32, pl.end)
    sums = pl.at("sa_sums", [P, HQ], F32, pl.end)
    rinv = pl.at("sa_rinv", [P, HQ], F32, pl.end)
    oT = [pl.at(f"sa_oT_{k}", [P, NQ // P, P], F32, pl.end) for k in ("head", "rest")]
    s = {k: pl.sem(f"sa_{k}") for k in (
        "w_in", "wo_in", "rs_in", "rstd", "xn", "xturned", "xT", "projected", "qkv", "cos", "sin", "rotated", "turned",
        "turned_scalar", "turned_vector", "scored", "soft", "exp", "pT", "valued", "oT", "oT_rest", "output", "added",
        "x_rest", "w_head", "w_rest")}
    NW = 5

    def weight_slices(n):
        if n < NW:
            return [x[:, :, n * 512:(n + 1) * 512] for x in (w, *wp)]
        return [x[:, 4 * (n - NW):4 * (n - NW) + 4, :] for x in (wo, *wop)]

    def each_tile(eng, first, step):
        first()
        for t in range(2):
            step(t, t, True)
        with eng.Fori(1, NT // 2 - 1) as u:
            for p in range(2):
                step(u * 2 + p, p, True)
        for p in range(2):
            step(NT - 2 + p, p, p == 0)

    with nc.Block() as block:
        @block.sync
        def _(eng):
            eng.dma_start(w[:, :, :], pl.ap["L0_wqkvT"]).then_inc(s["w_in"], 16)
            eng.dma_start(wo[:, :, :], pl.ap["L0_woT"]).then_inc(s["wo_in"], 16)

        @block.gpsimd
        def _(eng):
            pow_of_all(pl, eng, s)

            def sine(t):
                eng.wait_ge(s["rotated"], t * 3)
                for k in range(NW):
                    eng.wait_ge(s["qkv"], t * 6 + k + 1)
                    h = slice(8 * k, min(8 * k + 8, HQ + HKV))
                    for a in range(2):
                        eng.tensor_tensor(rsin[:, h, a, :], qk[:, h, 1 - a, :],
                                          pl.cst["sin64"][:, None, a * 32:a * 32 + 32].to_broadcast([P, h.stop - h.start, 32]),
                                          ALU.mult).then_inc(s["sin"], 1)
            each_tile(eng, lambda: sine(0), lambda t, p, more: sine(t + 1) if more else None)

        @block.vector
        def _(eng):
            rstd_of_all(pl, eng, s)

            def norm(t):
                eng.wait_ge(s["xturned"], t)
                eng.tensor_scalar(xn[:, :], pl.x[:, t, :] if isinstance(t, int) else pl.x[:, bass.ds(t, 1), :].rearrange("p a d -> p (a d)"),
                                  pl.mv[:, t, 0:1], pl.rstd[:, bass.ds(t, 1)], ALU.subtract, ALU.mult).then_inc(s["xn"], 1)

            def weight_rest(n):
                eng.wait_ge(s["w_head"], n + 1)
                rest_of(eng, *weight_slices(n)).then_inc(s["w_rest"], 1)

            def x_rest(t):
                eng.wait_ge(s["xT"], t + 1)
                rest_of(eng, ps[:, 6, 0:KC * P].rearrange("p (k n) -> p k n", k=KC), xT[0][:, :, :], xT[1][:, :, :]).then_inc(s["x_rest"], 1)

            def output_rest(t):
                for b in range(NB):
                    eng.wait_ge(s["oT"], t * 4 + b + 1)
                    eng.wait_ge(s["output"], t)
                    c = slice(b * S, (b + 1) * S)
                    rest_of(eng, ps[:, 2 + b, :].rearrange("p (c q) -> p c q", q=S), oT[0][:, :, c], oT[1][:, :, c]).then_inc(s["oT_rest"], 1)

            def cosine(t):
                eng.wait_ge(s["qkv"], t * 6 + 5)
                eng.wait_ge(s["turned"], t * 5)
                eng.tensor_tensor(rot[:, :, :, :].rearrange("p h a e -> p h (a e)"), qk[:, :, :, :].rearrange("p h a e -> p h (a e)"),
                                  pl.cst["cos64"][:, None, :].to_broadcast([P, HQ + HKV, E]), ALU.mult).then_inc(s["cos"], 1)

            def rotate(t):
                eng.wait_ge(s["cos"], t + 1)
                eng.wait_ge(s["sin"], (t + 1) * 2 * NW)
                f = lambda a: a.rearrange("p h a e -> p h (a e)")
                eng.tensor_tensor(f(rot[:, 0:HQ]), f(rot[:, 0:HQ]), f(rsin[:, 0:HQ]), ALU.add).then_inc(s["rotated"], 1)
                for a in range(2):
                    eng.tensor_tensor(kd[:, :, a, :], f(rot[:, HQ:]), f(rsin[:, HQ:]), ALU.add).then_inc(s["rotated"], 1)

            def take_turned(t):
                for k in (1, 3):
                    eng.wait_ge(s["turned"], t * 5 + k + 1)
                    eng.wait_ge(s["scored"], t)
                    eng.tensor_copy(qT[:, 4 * k:4 * k + 4, :], ps[:, 6 + (7 + k) % 2, :].rearrange("p (c n) -> p c n", c=4)).then_inc(s["turned_vector"], 1)

            def softmax(t):
                n = t * 6
                eng.wait_ge(s["scored"], t + 1)
                eng.tensor_tensor(sc[:, :, :], ps[:, 0:2, :].rearrange("p a (h k) -> p (a h) k", k=S),
                                  pl.cst["causal"][:, None, :].to_broadcast([P, HQ, S]), ALU.add).then_inc(s["soft"], 1)
                eng.wait_ge(s["soft"], n + 1)
                eng.tensor_reduce(mx[:, :], sc[:, :, :], AX.X, ALU.max).then_inc(s["soft"], 1)
                eng.wait_ge(s["soft"], n + 2)
                eng.tensor_tensor(sc[:, :, :], sc[:, :, :], mx[:, :, None].to_broadcast([P, HQ, S]), ALU.subtract).then_inc(s["soft"], 1)
                eng.wait_ge(s["exp"], t + 1)
                eng.tensor_reduce(sums[:, :], sc[:, :, :], AX.X, ALU.add).then_inc(s["soft"], 1)
                eng.wait_ge(s["soft"], n + 4)
                eng.reciprocal(rinv[:, :], sums[:, :]).then_inc(s["soft"], 1)
                eng.wait_ge(s["soft"], n + 5)
                eng.tensor_tensor(sc[:, :, :], sc[:, :, :], rinv[:, :, None].to_broadcast([P, HQ, S]), ALU.mult).then_inc(s["soft"], 1)
                eng.wait_ge(s["soft"], n + 6)
                eng.wait_ge(s["valued"], t * 4)
                eng.transpose(pT[:, :, :].rearrange("p h q -> p (h q)"), sc[:, :, :].rearrange("p h k -> p (h k)")).then_inc(s["pT"], 1)

            def add(t):
                eng.wait_ge(s["output"], t + 1)
                xt = pl.x[:, t, :]
                eng.tensor_tensor(xt, ps[:, 6, 0:D], xt, ALU.add).then_inc(s["added"], 1)
                eng.wait_ge(s["added"], t + 1)
                token_stats(pl, eng, t)

            def first():
                norm(0)
                weight_rest(0)
                x_rest(0)
                for n in range(1, NW + 4):
                    weight_rest(n)
                cosine(0)
                rotate(0)
                take_turned(0)
                norm(1)

            def step(t, p, more):
                if more:
                    x_rest(t + 1)
                softmax(t)
                if more:
                    cosine(t + 1)
                    rotate(t + 1)
                if not (isinstance(t, int) and t == 0):
                    add(t - 1)
                if more:
                    take_turned(t + 1)
                if not isinstance(t, int) or t + 2 < NT:
                    norm(t + 2)
                output_rest(t)
                if not more:
                    add(t)
            each_tile(eng, first, step)
            pl.stats_n += 3 * NT

        @block.scalar
        def _(eng):
            eng.preload_act_table(ACT.Exp)

            def take_xT(t):
                eng.wait_ge(s["xturned"], t + 1)
                eng.wait_ge(s["projected"], t * NW)
                eng.activation(xT[0][:, :, :].bitcast(F32R), ps[:, 6, 0:KC * P].rearrange("p (k n) -> p k n", k=KC), ACT.Copy).then_inc(s["xT"], 1)

            def take_qkv(t, p, lo, hi):
                for k in range(lo, hi):
                    eng.wait_ge(s["projected"], t * NW + k + 1)
                    eng.wait_ge(s["cos"], t)
                    eng.wait_ge(s["sin"], 2 * NW * t)
                    bank = ps[:, 6 + (1 + k) % 2, :]
                    if k < NW - 1:
                        eng.activation(qk[:, 8 * k:8 * k + 8, :, :].rearrange("p h a e -> p (h a e)"), bank, ACT.Copy).then_inc(s["qkv"], 1)
                    else:
                        eng.activation(qk[:, HQ:, :, :].rearrange("p h a e -> p (h a e)"), bank[:, 0:NKV], ACT.Copy).then_inc(s["qkv"], 1)
                        eng.activation(v[p][:, :], bank[:, NKV:2 * NKV], ACT.Copy).then_inc(s["qkv"], 1)

            def take_turned(t):
                for k in (0, 2, 4):
                    eng.wait_ge(s["turned"], t * 5 + k + 1)
                    eng.wait_ge(s["scored"], t)
                    dst = qT[:, 4 * k:4 * k + 4, :] if k < 4 else kT[:, :, :]
                    eng.activation(dst, ps[:, 6 + (7 + k) % 2, :].rearrange("p (c n) -> p c n", c=4), ACT.Copy).then_inc(s["turned_scalar"], 1)

            def weight_head(n):
                if n in (0, NW):
                    eng.wait_ge(s["w_in"] if n == 0 else s["wo_in"], 16)
                src, dst, _ = weight_slices(n)
                eng.activation(dst.bitcast(F32R), src, ACT.Copy).then_inc(s["w_head"], 1)

            def first():
                weight_head(0)
                take_xT(0)
                for n in range(1, NW + 4):
                    weight_head(n)
                take_qkv(0, 0, 0, NW)
                take_turned(0)

            def step(t, p, more):
                if more:
                    take_xT(t + 1)
                    take_qkv(t + 1, 1 - p, 0, 2)
                eng.wait_ge(s["soft"], t * 6 + 3)
                eng.activation(sc[:, :, :], sc[:, :, :], ACT.Exp, scale=SC).then_inc(s["exp"], 1)
                if more:
                    take_qkv(t + 1, 1 - p, 2, NW)
                for b in range(NB):
                    eng.wait_ge(s["valued"], t * 4 + b + 1)
                    eng.wait_ge(s["output"], t)
                    eng.activation(oT[0][:, :, b * S:(b + 1) * S].bitcast(F32R), ps[:, 2 + b, :].rearrange("p (c q) -> p c q", q=S),
                                   ACT.Copy).then_inc(s["oT"], 1)
                if more:
                    take_turned(t + 1)
            each_tile(eng, first, step)

        @block.tensor
        def _(eng):
            def turn_x(t):
                eng.wait_ge(s["xn"], t + 1)
                eng.wait_ge(s["turned_vector"], 2 * t)
                for k in range(KC):
                    mm = eng.transpose(ps[:, 6, k * P:(k + 1) * P], xn[:, k * P:(k + 1) * P], pl.ident[:, :])
                mm.then_inc(s["xturned"], 1)

            def project(t):
                eng.wait_ge(s["x_rest"], t + 1)
                eng.wait_ge(s["turned_scalar"], 3 * t)
                for n in range(NW):
                    if n >= 2:
                        eng.wait_ge(s["qkv"], t * 6 + n - 1)
                    if isinstance(t, int) and t == 0:
                        eng.wait_ge(s["w_rest"], n + 1)
                    for k in range(KC):
                        mm = split_product(eng, ps[:, 6 + (1 + n) % 2, :], [x[:, k, :] for x in xT],
                                           [x[:, k, n * 512:(n + 1) * 512] for x in wp], k == 0, k == KC - 1)
                    mm.then_inc(s["projected"], 1)

            def turn(t):
                eng.wait_ge(s["rotated"], t * 3 + 3)
                for n in range(5):
                    if n == 0:
                        eng.wait_ge(s["qkv"], t * 6 + 6)
                    elif n == 1:
                        if not (isinstance(t, int) and t == 0):
                            eng.wait_ge(s["added"], t - 1)
                    elif n % 2 == 0:
                        eng.wait_ge(s["turned_scalar"], t * 3 + n // 2)
                    else:
                        eng.wait_ge(s["turned_vector"], t * 2 + 1)
                    for j in range(4):
                        src = rot[:, 8 * n + 2 * j:8 * n + 2 * j + 2, :, :].rearrange("p h a e -> p (h a e)") if n < 4 else \
                            kd[:, j, :, :].rearrange("p a e -> p (a e)")
                        mm = eng.transpose(ps[:, 6 + (7 + n) % 2, j * P:(j + 1) * P], src, pl.ident[:, :])
                    mm.then_inc(s["turned"], 1)

            def output(t, more):
                eng.wait_ge(s["oT_rest"], 4 * t + 4)
                if more:
                    eng.wait_ge(s["qkv"], (t + 2) * 6 + 4)
                else:
                    eng.wait_ge(s["added"], t)
                for c in range(NQ // P):
                    mm = split_product(eng, ps[:, 6, 0:D], [x[:, c, :] for x in oT], [x[:, c, :] for x in wop], c == 0, c == NQ // P - 1)
                mm.then_inc(s["output"], 1)

            def first():
                turn_x(0)
                project(0)
                turn(0)
                eng.wait_ge(s["w_rest"], NW + 4)

            def step(t, p, more):
                eng.wait_ge(s["turned_scalar"], 3 * t + 3)
                eng.wait_ge(s["turned_vector"], 2 * t + 2)
                if more:
                    turn_x(t + 1)
                eng.wait_ge(s["soft"], 6 * t)
                apart(pl, eng)
                for h in range(HQ):
                    a = (h % 2) * E
                    for b in range(NB):
                        mm = eng.matmul(ps[b * S:(b + 1) * S, h % 2, (h // 2) * S:(h // 2 + 1) * S],
                                        qT[a:a + E, h // 2, b * S:(b + 1) * S], kT[a:a + E, h // 8, b * S:(b + 1) * S],
                                        start=True, stop=True)
                mm.then_inc(s["scored"], 1)
                if more:
                    project(t + 1)
                if not (isinstance(t, int) and t == 0):
                    output(t - 1, more)
                eng.wait_ge(s["pT"], t + 1)
                eng.wait_ge(s["oT_rest"], 4 * t)
                for b in range(NB):
                    for k in range(HKV):
                        for a in range(2):
                            mm = eng.matmul(ps[a * E:(a + 1) * E, 2 + b, k * P:(k + 1) * P], v[p][b * S:(b + 1) * S, k * E:(k + 1) * E],
                                            pT[b * S:(b + 1) * S, NQ // P * a + 4 * k:NQ // P * a + 4 * k + 4, :], start=True, stop=True)
                    mm.then_inc(s["valued"], 1)
                if more:
                    turn(t + 1)
                else:
                    output(t, False)
            each_tile(eng, first, step)


def experts(pl):
    nc, ps = pl.nc, pl.ps
    NE, F, TOPK, EB = 32, 96, 4, 4
    W = EB * F
    NS = NE // EB
    CB = W // P
    pl.end = L_OFF
    parts, wraw = [], []
    for k, shape in (("wg", [P, KC, NE * F]), ("wu", [P, KC, NE * F]), ("wd", [P, NE * F // P, D])):
        head = pl.at(f"ex_{k}_head", shape, F32, pl.end)
        wraw.append(pl.at(f"ex_{k}_loaded", shape, F32, pl.end))
        parts.append((head, pl.at(f"ex_{k}_rest", shape, F32, pl.end - 4 * KC * NE * F)))
    wg, wu, wd = parts
    gate = pl.at("ex_gate", [P, KC, NE], F32, pl.end)
    xn = pl.at("ex_xn", [P, D], F32, pl.end)
    xT = [pl.at(f"ex_xT{j}", [P, KC, P], F32, pl.end) for j in range(2)]
    sg = [pl.at(f"ex_sg{j}", [P, W], F32, pl.end) for j in range(2)]
    h = [pl.at(f"ex_h{j}", [P, W], F32, pl.end) for j in range(2)]
    xTp = [[pl.at(f"ex_xT{j}_{k}", [P, KC, P], F32, pl.end) for k in ("head", "rest")] for j in range(2)]
    hTp = [[pl.at(f"ex_hT{j}_{k}", [P, CB, P], F32, pl.end) for k in ("head", "rest")] for j in range(2)]
    route = pl.at("ex_route", [P, NT, NE], F32, pl.end)
    e, gt, eq, cum, le, one = (pl.at(f"ex_{k}", [P, NE], F32, pl.end) for k in ("e", "gt", "eq", "cum", "le", "one"))
    m8 = pl.at("ex_m8", [P, 8], F32, pl.end)
    nm, cnt, tot, inv = (pl.at(f"ex_{k}", [P, 1], F32, pl.end) for k in ("nm", "cnt", "tot", "inv"))
    s = {k: pl.sem(f"ex_{k}") for k in (
        "gate_in", "w_head", "w_rest", "wd_rest", "x_parts", "h_head", "h_rest", "down", "rs_in", "rstd", "xn", "xturned", "xT", "logits", "routed", "exp", "one", "gates", "ups", "silu",
        "gated", "turned", "added")}
    w_in = [pl.sem(f"ex_weights_loaded{j}") for j in range(NS)]
    LW = KC * 2 * 688 + 6 * D
    PIECE = LW // NT
    NLUT = 16
    assert LW % NT == 0 and NLUT == 2 * NS
    idx, acc, hit = ([pl.at(f"lu_{k}{j}", [P, PIECE], dt, pl.end) for j in range(2)] for k, dt in (("idx", I32), ("acc", F32), ("hit", F32)))
    lut = pl.at("lu_lut", [P, NLUT], F32, pl.end)
    kv = pl.at("lu_entry", [P, NLUT], F32, pl.end)
    pl.lut_dram = nc.dram_tensor("lut_scratch", (P, LW), F32, kind="Internal").ap()
    l_in, l_step = pl.sem("lu_in"), pl.sem("lu_step")
    l_stored = [pl.sem(f"lu_stored{j}") for j in range(2)]
    idx_in = [pl.sem(f"lu_index_loaded{j}") for j in range(2)]
    NL = 2 * NLUT - 1
    NR = 11

    def each_tile(eng, first, step):
        first()
        for t in range(2):
            step(t, t, True)
        with eng.Fori(1, NT // 2 - 1) as u:
            for p in range(2):
                step(u * 2 + p, p, True)
        for p in range(2):
            step(NT - 2 + p, p, p == 0)

    with nc.Block() as block:
        @block.sync
        def _(eng):
            eng.dma_start(gate[:, :, :], pl.ap["L0_gate"]).then_inc(s["gate_in"], 16)
            for j in range(NS):
                c, d = slice(j * W, (j + 1) * W), slice(j * CB, (j + 1) * CB)
                eng.dma_start(wraw[0][:, :, c], pl.ap["L0_wg"][:, :, c]).then_inc(w_in[j], 16)
                eng.dma_start(wraw[1][:, :, c], pl.ap["L0_wu"][:, :, c]).then_inc(w_in[j], 16)
                eng.dma_start(wraw[2][:, d, :], pl.ap["L0_wd"][:, d, :]).then_inc(w_in[j], 16)
                if j == 0:
                    eng.dma_start(lut[:, :], pl.ap["L1_lut"].to_broadcast([P, NLUT])).then_inc(l_in, 16)
                    eng.dma_start(kv[:, :], pl.ap["entries"]).then_inc(l_in, 16)
                    for p in range(2):
                        eng.dma_start(idx[p][:, :], pl.ap["L1_idx"][:, p * PIECE:(p + 1) * PIECE]).then_inc(idx_in[p], 16)

            def piece_done(t, p, more):
                eng.wait_ge(l_step, (t + 1) * NL)
                eng.dma_start(pl.lut_dram[:, bass.ds(t * PIECE, PIECE)], acc[p][:, :]).then_inc(l_stored[p], 16)
                if more:
                    eng.dma_start(idx[p][:, :], pl.ap["L1_idx"][:, bass.ds((t + 2) * PIECE, PIECE)]).then_inc(idx_in[p], 16)
            with eng.Fori(0, NT // 2 - 1) as u:
                for p in range(2):
                    piece_done(u * 2 + p, p, True)
            for p in range(2):
                piece_done(NT - 2 + p, p, False)
            for p in range(2):
                eng.wait_ge(l_stored[p], 8 * NT)

        @block.gpsimd
        def _(eng):
            pow_of_all(pl, eng, s)

            for j in range(NS):
                d = slice(j * CB, (j + 1) * CB)
                eng.wait_ge(s["w_head"], 3 * j + 3)
                rest_of(eng, wraw[2][:, d, :], wd[0][:, d, :], wd[1][:, d, :]).then_inc(s["wd_rest"], 1)

        @block.vector
        def _(eng):
            eng.memset(one[:, :], 1.0).then_inc(s["one"], 1)
            rstd_of_all(pl, eng, s)

            def norm(t):
                eng.wait_ge(s["xturned"], t)
                eng.tensor_scalar(xn[:, :], pl.x[:, t, :], pl.mv[:, t, 0:1], pl.rstd[:, bass.ds(t, 1)],
                                  ALU.subtract, ALU.mult).then_inc(s["xn"], 1)

            def logit_maximum(t):
                eng.wait_ge(s["logits"], t + 1)
                eng.tensor_reduce(nm[:, :], ps[:, 7, KC * P:KC * P + NE], AX.X, ALU.max, negate=True).then_inc(s["routed"], 1)

            def routing(t):
                n = t * NR
                r = s["routed"]
                eng.wait_ge(s["exp"], t + 1)
                apart(pl, eng)
                eng.max(m8[:, :], e[:, :]).then_inc(r, 1)
                eng.wait_ge(r, n + 2)
                kth = m8[:, TOPK - 1:TOPK]
                eng.tensor_scalar(gt[:, :], e[:, :], kth, None, ALU.is_gt).then_inc(r, 1)
                eng.tensor_scalar(eq[:, :], e[:, :], kth, None, ALU.is_equal).then_inc(r, 1)
                eng.wait_ge(r, n + 4)
                eng.tensor_reduce(cnt[:, :], gt[:, :], AX.X, ALU.add).then_inc(r, 1)
                eng.tensor_tensor_scan(cum[:, :], one[:, :], eq[:, :], 0.0, ALU.mult, ALU.add).then_inc(r, 1)

            def routing_weights(t):
                n = t * NR
                r = s["routed"]
                eng.wait_ge(r, n + 6)
                eng.tensor_scalar(le[:, :], cum[:, :], cnt[:, 0:1], float(TOPK), ALU.add, ALU.is_le).then_inc(r, 1)
                eng.wait_ge(r, n + 7)
                eng.tensor_tensor(le[:, :], le[:, :], eq[:, :], ALU.mult).then_inc(r, 1)
                eng.wait_ge(r, n + 8)
                eng.tensor_tensor(le[:, :], le[:, :], gt[:, :], ALU.add).then_inc(r, 1)
                eng.wait_ge(r, n + 9)
                eng.tensor_tensor_reduce(out=le[:, :], in0=le[:, :], in1=e[:, :], scale=1.0, scalar=0.0,
                                         op0=ALU.mult, op1=ALU.add, accum_out=tot[:, :]).then_inc(r, 1)
                eng.wait_ge(r, n + 10)
                eng.reciprocal(inv[:, :], tot[:, :]).then_inc(r, 1)
                eng.wait_ge(r, n + 11)
                eng.tensor_scalar(route[:, t, :], le[:, :], inv[:, 0:1], None, ALU.mult).then_inc(s["one"], 1)

            def look_up(t, p, j):
                n = t * NL + max(0, 4 * j - 1)
                if j == 0:
                    eng.wait_ge(idx_in[p], (t - p) * 8 + 16)
                    if not early(t):
                        eng.wait_ge(l_stored[p], (t - p) * 8)
                eng.wait_ge(l_step, n)
                for i in range(2):
                    e = 2 * j + i
                    out = acc[p] if e == 0 else hit[i]
                    eng.tensor_scalar(out[:, :], idx[p][:, :], kv[:, e:e + 1], lut[:, e:e + 1], ALU.is_equal, ALU.mult).then_inc(l_step, 1)
                for i in range(2):
                    if 2 * j + i > 0:
                        eng.wait_ge(l_step, n + 2 + (i if j > 0 else 0))
                        eng.tensor_tensor(acc[p][:, :], acc[p][:, :], hit[i][:, :], ALU.add).then_inc(l_step, 1)

            def weight_parts(j):
                eng.wait_ge(w_in[j], 48)
                c, d = slice(j * W, (j + 1) * W), slice(j * CB, (j + 1) * CB)
                for i, (w, part) in enumerate(((wg, (slice(None), slice(None), c)), (wu, (slice(None), slice(None), c)),
                                               (wd, (slice(None), d, slice(None))))):
                    leading_bits(eng, wraw[i][part], w[0][part]).then_inc(s["w_head"], 1)
                    if i < 2:
                        eng.wait_ge(s["w_head"], 3 * j + i + 1)
                        rest_of(eng, wraw[i][part], w[0][part], w[1][part]).then_inc(s["w_rest"], 1)

            def x_parts(t, p):
                eng.wait_ge(s["xT"], t + 1)
                leading_bits(eng, xT[p][:, :, :], xTp[p][0][:, :, :]).then_inc(s["x_parts"], 1)
                eng.wait_ge(s["x_parts"], 2 * t + 1)
                rest_of(eng, xT[p][:, :, :], xTp[p][0][:, :, :], xTp[p][1][:, :, :]).then_inc(s["x_parts"], 1)

            def add_up(t):
                eng.wait_ge(s["down"], (t + 1) * NS)
                eng.tensor_tensor(pl.x[:, t, :], ps[:, 6, 0:D], pl.x[:, t, :], ALU.add).then_inc(s["added"], 1)
                eng.wait_ge(s["added"], t + 1)
                token_stats(pl, eng, t)

            def first():
                norm(0)
                weight_parts(0)
                x_parts(0, 0)
                logit_maximum(0)
                routing(0)
                routing_weights(0)
                weight_parts(1)
                eng.wait_ge(l_in, 32)

            def step(t, p, more):
                opening = isinstance(t, int) and t == 0
                for j in range(NS):
                    k = t * NS + j
                    if j == 0:
                        eng.wait_ge(s["one"], t + 2)
                    eng.wait_ge(s["silu"], k + 1)
                    eng.wait_ge(s["ups"], k + 1)
                    for i in range(EB):
                        ex = j * EB + i
                        st = eng.scalar_tensor_tensor(out=h[j % 2][:, i * F:(i + 1) * F], in0=ps[:, 2 + j % 2, i * F:(i + 1) * F],
                                                      scalar=route[:, t, ex:ex + 1], in1=sg[j % 2][:, i * F:(i + 1) * F],
                                                      op0=ALU.mult, op1=ALU.mult)
                    st.then_inc(s["gated"], 1)
                    if j == 1 and not opening:
                        add_up(t - 1)
                    if opening and j + 2 < NS:
                        weight_parts(j + 2)
                    if more and j == 0:
                        norm(t + 1)
                    if more and j == 5:
                        logit_maximum(t + 1)
                    if more and j == 6:
                        routing(t + 1)
                    if more and j == 7:
                        routing_weights(t + 1)
                    look_up(t, p, j)
                    eng.wait_ge(s["h_head"], k + 1)
                    if not (isinstance(t, int) and k < 2):
                        eng.wait_ge(s["down"], k - 1)
                    rest_of(eng, ps[:, 4 + j % 2, 0:W].rearrange("p (c n) -> p c n", c=CB), hTp[j % 2][0][:, :, :],
                            hTp[j % 2][1][:, :, :]).then_inc(s["h_rest"], 1)
                    if more and j == 3:
                        x_parts(t + 1, 1 - p)
                if not more:
                    add_up(t)
            each_tile(eng, first, step)
            pl.stats_n += 3 * NT

        @block.scalar
        def _(eng):
            def take_xT(t, p):
                eng.wait_ge(s["xturned"], t + 1)
                eng.activation(xT[p][:, :, :], ps[:, 7, 0:KC * P].rearrange("p (k n) -> p k n", k=KC), ACT.Copy).then_inc(s["xT"], 1)

            def silu(k, q):
                eng.wait_ge(s["gates"], k + 1)
                if not (isinstance(k, int) and k < 2):
                    eng.wait_ge(s["gated"], k - 1)
                eng.activation(sg[q][:, :], ps[:, q, 0:W], ACT.Silu).then_inc(s["silu"], 1)

            def exp_logits(t):
                eng.wait_ge(s["routed"], t * NR + 1)
                eng.activation(e[:, :], ps[:, 7, KC * P:KC * P + NE], ACT.Exp, bias=nm[:, 0:1]).then_inc(s["exp"], 1)

            def first():
                take_xT(0, 0)
                exp_logits(0)
                silu(0, 0)

            def step(t, p, more):
                for j in range(NS):
                    k = t * NS + j
                    if j + 1 < NS or more:
                        silu(k + 1, (j + 1) % 2)
                    eng.wait_ge(s["turned"], k + 1)
                    if not (isinstance(t, int) and k < 2):
                        eng.wait_ge(s["down"], k - 1)
                    eng.activation(hTp[j % 2][0][:, :, :].bitcast(F32R), ps[:, 4 + j % 2, 0:W].rearrange("p (c n) -> p c n", c=CB),
                                   ACT.Copy).then_inc(s["h_head"], 1)
                    if more and j == 2:
                        take_xT(t + 1, 1 - p)
                    if more and j == 5:
                        exp_logits(t + 1)
            each_tile(eng, first, step)

        @block.tensor
        def _(eng):
            def turn_x(t):
                eng.wait_ge(s["xn"], t + 1)
                for k in range(KC):
                    mm = eng.transpose(ps[:, 7, k * P:(k + 1) * P], xn[:, k * P:(k + 1) * P], pl.ident[:, :])
                mm.then_inc(s["xturned"], 1)

            def logits(t, p):
                eng.wait_ge(s["xT"], t + 1)
                for k in range(KC):
                    mm = eng.matmul(ps[:, 7, KC * P:KC * P + NE], xT[p][:, k, :], gate[:, k, :], start=(k == 0), stop=(k == KC - 1))
                mm.then_inc(s["logits"], 1)

            def product(w, bank, p, j, sem):
                for k in range(KC):
                    mm = split_product(eng, ps[:, bank, 0:W], [x[:, k, :] for x in xTp[p]], [x[:, k, j * W:(j + 1) * W] for x in w],
                                       k == 0, k == KC - 1)
                mm.then_inc(sem, 1)

            def down(k, j):
                eng.wait_ge(s["h_rest"], k + 1)
                if isinstance(k, int) and k < NS:
                    eng.wait_ge(s["wd_rest"], j + 1)
                for c in range(CB):
                    n = j * CB + c
                    mm = split_product(eng, ps[:, 6, 0:D], [x[:, c, :] for x in hTp[j % 2]], [x[:, n, :] for x in wd],
                                       n == 0, n == NS * CB - 1)
                mm.then_inc(s["down"], 1)

            def first():
                turn_x(0)
                eng.wait_ge(s["gate_in"], 16)
                logits(0, 0)
                eng.wait_ge(s["x_parts"], 2)
                eng.wait_ge(s["w_rest"], 1)
                product(wg, 0, 0, 0, s["gates"])
                eng.wait_ge(s["w_rest"], 2)
                product(wu, 2, 0, 0, s["ups"])

            def step(t, p, more):
                opening = isinstance(t, int) and t == 0
                for j in range(NS):
                    k = t * NS + j
                    nxt = j + 1 < NS or more
                    np_, nj = (p, j + 1) if j + 1 < NS else (1 - p, 0)
                    if nxt:
                        eng.wait_ge(s["gated"], k)
                        if opening and j + 1 < NS:
                            eng.wait_ge(s["w_rest"], 2 * j + 3)
                        if nj == 0:
                            eng.wait_ge(s["x_parts"], t * 2 + 4)
                        product(wg, nj % 2, np_, nj, s["gates"])
                    eng.wait_ge(s["gated"], k + 1)
                    for c in range(CB):
                        mm = eng.transpose(ps[:, 4 + j % 2, c * P:(c + 1) * P], h[j % 2][:, c * P:(c + 1) * P], pl.ident[:, :])
                    mm.then_inc(s["turned"], 1)
                    if nxt:
                        if opening and j + 1 < NS:
                            eng.wait_ge(s["w_rest"], 2 * j + 4)
                        product(wu, 2 + nj % 2, np_, nj, s["ups"])
                    if j == 1:
                        eng.wait_ge(s["added"], t)
                    if j > 0 or not opening:
                        down(k - 1, (j - 1) % NS)
                    if more and j == 2:
                        turn_x(t + 1)
                    if more and j == 4:
                        logits(t + 1, 1 - p)
                if not more:
                    down(t * NS + NS - 1, NS - 1)
            each_tile(eng, first, step)


def inverse_root(pl, eng, x, y, t, sem, n, root):
    eng.wait_ge(root, 1)
    eng.reciprocal(y, y).then_inc(sem, 1)
    eng.wait_ge(sem, n + 1)
    eng.tensor_tensor(t, y, y, ALU.mult).then_inc(sem, 1)
    eng.wait_ge(sem, n + 2)
    eng.tensor_tensor(t, t, x, ALU.mult).then_inc(sem, 1)
    eng.wait_ge(sem, n + 3)
    eng.tensor_scalar(t, t, -0.5, 1.5, ALU.mult, ALU.add).then_inc(sem, 1)
    eng.wait_ge(sem, n + 4)
    eng.tensor_tensor(y, y, t, ALU.mult).then_inc(sem, 1)
    eng.wait_ge(sem, n + 5)


def key_norms(pl):
    nc, ps = pl.nc, pl.ps
    R = B * CS
    NC = -(-R // P)
    LAST = R - (NC - 1) * P
    G = 4
    pl.rq = pl.at("rq", [P, B, GQ], F32, L_OFF)
    pl.pick = pl.at("pick", [3 * NH, GQ, P], BF16, pl.end)
    pl.low1_off = pl.end
    pl.WkTg = pl.at("WkTg", [P, NH, CD], F32, pl.end)
    pl.tmp1_off = pl.end
    sq = [pl.at(f"kn_sq{j}", [P, 2, 512], F32, pl.end) for j in range(4)]
    assert pl.end <= QO_OFF
    pickf = pl.at("kn_pickf", [3 * NH, GQ, P], F32, QO_OFF)
    keys_off = pl.end
    wk = pl.at("kn_wk", [P, NH * HD], F32, keys_off)
    wkp = [pl.at(f"kn_wk_{k}", [P, NH * HD], F32, pl.end) for k in ("head", "rest")]
    ct, cth, ctl = ([pl.at(f"kn_{k}{j}", [P, G * P], F32, pl.end) for j in range(2)] for k in ("ctx", "ctx_head", "ctx_rest"))
    wv = pl.at("kn_wv", [P, NH, CD], F32, pl.end)
    wo = pl.at("kn_wo", [P, NH, D], F32, pl.end)
    bw = pl.at("kn_bw", [P, NH, D], F32, pl.end)
    g2 = pl.at("kn_g", [P, 2], F32, pl.end)
    gg = pl.at("kn_gg", [P, 1], F32, pl.end)
    ss = pl.at("kn_ss", [P, NC, NH], F32, pl.end)
    rs, nt = (pl.at(f"kn_{k}", [P, NC, NH], F32, pl.end) for k in ("rs", "newton"))
    parts = pl.at("kn_parts", [P, NC, 3, NH], BF16, pl.end)
    rkT = pl.at("kn_rkT", [3 * NH, NC * P], BF16, keys_off)
    pl.rk_dram = nc.dram_tensor("rk_scratch", (3 * NH, R), BF16, kind="Internal").ap()
    s = {k: pl.sem(f"kn_{k}") for k in (
        "wk_in", "w_in", "k", "sq", "ss", "made", "made_v", "made_s", "fin", "root", "newton", "turned", "rk_s", "rk_v", "stored", "mh", "gain", "wk_parts", "heads", "rests")}
    c_in = [pl.sem(f"kn_ctx_loaded{j}") for j in range(2)]
    pl.bw1_dram = nc.dram_tensor("bw1_scratch", (P, NH, D), F32, kind="Internal").ap()
    NG = (NC - 1) // G
    NB2 = NH // 2
    assert (NC - 1) % G == 0 and NG % 2 == 0

    with nc.Block() as block:
        @block.sync
        def _(eng):
            eng.dma_start(wk[:, :], pl.ap["L1_Wk"]).then_inc(s["wk_in"], 16)

            def load(u, p):
                if not isinstance(u, int):
                    eng.wait_ge(s["rests"], u * 2 + p - 1)
                eng.dma_start(ct[p][:, :], pl.ap["ctxT"][:, bass.ds((u * 2 + p) * G * P, G * P)]).then_inc(c_in[p], 16)
            load(0, 0)
            load(0, 1)
            for d, n in ((wv, "L1_WvT"), (wo, "L1_Wo"), (pl.WkTg, "L1_WkT"), (pickf, "pick")):
                eng.dma_start(d[:, :, :], pl.ap[n]).then_inc(s["w_in"], 16)
            eng.dma_start(g2[:, :], pl.ap["L1_g"]).then_inc(s["w_in"], 16)
            with eng.Fori(1, NG // 2) as u:
                for p in range(2):
                    load(u, p)
            eng.wait_ge(s["rests"], NG - 1)
            eng.dma_start(ct[0][:, 0:LAST], pl.ap["ctxT"][:, NG * G * P:R]).then_inc(c_in[0], 16)
            eng.wait_ge(s["made_s"], NB2 // 2)
            eng.wait_ge(s["made_v"], NB2 // 2)
            eng.dma_start(pl.bw1_dram, bw[:, :, :]).then_inc(s["stored"], 16)
            eng.wait_ge(s["rk_s"], (NC - 1) // 8)
            eng.wait_ge(s["rk_v"], (NC - 1) // 8 + 1)
            eng.dma_start(pl.rk_dram, rkT[:, 0:R]).then_inc(s["stored"], 16)
            eng.wait_ge(s["stored"], 32)

        @block.gpsimd
        def _(eng):
            eng.memset(ss[:, NC - 1, :], 1.0).then_inc(s["mh"], 1)

            def rest(g, p, m):
                eng.wait_ge(s["heads"], g + 1)
                rest_of(eng, ct[p][:, 0:m], cth[p][:, 0:m], ctl[p][:, 0:m]).then_inc(s["rests"], 1)
            with eng.Fori(0, NG // 2) as u:
                for p in range(2):
                    rest(u * 2 + p, p, G * P)
            rest(NG, 0, LAST)

        @block.scalar
        def _(eng):
            eng.preload_act_table(ACT.Square)

            def squares(c, odd, m):
                for n in range(2):
                    k = c * 2 + n
                    eng.wait_ge(s["k"], k + 1)
                    if not (isinstance(c, int) and c < 2):
                        eng.wait_ge(s["ss"], k - 3)
                    b = 4 * odd + 2 * n
                    eng.activation(sq[2 * odd + n][0:m, :, :], ps[0:m, b:b + 2, :], ACT.Square).then_inc(s["sq"], 1)
            squares(0, 0, P)
            squares(1, 1, P)
            with eng.Fori(1, (NC - 1) // 2) as u:
                squares(u * 2, 0, P)
                squares(u * 2 + 1, 1, P)
            squares(NC - 1, 0, LAST)
            eng.wait_ge(s["fin"], 1)
            eng.activation(rs[:, :, :], ss[:, :, :], ACT.Sqrt).then_inc(s["root"], 1)
            for k in range(1, NB2, 2):
                eng.wait_ge(s["made"], k + 1)
                eng.activation(bw[:, 2 * k:2 * k + 2, :], ps[:, 4 + k % 4, :].rearrange("p (h c) -> p h c", h=2), ACT.Copy).then_inc(s["made_s"], 1)
            for k in range(0, (NC - 1) // 8, 1):
                eng.wait_ge(s["turned"], 2 * k + 1)
                eng.activation(rkT[:, 8 * k * P:(8 * k + 4) * P], ps[0:3 * NH, 0, 0:256].bitcast(BF16), ACT.Copy).then_inc(s["rk_s"], 1)

        @block.vector
        def _(eng):
            eng.wait_ge(s["wk_in"], 16)
            split(eng, wk[:, :], wkp[0][:, :], wkp[1][:, :], s["wk_parts"], 0)

            def head(u, p, m):
                g = u * 2 + p
                eng.wait_ge(c_in[p], u * 16 + 16)
                if not (isinstance(u, int) and u == 0):
                    eng.wait_ge(s["k"], (g - 1) * 2 * G)
                leading_bits(eng, ct[p][:, 0:m], cth[p][:, 0:m]).then_inc(s["heads"], 1)
            head(0, 0, G * P)
            head(0, 1, G * P)
            eng.wait_ge(s["w_in"], 80)
            eng.tensor_copy(pl.pick[:, :, :], pickf[:, :, :]).then_inc(s["gain"], 1)
            eng.tensor_tensor(gg[:, :], g2[:, 0:1], g2[:, 1:2], ALU.mult).then_inc(s["gain"], 1)
            eng.wait_ge(s["gain"], 2)
            eng.tensor_scalar(pl.WkTg[:, :, :], pl.WkTg[:, :, :], gg[:, 0:1], None, ALU.mult).then_inc(s["gain"], 1)

            def sums(c, odd, m):
                for n in range(2):
                    eng.wait_ge(s["sq"], c * 2 + n + 1)
                    eng.tensor_reduce(ss[0:m, c, 8 * n:8 * n + 8], sq[2 * odd + n][0:m, :, :].rearrange("p b (h d) -> p (b h) d", h=4),
                                      AX.X, ALU.add).then_inc(s["ss"], 1)
            def sums_of_load(u, p):
                for j in range(G):
                    sums((u * 2 + p) * G + j, j % 2, P)
            with eng.Fori(0, NG // 2 - 1) as u:
                for p in range(2):
                    sums_of_load(u, p)
                    head(u + 1, p, G * P)
            sums_of_load(NG // 2 - 1, 0)
            head(NG // 2, 0, LAST)
            sums_of_load(NG // 2 - 1, 1)
            eng.wait_ge(s["mh"], 1)
            sums(NC - 1, 0, LAST)
            eng.wait_ge(s["ss"], 2 * NC)
            eng.tensor_scalar(ss[:, :, :], ss[:, :, :], 1.0 / HD, EPS, ALU.mult, ALU.add).then_inc(s["fin"], 1)
            for k in range(0, NB2, 2):
                eng.wait_ge(s["made"], k + 1)
                eng.tensor_copy(bw[:, 2 * k:2 * k + 2, :], ps[:, 4 + k % 4, :].rearrange("p (h c) -> p h c", h=2)).then_inc(s["made_v"], 1)
            inverse_root(pl, eng, ss[:, :, :], rs[:, :, :], nt[:, :, :], s["newton"], 0, s["root"])
            for j in range(3):
                eng.tensor_copy(parts[:, :, j, :], rs[:, :, :]).then_inc(s["fin"], 1)
                if j < 2:
                    eng.wait_ge(s["fin"], 2 * j + 2)
                    eng.tensor_tensor(rs[:, :, :], rs[:, :, :], parts[:, :, j, :], ALU.subtract).then_inc(s["fin"], 1)
                    eng.wait_ge(s["fin"], 2 * j + 3)
            for k in range((NC - 1) // 8):
                eng.wait_ge(s["turned"], 2 * k + 2)
                eng.tensor_copy(rkT[:, (8 * k + 4) * P:(8 * k + 8) * P], ps[0:3 * NH, 1, 0:256].bitcast(BF16)).then_inc(s["rk_v"], 1)
            eng.wait_ge(s["turned"], 2 * ((NC - 1) // 8) + 1)
            eng.tensor_copy(rkT[:, (NC - 1) * P:R], ps[0:3 * NH, 2, 0:LAST // 2].bitcast(BF16)).then_inc(s["rk_v"], 1)

        @block.tensor
        def _(eng):
            def keys(c, p, j, m):
                for n in range(2):
                    if not (isinstance(c, int) and c < 2):
                        eng.wait_ge(s["sq"], c * 2 + n - 3)
                    for a in range(2):
                        w = (2 * n + a) * 512
                        mm = split_product(eng, ps[0:m, 4 * (j % 2) + 2 * n + a, :], [x[p][:, j * P:j * P + m] for x in (cth, ctl)],
                                           [x[:, w:w + 512] for x in wkp])
                    mm.then_inc(s["k"], 1)

            eng.wait_ge(s["wk_parts"], 2)
            for p in range(2):
                eng.wait_ge(s["rests"], p + 1)
                for j in range(G):
                    keys(p * G + j, p, j, P)
            with eng.Fori(1, NG // 2) as u:
                for p in range(2):
                    eng.wait_ge(s["rests"], u * 2 + p + 1)
                    for j in range(G):
                        keys(u * 2 * G + p * G + j, p, j, P)
            eng.wait_ge(s["rests"], NG + 1)
            keys(NC - 1, 0, 0, LAST)
            eng.wait_ge(s["w_in"], 80)
            eng.wait_ge(s["sq"], 2 * NC)
            for k in range(NB2):
                if k >= 4:
                    eng.wait_ge((s["made_v"], s["made_s"])[k % 2], (k - 4) // 2 + 1)
                for j in range(2):
                    h = 2 * k + j
                    mm = eng.matmul(ps[:, 4 + k % 4, j * D:(j + 1) * D], wv[:, h, :], wo[:, h, :], start=True, stop=True)
                mm.then_inc(s["made"], 1)
            eng.wait_ge(s["fin"], 6)
            for k in range(2 * ((NC - 1) // 8)):
                if k >= 2:
                    eng.wait_ge((s["rk_s"], s["rk_v"])[k % 2], k // 2)
                for j in range(4):
                    mm = eng.transpose(ps[0:3 * NH, k % 2, j * P // 2:(j + 1) * P // 2].bitcast(BF16),
                                       parts[:, 4 * k + j, :, :].rearrange("p a h -> p (a h)"), pl.identb[:, :])
                mm.then_inc(s["turned"], 1)
            eng.transpose(ps[0:3 * NH, 2, 0:LAST // 2].bitcast(BF16), parts[0:LAST, NC - 1, :, :].rearrange("p a h -> p (a h)"),
                          pl.identb[0:LAST, 0:LAST]).then_inc(s["turned"], 1)


def l1x_queries(pl):
    nc, ps = pl.nc, pl.ps
    QO = pl.QO = pl.at("QO1", [P, NH, TOK], F32, QO_OFF)
    xT = pl.at("l1q_xT", [P, KC, ST], F32, pl.tmp1_off)
    xn = pl.at("l1q_xn", [P, 4, D], F32, pl.end)
    wq = pl.at("l1q_wq", [P, KC, NH * HD], F32, pl.end)
    qT = [pl.at(f"l1q_qT{j}", [P, ST], F32, pl.end) for j in range(2)]
    sq = pl.at("l1q_sq", [P, 4, ST], F32, pl.end)
    ones = pl.at("l1q_ones", [P, S], F32, pl.end)
    qs, nt = (pl.at(f"l1q_{k}", [P, B, GQ], F32, pl.end) for k in ("qs", "newton"))
    assert pl.end <= QO_OFF, pl.end - QO_OFF
    s = layer_norm_steps(pl, "l1q")
    for k in ("w_in", "ones", "q", "sq", "qT", "made", "out", "sums", "diag", "fin", "root", "newton"):
        s[k] = pl.sem(f"l1q_{k}")
    NBS = ST // S

    def supertiles(eng, step):
        step(0, True)
        with eng.Fori(1, SUP - 1) as i:
            step(i, True)
        step(SUP - 1, False)

    def first(i, h, lim):
        return isinstance(i, int) and i * NH + h < lim

    with nc.Block() as block:
        @block.sync
        def _(eng):
            eng.dma_start(wq[:, :, :], pl.ap["L1_WqT"]).then_inc(s["w_in"], 16)

        @block.gpsimd
        def _(eng):
            pow_of_all(pl, eng, s)
            eng.memset(ones[:, :], 1.0).then_inc(s["ones"], 1)

        @block.vector
        def _(eng):
            rstd_of_all(pl, eng, s)

            def norm(i):
                eng.wait_ge(s["turned"], i * 2)
                for j in range(4):
                    eng.tensor_scalar(xn[:, j, :], pl.x[:, i * 4 + j, :], pl.mv[:, i * 4 + j, 0:1], pl.rstd[:, bass.ds(i * 4 + j, 1)],
                                      ALU.subtract, ALU.mult).then_inc(s["xn"], 1)

            def take_xT(i):
                eng.wait_ge(s["q"], i * NH)
                for m in range(2):
                    eng.wait_ge(s["turned"], i * 2 + m + 1)
                    eng.tensor_copy(xT[:, :, m * 256:(m + 1) * 256], ps[:, 6 + m, :].rearrange("p (k n) -> p k n", k=KC)).then_inc(s["xT"], 1)

            def step(i, more):
                for h in range(NH):
                    k = i * NH + h
                    eng.wait_ge(s["q"], k + 1)
                    if not first(i, h, 2):
                        eng.wait_ge(s["made"], k - 1)
                        eng.wait_ge(s["sq"], k - 1)
                    eng.tensor_copy(qT[h % 2][:, :], ps[:, h % 2, :]).then_inc(s["qT"], 1)
                    if more and h == 5:
                        norm(i + 1)
                    if h % 4 == 3:
                        m = i * 4 + h // 4
                        eng.wait_ge(s["sums"], m + 1)
                        v = ps[:, 4, :].rearrange("p (b s) -> p b s", s=S)
                        eng.tensor_tensor(v, v, pl.cst["diag"][:, None, :].to_broadcast([P, NBS, S]), ALU.mult).then_inc(s["diag"], 1)
                        eng.wait_ge(s["diag"], m * 2 + 1)
                        apart(pl, eng)
                        eng.tensor_reduce(qs[:, bass.ds(i * NBS, NBS), h // 4], v, AX.X, ALU.add).then_inc(s["diag"], 1)
                if more:
                    take_xT(i + 1)

            norm(0)
            take_xT(0)
            supertiles(eng, step)
            eng.wait_ge(s["diag"], 2 * 4 * SUP)
            eng.tensor_scalar(qs[:, :, :], qs[:, :, :], 1.0 / HD, EPS, ALU.mult, ALU.add).then_inc(s["fin"], 1)
            inverse_root(pl, eng, qs[:, :, :], pl.rq[:, :, :], nt[:, :, :], s["newton"], 0, s["root"])
            eng.tensor_scalar(pl.rq[:, :, :], pl.rq[:, :, :], float(HD) ** -0.5, None, ALU.mult).then_inc(s["fin"], 1)

        @block.scalar
        def _(eng):
            eng.preload_act_table(ACT.Square)

            def out(i, h):
                eng.wait_ge(s["made"], i * NH + h + 1)
                eng.activation(QO[:, h, bass.ds(i * ST, ST)], ps[:, 2 + h % 2, :], ACT.Copy).then_inc(s["out"], 1)

            def step(i, more):
                for h in range(NH):
                    eng.wait_ge(s["qT"], i * NH + h + 1)
                    if not first(i, h, 4):
                        eng.wait_ge(s["sums"], i * 4 + h // 4)
                    eng.activation(sq[:, h % 4, :], qT[h % 2][:, :], ACT.Square).then_inc(s["sq"], 1)
                    if h >= 1:
                        out(i, h - 1)
                out(i, NH - 1)
            supertiles(eng, step)
            eng.wait_ge(s["fin"], 1)
            eng.activation(pl.rq[:, :, :], qs[:, :, :], ACT.Sqrt).then_inc(s["root"], 1)

        @block.tensor
        def _(eng):
            def through_wk(i, h):
                k = i * NH + h
                eng.wait_ge(s["qT"], k + 1)
                if not first(i, h, 2):
                    eng.wait_ge(s["out"], k - 1)
                eng.matmul(ps[:, 2 + h % 2, :], pl.WkTg[:, h, :], qT[h % 2][:, :], start=True, stop=True).then_inc(s["made"], 1)

            def step(i, more):
                eng.wait_ge(s["xT"], i * 2 + 2)
                for h in range(NH):
                    k = i * NH + h
                    if not first(i, h, 2):
                        eng.wait_ge(s["qT"], k - 1)
                    for c in range(KC):
                        mm = eng.matmul(ps[:, h % 2, :], wq[:, c, h * HD:(h + 1) * HD], xT[:, c, :], start=(c == 0), stop=(c == KC - 1))
                    mm.then_inc(s["q"], 1)
                    if more and h == 8:
                        turn_supertile(pl, eng, s, xn, i + 1)
                    if h >= 1:
                        through_wk(i, h - 1)
                    if h % 4 == 3:
                        m = i * 4 + h // 4
                        eng.wait_ge(s["sq"], k + 1)
                        eng.wait_ge(s["diag"], 2 * m)
                        apart(pl, eng)
                        for j in range(4):
                            mm = eng.matmul(ps[j * S:(j + 1) * S, 4, :], ones[:, :], sq[:, j, :], start=True, stop=True)
                        mm.then_inc(s["sums"], 1)
                through_wk(i, NH - 1)

            turn_supertile(pl, eng, s, xn, 0)
            eng.wait_ge(s["w_in"], 16)
            eng.wait_ge(s["ones"], 1)
            supertiles(eng, step)


MAGIC = 12582912.0


def staggered(eng, pieces):
    top = max(lag for lag, _ in pieces)

    def turn(n, slot):
        for lag, piece in pieces:
            t = n - lag
            if isinstance(t, int) and not 0 <= t < NT:
                continue
            piece(t, (slot - lag) % 2)
    lo = -(-(top + 2) // 2) * 2
    hi = NT // 2 * 2
    for n in range(lo):
        turn(n, n % 2)
    with eng.Fori(lo // 2, hi // 2) as u:
        for p in range(2):
            turn(u * 2 + p, p)
    for n in range(hi, NT + top):
        turn(n, n % 2)


def early(t):
    return isinstance(t, int) and t < 2


def quantise(eng, src, rounded, out, st, sem, n, ready):
    eng.tensor_reduce(st[:, 3:4], src, AX.X, ALU.max, apply_absolute_value=True).then_inc(sem, 1)
    eng.wait_ge(sem, n + 1)
    eng.tensor_scalar(st[:, 0:1], st[:, 3:4], 1e-5, None, ALU.max).then_inc(sem, 1)
    eng.wait_ge(sem, n + 2)
    eng.reciprocal(st[:, 1:2], st[:, 0:1]).then_inc(sem, 1)
    eng.wait_ge(sem, n + 3)
    eng.tensor_scalar(st[:, 2:3], st[:, 1:2], 127.0, None, ALU.mult).then_inc(sem, 1)
    eng.wait_ge(sem, n + 4)
    eng.tensor_scalar(rounded, src, st[:, 2:3], MAGIC, ALU.mult, ALU.add).then_inc(sem, 1)
    eng.wait_ge(sem, n + 5)
    eng.tensor_scalar(out, rounded, -MAGIC, None, ALU.add).then_inc(ready, 1)


NQS = 5


def block_attention(pl):
    nc, ps = pl.nc, pl.ps
    H, E, BT = 16, 16, 4
    pl.x1 = pl.at("x1", [P, NT, D], F32, L_OFF)
    pl.wd = pl.at("bl_wd", [P, 4, D], BF16, pl.end)
    pl.deq = pl.at("bl_deq", [P, 3], F32, pl.end)
    pl.ms = pl.at("bl_ms", [P, NT], F32, pl.end)
    pl.rs2 = pl.at("bl_rs2", [P, NT], F32, pl.end)
    pl.blk_low = pl.end
    sizes = {"qkv": KC * 3 * D, "o": KC * D, "down": 4 * D}
    wf = {k: pl.at(f"bl_{k}_f", [P, n], F32, pl.end) for k, n in sizes.items()}
    wqkv = pl.at("bl_wqkv", [P, KC, 3 * D], BF16, pl.end)
    wo = pl.at("bl_wo", [P, KC, D], BF16, pl.end)
    wn = pl.at("bl_wn", [P, D], F32, pl.end)
    sh = pl.at("bl_shift", [P, 3, P], F32, pl.end)
    bm = pl.at("bl_mask", [P, BT], F32, pl.end)
    cos = pl.at("bl_cos", [P, E], F32, pl.end)
    sin = pl.at("bl_sin", [P, E], F32, pl.end)
    ones = pl.at("bl_ones", [P, P], F32, pl.end)
    wsum = pl.at("bl_wsum", [P, 3], F32, pl.end)
    wmean = pl.at("bl_wmean", [P, 3], F32, pl.end)
    wscale = pl.at("bl_wscale", [P, 3], F32, pl.end)
    two = lambda name, shape, dt=F32: [pl.at(f"bl_{name}{j}", shape, dt, pl.end) for j in range(2)]
    h, hr, hq = two("h", [P, D]), two("hr", [P, D]), two("hq", [P, D], BF16)
    hqT = two("hqT", [P, KC, P], BF16)
    st, fac = two("st", [P, 4]), two("fac", [P, 1])
    R = two("R", [P, 3, H, 2, E // 2])
    rc, rsn = two("rc", [P, 2 * H, 2, E // 2]), two("rs", [P, 2 * H, 2, E // 2])
    prod = two("prod", [P, BT, H, E])
    sc, sx = two("sc", [P, BT, H]), two("sx", [P, BT, H])
    mx, sm_, inv = two("mx", [P, H]), two("sum", [P, H]), two("inv", [P, H])
    cx, cr, cq = two("cx", [P, D]), two("cr", [P, D]), two("cq", [P, D], BF16)
    cqT = two("cqT", [P, KC, P], BF16)
    st2, fac2 = two("st2", [P, 4]), two("fac2", [P, 1])
    s = {k: pl.sem(f"bl_{k}") for k in (
        "w_in", "wq", "wabs", "ones", "wsummed", "rs_in", "rstd", "pow2", "ln", "q1", "hq", "fac", "hturned", "hqT", "qkv",
        "R", "cos", "sin", "rot", "shifted", "att", "exp", "ctx", "q2", "cq", "cturned", "cqT", "proj", "x1", "ms", "wst", "sqs")}
    sqj = pl.at("bl_sqj", [P, D], F32, pl.end)
    ms1 = pl.at("bl_ms1", [P, 1], F32, pl.end)
    names = ("qkv", "o", "down")

    with nc.Block() as block:
        @block.sync
        def _(eng):
            for k in names:
                eng.dma_start(wf[k][:, :], pl.ap[f"L1_{k}T"]).then_inc(s["w_in"], 16)
            eng.dma_start(wn[:, :], pl.ap["L1_attn_norm"].to_broadcast([P, D])).then_inc(s["w_in"], 16)
            for d, n in ((sh, "shift"),):
                eng.dma_start(d[:, :, :], pl.ap[n]).then_inc(s["w_in"], 16)
            for d, n in ((bm, "bmask"), (cos, "cos16"), (sin, "sin16")):
                eng.dma_start(d[:, :], pl.ap[n]).then_inc(s["w_in"], 16)

        @block.gpsimd
        def _(eng):
            eng.memset(ones[:, :], 1.0).then_inc(s["ones"], 1)
            pow_of_all(pl, eng, s)
            eng.wait_ge(s["pow2"], 2)
            eng.tensor_tensor(pl.rs2[:, :], pl.rs2[:, :], pl.mhalf[:, :], ALU.pow).then_inc(s["pow2"], 1)

            def parts_of_rotation(t, p):
                eng.wait_ge(s["R"], 2 * t + 2)
                eng.wait_ge(s["w_in"], 128)
                if not early(t):
                    eng.wait_ge(s["rot"], t - 1)
                qk = R[p][:, 0:2].rearrange("p n h a e -> p (n h) a e")
                eng.tensor_tensor(rc[p][:, :, :, :].rearrange("p h a e -> p h (a e)"), qk.rearrange("p h a e -> p h (a e)"),
                                  cos[:, None, :].to_broadcast([P, 2 * H, E]), ALU.mult).then_inc(s["cos"], 1)
                for a in range(2):
                    eng.tensor_tensor(rsn[p][:, :, a, :], qk[:, :, 1 - a, :],
                                      sin[:, None, a * 8:a * 8 + 8].to_broadcast([P, 2 * H, 8]), ALU.mult).then_inc(s["sin"], 1)
            staggered(eng, [(0, parts_of_rotation)])

        @block.vector
        def _(eng):
            eng.wait_ge(s["w_in"], 128)
            for j, k in enumerate(names):
                eng.tensor_reduce(wsum[:, j:j + 1], wf[k][:, :], AX.X, ALU.add, apply_absolute_value=True).then_inc(s["wabs"], 1)
            eng.wait_ge(s["wsummed"], 1)
            for j, k in enumerate(names):
                eng.tensor_scalar(wmean[:, j:j + 1], ps[:, 0, j:j + 1], 1.0 / (P * sizes[k]), 1e-5, ALU.mult, ALU.max).then_inc(s["wq"], 1)
            eng.wait_ge(s["wq"], 3)
            eng.reciprocal(wscale[:, :], wmean[:, :]).then_inc(s["wq"], 1)
            eng.tensor_scalar(pl.deq[:, :], wmean[:, :], 1.0 / 127.0, None, ALU.mult).then_inc(s["wq"], 1)
            eng.wait_ge(s["wq"], 5)
            for j, (k, d) in enumerate(zip(names, (wqkv, wo, pl.wd))):
                eng.tensor_scalar(wf[k][:, :], wf[k][:, :], wscale[:, j:j + 1], MAGIC, ALU.mult, ALU.add).then_inc(s["wq"], 1)
                eng.wait_ge(s["wq"], 6 + 3 * j)
                eng.tensor_scalar(wf[k][:, :], wf[k][:, :], -MAGIC, -1.0, ALU.add, ALU.max).then_inc(s["wq"], 1)
                eng.wait_ge(s["wq"], 7 + 3 * j)
                eng.tensor_scalar(d[:, :, :].rearrange("p a b -> p (a b)"), wf[k][:, :], 1.0, None, ALU.min).then_inc(s["wq"], 1)
            rstd_of_all(pl, eng, s)
            eng.tensor_tensor(pl.rs2[:, :], pl.rstd[:, :], pl.rstd[:, :], ALU.mult).then_inc(s["ms"], 1)
            eng.wait_ge(s["ms"], 1)
            eng.tensor_tensor(pl.rs2[:, :], pl.rs2[:, :], pl.mv[:, :, 1], ALU.mult).then_inc(s["pow2"], 1)
            eng.wait_ge(s["pow2"], 1)
            eng.tensor_scalar(pl.rs2[:, :], pl.rs2[:, :], EPS, None, ALU.add).then_inc(s["pow2"], 1)
            eng.wait_ge(s["pow2"], 3)

            def norm_quantise(t, p):
                eng.tensor_scalar(pl.x1[:, t, :], pl.x[:, t, :], pl.mv[:, t, 0:1], pl.rstd[:, bass.ds(t, 1)],
                                  ALU.subtract, ALU.mult).then_inc(s["ln"], 1)
                eng.wait_ge(s["ln"], 2 * t + 1)
                eng.scalar_tensor_tensor(out=h[p][:, :], in0=pl.x1[:, t, :], scalar=pl.rs2[:, bass.ds(t, 1)], in1=wn[:, :],
                                         op0=ALU.mult, op1=ALU.mult).then_inc(s["ln"], 1)
                eng.wait_ge(s["ln"], 2 * t + 2)
                if not early(t):
                    eng.wait_ge(s["hturned"], t - 1)
                    eng.wait_ge(s["R"], 2 * t - 2)
                quantise(eng, h[p][:, :], hr[p][:, :], hq[p][:, :], st[p], s["q1"], t * NQS, s["hq"])
                eng.tensor_tensor(fac[p][:, :], st[p][:, 0:1], pl.deq[:, 0:1], ALU.mult).then_inc(s["fac"], 1)

            def rotate(t, p):
                eng.wait_ge(s["R"], 2 * t + 2)
                qk = R[p][:, 0:2].rearrange("p n h a e -> p (n h) (a e)")
                f = lambda a: a[:, :, :, :].rearrange("p h a e -> p h (a e)")
                eng.wait_ge(s["cos"], t + 1)
                eng.wait_ge(s["sin"], 2 * t + 2)
                eng.tensor_tensor(qk, f(rc[p]), f(rsn[p]), ALU.add).then_inc(s["rot"], 1)

            def scores(t, p):
                a = s["att"]
                n = t * 8
                q = R[p][:, 0].rearrange("p h a e -> p h (a e)")
                eng.wait_ge(s["rot"], t + 1)
                for j in range(BT):
                    if j == 1:
                        eng.wait_ge(s["shifted"], t + 1)
                    k = R[p][:, 1].rearrange("p h a e -> p h (a e)") if j == 0 else ps[:, 3 + j, 0:D].rearrange("p (h e) -> p h e", h=H)
                    eng.tensor_tensor(prod[p][:, j, :, :], k, q, ALU.mult).then_inc(a, 1)
                eng.wait_ge(a, n + 4)
                eng.tensor_reduce(sc[p][:, :, :], prod[p][:, :, :, :], AX.X, ALU.add).then_inc(a, 1)
                eng.wait_ge(a, n + 5)
                eng.tensor_tensor(sc[p][:, :, :], sc[p][:, :, :], bm[:, :, None].to_broadcast([P, BT, H]), ALU.add).then_inc(a, 1)
                eng.wait_ge(a, n + 6)
                eng.tensor_reduce(mx[p][:, :], sc[p][:, :, :].rearrange("p j h -> p h j"), AX.X, ALU.max).then_inc(a, 1)
                eng.wait_ge(a, n + 7)
                if not early(t):
                    eng.wait_ge(s["ctx"], t - 1)
                eng.tensor_tensor(sx[p][:, :, :], sc[p][:, :, :], mx[p][:, None, :].to_broadcast([P, BT, H]), ALU.subtract).then_inc(a, 1)

            def weigh(t, p):
                base = s["wst"]
                m = t * 8
                eng.wait_ge(s["exp"], t + 1)
                eng.tensor_reduce(sm_[p][:, :], sx[p][:, :, :].rearrange("p j h -> p h j"), AX.X, ALU.add).then_inc(base, 1)
                eng.wait_ge(base, m + 1)
                eng.reciprocal(inv[p][:, :], sm_[p][:, :]).then_inc(base, 1)
                eng.wait_ge(base, m + 2)
                eng.tensor_tensor(sx[p][:, :, :], sx[p][:, :, :], inv[p][:, None, :].to_broadcast([P, BT, H]), ALU.mult).then_inc(base, 1)
                eng.wait_ge(base, m + 3)
                for j in range(BT):
                    v = R[p][:, 2].rearrange("p h a e -> p h (a e)") if j == 0 else ps[:, 3 + j, D:2 * D].rearrange("p (h e) -> p h e", h=H)
                    eng.tensor_tensor(prod[p][:, j, :, :], v, sx[p][:, j, :, None].to_broadcast([P, H, E]), ALU.mult).then_inc(base, 1)
                eng.wait_ge(base, m + 7)
                eng.tensor_reduce(cx[p][:, :], prod[p][:, :, :, :].rearrange("p j h e -> p (h e) j"), AX.X, ALU.add).then_inc(base, 1)
                eng.wait_ge(base, m + 8)
                if not early(t):
                    eng.wait_ge(s["cturned"], t - 1)
                quantise(eng, cx[p][:, :], cr[p][:, :], cq[p][:, :], st2[p], s["q2"], t * NQS, s["cq"])
                eng.tensor_tensor(fac2[p][:, :], st2[p][:, 0:1], pl.deq[:, 1:2], ALU.mult).then_inc(s["ctx"], 1)

            def residual(t, p):
                eng.wait_ge(s["proj"], t + 1)
                eng.wait_ge(s["ctx"], t + 1)
                eng.scalar_tensor_tensor(out=pl.x1[:, t, :], in0=ps[:, 7, 0:D], scalar=fac2[p][:, 0:1], in1=pl.x1[:, t, :],
                                         op0=ALU.mult, op1=ALU.add).then_inc(s["x1"], 1)

            staggered(eng, [(0, norm_quantise), (2, scores), (2, weigh), (1, rotate), (3, residual)])

        @block.scalar
        def _(eng):
            eng.preload_act_table(ACT.Exp)

            def take_hq(t, p):
                eng.wait_ge(s["hturned"], t + 1)
                if not early(t):
                    eng.wait_ge(s["qkv"], 2 * t - 2)
                eng.activation(hqT[p][:, :, :], ps[:, 0, 0:P].bitcast(BF16).rearrange("p (k n) -> p k n", k=KC), ACT.Copy).then_inc(s["hqT"], 1)

            def take_qkv(t, p):
                eng.wait_ge(s["fac"], t + 1)
                if not early(t):
                    eng.wait_ge(s["shifted"], t - 1)
                    eng.wait_ge(s["ctx"], t - 1)
                f = R[p][:, :, :, :, :].rearrange("p n h a e -> p (n h a e)")
                eng.wait_ge(s["qkv"], 2 * t + 1)
                eng.activation(f[:, 0:2 * D], ps[:, 2, :], ACT.Copy, scale=fac[p][:, 0:1]).then_inc(s["R"], 1)
                eng.wait_ge(s["qkv"], 2 * t + 2)
                eng.activation(f[:, 2 * D:3 * D], ps[:, 3, 0:D], ACT.Copy, scale=fac[p][:, 0:1]).then_inc(s["R"], 1)

            def exponential(t, p):
                eng.wait_ge(s["att"], t * 8 + 8)
                eng.activation(sx[p][:, :, :], sx[p][:, :, :], ACT.Exp, scale=float(E) ** -0.5).then_inc(s["exp"], 1)

            def take_cq(t, p):
                eng.wait_ge(s["cturned"], t + 1)
                if not early(t):
                    eng.wait_ge(s["proj"], t - 1)
                eng.activation(cqT[p][:, :, :], ps[:, 1, 0:P].bitcast(BF16).rearrange("p (k n) -> p k n", k=KC), ACT.Copy).then_inc(s["cqT"], 1)

            def square(t, p):
                eng.wait_ge(s["sqs"], 2 * t)
                eng.wait_ge(s["x1"], t + 1)
                eng.activation(sqj[:, :], pl.x1[:, t, :], ACT.Square, accum_out=ms1[:, :]).then_inc(s["sqs"], 1)
                eng.wait_ge(s["sqs"], 2 * t + 1)
                eng.activation(pl.ms[:, bass.ds(t, 1)], ms1[:, :], ACT.Copy).then_inc(s["sqs"], 1)

            staggered(eng, [(0, take_hq), (2, exponential), (0, take_qkv), (2, take_cq), (3, square)])

        @block.tensor
        def _(eng):
            eng.wait_ge(s["ones"], 1)
            eng.wait_ge(s["wabs"], 3)
            eng.matmul(ps[:, 0, 0:3], ones[:, :], wsum[:, :], start=True, stop=True).then_inc(s["wsummed"], 1)
            eng.wait_ge(s["wq"], 14)

            def turn_h(t, p):
                eng.wait_ge(s["hq"], t + 1)
                eng.wait_ge(s["hqT"], t)
                for k in range(KC):
                    mm = eng.transpose(ps[:, 0, k * P // 2:(k + 1) * P // 2].bitcast(BF16), hq[p][:, k * P:(k + 1) * P], pl.identb[:, :])
                mm.then_inc(s["hturned"], 1)

            def project(t, p):
                eng.wait_ge(s["hqT"], t + 1)
                eng.wait_ge(s["R"], 2 * t)
                for n, w in ((0, 2 * D), (1, D)):
                    for k in range(KC):
                        mm = eng.matmul(ps[:, 2 + n, 0:w], hqT[p][:, k, :], wqkv[:, k, n * 512:n * 512 + w], start=(k == 0), stop=(k == KC - 1))
                    mm.then_inc(s["qkv"], 1)

            def shift(t, p):
                eng.wait_ge(s["rot"], t + 1)
                eng.wait_ge(s["wst"], 8 * t)
                kv = R[p][:, 1:3].rearrange("p n h a e -> p (n h a e)")
                for j in range(3):
                    mm = eng.matmul(ps[:, 4 + j, :], sh[:, j, :], kv, start=True, stop=True)
                mm.then_inc(s["shifted"], 1)

            def turn_c(t, p):
                eng.wait_ge(s["cq"], t + 1)
                eng.wait_ge(s["cqT"], t)
                for k in range(KC):
                    mm = eng.transpose(ps[:, 1, k * P // 2:(k + 1) * P // 2].bitcast(BF16), cq[p][:, k * P:(k + 1) * P], pl.identb[:, :])
                mm.then_inc(s["cturned"], 1)

            def output(t, p):
                eng.wait_ge(s["cqT"], t + 1)
                eng.wait_ge(s["x1"], t)
                for k in range(KC):
                    mm = eng.matmul(ps[:, 7, 0:D], cqT[p][:, k, :], wo[:, k, :], start=(k == 0), stop=(k == KC - 1))
                mm.then_inc(s["proj"], 1)

            staggered(eng, [(0, turn_h), (0, project), (1, shift), (2, turn_c), (2, output)])


def block_ffn(pl):
    nc, ps = pl.nc, pl.ps
    I = 2 * D
    up = pl.at("bf_up", [P, KC, 2 * I], F32, pl.blk_low)
    wn = pl.at("bf_wn", [P, D], F32, pl.end)
    two = lambda name, shape, dt=F32: [pl.at(f"bf_{name}{j}", shape, dt, pl.end) for j in range(2)]
    hn = two("hn", [P, D])
    hT = two("hT", [P, KC, P])
    sg, g, gr = two("sg", [P, I]), two("g", [P, I]), two("gr", [P, I])
    gq = two("gq", [P, I], BF16)
    gT = two("gT", [P, 4, P], BF16)
    st, fac = two("st", [P, 4]), two("fac", [P, 1])
    s = {k: pl.sem(f"bf_{k}") for k in (
        "w_in", "ms", "rs", "hn", "hturned", "hT", "gate", "val", "silu", "g", "q", "gq", "fac", "gturned", "gT", "down", "res", "added")}

    with nc.Block() as block:
        @block.sync
        def _(eng):
            eng.dma_start(up[:, :, :], pl.ap["L1_upT"]).then_inc(s["w_in"], 16)
            eng.dma_start(wn[:, :], pl.ap["L1_ffn_norm"].to_broadcast([P, D])).then_inc(s["w_in"], 16)

        @block.gpsimd
        def _(eng):
            eng.wait_ge(s["ms"], 1)
            eng.tensor_tensor(pl.rs2[:, :], pl.rs2[:, :], pl.mhalf[:, :], ALU.pow).then_inc(s["rs"], 1)

        @block.vector
        def _(eng):
            eng.tensor_scalar(pl.rs2[:, :], pl.ms[:, :], 1.0 / D, EPS, ALU.mult, ALU.add).then_inc(s["ms"], 1)
            eng.wait_ge(s["rs"], 1)
            eng.wait_ge(s["w_in"], 32)

            def norm(t, p):
                if not early(t):
                    eng.wait_ge(s["hturned"], t - 1)
                eng.scalar_tensor_tensor(out=hn[p][:, :], in0=pl.x1[:, t, :], scalar=pl.rs2[:, bass.ds(t, 1)], in1=wn[:, :],
                                         op0=ALU.mult, op1=ALU.mult).then_inc(s["hn"], 1)

            def gated(t, p):
                eng.wait_ge(s["silu"], t + 1)
                eng.wait_ge(s["val"], t + 1)
                eng.tensor_tensor(g[p][:, :], ps[:, 2, :], sg[p][:, :], ALU.mult).then_inc(s["g"], 1)
                eng.wait_ge(s["g"], t + 1)
                if not early(t):
                    eng.wait_ge(s["gturned"], t - 1)
                quantise(eng, g[p][:, :], gr[p][:, :], gq[p][:, :], st[p], s["q"], t * NQS, s["gq"])
                eng.tensor_tensor(fac[p][:, :], st[p][:, 0:1], pl.deq[:, 2:3], ALU.mult).then_inc(s["fac"], 1)

            def residual(t, p):
                eng.wait_ge(s["down"], t + 1)
                eng.wait_ge(s["fac"], t + 1)
                eng.scalar_tensor_tensor(out=pl.x1[:, t, :], in0=ps[:, 6, 0:D], scalar=fac[p][:, 0:1], in1=pl.x1[:, t, :],
                                         op0=ALU.mult, op1=ALU.add).then_inc(s["res"], 1)
                eng.wait_ge(s["res"], t + 1)
                eng.tensor_tensor(pl.x[:, t, :], pl.x[:, t, :], pl.x1[:, t, :], ALU.add).then_inc(s["added"], 1)
                eng.wait_ge(s["added"], t + 1)
                token_stats(pl, eng, t)

            staggered(eng, [(0, norm), (1, gated), (2, residual)])
            pl.stats_n += 3 * NT

        @block.scalar
        def _(eng):
            eng.preload_act_table(ACT.Silu)

            def take_h(t, p):
                eng.wait_ge(s["hturned"], t + 1)
                if not early(t):
                    eng.wait_ge(s["val"], t - 1)
                eng.activation(hT[p][:, :, :], ps[:, 0, 0:KC * P].rearrange("p (k n) -> p k n", k=KC), ACT.Copy).then_inc(s["hT"], 1)

            def silu(t, p):
                eng.wait_ge(s["gate"], t + 1)
                if not early(t):
                    eng.wait_ge(s["g"], t - 1)
                eng.activation(sg[p][:, :], ps[:, 1, :], ACT.Silu).then_inc(s["silu"], 1)

            def take_g(t, p):
                eng.wait_ge(s["gturned"], t + 1)
                if not early(t):
                    eng.wait_ge(s["down"], t - 1)
                eng.activation(gT[p][:, :, :], ps[:, 3, 0:2 * P].bitcast(BF16).rearrange("p (k n) -> p k n", k=4), ACT.Copy).then_inc(s["gT"], 1)

            staggered(eng, [(0, take_h), (0, silu), (1, take_g)])

        @block.tensor
        def _(eng):
            eng.wait_ge(s["w_in"], 32)

            def turn_h(t, p):
                eng.wait_ge(s["hn"], t + 1)
                eng.wait_ge(s["hT"], t)
                for k in range(KC):
                    mm = eng.transpose(ps[:, 0, k * P:(k + 1) * P], hn[p][:, k * P:(k + 1) * P], pl.ident[:, :])
                mm.then_inc(s["hturned"], 1)

            def ups(t, p):
                eng.wait_ge(s["hT"], t + 1)
                for n, (bank, sem, free) in enumerate(((1, s["gate"], s["silu"]), (2, s["val"], s["g"]))):
                    eng.wait_ge(free, t)
                    for k in range(KC):
                        mm = eng.matmul(ps[:, bank, :], hT[p][:, k, :], up[:, k, n * I:(n + 1) * I], start=(k == 0), stop=(k == KC - 1))
                    mm.then_inc(sem, 1)

            def turn_g(t, p):
                eng.wait_ge(s["gq"], t + 1)
                eng.wait_ge(s["gT"], t)
                for k in range(4):
                    mm = eng.transpose(ps[:, 3, k * P // 2:(k + 1) * P // 2].bitcast(BF16), gq[p][:, k * P:(k + 1) * P], pl.identb[:, :])
                mm.then_inc(s["gturned"], 1)

            def down(t, p):
                eng.wait_ge(s["gT"], t + 1)
                eng.wait_ge(s["res"], t)
                for k in range(4):
                    mm = eng.matmul(ps[:, 6, 0:D], gT[p][:, k, :], pl.wd[:, k, :], start=(k == 0), stop=(k == 3))
                mm.then_inc(s["down"], 1)

            staggered(eng, [(0, turn_h), (0, ups), (1, turn_g), (1, down)])


def lut_ffn(pl):
    nc, ps = pl.nc, pl.ps
    I = 688
    half = I // 2
    NC = -(-I // P)
    LAST = I - (NC - 1) * P
    wgu = pl.at("lf_wgu", [P, KC, 2, I], F32, L_OFF)
    wdn = pl.at("lf_wdn", [P, NC, D], F32, pl.end)
    two = lambda name, shape, dt=F32: [pl.at(f"lf_{name}{j}", shape, dt, pl.end) for j in range(2)]
    xn, xT = two("xn", [P, D]), two("xT", [P, KC, P])
    sg, h = two("sg", [P, I]), two("h", [P, I])
    hT = two("hT", [P, NC, P])
    s = {k: pl.sem(f"lf_{k}") for k in (
        "w_in", "rs_in", "rstd", "xn", "xturned", "xT", "gate", "up", "silu", "h", "hturned", "hT", "down", "added", "stored")}

    with nc.Block() as block:
        @block.sync
        def _(eng):
            n = KC * 2 * I
            eng.dma_start(wgu[:, :, :, :].rearrange("p k a n -> p (k a n)"), pl.lut_dram[:, 0:n]).then_inc(s["w_in"], 16)
            eng.dma_start(wdn[:, :, :].rearrange("p k n -> p (k n)"), pl.lut_dram[:, n:]).then_inc(s["w_in"], 16)

            def store(t, p):
                eng.wait_ge(s["added"], t + 1)
                eng.dma_start(pl.out[:, t, :], pl.x[:, t, :]).then_inc(s["stored"], 16)
            staggered(eng, [(0, store)])
            eng.wait_ge(s["stored"], 16 * NT)

        @block.gpsimd
        def _(eng):
            pow_of_all(pl, eng, s)

        @block.vector
        def _(eng):
            rstd_of_all(pl, eng, s)

            def norm(t, p):
                if not early(t):
                    eng.wait_ge(s["xturned"], t - 1)
                eng.tensor_scalar(xn[p][:, :], pl.x[:, t, :], pl.mv[:, t, 0:1], pl.rstd[:, bass.ds(t, 1)],
                                  ALU.subtract, ALU.mult).then_inc(s["xn"], 1)

            def gated(t, p):
                eng.wait_ge(s["silu"], t + 1)
                eng.wait_ge(s["up"], t + 1)
                if not early(t):
                    eng.wait_ge(s["hturned"], 2 * t - 2)
                eng.tensor_tensor(h[p][:, :].rearrange("p (a n) -> p a n", a=2), ps[:, 2:4, 0:half],
                                  sg[p][:, :].rearrange("p (a n) -> p a n", a=2), ALU.mult).then_inc(s["h"], 1)

            def add(t, p):
                eng.wait_ge(s["down"], t + 1)
                eng.tensor_tensor(pl.x[:, t, :], ps[:, 6, 0:D], pl.x[:, t, :], ALU.add).then_inc(s["added"], 1)

            staggered(eng, [(0, norm), (1, gated), (2, add)])

        @block.scalar
        def _(eng):
            eng.preload_act_table(ACT.Silu)

            def take_x(t, p):
                eng.wait_ge(s["xturned"], t + 1)
                if not early(t):
                    eng.wait_ge(s["up"], t - 1)
                eng.activation(xT[p][:, :, :], ps[:, 7, 0:KC * P].rearrange("p (k n) -> p k n", k=KC), ACT.Copy).then_inc(s["xT"], 1)

            def silu(t, p):
                eng.wait_ge(s["gate"], t + 1)
                if not early(t):
                    eng.wait_ge(s["h"], t - 1)
                eng.activation(sg[p][:, :].rearrange("p (a n) -> p a n", a=2), ps[:, 0:2, 0:half], ACT.Silu).then_inc(s["silu"], 1)

            def take_h(t, p):
                eng.wait_ge(s["hturned"], 2 * t + 2)
                if not early(t):
                    eng.wait_ge(s["down"], t - 1)
                eng.activation(hT[p][:, 0:4, :], ps[:, 4, :].rearrange("p (c n) -> p c n", c=4), ACT.Copy).then_inc(s["hT"], 1)
                eng.activation(hT[p][:, 4, :], ps[:, 5, 0:P], ACT.Copy).then_inc(s["hT"], 1)
                eng.activation(hT[p][0:LAST, 5, :], ps[0:LAST, 5, P:2 * P], ACT.Copy).then_inc(s["hT"], 1)

            staggered(eng, [(0, take_x), (0, silu), (1, take_h)])

        @block.tensor
        def _(eng):
            eng.wait_ge(s["w_in"], 32)

            def turn_x(t, p):
                eng.wait_ge(s["xn"], t + 1)
                eng.wait_ge(s["xT"], t)
                for k in range(KC):
                    mm = eng.transpose(ps[:, 7, k * P:(k + 1) * P], xn[p][:, k * P:(k + 1) * P], pl.ident[:, :])
                mm.then_inc(s["xturned"], 1)

            def ups(t, p):
                eng.wait_ge(s["xT"], t + 1)
                for a, (sem, free) in enumerate(((s["gate"], s["silu"]), (s["up"], s["h"]))):
                    eng.wait_ge(free, t)
                    for m in range(2):
                        for k in range(KC):
                            mm = eng.matmul(ps[:, 2 * a + m, 0:half], xT[p][:, k, :], wgu[:, k, a, m * half:(m + 1) * half],
                                            start=(k == 0), stop=(k == KC - 1))
                    mm.then_inc(sem, 1)

            def turn_h(t, p):
                eng.wait_ge(s["h"], t + 1)
                eng.wait_ge(s["hT"], 3 * t)
                for c in range(NC):
                    m = P if c < NC - 1 else LAST
                    mm = eng.transpose(ps[0:m, 4 + c // 4, c % 4 * P:c % 4 * P + P], h[p][:, c * P:c * P + m], pl.ident[:, :])
                    if c in (3, NC - 1):
                        mm.then_inc(s["hturned"], 1)

            def down(t, p):
                eng.wait_ge(s["hT"], 3 * t + 3)
                eng.wait_ge(s["added"], t)
                for c in range(NC):
                    m = P if c < NC - 1 else LAST
                    mm = eng.matmul(ps[:, 6, 0:D], hT[p][0:m, c, :], wdn[0:m, c, :], start=(c == 0), stop=(c == NC - 1))
                mm.then_inc(s["down"], 1)

            staggered(eng, [(0, turn_x), (0, ups), (1, turn_h), (1, down)])


def store(pl, out):
    done = pl.sem("stored")
    with pl.nc.Block() as block:
        @block.sync
        def _(eng):
            eng.dma_start(out.rearrange("(t p) d -> p t d", p=P), pl.x[:, :, :]).then_inc(done, 16)
            eng.wait_ge(done, 16)


def build(nc, ap, out, start=0, stop=6):
    with ExitStack() as ctx:
        pl = Plan(nc, ctx, ap)
        common(pl)
        setup(pl)
        if start < 1 <= stop:
            l0x_queries(pl)
            xattn_batches(pl, "l0x", L_OFF, pl.tmp_off, True)
            xattn_project(pl, "l0xo", pl.Bw, pl.tmp_off)
            pl.clear_layer()
        if start < 2 <= stop:
            self_attention(pl)
        if start < 3 <= stop:
            experts(pl)
            pl.clear_layer()
        if start < 4 <= stop:
            key_norms(pl)
            l1x_queries(pl)
            xattn_batches(pl, "l1x", pl.low1_off, None, False, normed=True)
            xattn_project(pl, "l1xo", pl.Bw1, pl.low1_off, pl.bw1_in)
            pl.clear_layer()
        if start < 5 <= stop:
            block_attention(pl)
            block_ffn(pl)
        pl.out = out.rearrange("(t p) d -> p t d", p=P)
        if stop >= 6:
            lut_ffn(pl)
        else:
            store(pl, out)


def layout(inputs):
    a = {k: np.asarray(v) for k, v in inputs.items()}
    c = np.ascontiguousarray
    heads = lambda w, n: w.reshape(w.shape[0], n, -1)
    turned = lambda w: w.T.reshape(-1, P, w.shape[0]).transpose(1, 0, 2).reshape(P, -1)
    gu = np.stack([a["L1_ffn_gate_idx"].T, a["L1_ffn_up_idx"].T], 1)
    gu = gu.reshape(KC, P, -1).transpose(1, 0, 2).reshape(P, -1)
    dn = a["L1_ffn_down_idx"].T
    dn = np.concatenate([dn, np.zeros((-dn.shape[0] % P, D), dn.dtype)])
    idx = np.concatenate([gu, dn.reshape(-1, P, D).transpose(1, 0, 2).reshape(P, -1)], 1)
    return {
        **tables(),
        "x": c(a["x"].reshape(NT, P, D).transpose(1, 0, 2)),
        "ctx": c(a["ctx_1024"]),
        "ctxT": c(a["ctx_1024"].reshape(B * CS, CD).T),
        "mask": c(a["mask_BxS2_bf1"]).view(np.uint8),
        "L0_WqT": c(heads(a["L0_xattn_Wq"], NH).transpose(2, 1, 0)),
        "L0_WkT": c(heads(a["L0_xattn_Wk"], 8).transpose(2, 1, 0)),
        "L0_WvT": c(heads(a["L0_xattn_Wv"], 8).transpose(2, 1, 0)),
        "L0_wqkvT": c(a["L0_attn_w_qkv"].T.reshape(KC, P, -1).transpose(1, 0, 2)),
        "L0_woT": c(a["L0_attn_w_o"].T.reshape(NT, P, D).transpose(1, 0, 2)),
        "L1_WqT": c(a["L1_xattn_Wq"].reshape(KC, P, -1).transpose(1, 0, 2)),
        "L1_Wk": c(a["L1_xattn_Wk"]),
        "L1_WkT": c(heads(a["L1_xattn_Wk"], NH).transpose(2, 1, 0)),
        "L1_WvT": c(heads(a["L1_xattn_Wv"], NH).transpose(2, 1, 0)),
        "L1_Wo": c(a["L1_xattn_Wo"].reshape(NH, HD, D).transpose(1, 0, 2)),
        "L1_g": c(np.stack([a["L1_xattn_gq"], a["L1_xattn_gk"]], 1)),
        "L1_qkvT": c(turned(a["L1_attn_qkv_w"])),
        "L1_oT": c(turned(a["L1_attn_o_w"])),
        "L1_downT": c(turned(a["L1_attn_ffn_down_w"])),
        "L1_upT": c(turned(a["L1_attn_ffn_up_w"]).reshape(P, KC, -1)),
        "L1_attn_norm": c(a["L1_attn_attn_norm_w"][None]),
        "L1_ffn_norm": c(a["L1_attn_ffn_norm_w"][None]),
        "L1_lut": c(a["L1_ffn_lut"][None]),
        "L1_idx": c(idx),
        "entries": np.ascontiguousarray(np.broadcast_to(np.arange(NT, dtype=np.float32), (P, NT))),
        "L0_gate": c(a["L0_ffn_gate"].reshape(KC, P, -1).transpose(1, 0, 2)),
        "L0_wg": c(a["L0_ffn_gate_up_proj"][:, :, :96].transpose(1, 0, 2).reshape(KC, P, -1).transpose(1, 0, 2)),
        "L0_wu": c(a["L0_ffn_gate_up_proj"][:, :, 96:].transpose(1, 0, 2).reshape(KC, P, -1).transpose(1, 0, 2)),
        "L0_wd": c(a["L0_ffn_down_proj"].reshape(-1, P, D).transpose(1, 0, 2)),
        "L0_Wo": c(a["L0_xattn_Wo"].reshape(NH, HD, D).transpose(1, 0, 2)),
    }


def kernel(**inputs):
    import concourse.bacc as _bacc
    from concourse import mybir as _mybir
    from concourse.bass_utils import run_bass_kernel_spmd as _run

    nc = _bacc.Bacc("TRN2", target_bir_lowering=False, num_devices=1)
    arrays = layout(inputs)
    ap = {k: nc.dram_tensor(k, a.shape, _mybir.dt.from_np(a.dtype), kind="ExternalInput").ap() for k, a in arrays.items()}
    out = nc.dram_tensor("out", (TOK, D), F32, kind="ExternalOutput").ap()
    build(nc, ap, out)
    r = _run(nc, [arrays], core_ids=[0])
    return r.results[0]["out"].reshape(B, S, D)
```

```python
from contextlib import ExitStack

import numpy as np
import concourse.bass as bass
from concourse import mybir
from concourse.alu_op_type import AluOpType as ALU

F32 = mybir.dt.float32
BF16 = mybir.dt.bfloat16
U8 = mybir.dt.uint8
I32 = mybir.dt.int32
F32R = mybir.dt.float32r
ACT = mybir.ActivationFunctionType
AX = mybir.AxisListType

P = 128
B, S, D = 64, 32, 256
TOK = B * S
NT = TOK // P
KC = D // P
SUP = 4
ST = TOK // SUP
CD, CS = 128, 257
NH, HD = 16, 128
GQ = 4
EPS = 1e-5
NEG = -1e30

SB0 = 16512
X_OFF = SB0
C_OFF = X_OFF + NT * D * 4
L_OFF = C_OFF + 8192
TOP = 229344
QO_OFF = TOP - NH * TOK * 4

CONSTS = {"cos64": 64, "sin64": 64, "causal": S, "diag": S}


def tables():
    pos = np.arange(P) % S
    out = {}
    for d in (64, 16):
        inv = (1.0 / np.float32(10000.0) ** (np.arange(0, d, 2, dtype=np.float32) / np.float32(d))).astype(np.float32)
        ang = pos.astype(np.float32)[:, None] * inv
        co, si = np.cos(ang).astype(np.float32), np.sin(ang).astype(np.float32)
        out[f"cos{d}"] = np.concatenate([co, co], 1)
        out[f"sin{d}"] = np.concatenate([-si, si], 1)
    out["causal"] = np.where(np.arange(S)[None, :] <= pos[:, None], 0.0, NEG).astype(np.float32)
    out["diag"] = (np.arange(S)[None, :] == pos[:, None]).astype(np.float32)
    out["shift"] = (np.arange(P)[:, None, None] == np.arange(P)[None, None] - np.arange(1, 4)[None, :, None]).astype(np.float32)
    out["bmask"] = np.where(np.arange(4)[None, :] <= (np.arange(P) % 4)[:, None], 0.0, NEG).astype(np.float32)
    row_head = np.arange(4)[:, None] * 4 + (np.arange(P) // S)[None, :]
    pick = (np.arange(3 * NH)[:, None, None] % NH == row_head[None]).astype(np.float32)
    out["pick"] = pick
    return out


class Plan:

    def __init__(self, nc, ctx, ap):
        self.nc, self.ctx, self.ap = nc, ctx, ap
        self.layer_sems = []

    def at(self, name, shape, dt, off):
        t = self.nc.alloc_sbuf_tensor_at(name, shape, dt, offset=off)
        size = {F32: 4, I32: 4, BF16: 2, U8: 1}[dt]
        for n in shape[1:]:
            size *= n
        assert off + size <= TOP, (name, off + size - TOP)
        self.end = -(-(off + size) // 32) * 32
        return t

    def sem(self, name):
        s = self.nc.alloc_semaphore(name)
        self.layer_sems.append(s)
        return s

    def clear_layer(self):
        self.nc.clear_and_free_semaphores(self.layer_sems)
        self.layer_sems = []
        self.nc.all_engine_barrier()


def common(pl):
    nc = pl.nc
    pl.x = pl.at("x_sb", [P, NT, D], F32, X_OFF)
    pl.ident = pl.at("ident", [P, P], F32, C_OFF)
    pl.identb = pl.at("identb", [P, P], BF16, pl.end)
    pl.mv = pl.at("mv_all", [P, NT, 2], F32, pl.end)
    pl.rstd = pl.at("rstd_all", [P, NT], F32, pl.end)
    pl.veps = pl.at("veps_all", [P, NT], F32, pl.end)
    pl.bn = pl.at("bn_out", [P, 6], F32, pl.end)
    pl.bn4 = pl.at("bn_out4", [P, 4, 6], F32, pl.end)
    pl.mv1 = pl.at("mv_one", [P, 2], F32, pl.end)
    pl.mhalf = pl.at("minus_half", [P, NT], F32, pl.end)
    pl.maskb = pl.at("mask_bias", [B, CS], BF16, pl.end)
    pl.flag = pl.at("any_valid", [P, B], F32, pl.end)
    pl.cst = {n: pl.at(n, [P, w], F32, pl.end) for n, w in CONSTS.items()}
    pl.const_end = pl.end
    assert pl.end <= L_OFF
    pl.ps = pl.ctx.enter_context(nc.psum_tensor("ps", [P, 8, 512], F32))
    pl.x_loaded = nc.alloc_semaphore("x_loaded")
    pl.stats = nc.alloc_semaphore("stats_step")
    pl.stats_n = 0


def apart(pl, eng):
    eng.nop(nofuse=True)




def leading_bits(eng, src, head):
    return eng.tensor_copy(head.bitcast(F32R), src)


def rest_of(eng, src, head, rest):
    return eng.tensor_tensor(rest.bitcast(F32R), src, head, ALU.subtract)


def split(eng, src, head, rest, sem, n):
    leading_bits(eng, src, head).then_inc(sem, 1)
    eng.wait_ge(sem, n + 1)
    rest_of(eng, src, head, rest).then_inc(sem, 1)


def bfloat_parts(eng, src, parts, rests, sem, n):
    left = [src, *rests]
    for j in range(3):
        if j > 0:
            eng.wait_ge(sem, n + 2 * j - 1)
            eng.tensor_tensor(left[j], left[j - 1], parts[j - 1], ALU.subtract).then_inc(sem, 1)
            eng.wait_ge(sem, n + 2 * j)
        eng.tensor_copy(parts[j], left[j]).then_inc(sem, 1)


def split_product(eng, out, a, b, start=True, stop=True):
    r = [[x.bitcast(F32R) for x in y] for y in (a, b)]
    eng.matmul(out, r[0][0], r[1][0], start=start, stop=False)
    eng.matmul(out, r[0][0], r[1][1], start=False, stop=False)
    return eng.matmul(out, r[0][1], r[1][0], start=False, stop=stop)


def token_stats(pl, eng, t):
    n = t * 3 + pl.stats_n
    apart(pl, eng)
    eng.bn_stats(pl.bn[:, :], pl.x[:, t, :]).then_inc(pl.stats, 1)
    eng.wait_ge(pl.stats, n + 1)
    apart(pl, eng)
    eng.bn_aggr(pl.mv1[:, :], pl.bn[:, :]).then_inc(pl.stats, 1)
    eng.wait_ge(pl.stats, n + 2)
    apart(pl, eng)
    eng.tensor_copy(pl.mv[:, t, :], pl.mv1[:, :]).then_inc(pl.stats, 1)


def tiles_stats(pl, eng, lo):
    for t in range(lo, lo + 4):
        if t >= 4:
            eng.wait_ge(pl.stats, pl.stats_n + 2 * lo)
        eng.bn_stats(pl.bn4[:, t - lo, :], pl.x[:, t, :]).then_inc(pl.stats, 1)
    for t in range(lo, lo + 4):
        eng.wait_ge(pl.stats, pl.stats_n + 2 * lo + t - lo + 1)
        eng.bn_aggr(pl.mv[:, t, :], pl.bn4[:, t - lo, :]).then_inc(pl.stats, 1)


def setup(pl):
    nc, ap = pl.nc, pl.ap
    pl.Aw = pl.at("Aw", [P, KC, NH, CD], F32, L_OFF)
    pl.Bw = pl.at("Bw", [P, NH, D], F32, pl.end)
    pl.tmp_off = pl.end
    wq = pl.at("s_wqT", [P, NH, D], F32, QO_OFF)
    wk = pl.at("s_wkT", [P, 8, CD], F32, pl.end)
    wv = pl.at("s_wvT", [P, 8, CD], F32, pl.end)
    wo = pl.at("s_wo", [P, NH, D], F32, pl.end)
    mask8 = pl.at("s_mask8", [B, CS], U8, pl.end)
    maskf = pl.at("s_maskf", [B, CS], F32, pl.end)
    vflag = pl.at("s_vflag", [B, 1], F32, pl.end)
    dflag = pl.at("s_dflag", [B, B], F32, pl.end)
    ones = pl.at("s_ones", [B, P], F32, pl.end)
    last, lrest0, lrest1 = (pl.at(f"s_last{j}", [B, CD], F32, pl.end) for j in range(3))
    lparts = pl.at("s_last_parts", [B, 3, CD], BF16, pl.end)
    pl.last_dram = nc.dram_tensor("last_row_scratch", (B, 9, CD), BF16, kind="Internal").ap()
    last_in, last_step, last_stored = pl.sem("set_last_loaded"), pl.sem("set_last_step"), pl.sem("set_last_stored")
    w_loaded, vo_loaded, mask_loaded = pl.sem("set_w_loaded"), pl.sem("set_vo_loaded"), pl.sem("set_mask_loaded")
    ones_set, filled = pl.sem("set_ones"), pl.sem("set_filled")
    evac = pl.sem("set_bank_read")
    ident_set, ident_zero, mstep = pl.sem("ident_set"), pl.sem("ident_zero"), pl.sem("set_mask_step")
    fl_done = pl.sem("set_flag_product")
    pl.ident_set = ident_set
    ps = pl.ps
    NA, NBK = KC * NH // 4, NH // 2

    consts_in = pl.sem("consts_loaded")
    with nc.Block() as block:
        @block.sync
        def _(eng):
            eng.dma_start(wq[:, :, :], ap["L0_WqT"]).then_inc(w_loaded, 16)
            eng.dma_start(wk[:, :, :], ap["L0_WkT"]).then_inc(w_loaded, 16)
            eng.dma_start(mask8[:, :], ap["mask"]).then_inc(mask_loaded, 16)
            eng.dma_start(wv[:, :, :], ap["L0_WvT"]).then_inc(vo_loaded, 16)
            eng.dma_start(wo[:, :, :], ap["L0_Wo"]).then_inc(vo_loaded, 16)
            eng.dma_start(last[:, :], ap["ctx"][:, CS - 1, :]).then_inc(last_in, 16)
            for name in CONSTS:
                eng.dma_start(pl.cst[name][:, :], ap[name]).then_inc(consts_in, 16)
            eng.wait_ge(last_step, 5)
            for r in range(3):
                eng.dma_start(pl.last_dram[:, 3 * r:3 * r + 3, :], lparts[:, :, :]).then_inc(last_stored, 16)
            eng.wait_ge(last_stored, 48)

        @block.scalar
        def _(eng):
            eng.dma_start(pl.x[:, :, :], ap["x"]).then_inc(pl.x_loaded, 16)
            for k in range(NA + NBK):
                eng.wait_ge(filled, k + 1)
                dst = pl.Aw[:, k * 4 // NH, k * 4 % NH:k * 4 % NH + 4, :] if k < NA else pl.Bw[:, 2 * (k - NA):2 * (k - NA) + 2, :]
                src = ps[:, k % 8, :].rearrange("p (h c) -> p h c", h=4 if k < NA else 2)
                eng.activation(dst, src, ACT.Copy).then_inc(evac, 1)

        @block.gpsimd
        def _(eng):
            eng.memset(pl.ident[:, :], 0.0).then_inc(ident_zero, 1)
            eng.memset(pl.identb[:, :], 0.0).then_inc(ident_zero, 1)
            eng.wait_ge(ident_zero, 2)
            for m in (pl.ident, pl.identb):
                eng.affine_select(out=m[:, :], in_=m[:, :], compare_op=ALU.not_equal, fill=1.0, base=0,
                                  pattern=[[-1, P]], channel_multiplier=1).then_inc(ident_set, 1)
            eng.memset(ones[:, :], 1.0).then_inc(ones_set, 1)
            eng.memset(pl.mhalf[:, :], -0.5).then_inc(ones_set, 1)

        @block.vector
        def _(eng):
            eng.wait_ge(pl.x_loaded, 16)
            for t in range(0, NT, 4):
                tiles_stats(pl, eng, t)
            pl.stats_n += 2 * NT
            eng.wait_ge(mask_loaded, 16)
            eng.tensor_copy(maskf[:, :], mask8[:, :]).then_inc(mstep, 1)
            eng.wait_ge(mstep, 1)
            eng.tensor_scalar(pl.maskb[:, :], maskf[:, :], -1.0, -NEG, ALU.add, ALU.mult).then_inc(mstep, 1)
            eng.tensor_reduce(vflag[:, :], maskf[:, :], AX.X, ALU.max).then_inc(mstep, 1)
            eng.wait_ge(mstep, 3)
            eng.wait_ge(ident_set, 2)
            eng.tensor_scalar(dflag[:, :], pl.ident[0:B, 0:B], vflag[:, 0:1], None, ALU.mult).then_inc(mstep, 1)
            eng.wait_ge(fl_done, 1)
            eng.tensor_copy(pl.flag[:, :], ps[:, 7, 0:B]).then_inc(mstep, 1)
            eng.wait_ge(last_in, 16)
            bfloat_parts(eng, last[:, :], [lparts[:, j, :] for j in range(3)], (lrest0[:, :], lrest1[:, :]), last_step, 0)
            eng.wait_ge(consts_in, 16 * len(CONSTS))

        @block.tensor
        def _(eng):
            eng.wait_ge(w_loaded, 32)
            for k in range(NA):
                if k >= 8:
                    eng.wait_ge(evac, k - 7)
                for j in range(4):
                    c, h = divmod(4 * k + j, NH)
                    mm = eng.matmul(ps[:, k % 8, j * CD:(j + 1) * CD], wq[:, h, c * P:(c + 1) * P], wk[:, h // 2, :],
                                    start=True, stop=True)
                mm.then_inc(filled, 1)
            eng.wait_ge(vo_loaded, 32)
            for k in range(NA, NA + NBK):
                eng.wait_ge(evac, k - 7)
                for j in range(2):
                    h = 2 * (k - NA) + j
                    mm = eng.matmul(ps[:, k % 8, j * D:(j + 1) * D], wv[:, h // 2, :], wo[:, h, :], start=True, stop=True)
                mm.then_inc(filled, 1)
            eng.wait_ge(mstep, 4)
            eng.wait_ge(ones_set, 1)
            eng.wait_ge(evac, NA + NBK)
            eng.matmul(ps[:, 7, 0:B], ones[:, :], dflag[:, :], start=True, stop=True).then_inc(fl_done, 1)


def layer_norm_steps(pl, name):
    return {k: pl.sem(f"{name}_{k}") for k in ("rs_in", "rstd", "xn", "turned", "xT")}


def rstd_of_all(pl, eng, s, meanwhile=None):
    eng.wait_ge(pl.stats, pl.stats_n)
    eng.tensor_scalar(pl.veps[:, :], pl.mv[:, :, 1], EPS, None, ALU.add).then_inc(s["rs_in"], 1)
    if meanwhile:
        meanwhile()
    eng.wait_ge(s["rstd"], 1)


def pow_of_all(pl, eng, s):
    eng.wait_ge(s["rs_in"], 1)
    eng.tensor_tensor(pl.rstd[:, :], pl.veps[:, :], pl.mhalf[:, :], ALU.pow).then_inc(s["rstd"], 1)


def norm_supertile(pl, eng, s, xn, xT, i):
    for j in range(4):
        if j == 0:
            eng.wait_ge(s["turned"], i * 2)
        eng.tensor_scalar(xn[:, j, :], pl.x[:, i * 4 + j, :], pl.mv[:, i * 4 + j, 0:1], pl.rstd[:, bass.ds(i * 4 + j, 1)],
                          ALU.subtract, ALU.mult).then_inc(s["xn"], 1)
    for m in range(2):
        eng.wait_ge(s["turned"], i * 2 + m + 1)
        eng.tensor_copy(xT[:, :, bass.ds(i * ST + m * 256, 256)],
                        pl.ps[:, 6 + m, :].rearrange("p (k n) -> p k n", k=KC)).then_inc(s["xT"], 1)


def turn_supertile(pl, eng, s, xn, i):
    for m in range(2):
        eng.wait_ge(s["xn"], i * 4 + 2 * m + 2)
        eng.wait_ge(s["xT"], i * 2)
        for j in range(2):
            for k in range(KC):
                mm = eng.transpose(pl.ps[:, 6 + m, k * 256 + j * P:k * 256 + j * P + P],
                                   xn[:, 2 * m + j, k * P:(k + 1) * P], pl.ident[:, :])
        mm.then_inc(s["turned"], 1)


def l0x_queries(pl):
    nc = pl.nc
    pl.QO = pl.at("QO", [P, NH, TOK], F32, QO_OFF)
    xT = pl.at("l0x_xT", [P, KC, TOK], F32, pl.tmp_off)
    xn = pl.at("l0x_xn", [P, 4, D], F32, pl.end)
    assert pl.end <= QO_OFF
    s = layer_norm_steps(pl, "l0xq")
    look_up = LookUp(pl, 0, pl.const_end, pl.end)
    assert pl.end <= QO_OFF
    filled, evac = pl.sem("l0xq_filled"), pl.sem("l0xq_bank_free")

    with nc.Block() as block:
        @block.sync
        def _(eng):
            look_up.sync(eng)

        @block.gpsimd
        def _(eng):
            pow_of_all(pl, eng, s)

        @block.vector
        def _(eng):
            rstd_of_all(pl, eng, s)
            for i in range(SUP):
                norm_supertile(pl, eng, s, xn, xT, i)
                look_up.vector(eng, i)

        @block.scalar
        def _(eng):
            eng.sem_inc(evac, 4)
            with eng.Fori(0, SUP) as i:
                for h in range(NH):
                    eng.wait_ge(filled, i * NH + h + 1)
                    eng.activation(pl.QO[:, h, bass.ds(i * ST, ST)], pl.ps[:, h % 4, :], ACT.Copy).then_inc(evac, 1)

        @block.tensor
        def _(eng):
            def heads(i, lo, hi):
                for h in range(lo, hi):
                    eng.wait_ge(evac, i * NH + h + 1)
                    for k in range(KC):
                        mm = eng.matmul(pl.ps[:, h % 4, :], pl.Aw[:, k, h, :], xT[:, k, bass.ds(i * ST, ST)],
                                        start=(k == 0), stop=(k == KC - 1))
                    mm.then_inc(filled, 1)

            turn_supertile(pl, eng, s, xn, 0)
            with eng.Fori(0, SUP - 1) as i:
                eng.wait_ge(s["xT"], i * 2 + 2)
                heads(i, 0, NH // 2)
                turn_supertile(pl, eng, s, xn, i + 1)
                heads(i, NH // 2, NH)
            eng.wait_ge(s["xT"], SUP * 2)
            heads(SUP - 1, 0, NH)


UB = 4


def xattn_batches(pl, name, low, high, masked, normed=False):
    nc, ps, QO = pl.nc, pl.ps, pl.QO
    SC = float(HD) ** -0.5
    sm = {}
    qb = [pl.at(f"{name}_qb{j}", [P, NH, S], F32, low if j == 0 else pl.end) for j in range(2)]
    ctxT = [pl.at(f"{name}_ctxT{j}", [P, CS], F32, pl.end) for j in range(UB)]
    ctxn = [pl.at(f"{name}_ctx{j}", [P, 2, CD], F32, pl.end) for j in range(UB)]
    ctxl = [pl.at(f"{name}_ctxl{j}", [9, CD], BF16, pl.end) for j in range(UB)]
    if normed:
        rk = [pl.at(f"{name}_rk{j}", [3 * NH, CS], BF16, pl.end) for j in range(UB)]
        rkr = [pl.at(f"{name}_rkr{j}", [P, CS], F32, pl.end) for j in range(2)]
    assert high is None or pl.end <= high, pl.end
    prob = [pl.at(f"{name}_prob{j}", [P, GQ, CS], F32, high if high and j == 0 else pl.end) for j in range(2)]
    pT = pl.at(f"{name}_pT", [P, 2, 512], F32, pl.end)
    pTl = pl.at(f"{name}_pTl", [9, 512], BF16, pl.end)
    pl9 = [pl.at(f"{name}_last{j}", [P, GQ, 9], BF16, pl.end) for j in range(2)]
    lr = [pl.at(f"{name}_last_rest{j}", [P, GQ], F32, pl.end) for j in range(3)]
    mx = [pl.at(f"{name}_mx{j}", [P, GQ], F32, pl.end) for j in range(2)]
    nb = [pl.at(f"{name}_nb{j}", [P, GQ], F32, pl.end) for j in range(2)]
    sums = [pl.at(f"{name}_sum{j}", [P, GQ], F32, pl.end) for j in range(2)]
    rinv = [pl.at(f"{name}_rinv{j}", [P, GQ], F32, pl.end) for j in range(2)]
    rfl = [pl.at(f"{name}_rfl{j}", [P, GQ], F32, pl.end) for j in range(2)]
    mx_end = pl.end
    if normed:
        bw = pl.Bw1 = pl.at("Bw1", [P, NH, D], F32, QO_OFF - NH * D * 4)
        bw_in = pl.bw1_in = pl.sem(f"{name}_bw_loaded")
        assert pl.end >= QO_OFF - 32
        assert mx_end <= QO_OFF - NH * D * 4, mx_end
        pl.end = mx_end
    assert pl.end <= QO_OFF, pl.end - QO_OFF
    T0, T1, TL, O = 4, 5, 6, 7
    ctxT_in = [pl.sem(f"{name}_ctxT_loaded{j}") for j in range(UB)]
    ctxn_in = [pl.sem(f"{name}_ctx_loaded{j}") for j in range(UB)]
    rk_in = [pl.sem(f"{name}_rk_loaded{j}") for j in range(UB)] if normed else None
    for k in ("qb", "rep", "rep_out", "scaled", "scored", "mx", "nb", "exp", "rinv", "rfl", "norm", "turned",
              "pT_scalar", "pT_vector", "attended", "out_read", "last"):
        sm[k] = pl.sem(f"{name}_{k}")
    NI = B // UB

    with nc.Block() as block:
        @block.sync
        def _(eng):
            def load(i, p):
                b = i * UB + p
                eng.wait_ge(sm["scored"], (i - 1) * UB * GQ + (p + 1) * GQ) if not isinstance(i, int) else None
                eng.dma_start(ctxT[p][:, :], pl.ap["ctxT"][:, bass.ds(b * CS, CS)]).then_inc(ctxT_in[p], 16)
                if normed:
                    eng.dma_start(rk[p][:, :], pl.rk_dram[:, bass.ds(b * CS, CS)]).then_inc(rk_in[p], 16)
                eng.wait_ge(sm["attended"], (i - 1) * UB + p + 1) if not isinstance(i, int) else None
                eng.dma_start(ctxn[p][:, :, :], pl.ap["ctx"][b, 0:2 * P, :].rearrange("(c p) d -> p c d", p=P) if isinstance(b, int)
                              else pl.ap["ctx"][bass.ds(b, 1), 0:2 * P, :].rearrange("b (c p) d -> p (b c) d", p=P)).then_inc(ctxn_in[p], 16)
                eng.dma_start(ctxl[p][:, :], pl.last_dram[bass.ds(b, 1), :, :].rearrange("b r d -> (b r) d")).then_inc(ctxn_in[p], 16)
            for p in range(UB):
                load(0, p)
            if normed:
                eng.dma_start(bw[:, :, :], pl.bw1_dram).then_inc(bw_in, 16)
            with eng.Fori(1, NI) as i:
                for p in range(UB):
                    load(i, p)

        def each_batch(eng, first, step):
            first()
            for p in range(UB):
                step(0, p, True)
            with eng.Fori(1, NI - 1) as i:
                for p in range(UB):
                    step(i, p, True)
            for p in range(UB):
                step(NI - 1, p, p < UB - 1)

        @block.gpsimd
        def _(eng):
            def copy_q(i, p):
                b = i * UB + p
                if not (isinstance(i, int) and i * UB + p < 2):
                    eng.wait_ge(sm["scored"], b * GQ - GQ)
                eng.tensor_copy(qb[p % 2][:, :, :], QO[:, :, bass.ds(b * S, S)]).then_inc(sm["qb"], 1)

            def first():
                copy_q(0, 0)
                copy_q(0, 1)

            def step(i, p, more):
                if not (isinstance(i, int) and i == NI - 1 and p >= UB - 2):
                    b = i * UB + p + 2
                    eng.wait_ge(sm["scored"], b * GQ - GQ)
                    eng.tensor_copy(qb[p % 2][:, :, :], QO[:, :, bass.ds(b * S, S)]).then_inc(sm["qb"], 1)
            each_batch(eng, first, step)

        @block.vector
        def _(eng):
            def scaled_maxima(i, p, m):
                b = i * UB + p
                for g in (2 * m, 2 * m + 1):
                    eng.wait_ge(sm["rep_out"], b * GQ + g + 1)
                    eng.wait_ge(sm["scored"], b * GQ + g + 1)
                    if g == 0 and not (isinstance(i, int) and b < 2):
                        eng.wait_ge(sm["turned"], b - 1)
                    apart(pl, eng)
                    eng.tensor_tensor_reduce(out=prob[p % 2][:, g, :], in0=ps[:, g % 2, 0:CS], in1=rkr[g % 2][:, :], scale=1.0,
                                             scalar=-3.0e38, op0=ALU.mult, op1=ALU.max, accum_out=mx[p % 2][:, g:g + 1]).then_inc(sm["scaled"], 1)
                eng.wait_ge(sm["scaled"], b * GQ + 2 * m + 2)
                eng.scalar_tensor_tensor(out=nb[p % 2][:, 2 * m:2 * m + 2], in0=mx[p % 2][:, 2 * m:2 * m + 2], scalar=-1.0,
                                         in1=pl.rq[:, bass.ds(b, 1), 2 * m:2 * m + 2].rearrange("p a g -> p (a g)"),
                                         op0=ALU.mult, op1=ALU.mult).then_inc(sm["nb"], 1)

            def maxima(i, p, m):
                b = i * UB + p
                if normed:
                    return scaled_maxima(i, p, m)
                eng.wait_ge(sm["scored"], b * GQ + 2 * m + 2)
                eng.tensor_reduce(mx[p % 2][:, 2 * m:2 * m + 2], ps[:, 2 * m:2 * m + 2, 0:CS], AX.X, ALU.max).then_inc(sm["mx"], 1)
                eng.wait_ge(sm["mx"], b * 2 + m + 1)
                eng.tensor_scalar(nb[p % 2][:, 2 * m:2 * m + 2], mx[p % 2][:, 2 * m:2 * m + 2], -SC, None,
                                  ALU.mult).then_inc(sm["nb"], 1)

            def inverse(i, p):
                b = i * UB + p
                factor = rfl if masked else rinv
                q, n = p % 2, b * 6

                def norm(g):
                    eng.tensor_scalar(prob[q][:, g, 0:CS - 1], prob[q][:, g, 0:CS - 1], factor[q][:, g:g + 1], None,
                                      ALU.mult).then_inc(sm["norm"], 1)
                for m in range(2):
                    c = slice(2 * m, 2 * m + 2)
                    eng.wait_ge(sm["exp"], b * GQ + 2 * m + 2)
                    eng.reciprocal(rinv[q][:, c], sums[q][:, c]).then_inc(sm["rinv"], 1)
                    eng.wait_ge(sm["rinv"], b * 2 + m + 1)
                    if masked:
                        eng.tensor_scalar(rfl[q][:, c], rinv[q][:, c], pl.flag[:, bass.ds(b, 1)], None, ALU.mult).then_inc(sm["rfl"], 1)
                        eng.wait_ge(sm["rfl"], b * 2 + m + 1)
                    if m == 0:
                        norm(0)
                if not (isinstance(i, int) and b < 2):
                    eng.wait_ge(sm["turned"], b - 1)
                eng.tensor_tensor(lr[0][:, :], prob[q][:, :, CS - 1], factor[q][:, :], ALU.mult).then_inc(sm["last"], 1)
                for k, g in enumerate((1, 2, 3, None)):
                    if g:
                        norm(g)
                    eng.wait_ge(sm["last"], n + k + 1)
                    j = k // 2
                    if k % 2 == 0:
                        eng.tensor_copy(pl9[q][:, :, 3 * j:3 * j + 3], lr[j][:, :, None].to_broadcast([P, GQ, 3])).then_inc(sm["last"], 1)
                    else:
                        eng.tensor_tensor(lr[j + 1][:, :], lr[j][:, :], pl9[q][:, :, 3 * j], ALU.subtract).then_inc(sm["last"], 1)
                eng.wait_ge(sm["last"], n + 5)
                eng.tensor_copy(pl9[q][:, :, 6:9], lr[2][:, :, None].to_broadcast([P, GQ, 3])).then_inc(sm["last"], 1)

            def take_last(b):
                eng.wait_ge(sm["turned"], b + 1)
                eng.wait_ge(sm["attended"], b)
                eng.tensor_copy(pTl[:, :], ps[0:9, TL, 0:256].bitcast(BF16)).then_inc(sm["pT_vector"], 1)

            def first():
                maxima(0, 0, 0)
                maxima(0, 0, 1)
                inverse(0, 0)

            def step(i, p, more):
                b = i * UB + p
                n = i + (p + 1) // UB, (p + 1) % UB
                if more:
                    maxima(*n, 0)
                if not (isinstance(b, int) and b == 0):
                    take_last(b - 1)
                if more:
                    maxima(*n, 1)
                    inverse(*n)
                else:
                    take_last(b)
            each_batch(eng, first, step)

        @block.scalar
        def _(eng):
            eng.preload_act_table(ACT.Exp)

            def take_pT(b, c):
                eng.wait_ge(sm["turned"], b + 1)
                eng.wait_ge(sm["attended"], b)
                eng.activation(pT[:, c, :], ps[:, (T0, T1)[c], :], ACT.Copy).then_inc(sm["pT_scalar"], 1)

            def exps(i, p):
                b = i * UB + p
                if not normed and not (isinstance(i, int) and b < 2):
                    take_pT(b - 2, 1)
                if normed:
                    for g in range(GQ):
                        eng.wait_ge(sm["rep"], b * GQ + g + 1)
                        if g >= 2 or not (isinstance(i, int) and b == 0):
                            eng.wait_ge(sm["scaled"], b * GQ + g - 1)
                        eng.activation(rkr[g % 2][:, :], ps[:, 2 + g % 2, 0:CS], ACT.Copy).then_inc(sm["rep_out"], 1)
                        if g == 1 and not (isinstance(i, int) and b < 2):
                            take_pT(b - 2, 1)
                for g in range(GQ):
                    if g % 2 == 0:
                        eng.wait_ge(sm["nb"], b * 2 + g // 2 + 1)
                    if g == 0 and not (isinstance(i, int) and b < 2):
                        eng.wait_ge(sm["turned"], b - 1)
                    src, scale = (prob[p % 2][:, g, :], pl.rq[:, b, g:g + 1]) if normed else (ps[:, g, 0:CS], SC)
                    eng.activation(prob[p % 2][:, g, :], src, ACT.Exp, bias=nb[p % 2][:, g:g + 1], scale=scale,
                                   accum_out=sums[p % 2][:, g:g + 1]).then_inc(sm["exp"], 1)

            def take_output(b):
                eng.wait_ge(sm["attended"], b + 1)
                eng.activation(QO[:, :, bass.ds(b * S, S)], ps[:, O, :].rearrange("p (h s) -> p h s", s=S), ACT.Copy).then_inc(sm["out_read"], 1)

            def step(i, p, more):
                b = i * UB + p
                if more:
                    exps(i + (p + 1) // UB, (p + 1) % UB)
                else:
                    take_pT(b - 1, 1)
                if not (isinstance(b, int) and b == 0):
                    take_output(b - 1)
                take_pT(b, 0)
                if not more:
                    take_pT(b, 1)
                    take_output(b)
            each_batch(eng, lambda: exps(0, 0), step)

        @block.tensor
        def _(eng):
            def scores(i, p, groups):
                b = i * UB + p
                if groups[0] == 0:
                    eng.wait_ge(ctxT_in[p], i * 16 + 16)
                    eng.wait_ge(sm["qb"], b + 1)
                    if normed:
                        eng.wait_ge(rk_in[p], i * 16 + 16)
                for g in groups:
                    if normed:
                        if g >= 2 or not (isinstance(i, int) and b == 0):
                            eng.wait_ge(sm["rep_out"], b * GQ + g - 1)
                        eng.matmul(ps[:, 2 + g % 2, 0:CS], pl.pick[:, g, :], rk[p][:, :], start=True, stop=True).then_inc(sm["rep"], 1)
                        if g >= 2 or not (isinstance(i, int) and b == 0):
                            eng.wait_ge(sm["scaled"], b * GQ + g - 1)
                        eng.matmul(ps[:, g % 2, 0:CS], qb[p % 2][:, 4 * g:4 * g + 4, :], ctxT[p][:, :], start=True, stop=True).then_inc(sm["scored"], 1)
                        continue
                    if not (isinstance(i, int) and b == 0):
                        eng.wait_ge(sm["exp"], b * GQ - GQ + g + 1)
                    mm = eng.matmul(ps[:, g, 0:CS], qb[p % 2][:, 4 * g:4 * g + 4, :], ctxT[p][:, :], start=True, stop=not masked)
                    if masked:
                        mm = eng.matmul(ps[:, g, 0:CS], pl.identb[0:B, bass.ds(b, 1)].to_broadcast([B, P]), pl.maskb[:, :],
                                        start=False, stop=True)
                    mm.then_inc(sm["scored"], 1)

            def products(i, p):
                b = i * UB + p
                eng.wait_ge(ctxn_in[p], i * 32 + 32)
                eng.wait_ge(sm["out_read"], b)
                eng.wait_ge(sm["pT_scalar"], 2 * b + 1)
                eng.matmul(ps[:, O, :], ctxn[p][:, 0, :], pT[:, 0, :], start=True, stop=False)
                eng.wait_ge(sm["pT_scalar"], 2 * b + 2)
                eng.matmul(ps[:, O, :], ctxn[p][:, 1, :], pT[:, 1, :], start=False, stop=False)
                eng.wait_ge(sm["pT_vector"], b + 1)
                eng.matmul(ps[:, O, :], ctxl[p][:, :], pTl[:, :], start=False, stop=True).then_inc(sm["attended"], 1)

            def step(i, p, more):
                b = i * UB + p
                if more:
                    scores(i + (p + 1) // UB, (p + 1) % UB, range(GQ))
                if not (isinstance(b, int) and b == 0):
                    products(i - (p == 0), (p - 1) % UB)
                eng.wait_ge(sm["pT_scalar"], 2 * b)
                eng.wait_ge(sm["pT_vector"], b)
                for g in range(GQ):
                    eng.wait_ge(sm["norm"], b * GQ + g + 1)
                    for c, bank in enumerate((T0, T1)):
                        eng.transpose(ps[:, bank, g * P:(g + 1) * P], prob[p % 2][:, g, c * P:(c + 1) * P], pl.ident[:, :])
                eng.wait_ge(sm["last"], b * 6 + 6)
                for g in range(GQ):
                    mm = eng.transpose(ps[0:9, TL, g * P // 2:(g + 1) * P // 2].bitcast(BF16), pl9[p % 2][:, g, :], pl.identb[:, :])
                mm.then_inc(sm["turned"], 1)
                if not more:
                    products(i, p)
            each_batch(eng, lambda: scores(0, 0, range(GQ)), step)


def xattn_project(pl, name, Bw, low, share, bw_in=None, weights=None):
    nc, ps, QO = pl.nc, pl.ps, pl.QO
    yT = [pl.at(f"{name}_yT{j}", [P, KC, 512], F32, low if j == 0 else pl.end) for j in range(2)]
    assert pl.end <= QO_OFF - (NH * D * 4 if bw_in is not None else 0)
    look_up = LookUp(pl, share, pl.const_end, pl.end)
    made, y, turned, added = (pl.sem(f"{name}_{k}") for k in ("made", "y", "turned", "added"))

    with nc.Block() as block:
        @block.sync
        def _(eng):
            if weights:
                weights.sync(eng)
            look_up.sync(eng)

        if weights:
            @block.gpsimd
            def _(eng):
                weights.gpsimd(eng)

        @block.tensor
        def _(eng):
            def products(s):
                for k in range(KC):
                    if s >= 2:
                        eng.wait_ge(y, 2 * (s - 2) + k + 1)
                    for h in range(NH):
                        mm = eng.matmul(ps[:, 2 * (s % 2) + k, :], Bw[:, h, k * P:(k + 1) * P], QO[:, h, s * ST:(s + 1) * ST],
                                        start=(h == 0), stop=(h == NH - 1))
                    mm.then_inc(made, 1)

            def turn(s):
                eng.wait_ge(y, 2 * s + 2)
                if s >= 1:
                    eng.wait_ge(added, 2 * s)
                for m in range(2):
                    for j in range(2):
                        for k in range(KC):
                            mm = eng.transpose(ps[:, 4 + m, j * D + k * P:j * D + (k + 1) * P],
                                               yT[s % 2][:, k, (2 * m + j) * P:(2 * m + j + 1) * P], pl.ident[:, :])
                    mm.then_inc(turned, 1)

            if bw_in is not None:
                eng.wait_ge(bw_in, 16)
            products(0)
            if weights:
                weights.tensor(eng)
            for s in range(SUP):
                if s + 1 < SUP:
                    products(s + 1)
                turn(s)

        @block.scalar
        def _(eng):
            for s in range(SUP):
                if s >= 2:
                    eng.wait_ge(turned, 2 * (s - 1))
                for k in range(KC):
                    eng.wait_ge(made, 2 * s + k + 1)
                    eng.activation(yT[s % 2][:, k, :], ps[:, 2 * (s % 2) + k, :], ACT.Copy).then_inc(y, 1)

        @block.vector
        def _(eng):
            def add(s):
                for m in range(2):
                    t = 4 * s + 2 * m
                    eng.wait_ge(turned, 2 * s + m + 1)
                    eng.tensor_tensor(pl.x[:, t:t + 2, :], ps[:, 4 + m, :].rearrange("p (t d) -> p t d", t=2),
                                      pl.x[:, t:t + 2, :], ALU.add).then_inc(added, 1)
                eng.wait_ge(added, 2 * s + 2)
                tiles_stats(pl, eng, 4 * s)

            if weights:
                weights.vector_sums(eng)
            look_up.vector(eng, 0)
            if weights:
                weights.vector_ternary(eng)
            look_up.vector(eng, 1)
            for s in range(SUP):
                add(s)
                if s < 2:
                    look_up.vector(eng, 2 + s)
            pl.stats_n += 2 * NT


def self_attention(pl):
    nc, ps = pl.nc, pl.ps
    HQ, HKV, E = 32, 4, 64
    NQ, NKV = HQ * E, HKV * E
    NB = P // S
    SC = float(E) ** -0.5
    w = pl.at("sa_wqkv", [P, KC, NQ + 2 * NKV], F32, L_OFF)
    wo = pl.at("sa_wo", [P, NQ // P, D], F32, pl.end)
    wp = [pl.at(f"sa_wqkv_{k}", [P, KC, NQ + 2 * NKV], F32, pl.end) for k in ("head", "rest")]
    wop = [pl.at(f"sa_wo_{k}", [P, NQ // P, D], F32, pl.end) for k in ("head", "rest")]
    xn = pl.at("sa_xn", [P, D], F32, pl.end)
    xT = [pl.at(f"sa_xT_{k}", [P, KC, P], F32, pl.end) for k in ("head", "rest")]
    qk = pl.at("sa_qk", [P, HQ + HKV, 2, E // 2], F32, pl.end)
    v = [pl.at(f"sa_v{j}", [P, NKV], F32, pl.end) for j in range(2)]
    rot = pl.at("sa_rot", [P, HQ + HKV, 2, E // 2], F32, pl.end)
    rsin = pl.at("sa_rsin", [P, HQ + HKV, 2, E // 2], F32, pl.end)
    kd = pl.at("sa_kd", [P, HKV, 2, E], F32, pl.end)
    qT = pl.at("sa_qT", [P, NQ // P, P], F32, pl.end)
    kT = pl.at("sa_kT", [P, HKV, P], F32, pl.end)
    sc = pl.at("sa_sc", [P, HQ, S], F32, pl.end)
    pT = pl.at("sa_pT", [P, HQ, S], F32, pl.end)
    mx = pl.at("sa_mx", [P, HQ], F32, pl.end)
    sums = pl.at("sa_sums", [P, HQ], F32, pl.end)
    rinv = pl.at("sa_rinv", [P, HQ], F32, pl.end)
    oT = [pl.at(f"sa_oT_{k}", [P, NQ // P, P], F32, pl.end) for k in ("head", "rest")]
    s = {k: pl.sem(f"sa_{k}") for k in (
        "w_in", "wo_in", "rs_in", "rstd", "xn", "xturned", "xT", "projected", "qkv", "cos", "sin", "rotated", "turned",
        "turned_scalar", "turned_vector", "scored", "soft", "exp", "pT", "valued", "oT", "oT_rest", "output", "added",
        "x_rest", "w_head", "w_rest")}
    NW = 5

    def weight_slices(n):
        if n < NW:
            return [x[:, :, n * 512:(n + 1) * 512] for x in (w, *wp)]
        return [x[:, 4 * (n - NW):4 * (n - NW) + 4, :] for x in (wo, *wop)]

    def each_tile(eng, first, step):
        first()
        for t in range(2):
            step(t, t, True)
        with eng.Fori(1, NT // 2 - 1) as u:
            for p in range(2):
                step(u * 2 + p, p, True)
        for p in range(2):
            step(NT - 2 + p, p, p == 0)

    with nc.Block() as block:
        @block.sync
        def _(eng):
            eng.dma_start(w[:, :, :], pl.ap["L0_wqkvT"]).then_inc(s["w_in"], 16)
            eng.dma_start(wo[:, :, :], pl.ap["L0_woT"]).then_inc(s["wo_in"], 16)

        @block.gpsimd
        def _(eng):
            pow_of_all(pl, eng, s)

            def sine(t):
                eng.wait_ge(s["rotated"], t * 3)
                for k in range(NW):
                    eng.wait_ge(s["qkv"], t * 6 + k + 1)
                    h = slice(8 * k, min(8 * k + 8, HQ + HKV))
                    for a in range(2):
                        eng.tensor_tensor(rsin[:, h, a, :], qk[:, h, 1 - a, :],
                                          pl.cst["sin64"][:, None, a * 32:a * 32 + 32].to_broadcast([P, h.stop - h.start, 32]),
                                          ALU.mult).then_inc(s["sin"], 1)
            each_tile(eng, lambda: sine(0), lambda t, p, more: sine(t + 1) if more else None)

        @block.vector
        def _(eng):
            rstd_of_all(pl, eng, s)

            def norm(t):
                eng.wait_ge(s["xturned"], t)
                eng.tensor_scalar(xn[:, :], pl.x[:, t, :] if isinstance(t, int) else pl.x[:, bass.ds(t, 1), :].rearrange("p a d -> p (a d)"),
                                  pl.mv[:, t, 0:1], pl.rstd[:, bass.ds(t, 1)], ALU.subtract, ALU.mult).then_inc(s["xn"], 1)

            def weight_rest(n):
                eng.wait_ge(s["w_head"], n + 1)
                rest_of(eng, *weight_slices(n)).then_inc(s["w_rest"], 1)

            def x_rest(t):
                eng.wait_ge(s["xT"], t + 1)
                rest_of(eng, ps[:, 6, 0:KC * P].rearrange("p (k n) -> p k n", k=KC), xT[0][:, :, :], xT[1][:, :, :]).then_inc(s["x_rest"], 1)

            def output_rest(t):
                for b in range(NB):
                    eng.wait_ge(s["oT"], t * 4 + b + 1)
                    eng.wait_ge(s["output"], t)
                    c = slice(b * S, (b + 1) * S)
                    rest_of(eng, ps[:, 2 + b, :].rearrange("p (c q) -> p c q", q=S), oT[0][:, :, c], oT[1][:, :, c]).then_inc(s["oT_rest"], 1)

            def cosine(t):
                eng.wait_ge(s["qkv"], t * 6 + 5)
                eng.wait_ge(s["turned"], t * 5)
                eng.tensor_tensor(rot[:, :, :, :].rearrange("p h a e -> p h (a e)"), qk[:, :, :, :].rearrange("p h a e -> p h (a e)"),
                                  pl.cst["cos64"][:, None, :].to_broadcast([P, HQ + HKV, E]), ALU.mult).then_inc(s["cos"], 1)

            def rotate(t):
                eng.wait_ge(s["cos"], t + 1)
                eng.wait_ge(s["sin"], (t + 1) * 2 * NW)
                f = lambda a: a.rearrange("p h a e -> p h (a e)")
                eng.tensor_tensor(f(rot[:, 0:HQ]), f(rot[:, 0:HQ]), f(rsin[:, 0:HQ]), ALU.add).then_inc(s["rotated"], 1)
                for a in range(2):
                    eng.tensor_tensor(kd[:, :, a, :], f(rot[:, HQ:]), f(rsin[:, HQ:]), ALU.add).then_inc(s["rotated"], 1)

            def take_turned(t):
                for k in (1, 3):
                    eng.wait_ge(s["turned"], t * 5 + k + 1)
                    eng.wait_ge(s["scored"], t)
                    eng.tensor_copy(qT[:, 4 * k:4 * k + 4, :], ps[:, 6 + (7 + k) % 2, :].rearrange("p (c n) -> p c n", c=4)).then_inc(s["turned_vector"], 1)

            def softmax(t):
                n = t * 6
                eng.wait_ge(s["scored"], t + 1)
                eng.tensor_tensor(sc[:, :, :], ps[:, 0:2, :].rearrange("p a (h k) -> p (a h) k", k=S),
                                  pl.cst["causal"][:, None, :].to_broadcast([P, HQ, S]), ALU.add).then_inc(s["soft"], 1)
                eng.wait_ge(s["soft"], n + 1)
                eng.tensor_reduce(mx[:, :], sc[:, :, :], AX.X, ALU.max).then_inc(s["soft"], 1)
                eng.wait_ge(s["soft"], n + 2)
                eng.tensor_tensor(sc[:, :, :], sc[:, :, :], mx[:, :, None].to_broadcast([P, HQ, S]), ALU.subtract).then_inc(s["soft"], 1)
                eng.wait_ge(s["exp"], t + 1)
                eng.tensor_reduce(sums[:, :], sc[:, :, :], AX.X, ALU.add).then_inc(s["soft"], 1)
                eng.wait_ge(s["soft"], n + 4)
                eng.reciprocal(rinv[:, :], sums[:, :]).then_inc(s["soft"], 1)
                eng.wait_ge(s["soft"], n + 5)
                eng.tensor_tensor(sc[:, :, :], sc[:, :, :], rinv[:, :, None].to_broadcast([P, HQ, S]), ALU.mult).then_inc(s["soft"], 1)
                eng.wait_ge(s["soft"], n + 6)
                eng.wait_ge(s["valued"], t * 4)
                eng.transpose(pT[:, :, :].rearrange("p h q -> p (h q)"), sc[:, :, :].rearrange("p h k -> p (h k)")).then_inc(s["pT"], 1)

            def add(t):
                eng.wait_ge(s["output"], t + 1)
                xt = pl.x[:, t, :]
                eng.tensor_tensor(xt, ps[:, 6, 0:D], xt, ALU.add).then_inc(s["added"], 1)
                eng.wait_ge(s["added"], t + 1)
                token_stats(pl, eng, t)

            def first():
                norm(0)
                weight_rest(0)
                x_rest(0)
                for n in range(1, NW + 4):
                    weight_rest(n)
                cosine(0)
                rotate(0)
                take_turned(0)
                norm(1)

            def step(t, p, more):
                if more:
                    x_rest(t + 1)
                softmax(t)
                if more:
                    cosine(t + 1)
                    rotate(t + 1)
                if not (isinstance(t, int) and t == 0):
                    add(t - 1)
                if more:
                    take_turned(t + 1)
                if not isinstance(t, int) or t + 2 < NT:
                    norm(t + 2)
                output_rest(t)
                if not more:
                    add(t)
            each_tile(eng, first, step)
            pl.stats_n += 3 * NT

        @block.scalar
        def _(eng):
            eng.preload_act_table(ACT.Exp)

            def take_xT(t):
                eng.wait_ge(s["xturned"], t + 1)
                eng.wait_ge(s["projected"], t * NW)
                eng.activation(xT[0][:, :, :].bitcast(F32R), ps[:, 6, 0:KC * P].rearrange("p (k n) -> p k n", k=KC), ACT.Copy).then_inc(s["xT"], 1)

            def take_qkv(t, p, lo, hi):
                for k in range(lo, hi):
                    eng.wait_ge(s["projected"], t * NW + k + 1)
                    eng.wait_ge(s["cos"], t)
                    eng.wait_ge(s["sin"], 2 * NW * t)
                    bank = ps[:, 6 + (1 + k) % 2, :]
                    if k < NW - 1:
                        eng.activation(qk[:, 8 * k:8 * k + 8, :, :].rearrange("p h a e -> p (h a e)"), bank, ACT.Copy).then_inc(s["qkv"], 1)
                    else:
                        eng.activation(qk[:, HQ:, :, :].rearrange("p h a e -> p (h a e)"), bank[:, 0:NKV], ACT.Copy).then_inc(s["qkv"], 1)
                        eng.activation(v[p][:, :], bank[:, NKV:2 * NKV], ACT.Copy).then_inc(s["qkv"], 1)

            def take_turned(t):
                for k in (0, 2, 4):
                    eng.wait_ge(s["turned"], t * 5 + k + 1)
                    eng.wait_ge(s["scored"], t)
                    dst = qT[:, 4 * k:4 * k + 4, :] if k < 4 else kT[:, :, :]
                    eng.activation(dst, ps[:, 6 + (7 + k) % 2, :].rearrange("p (c n) -> p c n", c=4), ACT.Copy).then_inc(s["turned_scalar"], 1)

            def weight_head(n):
                if n in (0, NW):
                    eng.wait_ge(s["w_in"] if n == 0 else s["wo_in"], 16)
                src, dst, _ = weight_slices(n)
                eng.activation(dst.bitcast(F32R), src, ACT.Copy).then_inc(s["w_head"], 1)

            def first():
                weight_head(0)
                take_xT(0)
                for n in range(1, NW + 4):
                    weight_head(n)
                take_qkv(0, 0, 0, NW)
                take_turned(0)

            def step(t, p, more):
                if more:
                    take_xT(t + 1)
                    take_qkv(t + 1, 1 - p, 0, 2)
                eng.wait_ge(s["soft"], t * 6 + 3)
                eng.activation(sc[:, :, :], sc[:, :, :], ACT.Exp, scale=SC).then_inc(s["exp"], 1)
                if more:
                    take_qkv(t + 1, 1 - p, 2, NW)
                for b in range(NB):
                    eng.wait_ge(s["valued"], t * 4 + b + 1)
                    eng.wait_ge(s["output"], t)
                    eng.activation(oT[0][:, :, b * S:(b + 1) * S].bitcast(F32R), ps[:, 2 + b, :].rearrange("p (c q) -> p c q", q=S),
                                   ACT.Copy).then_inc(s["oT"], 1)
                if more:
                    take_turned(t + 1)
            each_tile(eng, first, step)

        @block.tensor
        def _(eng):
            def turn_x(t):
                eng.wait_ge(s["xn"], t + 1)
                eng.wait_ge(s["turned_vector"], 2 * t)
                for k in range(KC):
                    mm = eng.transpose(ps[:, 6, k * P:(k + 1) * P], xn[:, k * P:(k + 1) * P], pl.ident[:, :])
                mm.then_inc(s["xturned"], 1)

            def project(t):
                eng.wait_ge(s["x_rest"], t + 1)
                eng.wait_ge(s["turned_scalar"], 3 * t)
                for n in range(NW):
                    if n >= 2:
                        eng.wait_ge(s["qkv"], t * 6 + n - 1)
                    if isinstance(t, int) and t == 0:
                        eng.wait_ge(s["w_rest"], n + 1)
                    for k in range(KC):
                        mm = split_product(eng, ps[:, 6 + (1 + n) % 2, :], [x[:, k, :] for x in xT],
                                           [x[:, k, n * 512:(n + 1) * 512] for x in wp], k == 0, k == KC - 1)
                    mm.then_inc(s["projected"], 1)

            def turn(t):
                eng.wait_ge(s["rotated"], t * 3 + 3)
                for n in range(5):
                    if n == 0:
                        eng.wait_ge(s["qkv"], t * 6 + 6)
                    elif n == 1:
                        if not (isinstance(t, int) and t == 0):
                            eng.wait_ge(s["added"], t - 1)
                    elif n % 2 == 0:
                        eng.wait_ge(s["turned_scalar"], t * 3 + n // 2)
                    else:
                        eng.wait_ge(s["turned_vector"], t * 2 + 1)
                    for j in range(4):
                        src = rot[:, 8 * n + 2 * j:8 * n + 2 * j + 2, :, :].rearrange("p h a e -> p (h a e)") if n < 4 else \
                            kd[:, j, :, :].rearrange("p a e -> p (a e)")
                        mm = eng.transpose(ps[:, 6 + (7 + n) % 2, j * P:(j + 1) * P], src, pl.ident[:, :])
                    mm.then_inc(s["turned"], 1)

            def output(t, more):
                eng.wait_ge(s["oT_rest"], 4 * t + 4)
                if more:
                    eng.wait_ge(s["qkv"], (t + 2) * 6 + 4)
                else:
                    eng.wait_ge(s["added"], t)
                for c in range(NQ // P):
                    mm = split_product(eng, ps[:, 6, 0:D], [x[:, c, :] for x in oT], [x[:, c, :] for x in wop], c == 0, c == NQ // P - 1)
                mm.then_inc(s["output"], 1)

            def first():
                turn_x(0)
                project(0)
                turn(0)
                eng.wait_ge(s["w_rest"], NW + 4)

            def step(t, p, more):
                eng.wait_ge(s["turned_scalar"], 3 * t + 3)
                eng.wait_ge(s["turned_vector"], 2 * t + 2)
                if more:
                    turn_x(t + 1)
                eng.wait_ge(s["soft"], 6 * t)
                apart(pl, eng)
                for h in range(HQ):
                    a = (h % 2) * E
                    for b in range(NB):
                        mm = eng.matmul(ps[b * S:(b + 1) * S, h % 2, (h // 2) * S:(h // 2 + 1) * S],
                                        qT[a:a + E, h // 2, b * S:(b + 1) * S], kT[a:a + E, h // 8, b * S:(b + 1) * S],
                                        start=True, stop=True)
                mm.then_inc(s["scored"], 1)
                if more:
                    project(t + 1)
                if not (isinstance(t, int) and t == 0):
                    output(t - 1, more)
                eng.wait_ge(s["pT"], t + 1)
                eng.wait_ge(s["oT_rest"], 4 * t)
                for b in range(NB):
                    for k in range(HKV):
                        for a in range(2):
                            mm = eng.matmul(ps[a * E:(a + 1) * E, 2 + b, k * P:(k + 1) * P], v[p][b * S:(b + 1) * S, k * E:(k + 1) * E],
                                            pT[b * S:(b + 1) * S, NQ // P * a + 4 * k:NQ // P * a + 4 * k + 4, :], start=True, stop=True)
                    mm.then_inc(s["valued"], 1)
                if more:
                    turn(t + 1)
                else:
                    output(t, False)
            each_tile(eng, first, step)


class LookUp:
    ENTRIES, PIECES = 16, 16
    COLS = (KC * 2 * 688 + 6 * D) // PIECES
    BOUNDS = ((0, 1, 3, 5, 7), (0, 2, 3, 4, 5), (0, 1, 2, 3, 4))

    def __init__(self, pl, share, low, low2=None):
        self.pl, self.bounds = pl, self.BOUNDS[share]
        self.first, self.count = sum(b[-1] for b in self.BOUNDS[:share]), self.bounds[-1]
        assert sum(b[-1] for b in self.BOUNDS) == self.PIECES
        if share == 0:
            pl.lut_dram = pl.nc.dram_tensor("lut_scratch", (P, self.PIECES * self.COLS), F32, kind="Internal").ap()
        n = f"lu{share}_"
        pl.end = low
        self.idx, self.acc = ([pl.at(f"{n}{k}{j}", [P, self.COLS], dt, pl.end) for j in range(2)] for k, dt in (("idx", I32), ("acc", F32)))
        assert pl.end <= L_OFF
        if low2 is not None:
            pl.end = low2
        self.hit = [pl.at(f"{n}hit{j}", [P, self.COLS], F32, pl.end) for j in range(2)]
        self.lut, self.entry = (pl.at(f"{n}{k}", [P, self.ENTRIES], F32, pl.end) for k in ("table", "entry"))
        self.table_in, self.step = pl.sem(f"{n}table_loaded"), pl.sem(f"{n}step")
        self.idx_in, self.stored = ([pl.sem(f"{n}{k}{j}") for j in range(2)] for k in ("index_loaded", "stored"))
        self.steps = 2 * self.ENTRIES - 1

    def columns(self, k):
        return slice((self.first + k) * self.COLS, (self.first + k + 1) * self.COLS)

    def sync(self, eng):
        ap = self.pl.ap
        eng.dma_start(self.lut[:, :], ap["L1_lut"].to_broadcast([P, self.ENTRIES])).then_inc(self.table_in, 16)
        eng.dma_start(self.entry[:, :], ap["entries"]).then_inc(self.table_in, 16)
        for k in range(2):
            eng.dma_start(self.idx[k][:, :], ap["L1_idx"][:, self.columns(k)]).then_inc(self.idx_in[k], 16)
        for k in range(self.count):
            eng.wait_ge(self.step, (k + 1) * self.steps)
            eng.dma_start(self.pl.lut_dram[:, self.columns(k)], self.acc[k % 2][:, :]).then_inc(self.stored[k % 2], 16)
            if k + 2 < self.count:
                eng.dma_start(self.idx[k % 2][:, :], ap["L1_idx"][:, self.columns(k + 2)]).then_inc(self.idx_in[k % 2], 16)
        for p in range(2):
            eng.wait_ge(self.stored[p], 16 * ((self.count + 1 - p) // 2))

    def vector(self, eng, part):
        lo, hi = self.bounds[part:part + 2]
        if lo == 0:
            eng.wait_ge(self.table_in, 32)
        for k in range(lo, hi):
            idx, acc = self.idx[k % 2], self.acc[k % 2]
            eng.wait_ge(self.idx_in[k % 2], 16 * (k // 2 + 1))
            if k >= 2:
                eng.wait_ge(self.stored[k % 2], 16 * (k // 2))
            for j in range(self.ENTRIES // 2):
                n = k * self.steps + max(0, 4 * j - 1)
                if n > 0:
                    eng.wait_ge(self.step, n)
                for i in range(2):
                    e = 2 * j + i
                    out = acc if e == 0 else self.hit[i]
                    eng.tensor_scalar(out[:, :], idx[:, :], self.entry[:, e:e + 1], self.lut[:, e:e + 1],
                                      ALU.is_equal, ALU.mult).then_inc(self.step, 1)
                for i in range(2):
                    if 2 * j + i > 0:
                        eng.wait_ge(self.step, n + 2 + (i if j > 0 else 0))
                        eng.tensor_tensor(acc[:, :], acc[:, :], self.hit[i][:, :], ALU.add).then_inc(self.step, 1)


def experts(pl):
    nc, ps = pl.nc, pl.ps
    NE, F, TOPK, EB = 32, 96, 4, 4
    W = EB * F
    NS = NE // EB
    CB = W // P
    pl.end = L_OFF
    parts, wraw = [], []
    for k, shape in (("wg", [P, KC, NE * F]), ("wu", [P, KC, NE * F]), ("wd", [P, NE * F // P, D])):
        head = pl.at(f"ex_{k}_head", shape, F32, pl.end)
        wraw.append(pl.at(f"ex_{k}_loaded", shape, F32, pl.end))
        parts.append((head, pl.at(f"ex_{k}_rest", shape, F32, pl.end - 4 * KC * NE * F)))
    wg, wu, wd = parts
    gate = pl.at("ex_gate", [P, KC, NE], F32, pl.end)
    xn = pl.at("ex_xn", [P, D], F32, pl.end)
    xT = [pl.at(f"ex_xT{j}", [P, KC, P], F32, pl.end) for j in range(2)]
    sg = [pl.at(f"ex_sg{j}", [P, W], F32, pl.end) for j in range(2)]
    h = [pl.at(f"ex_h{j}", [P, W], F32, pl.end) for j in range(2)]
    xTp = [[pl.at(f"ex_xT{j}_{k}", [P, KC, P], F32, pl.end) for k in ("head", "rest")] for j in range(2)]
    hTp = [[pl.at(f"ex_hT{j}_{k}", [P, CB, P], F32, pl.end) for k in ("head", "rest")] for j in range(2)]
    route = pl.at("ex_route", [P, NT, NE], F32, pl.end)
    e, gt, eq, cum, le, one = (pl.at(f"ex_{k}", [P, NE], F32, pl.end) for k in ("e", "gt", "eq", "cum", "le", "one"))
    m8 = pl.at("ex_m8", [P, 8], F32, pl.end)
    nm, cnt, tot, inv = (pl.at(f"ex_{k}", [P, 1], F32, pl.end) for k in ("nm", "cnt", "tot", "inv"))
    s = {k: pl.sem(f"ex_{k}") for k in (
        "gate_in", "w_head", "w_rest", "wd_rest", "x_parts", "h_head", "h_rest", "down", "rs_in", "rstd", "xn", "xturned", "xT", "logits", "routed", "exp", "one", "gates", "ups", "silu",
        "gated", "turned", "added")}
    w_in = [pl.sem(f"ex_weights_loaded{j}") for j in range(NS)]
    NR = 11

    def each_tile(eng, first, step):
        first()
        for t in range(2):
            step(t, t, True)
        with eng.Fori(1, NT // 2 - 1) as u:
            for p in range(2):
                step(u * 2 + p, p, True)
        for p in range(2):
            step(NT - 2 + p, p, p == 0)

    with nc.Block() as block:
        @block.sync
        def _(eng):
            eng.dma_start(gate[:, :, :], pl.ap["L0_gate"]).then_inc(s["gate_in"], 16)
            for j in range(NS):
                c, d = slice(j * W, (j + 1) * W), slice(j * CB, (j + 1) * CB)
                eng.dma_start(wraw[0][:, :, c], pl.ap["L0_wg"][:, :, c]).then_inc(w_in[j], 16)
                eng.dma_start(wraw[1][:, :, c], pl.ap["L0_wu"][:, :, c]).then_inc(w_in[j], 16)
                eng.dma_start(wraw[2][:, d, :], pl.ap["L0_wd"][:, d, :]).then_inc(w_in[j], 16)

        @block.gpsimd
        def _(eng):
            pow_of_all(pl, eng, s)

            for j in range(NS):
                d = slice(j * CB, (j + 1) * CB)
                eng.wait_ge(s["w_head"], 3 * j + 3)
                rest_of(eng, wraw[2][:, d, :], wd[0][:, d, :], wd[1][:, d, :]).then_inc(s["wd_rest"], 1)

        @block.vector
        def _(eng):
            eng.memset(one[:, :], 1.0).then_inc(s["one"], 1)
            def norm(t):
                eng.wait_ge(s["xturned"], t)
                eng.tensor_scalar(xn[:, :], pl.x[:, t, :], pl.mv[:, t, 0:1], pl.rstd[:, bass.ds(t, 1)],
                                  ALU.subtract, ALU.mult).then_inc(s["xn"], 1)

            def logit_maximum(t):
                eng.wait_ge(s["logits"], t + 1)
                eng.tensor_reduce(nm[:, :], ps[:, 7, KC * P:KC * P + NE], AX.X, ALU.max, negate=True).then_inc(s["routed"], 1)

            def routing(t):
                n = t * NR
                r = s["routed"]
                eng.wait_ge(s["exp"], t + 1)
                apart(pl, eng)
                eng.max(m8[:, :], e[:, :]).then_inc(r, 1)
                eng.wait_ge(r, n + 2)
                kth = m8[:, TOPK - 1:TOPK]
                eng.tensor_scalar(gt[:, :], e[:, :], kth, None, ALU.is_gt).then_inc(r, 1)
                eng.tensor_scalar(eq[:, :], e[:, :], kth, None, ALU.is_equal).then_inc(r, 1)
                eng.wait_ge(r, n + 4)
                eng.tensor_reduce(cnt[:, :], gt[:, :], AX.X, ALU.add).then_inc(r, 1)
                eng.tensor_tensor_scan(cum[:, :], one[:, :], eq[:, :], 0.0, ALU.mult, ALU.add).then_inc(r, 1)

            def routing_weights(t):
                n = t * NR
                r = s["routed"]
                eng.wait_ge(r, n + 6)
                eng.tensor_scalar(le[:, :], cum[:, :], cnt[:, 0:1], float(TOPK), ALU.add, ALU.is_le).then_inc(r, 1)
                eng.wait_ge(r, n + 7)
                eng.tensor_tensor(le[:, :], le[:, :], eq[:, :], ALU.mult).then_inc(r, 1)
                eng.wait_ge(r, n + 8)
                eng.tensor_tensor(le[:, :], le[:, :], gt[:, :], ALU.add).then_inc(r, 1)
                eng.wait_ge(r, n + 9)
                eng.tensor_tensor_reduce(out=le[:, :], in0=le[:, :], in1=e[:, :], scale=1.0, scalar=0.0,
                                         op0=ALU.mult, op1=ALU.add, accum_out=tot[:, :]).then_inc(r, 1)
                eng.wait_ge(r, n + 10)
                eng.reciprocal(inv[:, :], tot[:, :]).then_inc(r, 1)
                eng.wait_ge(r, n + 11)
                eng.tensor_scalar(route[:, t, :], le[:, :], inv[:, 0:1], None, ALU.mult).then_inc(s["one"], 1)

            def weight_parts(j):
                eng.wait_ge(w_in[j], 48)
                c, d = slice(j * W, (j + 1) * W), slice(j * CB, (j + 1) * CB)
                for i, (w, part) in enumerate(((wg, (slice(None), slice(None), c)), (wu, (slice(None), slice(None), c)),
                                               (wd, (slice(None), d, slice(None))))):
                    leading_bits(eng, wraw[i][part], w[0][part]).then_inc(s["w_head"], 1)
                    if i < 2:
                        eng.wait_ge(s["w_head"], 3 * j + i + 1)
                        rest_of(eng, wraw[i][part], w[0][part], w[1][part]).then_inc(s["w_rest"], 1)

            rstd_of_all(pl, eng, s, lambda: weight_parts(0))

            def x_parts(t, p):
                eng.wait_ge(s["xT"], t + 1)
                leading_bits(eng, xT[p][:, :, :], xTp[p][0][:, :, :]).then_inc(s["x_parts"], 1)
                eng.wait_ge(s["x_parts"], 2 * t + 1)
                rest_of(eng, xT[p][:, :, :], xTp[p][0][:, :, :], xTp[p][1][:, :, :]).then_inc(s["x_parts"], 1)

            def add_up(t):
                eng.wait_ge(s["down"], (t + 1) * NS)
                eng.tensor_tensor(pl.x[:, t, :], ps[:, 6, 0:D], pl.x[:, t, :], ALU.add).then_inc(s["added"], 1)
                eng.wait_ge(s["added"], t + 1)
                token_stats(pl, eng, t)

            def first():
                norm(0)
                x_parts(0, 0)
                logit_maximum(0)
                routing(0)
                routing_weights(0)
                weight_parts(1)

            def step(t, p, more):
                opening = isinstance(t, int) and t == 0
                for j in range(NS):
                    k = t * NS + j
                    if j == 0:
                        eng.wait_ge(s["one"], t + 2)
                    eng.wait_ge(s["silu"], k + 1)
                    eng.wait_ge(s["ups"], k + 1)
                    for i in range(EB):
                        ex = j * EB + i
                        st = eng.scalar_tensor_tensor(out=h[j % 2][:, i * F:(i + 1) * F], in0=ps[:, 2 + j % 2, i * F:(i + 1) * F],
                                                      scalar=route[:, t, ex:ex + 1], in1=sg[j % 2][:, i * F:(i + 1) * F],
                                                      op0=ALU.mult, op1=ALU.mult)
                    st.then_inc(s["gated"], 1)
                    if j == 1 and not opening:
                        add_up(t - 1)
                    if opening and j + 2 < NS:
                        weight_parts(j + 2)
                    if more and j == 0:
                        norm(t + 1)
                    if more and j == 5:
                        logit_maximum(t + 1)
                    if more and j == 6:
                        routing(t + 1)
                    if more and j == 7:
                        routing_weights(t + 1)
                    eng.wait_ge(s["h_head"], k + 1)
                    if not (isinstance(t, int) and k < 2):
                        eng.wait_ge(s["down"], k - 1)
                    rest_of(eng, ps[:, 4 + j % 2, 0:W].rearrange("p (c n) -> p c n", c=CB), hTp[j % 2][0][:, :, :],
                            hTp[j % 2][1][:, :, :]).then_inc(s["h_rest"], 1)
                    if more and j == 3:
                        x_parts(t + 1, 1 - p)
                if not more:
                    add_up(t)
            each_tile(eng, first, step)
            pl.stats_n += 3 * NT

        @block.scalar
        def _(eng):
            def take_xT(t, p):
                eng.wait_ge(s["xturned"], t + 1)
                eng.activation(xT[p][:, :, :], ps[:, 7, 0:KC * P].rearrange("p (k n) -> p k n", k=KC), ACT.Copy).then_inc(s["xT"], 1)

            def silu(k, q):
                eng.wait_ge(s["gates"], k + 1)
                if not (isinstance(k, int) and k < 2):
                    eng.wait_ge(s["gated"], k - 1)
                eng.activation(sg[q][:, :], ps[:, q, 0:W], ACT.Silu).then_inc(s["silu"], 1)

            def exp_logits(t):
                eng.wait_ge(s["routed"], t * NR + 1)
                eng.activation(e[:, :], ps[:, 7, KC * P:KC * P + NE], ACT.Exp, bias=nm[:, 0:1]).then_inc(s["exp"], 1)

            def first():
                take_xT(0, 0)
                exp_logits(0)
                silu(0, 0)

            def step(t, p, more):
                for j in range(NS):
                    k = t * NS + j
                    if j + 1 < NS or more:
                        silu(k + 1, (j + 1) % 2)
                    eng.wait_ge(s["turned"], k + 1)
                    if not (isinstance(t, int) and k < 2):
                        eng.wait_ge(s["down"], k - 1)
                    eng.activation(hTp[j % 2][0][:, :, :].bitcast(F32R), ps[:, 4 + j % 2, 0:W].rearrange("p (c n) -> p c n", c=CB),
                                   ACT.Copy).then_inc(s["h_head"], 1)
                    if more and j == 2:
                        take_xT(t + 1, 1 - p)
                    if more and j == 5:
                        exp_logits(t + 1)
            each_tile(eng, first, step)

        @block.tensor
        def _(eng):
            def turn_x(t):
                eng.wait_ge(s["xn"], t + 1)
                for k in range(KC):
                    mm = eng.transpose(ps[:, 7, k * P:(k + 1) * P], xn[:, k * P:(k + 1) * P], pl.ident[:, :])
                mm.then_inc(s["xturned"], 1)

            def logits(t, p):
                eng.wait_ge(s["xT"], t + 1)
                for k in range(KC):
                    mm = eng.matmul(ps[:, 7, KC * P:KC * P + NE], xT[p][:, k, :], gate[:, k, :], start=(k == 0), stop=(k == KC - 1))
                mm.then_inc(s["logits"], 1)

            def product(w, bank, p, j, sem):
                for k in range(KC):
                    mm = split_product(eng, ps[:, bank, 0:W], [x[:, k, :] for x in xTp[p]], [x[:, k, j * W:(j + 1) * W] for x in w],
                                       k == 0, k == KC - 1)
                mm.then_inc(sem, 1)

            def down(k, j):
                eng.wait_ge(s["h_rest"], k + 1)
                if isinstance(k, int) and k < NS:
                    eng.wait_ge(s["wd_rest"], j + 1)
                for c in range(CB):
                    n = j * CB + c
                    mm = split_product(eng, ps[:, 6, 0:D], [x[:, c, :] for x in hTp[j % 2]], [x[:, n, :] for x in wd],
                                       n == 0, n == NS * CB - 1)
                mm.then_inc(s["down"], 1)

            def first():
                turn_x(0)
                eng.wait_ge(s["gate_in"], 16)
                logits(0, 0)
                eng.wait_ge(s["x_parts"], 2)
                eng.wait_ge(s["w_rest"], 1)
                product(wg, 0, 0, 0, s["gates"])
                eng.wait_ge(s["w_rest"], 2)
                product(wu, 2, 0, 0, s["ups"])

            def step(t, p, more):
                opening = isinstance(t, int) and t == 0
                for j in range(NS):
                    k = t * NS + j
                    nxt = j + 1 < NS or more
                    np_, nj = (p, j + 1) if j + 1 < NS else (1 - p, 0)
                    if nxt:
                        eng.wait_ge(s["gated"], k)
                        if opening and j + 1 < NS:
                            eng.wait_ge(s["w_rest"], 2 * j + 3)
                        if nj == 0:
                            eng.wait_ge(s["x_parts"], t * 2 + 4)
                        product(wg, nj % 2, np_, nj, s["gates"])
                    eng.wait_ge(s["gated"], k + 1)
                    for c in range(CB):
                        mm = eng.transpose(ps[:, 4 + j % 2, c * P:(c + 1) * P], h[j % 2][:, c * P:(c + 1) * P], pl.ident[:, :])
                    mm.then_inc(s["turned"], 1)
                    if nxt:
                        if opening and j + 1 < NS:
                            eng.wait_ge(s["w_rest"], 2 * j + 4)
                        product(wu, 2 + nj % 2, np_, nj, s["ups"])
                    if j == 1:
                        eng.wait_ge(s["added"], t)
                    if j > 0 or not opening:
                        down(k - 1, (j - 1) % NS)
                    if more and j == 2:
                        turn_x(t + 1)
                    if more and j == 4:
                        logits(t + 1, 1 - p)
                if not more:
                    down(t * NS + NS - 1, NS - 1)
            each_tile(eng, first, step)


def inverse_root(pl, eng, x, y, t, sem, n, root, roots=1):
    eng.wait_ge(root, roots)
    eng.reciprocal(y, y).then_inc(sem, 1)
    eng.wait_ge(sem, n + 1)
    eng.tensor_tensor(t, y, y, ALU.mult).then_inc(sem, 1)
    eng.wait_ge(sem, n + 2)
    eng.tensor_tensor(t, t, x, ALU.mult).then_inc(sem, 1)
    eng.wait_ge(sem, n + 3)
    eng.tensor_scalar(t, t, -0.5, 1.5, ALU.mult, ALU.add).then_inc(sem, 1)
    eng.wait_ge(sem, n + 4)
    eng.tensor_tensor(y, y, t, ALU.mult).then_inc(sem, 1)
    eng.wait_ge(sem, n + 5)


def key_norms(pl):
    nc, ps = pl.nc, pl.ps
    R = B * CS
    NC = -(-R // P)
    LAST = R - (NC - 1) * P
    G = 4
    pl.rq = pl.at("rq", [P, B, GQ], F32, L_OFF)
    pl.pick = pl.at("pick", [3 * NH, GQ, P], BF16, pl.end)
    pl.low1_off = pl.end
    pl.WkTg = pl.at("WkTg", [P, NH, CD], F32, pl.end)
    pl.tmp1_off = pl.end
    sq = [pl.at(f"kn_sq{j}", [P, 2, 512], F32, pl.end) for j in range(4)]
    assert pl.end <= QO_OFF
    pickf = pl.at("kn_pickf", [3 * NH, GQ, P], F32, QO_OFF)
    keys_off = pl.end
    wk = pl.at("kn_wk", [P, NH * HD], F32, keys_off)
    wkp = [pl.at(f"kn_wk_{k}", [P, NH * HD], F32, pl.end) for k in ("head", "rest")]
    ct, cth, ctl = ([pl.at(f"kn_{k}{j}", [P, G * P], F32, pl.end) for j in range(2)] for k in ("ctx", "ctx_head", "ctx_rest"))
    wv = pl.at("kn_wv", [P, NH, CD], F32, pl.end)
    wo = pl.at("kn_wo", [P, NH, D], F32, pl.end)
    bw = pl.at("kn_bw", [P, NH, D], F32, pl.end)
    g2 = pl.at("kn_g", [P, 2], F32, pl.end)
    gg = pl.at("kn_gg", [P, 1], F32, pl.end)
    ss = pl.at("kn_ss", [P, NC, NH], F32, pl.end)
    rs, nt = (pl.at(f"kn_{k}", [P, NC, NH], F32, pl.end) for k in ("rs", "newton"))
    parts = pl.at("kn_parts", [P, NC, 3, NH], BF16, pl.end)
    rkT = pl.at("kn_rkT", [3 * NH, NC * P], BF16, keys_off)
    pl.rk_dram = nc.dram_tensor("rk_scratch", (3 * NH, R), BF16, kind="Internal").ap()
    s = {k: pl.sem(f"kn_{k}") for k in (
        "wk_in", "w_in", "k", "sq", "ss", "made", "made_s", "fin", "root", "newton", "turned", "rk_s", "rk_v", "stored", "mh", "gain", "wk_parts", "heads", "rests")}
    c_in = [pl.sem(f"kn_ctx_loaded{j}") for j in range(2)]
    pl.bw1_dram = nc.dram_tensor("bw1_scratch", (P, NH, D), F32, kind="Internal").ap()
    NG = (NC - 1) // G
    NB2 = NH // 2
    assert (NC - 1) % G == 0 and NG % 4 == 0
    HC = (NC - 1) // 2
    halves = (slice(0, HC), slice(HC, NC))
    GT = (NC - 1) // 4

    def taken(k):
        if k < GT // 2:
            return s["rk_s"], k + 1
        return (s["rk_s"], GT // 2 + (k - GT // 2) // 2 + 1) if k % 2 == 0 else (s["rk_v"], (k - GT // 2) // 2 + 1)

    with nc.Block() as block:
        @block.sync
        def _(eng):
            eng.dma_start(wk[:, :], pl.ap["L1_Wk"]).then_inc(s["wk_in"], 16)

            def load(u, p):
                if not isinstance(u, int):
                    eng.wait_ge(s["rests"], u * 2 + p - 1)
                eng.dma_start(ct[p][:, :], pl.ap["ctxT"][:, bass.ds((u * 2 + p) * G * P, G * P)]).then_inc(c_in[p], 16)
            load(0, 0)
            load(0, 1)
            for d, n in ((wv, "L1_WvT"), (wo, "L1_Wo"), (pl.WkTg, "L1_WkT"), (pickf, "pick")):
                eng.dma_start(d[:, :, :], pl.ap[n]).then_inc(s["w_in"], 16)
            eng.dma_start(g2[:, :], pl.ap["L1_g"]).then_inc(s["w_in"], 16)
            with eng.Fori(1, NG // 2) as u:
                for p in range(2):
                    load(u, p)
            eng.wait_ge(s["rests"], NG - 1)
            eng.dma_start(ct[0][:, 0:LAST], pl.ap["ctxT"][:, NG * G * P:R]).then_inc(c_in[0], 16)
            eng.wait_ge(s["made_s"], NB2)
            eng.dma_start(pl.bw1_dram, bw[:, :, :]).then_inc(s["stored"], 16)
            eng.wait_ge(s["rk_s"], GT // 2)
            eng.dma_start(pl.rk_dram[:, 0:HC * P], rkT[:, 0:HC * P]).then_inc(s["stored"], 16)
            eng.wait_ge(s["rk_s"], GT // 2 + GT // 4)
            eng.wait_ge(s["rk_v"], GT // 4 + 1)
            eng.dma_start(pl.rk_dram[:, HC * P:R], rkT[:, HC * P:R]).then_inc(s["stored"], 16)
            eng.wait_ge(s["stored"], 48)

        @block.gpsimd
        def _(eng):
            eng.memset(ss[:, NC - 1, :], 1.0).then_inc(s["mh"], 1)

            def rest(g, p, m):
                eng.wait_ge(s["heads"], g + 1)
                rest_of(eng, ct[p][:, 0:m], cth[p][:, 0:m], ctl[p][:, 0:m]).then_inc(s["rests"], 1)
            with eng.Fori(0, NG // 2) as u:
                for p in range(2):
                    rest(u * 2 + p, p, G * P)
            rest(NG, 0, LAST)

        @block.scalar
        def _(eng):
            eng.preload_act_table(ACT.Square)

            def squares(c, odd, m):
                for n in range(2):
                    k = c * 2 + n
                    eng.wait_ge(s["k"], k + 1)
                    if not (isinstance(c, int) and c < 2):
                        eng.wait_ge(s["ss"], k - 3)
                    b = 4 * odd + 2 * n
                    eng.activation(sq[2 * odd + n][0:m, :, :], ps[0:m, b:b + 2, :], ACT.Square).then_inc(s["sq"], 1)
            squares(0, 0, P)
            squares(1, 1, P)

            def root(h):
                eng.wait_ge(s["fin"], 6 * h + 1)
                eng.activation(rs[:, halves[h], :], ss[:, halves[h], :], ACT.Sqrt).then_inc(s["root"], 1)

            def pairs(lo, hi):
                with eng.Fori(lo, hi) as u:
                    squares(u * 2, 0, P)
                    squares(u * 2 + 1, 1, P)
            pairs(1, HC // 2)
            root(0)
            eng.preload_act_table(ACT.Square)
            pairs(HC // 2, HC)
            squares(NC - 1, 0, LAST)
            root(1)
            for k in range(NB2):
                eng.wait_ge(s["made"], k + 1)
                eng.activation(bw[:, 2 * k:2 * k + 2, :], ps[:, 4 + k % 4, :].rearrange("p (h c) -> p h c", h=2), ACT.Copy).then_inc(s["made_s"], 1)
            for k in range(GT):
                if taken(k)[0] is s["rk_s"]:
                    eng.wait_ge(s["turned"], k + 1)
                    eng.activation(rkT[:, 4 * k * P:4 * (k + 1) * P], ps[0:3 * NH, k % 2, 0:256].bitcast(BF16), ACT.Copy).then_inc(s["rk_s"], 1)

        @block.vector
        def _(eng):
            eng.wait_ge(s["wk_in"], 16)
            split(eng, wk[:, :], wkp[0][:, :], wkp[1][:, :], s["wk_parts"], 0)

            def head(u, p, m):
                g = u * 2 + p
                eng.wait_ge(c_in[p], u * 16 + 16)
                if not (isinstance(u, int) and u == 0):
                    eng.wait_ge(s["k"], (g - 1) * 2 * G)
                leading_bits(eng, ct[p][:, 0:m], cth[p][:, 0:m]).then_inc(s["heads"], 1)
            head(0, 0, G * P)
            head(0, 1, G * P)
            eng.wait_ge(s["w_in"], 80)
            eng.tensor_copy(pl.pick[:, :, :], pickf[:, :, :]).then_inc(s["gain"], 1)
            eng.tensor_tensor(gg[:, :], g2[:, 0:1], g2[:, 1:2], ALU.mult).then_inc(s["gain"], 1)
            eng.wait_ge(s["gain"], 2)
            eng.tensor_scalar(pl.WkTg[:, :, :], pl.WkTg[:, :, :], gg[:, 0:1], None, ALU.mult).then_inc(s["gain"], 1)

            def sums(c, odd, m):
                for n in range(2):
                    eng.wait_ge(s["sq"], c * 2 + n + 1)
                    eng.tensor_reduce(ss[0:m, c, 8 * n:8 * n + 8], sq[2 * odd + n][0:m, :, :].rearrange("p b (h d) -> p (b h) d", h=4),
                                      AX.X, ALU.add).then_inc(s["ss"], 1)
            def sums_of_load(u, p):
                for j in range(G):
                    sums((u * 2 + p) * G + j, j % 2, P)
            def loads(lo, hi):
                with eng.Fori(lo, hi) as u:
                    for p in range(2):
                        sums_of_load(u, p)
                        head(u + 1, p, G * P)

            def finish(h):
                c, n = halves[h], 6 * h
                eng.wait_ge(s["ss"], 2 * c.stop)
                eng.tensor_scalar(ss[:, c, :], ss[:, c, :], 1.0 / HD, EPS, ALU.mult, ALU.add).then_inc(s["fin"], 1)
                inverse_root(pl, eng, ss[:, c, :], rs[:, c, :], nt[:, c, :], s["newton"], 5 * h, s["root"], h + 1)
                for j in range(3):
                    eng.tensor_copy(parts[:, c, j, :], rs[:, c, :]).then_inc(s["fin"], 1)
                    if j < 2:
                        eng.wait_ge(s["fin"], n + 2 * j + 2)
                        eng.tensor_tensor(rs[:, c, :], rs[:, c, :], parts[:, c, j, :], ALU.subtract).then_inc(s["fin"], 1)
                        eng.wait_ge(s["fin"], n + 2 * j + 3)

            loads(0, NG // 4)
            finish(0)
            loads(NG // 4, NG // 2 - 1)
            sums_of_load(NG // 2 - 1, 0)
            head(NG // 2, 0, LAST)
            sums_of_load(NG // 2 - 1, 1)
            eng.wait_ge(s["mh"], 1)
            sums(NC - 1, 0, LAST)
            finish(1)
            for k in range(GT):
                if taken(k)[0] is s["rk_v"]:
                    eng.wait_ge(s["turned"], k + 1)
                    eng.tensor_copy(rkT[:, 4 * k * P:4 * (k + 1) * P], ps[0:3 * NH, k % 2, 0:256].bitcast(BF16)).then_inc(s["rk_v"], 1)
            eng.wait_ge(s["turned"], GT + 1)
            eng.tensor_copy(rkT[:, (NC - 1) * P:R], ps[0:3 * NH, 2, 0:LAST // 2].bitcast(BF16)).then_inc(s["rk_v"], 1)

        @block.tensor
        def _(eng):
            def keys(c, p, j, m):
                for n in range(2):
                    if not (isinstance(c, int) and c < 2):
                        eng.wait_ge(s["sq"], c * 2 + n - 3)
                    for a in range(2):
                        w = (2 * n + a) * 512
                        mm = split_product(eng, ps[0:m, 4 * (j % 2) + 2 * n + a, :], [x[p][:, j * P:j * P + m] for x in (cth, ctl)],
                                           [x[:, w:w + 512] for x in wkp])
                    mm.then_inc(s["k"], 1)

            eng.wait_ge(s["wk_parts"], 2)
            for p in range(2):
                eng.wait_ge(s["rests"], p + 1)
                for j in range(G):
                    keys(p * G + j, p, j, P)
            with eng.Fori(1, NG // 2) as u:
                for p in range(2):
                    eng.wait_ge(s["rests"], u * 2 + p + 1)
                    for j in range(G):
                        keys(u * 2 * G + p * G + j, p, j, P)
            eng.wait_ge(s["rests"], NG + 1)
            keys(NC - 1, 0, 0, LAST)
            eng.wait_ge(s["w_in"], 80)
            eng.wait_ge(s["sq"], 2 * NC)
            for k in range(NB2):
                if k >= 4:
                    eng.wait_ge(s["made_s"], k - 3)
                for j in range(2):
                    h = 2 * k + j
                    mm = eng.matmul(ps[:, 4 + k % 4, j * D:(j + 1) * D], wv[:, h, :], wo[:, h, :], start=True, stop=True)
                mm.then_inc(s["made"], 1)
            for k in range(GT):
                if k in (0, GT // 2):
                    eng.wait_ge(s["fin"], 6 if k == 0 else 12)
                if k >= 2:
                    eng.wait_ge(*taken(k - 2))
                for j in range(4):
                    mm = eng.transpose(ps[0:3 * NH, k % 2, j * P // 2:(j + 1) * P // 2].bitcast(BF16),
                                       parts[:, 4 * k + j, :, :].rearrange("p a h -> p (a h)"), pl.identb[:, :])
                mm.then_inc(s["turned"], 1)
            eng.transpose(ps[0:3 * NH, 2, 0:LAST // 2].bitcast(BF16), parts[0:LAST, NC - 1, :, :].rearrange("p a h -> p (a h)"),
                          pl.identb[0:LAST, 0:LAST]).then_inc(s["turned"], 1)


def l1x_queries(pl):
    nc, ps = pl.nc, pl.ps
    QO = pl.QO = pl.at("QO1", [P, NH, TOK], F32, QO_OFF)
    xT = pl.at("l1q_xT", [P, KC, ST], F32, pl.tmp1_off)
    xn = pl.at("l1q_xn", [P, 4, D], F32, pl.end)
    wq = pl.at("l1q_wq", [P, KC, NH * HD], F32, pl.end)
    qT = [pl.at(f"l1q_qT{j}", [P, ST], F32, pl.end) for j in range(2)]
    sq = pl.at("l1q_sq", [P, 4, ST], F32, pl.end)
    ones = pl.at("l1q_ones", [P, S], F32, pl.end)
    qs, nt = (pl.at(f"l1q_{k}", [P, B, GQ], F32, pl.end) for k in ("qs", "newton"))
    assert pl.end <= QO_OFF, pl.end - QO_OFF
    s = layer_norm_steps(pl, "l1q")
    for k in ("w_in", "ones", "q", "sq", "qT", "made", "out", "sums", "diag", "fin", "root", "newton"):
        s[k] = pl.sem(f"l1q_{k}")
    NBS = ST // S

    def supertiles(eng, step):
        step(0, True)
        with eng.Fori(1, SUP - 1) as i:
            step(i, True)
        step(SUP - 1, False)

    def first(i, h, lim):
        return isinstance(i, int) and i * NH + h < lim

    with nc.Block() as block:
        @block.sync
        def _(eng):
            eng.dma_start(wq[:, :, :], pl.ap["L1_WqT"]).then_inc(s["w_in"], 16)

        @block.gpsimd
        def _(eng):
            pow_of_all(pl, eng, s)
            eng.memset(ones[:, :], 1.0).then_inc(s["ones"], 1)

        @block.vector
        def _(eng):
            rstd_of_all(pl, eng, s)

            def norm(i):
                eng.wait_ge(s["turned"], i * 2)
                for j in range(4):
                    eng.tensor_scalar(xn[:, j, :], pl.x[:, i * 4 + j, :], pl.mv[:, i * 4 + j, 0:1], pl.rstd[:, bass.ds(i * 4 + j, 1)],
                                      ALU.subtract, ALU.mult).then_inc(s["xn"], 1)

            def take_xT(i):
                eng.wait_ge(s["q"], i * NH)
                for m in range(2):
                    eng.wait_ge(s["turned"], i * 2 + m + 1)
                    eng.tensor_copy(xT[:, :, m * 256:(m + 1) * 256], ps[:, 6 + m, :].rearrange("p (k n) -> p k n", k=KC)).then_inc(s["xT"], 1)

            def step(i, more):
                for h in range(NH):
                    k = i * NH + h
                    eng.wait_ge(s["q"], k + 1)
                    if not first(i, h, 2):
                        eng.wait_ge(s["made"], k - 1)
                        eng.wait_ge(s["sq"], k - 1)
                    eng.tensor_copy(qT[h % 2][:, :], ps[:, h % 2, :]).then_inc(s["qT"], 1)
                    if more and h == 5:
                        norm(i + 1)
                    if h % 4 == 3:
                        m = i * 4 + h // 4
                        eng.wait_ge(s["sums"], m + 1)
                        v = ps[:, 4, :].rearrange("p (b s) -> p b s", s=S)
                        eng.tensor_tensor(v, v, pl.cst["diag"][:, None, :].to_broadcast([P, NBS, S]), ALU.mult).then_inc(s["diag"], 1)
                        eng.wait_ge(s["diag"], m * 2 + 1)
                        apart(pl, eng)
                        eng.tensor_reduce(qs[:, bass.ds(i * NBS, NBS), h // 4], v, AX.X, ALU.add).then_inc(s["diag"], 1)
                if more:
                    take_xT(i + 1)

            norm(0)
            take_xT(0)
            supertiles(eng, step)
            eng.wait_ge(s["diag"], 2 * 4 * SUP)
            eng.tensor_scalar(qs[:, :, :], qs[:, :, :], 1.0 / HD, EPS, ALU.mult, ALU.add).then_inc(s["fin"], 1)
            inverse_root(pl, eng, qs[:, :, :], pl.rq[:, :, :], nt[:, :, :], s["newton"], 0, s["root"])
            eng.tensor_scalar(pl.rq[:, :, :], pl.rq[:, :, :], float(HD) ** -0.5, None, ALU.mult).then_inc(s["fin"], 1)

        @block.scalar
        def _(eng):
            eng.preload_act_table(ACT.Square)

            def out(i, h):
                eng.wait_ge(s["made"], i * NH + h + 1)
                eng.activation(QO[:, h, bass.ds(i * ST, ST)], ps[:, 2 + h % 2, :], ACT.Copy).then_inc(s["out"], 1)

            def step(i, more):
                for h in range(NH):
                    eng.wait_ge(s["qT"], i * NH + h + 1)
                    if not first(i, h, 4):
                        eng.wait_ge(s["sums"], i * 4 + h // 4)
                    eng.activation(sq[:, h % 4, :], qT[h % 2][:, :], ACT.Square).then_inc(s["sq"], 1)
                    if h >= 1:
                        out(i, h - 1)
                out(i, NH - 1)
            supertiles(eng, step)
            eng.wait_ge(s["fin"], 1)
            eng.activation(pl.rq[:, :, :], qs[:, :, :], ACT.Sqrt).then_inc(s["root"], 1)

        @block.tensor
        def _(eng):
            def through_wk(i, h):
                k = i * NH + h
                eng.wait_ge(s["qT"], k + 1)
                if not first(i, h, 2):
                    eng.wait_ge(s["out"], k - 1)
                eng.matmul(ps[:, 2 + h % 2, :], pl.WkTg[:, h, :], qT[h % 2][:, :], start=True, stop=True).then_inc(s["made"], 1)

            def step(i, more):
                eng.wait_ge(s["xT"], i * 2 + 2)
                for h in range(NH):
                    k = i * NH + h
                    if not first(i, h, 2):
                        eng.wait_ge(s["qT"], k - 1)
                    for c in range(KC):
                        mm = eng.matmul(ps[:, h % 2, :], wq[:, c, h * HD:(h + 1) * HD], xT[:, c, :], start=(c == 0), stop=(c == KC - 1))
                    mm.then_inc(s["q"], 1)
                    if more and h == 8:
                        turn_supertile(pl, eng, s, xn, i + 1)
                    if h >= 1:
                        through_wk(i, h - 1)
                    if h % 4 == 3:
                        m = i * 4 + h // 4
                        eng.wait_ge(s["sq"], k + 1)
                        eng.wait_ge(s["diag"], 2 * m)
                        apart(pl, eng)
                        for j in range(4):
                            mm = eng.matmul(ps[j * S:(j + 1) * S, 4, :], ones[:, :], sq[:, j, :], start=True, stop=True)
                        mm.then_inc(s["sums"], 1)
                through_wk(i, NH - 1)

            turn_supertile(pl, eng, s, xn, 0)
            eng.wait_ge(s["w_in"], 16)
            eng.wait_ge(s["ones"], 1)
            supertiles(eng, step)


LUT_COLS = KC * 2 * 688 + 6 * D
MAGIC = 12582912.0


def staggered(eng, pieces):
    top = max(lag for lag, _ in pieces)

    def turn(n, slot):
        for lag, piece in pieces:
            t = n - lag
            if isinstance(t, int) and not 0 <= t < NT:
                continue
            piece(t, (slot - lag) % 2)
    lo = -(-(top + 2) // 2) * 2
    hi = NT // 2 * 2
    for n in range(lo):
        turn(n, n % 2)
    with eng.Fori(lo // 2, hi // 2) as u:
        for p in range(2):
            turn(u * 2 + p, p)
    for n in range(hi, NT + top):
        turn(n, n % 2)


def early(t):
    return isinstance(t, int) and t < 2


def quantise(eng, src, rounded, out, st, sem, n, ready):
    eng.tensor_reduce(st[:, 3:4], src, AX.X, ALU.max, apply_absolute_value=True).then_inc(sem, 1)
    eng.wait_ge(sem, n + 1)
    eng.tensor_scalar(st[:, 0:1], st[:, 3:4], 1e-5, None, ALU.max).then_inc(sem, 1)
    eng.wait_ge(sem, n + 2)
    eng.reciprocal(st[:, 1:2], st[:, 0:1]).then_inc(sem, 1)
    eng.wait_ge(sem, n + 3)
    eng.tensor_scalar(st[:, 2:3], st[:, 1:2], 127.0, None, ALU.mult).then_inc(sem, 1)
    eng.wait_ge(sem, n + 4)
    eng.tensor_scalar(rounded, src, st[:, 2:3], MAGIC, ALU.mult, ALU.add).then_inc(sem, 1)
    eng.wait_ge(sem, n + 5)
    eng.tensor_scalar(out, rounded, -MAGIC, None, ALU.add).then_inc(ready, 1)


NQS = 5


class BlockWeights:

    def __init__(self, pl):
        self.pl = pl
        self.sizes = {"qkv": KC * 3 * D, "o": KC * D, "down": 4 * D}
        pl.wd = pl.at("bl_wd", [P, 4, D], BF16, L_OFF + NT * D * 4)
        pl.deq = pl.at("bl_deq", [P, 3], F32, pl.end)
        pl.wqkv = pl.at("bl_wqkv", [P, KC, 3 * D], BF16, pl.end)
        pl.wo = pl.at("bl_wo", [P, KC, D], BF16, pl.end)
        pl.weights_end = pl.end
        self.loaded = {k: pl.at(f"bl_{k}_f", [P, n], F32, pl.end) for k, n in self.sizes.items()}
        self.ones = pl.at("bl_ones", [P, P], F32, pl.end)
        self.sum, self.mean, self.scale = (pl.at(f"bl_w{k}", [P, 3], F32, pl.end) for k in ("sum", "mean", "scale"))
        pl.scratch_end = pl.end
        self.s = {k: pl.sem(f"bl_{k}") for k in ("w_in", "wq", "wabs", "ones", "wsummed")}

    def sync(self, eng):
        for k in self.sizes:
            eng.dma_start(self.loaded[k][:, :], self.pl.ap[f"L1_{k}T"]).then_inc(self.s["w_in"], 16)

    def gpsimd(self, eng):
        eng.memset(self.ones[:, :], 1.0).then_inc(self.s["ones"], 1)

    def vector_sums(self, eng):
        eng.wait_ge(self.s["w_in"], 48)
        for j, k in enumerate(self.sizes):
            eng.tensor_reduce(self.sum[:, j:j + 1], self.loaded[k][:, :], AX.X, ALU.add, apply_absolute_value=True).then_inc(self.s["wabs"], 1)

    def tensor(self, eng):
        eng.wait_ge(self.s["ones"], 1)
        eng.wait_ge(self.s["wabs"], 3)
        eng.matmul(self.pl.ps[:, 7, 0:3], self.ones[:, :], self.sum[:, :], start=True, stop=True).then_inc(self.s["wsummed"], 1)

    def vector_ternary(self, eng):
        pl, s, wf = self.pl, self.s, self.loaded
        eng.wait_ge(s["wsummed"], 1)
        for j, n in enumerate(self.sizes.values()):
            eng.tensor_scalar(self.mean[:, j:j + 1], pl.ps[:, 7, j:j + 1], 1.0 / (P * n), 1e-5, ALU.mult, ALU.max).then_inc(s["wq"], 1)
        eng.wait_ge(s["wq"], 3)
        eng.reciprocal(self.scale[:, :], self.mean[:, :]).then_inc(s["wq"], 1)
        eng.tensor_scalar(pl.deq[:, :], self.mean[:, :], 1.0 / 127.0, None, ALU.mult).then_inc(s["wq"], 1)
        eng.wait_ge(s["wq"], 5)
        for j, (k, d) in enumerate(zip(self.sizes, (pl.wqkv, pl.wo, pl.wd))):
            eng.tensor_scalar(wf[k][:, :], wf[k][:, :], self.scale[:, j:j + 1], MAGIC, ALU.mult, ALU.add).then_inc(s["wq"], 1)
            eng.wait_ge(s["wq"], 6 + 3 * j)
            eng.tensor_scalar(wf[k][:, :], wf[k][:, :], -MAGIC, -1.0, ALU.add, ALU.max).then_inc(s["wq"], 1)
            eng.wait_ge(s["wq"], 7 + 3 * j)
            eng.tensor_scalar(d[:, :, :].rearrange("p a b -> p (a b)"), wf[k][:, :], 1.0, None, ALU.min).then_inc(s["wq"], 1)


def block_attention(pl):
    nc, ps = pl.nc, pl.ps
    H, E, BT = 16, 16, 4
    pl.x1 = pl.at("x1", [P, NT, D], F32, L_OFF)
    pl.end = pl.weights_end
    wqkv, wo = pl.wqkv, pl.wo
    pl.ms = pl.at("bl_ms", [P, NT], F32, pl.end)
    pl.rs2 = pl.at("bl_rs2", [P, NT], F32, pl.end)
    pl.blk_low = pl.end
    pl.lut_w = pl.at("lf_weights", [P, LUT_COLS], F32, TOP - LUT_COLS * 4)
    pl.up_w = pl.at("bf_up", [P, KC, 4 * D], F32, TOP - LUT_COLS * 4 - KC * 4 * D * 4)
    pl.ffn_norm = pl.at("bf_wn", [P, D], F32, TOP - LUT_COLS * 4 - KC * 4 * D * 4 - D * 4)
    pl.ahead_in, pl.lut_in = pl.sem("bf_weights_loaded"), pl.sem("lf_weights_loaded")
    pl.end = pl.blk_low
    wn = pl.at("bl_wn", [P, D], F32, pl.end)
    sh = pl.at("bl_shift", [P, 3, P], F32, pl.end)
    bm = pl.at("bl_mask", [P, BT], F32, pl.end)
    cos = pl.at("bl_cos", [P, E], F32, pl.end)
    sin = pl.at("bl_sin", [P, E], F32, pl.end)
    two = lambda name, shape, dt=F32: [pl.at(f"bl_{name}{j}", shape, dt, pl.end) for j in range(2)]
    h, hr, hq = two("h", [P, D]), two("hr", [P, D]), two("hq", [P, D], BF16)
    hqT = two("hqT", [P, KC, P], BF16)
    st, fac = two("st", [P, 4]), two("fac", [P, 1])
    R = two("R", [P, 3, H, 2, E // 2])
    rc, rsn = two("rc", [P, 2 * H, 2, E // 2]), two("rs", [P, 2 * H, 2, E // 2])
    prod = two("prod", [P, BT, H, E])
    sc, sx = two("sc", [P, BT, H]), two("sx", [P, BT, H])
    mx, sm_, inv = two("mx", [P, H]), two("sum", [P, H]), two("inv", [P, H])
    cx, cr, cq = two("cx", [P, D]), two("cr", [P, D]), two("cq", [P, D], BF16)
    cqT = two("cqT", [P, KC, P], BF16)
    st2, fac2 = two("st2", [P, 4]), two("fac2", [P, 1])
    s = {k: pl.sem(f"bl_{k}") for k in (
        "tables_in", "rs_in", "rstd", "pow2", "ln", "q1", "hq", "fac", "hturned", "hqT", "qkv",
        "R", "cos", "sin", "rot", "shifted", "att", "exp", "ctx", "q2", "cq", "cturned", "cqT", "proj", "x1", "ms", "wst", "sqs", "own_score", "own_value")}
    sqj = pl.at("bl_sqj", [P, D], F32, pl.end)
    ms1 = pl.at("bl_ms1", [P, 1], F32, pl.end)

    def moved(j, n, by_head=True):
        bank = 4 + n if j < 3 else 6 + n
        at = (j - 1) * D if j < 3 else D
        v = ps[:, bank, at:at + D]
        return v.rearrange("p (h e) -> p h e", h=H) if by_head else v

    with nc.Block() as block:
        @block.sync
        def _(eng):
            eng.dma_start(wn[:, :], pl.ap["L1_attn_norm"].to_broadcast([P, D])).then_inc(s["tables_in"], 16)
            for d, n in ((sh, "shift"),):
                eng.dma_start(d[:, :, :], pl.ap[n]).then_inc(s["tables_in"], 16)
            for d, n in ((bm, "bmask"), (cos, "cos16"), (sin, "sin16")):
                eng.dma_start(d[:, :], pl.ap[n]).then_inc(s["tables_in"], 16)
            eng.dma_start(pl.up_w[:, :, :], pl.ap["L1_upT"]).then_inc(pl.ahead_in, 16)
            eng.dma_start(pl.ffn_norm[:, :], pl.ap["L1_ffn_norm"].to_broadcast([P, D])).then_inc(pl.ahead_in, 16)
            eng.dma_start(pl.lut_w[:, :], pl.lut_dram).then_inc(pl.lut_in, 16)

        @block.gpsimd
        def _(eng):
            pow_of_all(pl, eng, s)
            eng.wait_ge(s["pow2"], 2)
            eng.tensor_tensor(pl.rs2[:, :], pl.rs2[:, :], pl.mhalf[:, :], ALU.pow).then_inc(s["pow2"], 1)

            def rotate(t, p):
                eng.wait_ge(s["R"], 2 * t + 2)
                eng.wait_ge(s["tables_in"], 80)
                if not early(t):
                    eng.wait_ge(s["rot"], t - 1)
                qk = R[p][:, 0:2].rearrange("p n h a e -> p (n h) a e")
                f = lambda a: a[:, :, :, :].rearrange("p h a e -> p h (a e)")
                eng.tensor_tensor(f(rc[p]), f(qk), cos[:, None, :].to_broadcast([P, 2 * H, E]), ALU.mult).then_inc(s["cos"], 1)
                for a in range(2):
                    eng.tensor_tensor(rsn[p][:, :, a, :], qk[:, :, 1 - a, :],
                                      sin[:, None, a * 8:a * 8 + 8].to_broadcast([P, 2 * H, 8]), ALU.mult).then_inc(s["sin"], 1)
                eng.wait_ge(s["cos"], t + 1)
                eng.wait_ge(s["sin"], 2 * t + 2)
                eng.tensor_tensor(f(qk), f(rc[p]), f(rsn[p]), ALU.add).then_inc(s["rot"], 1)
                eng.wait_ge(s["rot"], t + 1)
                if not early(t):
                    eng.wait_ge(s["wst"], 7 * t - 7)
                q, k = (R[p][:, i].rearrange("p h a e -> p h (a e)") for i in range(2))
                eng.tensor_tensor(prod[p][:, 0, :, :], k, q, ALU.mult).then_inc(s["own_score"], 1)

            def own_value(t, p):
                eng.wait_ge(s["wst"], 7 * t + 3)
                eng.tensor_tensor(prod[p][:, 0, :, :], R[p][:, 2].rearrange("p h a e -> p h (a e)"),
                                  sx[p][:, 0, :, None].to_broadcast([P, H, E]), ALU.mult).then_inc(s["own_value"], 1)

            staggered(eng, [(2, own_value), (0, rotate)])

        @block.vector
        def _(eng):
            rstd_of_all(pl, eng, s)
            eng.tensor_tensor(pl.rs2[:, :], pl.rstd[:, :], pl.rstd[:, :], ALU.mult).then_inc(s["ms"], 1)
            eng.wait_ge(s["ms"], 1)
            eng.tensor_tensor(pl.rs2[:, :], pl.rs2[:, :], pl.mv[:, :, 1], ALU.mult).then_inc(s["pow2"], 1)
            eng.wait_ge(s["pow2"], 1)
            eng.tensor_scalar(pl.rs2[:, :], pl.rs2[:, :], EPS, None, ALU.add).then_inc(s["pow2"], 1)
            eng.wait_ge(s["pow2"], 3)
            eng.wait_ge(s["tables_in"], 80)

            def norm_quantise(t, p):
                eng.tensor_scalar(pl.x1[:, t, :], pl.x[:, t, :], pl.mv[:, t, 0:1], pl.rstd[:, bass.ds(t, 1)],
                                  ALU.subtract, ALU.mult).then_inc(s["ln"], 1)
                eng.wait_ge(s["ln"], 2 * t + 1)
                eng.scalar_tensor_tensor(out=h[p][:, :], in0=pl.x1[:, t, :], scalar=pl.rs2[:, bass.ds(t, 1)], in1=wn[:, :],
                                         op0=ALU.mult, op1=ALU.mult).then_inc(s["ln"], 1)
                eng.wait_ge(s["ln"], 2 * t + 2)
                if not early(t):
                    eng.wait_ge(s["hturned"], t - 1)
                    eng.wait_ge(s["R"], 2 * t - 2)
                quantise(eng, h[p][:, :], hr[p][:, :], hq[p][:, :], st[p], s["q1"], t * NQS, s["hq"])
                eng.tensor_tensor(fac[p][:, :], st[p][:, 0:1], pl.deq[:, 0:1], ALU.mult).then_inc(s["fac"], 1)

            def scores(t, p):
                a = s["att"]
                n = t * 7
                q = R[p][:, 0].rearrange("p h a e -> p h (a e)")
                eng.wait_ge(s["rot"], t + 1)
                eng.wait_ge(s["shifted"], 2 * t + 1)
                if not early(t):
                    eng.wait_ge(s["wst"], 7 * t - 7)
                for j in range(1, BT):
                    eng.tensor_tensor(prod[p][:, j, :, :], moved(j, 0), q, ALU.mult).then_inc(a, 1)
                eng.wait_ge(a, n + 3)
                eng.wait_ge(s["own_score"], t + 1)
                eng.tensor_reduce(sc[p][:, :, :], prod[p][:, :, :, :], AX.X, ALU.add).then_inc(a, 1)
                eng.wait_ge(a, n + 4)
                eng.tensor_tensor(sc[p][:, :, :], sc[p][:, :, :], bm[:, :, None].to_broadcast([P, BT, H]), ALU.add).then_inc(a, 1)
                eng.wait_ge(a, n + 5)
                eng.tensor_reduce(mx[p][:, :], sc[p][:, :, :].rearrange("p j h -> p h j"), AX.X, ALU.max).then_inc(a, 1)
                eng.wait_ge(a, n + 6)
                if not early(t):
                    eng.wait_ge(s["ctx"], t - 1)
                eng.tensor_tensor(sx[p][:, :, :], sc[p][:, :, :], mx[p][:, None, :].to_broadcast([P, BT, H]), ALU.subtract).then_inc(a, 1)

            def weigh(t, p):
                base = s["wst"]
                m = t * 7
                eng.wait_ge(s["exp"], t + 1)
                eng.tensor_reduce(sm_[p][:, :], sx[p][:, :, :].rearrange("p j h -> p h j"), AX.X, ALU.add).then_inc(base, 1)
                eng.wait_ge(base, m + 1)
                eng.reciprocal(inv[p][:, :], sm_[p][:, :]).then_inc(base, 1)
                eng.wait_ge(base, m + 2)
                eng.tensor_tensor(sx[p][:, :, :], sx[p][:, :, :], inv[p][:, None, :].to_broadcast([P, BT, H]), ALU.mult).then_inc(base, 1)
                eng.wait_ge(base, m + 3)
                eng.wait_ge(s["shifted"], 2 * t + 2)
                for j in range(1, BT):
                    eng.tensor_tensor(prod[p][:, j, :, :], moved(j, 1), sx[p][:, j, :, None].to_broadcast([P, H, E]), ALU.mult).then_inc(base, 1)
                eng.wait_ge(base, m + 6)
                eng.wait_ge(s["own_value"], t + 1)
                eng.tensor_reduce(cx[p][:, :], prod[p][:, :, :, :].rearrange("p j h e -> p (h e) j"), AX.X, ALU.add).then_inc(base, 1)
                eng.wait_ge(base, m + 7)
                if not early(t):
                    eng.wait_ge(s["cturned"], t - 1)
                quantise(eng, cx[p][:, :], cr[p][:, :], cq[p][:, :], st2[p], s["q2"], t * NQS, s["cq"])
                eng.tensor_tensor(fac2[p][:, :], st2[p][:, 0:1], pl.deq[:, 1:2], ALU.mult).then_inc(s["ctx"], 1)

            def residual(t, p):
                eng.wait_ge(s["proj"], t + 1)
                eng.wait_ge(s["ctx"], t + 1)
                eng.scalar_tensor_tensor(out=pl.x1[:, t, :], in0=ps[:, 7, 0:D], scalar=fac2[p][:, 0:1], in1=pl.x1[:, t, :],
                                         op0=ALU.mult, op1=ALU.add).then_inc(s["x1"], 1)

            staggered(eng, [(0, norm_quantise), (2, scores), (3, residual), (2, weigh)])

        @block.scalar
        def _(eng):
            eng.preload_act_table(ACT.Exp)

            def take_hq(t, p):
                eng.wait_ge(s["hturned"], t + 1)
                if not early(t):
                    eng.wait_ge(s["qkv"], 2 * t - 2)
                eng.activation(hqT[p][:, :, :], ps[:, 0, 0:P].bitcast(BF16).rearrange("p (k n) -> p k n", k=KC), ACT.Copy).then_inc(s["hqT"], 1)

            def take_qkv(t, p):
                eng.wait_ge(s["fac"], t + 1)
                if not early(t):
                    eng.wait_ge(s["shifted"], 2 * t - 2)
                    eng.wait_ge(s["ctx"], t - 1)
                f = R[p][:, :, :, :, :].rearrange("p n h a e -> p (n h a e)")
                eng.wait_ge(s["qkv"], 2 * t + 1)
                eng.activation(f[:, 0:2 * D], ps[:, 2, :], ACT.Copy, scale=fac[p][:, 0:1]).then_inc(s["R"], 1)
                eng.wait_ge(s["qkv"], 2 * t + 2)
                eng.activation(f[:, 2 * D:3 * D], ps[:, 3, 0:D], ACT.Copy, scale=fac[p][:, 0:1]).then_inc(s["R"], 1)

            def exponential(t, p):
                eng.wait_ge(s["att"], t * 7 + 7)
                eng.activation(sx[p][:, :, :], sx[p][:, :, :], ACT.Exp, scale=float(E) ** -0.5).then_inc(s["exp"], 1)

            def take_cq(t, p):
                eng.wait_ge(s["cturned"], t + 1)
                if not early(t):
                    eng.wait_ge(s["proj"], t - 1)
                eng.activation(cqT[p][:, :, :], ps[:, 1, 0:P].bitcast(BF16).rearrange("p (k n) -> p k n", k=KC), ACT.Copy).then_inc(s["cqT"], 1)

            def square(t, p):
                eng.wait_ge(s["sqs"], 2 * t)
                eng.wait_ge(s["x1"], t + 1)
                eng.activation(sqj[:, :], pl.x1[:, t, :], ACT.Square, accum_out=ms1[:, :]).then_inc(s["sqs"], 1)
                eng.wait_ge(s["sqs"], 2 * t + 1)
                eng.activation(pl.ms[:, bass.ds(t, 1)], ms1[:, :], ACT.Copy).then_inc(s["sqs"], 1)

            staggered(eng, [(0, take_hq), (2, exponential), (0, take_qkv), (2, take_cq), (3, square)])

        @block.tensor
        def _(eng):
            eng.wait_ge(s["tables_in"], 80)

            def turn_h(t, p):
                eng.wait_ge(s["hq"], t + 1)
                eng.wait_ge(s["hqT"], t)
                for k in range(KC):
                    mm = eng.transpose(ps[:, 0, k * P // 2:(k + 1) * P // 2].bitcast(BF16), hq[p][:, k * P:(k + 1) * P], pl.identb[:, :])
                mm.then_inc(s["hturned"], 1)

            def project(t, p):
                eng.wait_ge(s["hqT"], t + 1)
                eng.wait_ge(s["R"], 2 * t)
                for n, w in ((0, 2 * D), (1, D)):
                    for k in range(KC):
                        mm = eng.matmul(ps[:, 2 + n, 0:w], hqT[p][:, k, :], wqkv[:, k, n * 512:n * 512 + w], start=(k == 0), stop=(k == KC - 1))
                    mm.then_inc(s["qkv"], 1)

            def shift(t, p):
                eng.wait_ge(s["rot"], t + 1)
                for n in range(2):
                    if not (isinstance(t, int) and t == 0):
                        eng.wait_ge(s["att"], 7 * t - 4) if n == 0 else eng.wait_ge(s["wst"], 7 * t - 1)
                        if n == 1:
                            eng.wait_ge(s["x1"], t - 1)
                    for j in range(1, BT):
                        mm = eng.matmul(moved(j, n, False), sh[:, j - 1, :], R[p][:, 1 + n].rearrange("p h a e -> p (h a e)"), start=True, stop=True)
                    mm.then_inc(s["shifted"], 1)

            def turn_c(t, p):
                eng.wait_ge(s["cq"], t + 1)
                eng.wait_ge(s["cqT"], t)
                for k in range(KC):
                    mm = eng.transpose(ps[:, 1, k * P // 2:(k + 1) * P // 2].bitcast(BF16), cq[p][:, k * P:(k + 1) * P], pl.identb[:, :])
                mm.then_inc(s["cturned"], 1)

            def output(t, p):
                eng.wait_ge(s["cqT"], t + 1)
                eng.wait_ge(s["x1"], t)
                for k in range(KC):
                    mm = eng.matmul(ps[:, 7, 0:D], cqT[p][:, k, :], wo[:, k, :], start=(k == 0), stop=(k == KC - 1))
                mm.then_inc(s["proj"], 1)

            staggered(eng, [(0, turn_h), (0, project), (1, shift), (2, turn_c), (2, output)])


def block_ffn(pl):
    nc, ps = pl.nc, pl.ps
    I = 2 * D
    wn = pl.ffn_norm
    up = [pl.at(f"bf_up_{k}", [P, KC, 2 * I], F32, pl.blk_low if k == "head" else pl.end) for k in ("head", "rest")]
    two = lambda name, shape, dt=F32: [pl.at(f"bf_{name}{j}", shape, dt, pl.end) for j in range(2)]
    hn = two("hn", [P, D])
    hT = [[pl.at(f"bf_hT{j}_{k}", [P, KC, P], F32, pl.end) for k in ("head", "rest")] for j in range(2)]
    sg, g, gr = two("sg", [P, I]), two("g", [P, I]), two("gr", [P, I])
    gq = two("gq", [P, I], BF16)
    gT = two("gT", [P, 4, P], BF16)
    st, fac = two("st", [P, 4]), two("fac", [P, 1])
    s = {k: pl.sem(f"bf_{k}") for k in (
        "w_head", "w_rest", "hT_rest", "ms", "rs", "hn", "hturned", "hT", "gate", "val", "silu", "g", "q", "gq", "fac", "gturned", "gT", "down", "res", "added")}

    with nc.Block() as block:
        @block.gpsimd
        def _(eng):
            eng.wait_ge(s["ms"], 1)
            eng.tensor_tensor(pl.rs2[:, :], pl.rs2[:, :], pl.mhalf[:, :], ALU.pow).then_inc(s["rs"], 1)

        @block.vector
        def _(eng):
            eng.tensor_scalar(pl.rs2[:, :], pl.ms[:, :], 1.0 / D, EPS, ALU.mult, ALU.add).then_inc(s["ms"], 1)
            for n in range(2):
                c = slice(n * I, (n + 1) * I)
                eng.wait_ge(s["w_head"], n + 1)
                rest_of(eng, pl.up_w[:, :, c], up[0][:, :, c], up[1][:, :, c]).then_inc(s["w_rest"], 1)
            eng.wait_ge(s["rs"], 1)

            def norm(t, p):
                if not early(t):
                    eng.wait_ge(s["hturned"], t - 1)
                eng.scalar_tensor_tensor(out=hn[p][:, :], in0=pl.x1[:, t, :], scalar=pl.rs2[:, bass.ds(t, 1)], in1=wn[:, :],
                                         op0=ALU.mult, op1=ALU.mult).then_inc(s["hn"], 1)

            def hT_rest(t, p):
                eng.wait_ge(s["hT"], t + 1)
                if not early(t):
                    eng.wait_ge(s["val"], t - 1)
                rest_of(eng, ps[:, 0, 0:KC * P].rearrange("p (k n) -> p k n", k=KC), hT[p][0][:, :, :], hT[p][1][:, :, :]).then_inc(s["hT_rest"], 1)

            def gated(t, p):
                eng.wait_ge(s["silu"], t + 1)
                eng.wait_ge(s["val"], t + 1)
                eng.tensor_tensor(g[p][:, :], ps[:, (2, 5)[p], :], sg[p][:, :], ALU.mult).then_inc(s["g"], 1)
                eng.wait_ge(s["g"], t + 1)
                if not early(t):
                    eng.wait_ge(s["gturned"], t - 1)
                quantise(eng, g[p][:, :], gr[p][:, :], gq[p][:, :], st[p], s["q"], t * NQS, s["gq"])
                eng.tensor_tensor(fac[p][:, :], st[p][:, 0:1], pl.deq[:, 2:3], ALU.mult).then_inc(s["fac"], 1)

            def residual(t, p):
                eng.wait_ge(s["down"], t + 1)
                eng.wait_ge(s["fac"], t + 1)
                eng.scalar_tensor_tensor(out=pl.x1[:, t, :], in0=ps[:, 6, 0:D], scalar=fac[p][:, 0:1], in1=pl.x1[:, t, :],
                                         op0=ALU.mult, op1=ALU.add).then_inc(s["res"], 1)
                eng.wait_ge(s["res"], t + 1)
                eng.tensor_tensor(pl.x[:, t, :], pl.x[:, t, :], pl.x1[:, t, :], ALU.add).then_inc(s["added"], 1)
                eng.wait_ge(s["added"], t + 1)
                token_stats(pl, eng, t)

            staggered(eng, [(2, gated), (0, norm), (3, residual), (0, hT_rest)])
            pl.stats_n += 3 * NT

        @block.scalar
        def _(eng):
            eng.preload_act_table(ACT.Silu)
            eng.wait_ge(pl.ahead_in, 32)
            for n in range(2):
                c = slice(n * I, (n + 1) * I)
                eng.activation(up[0][:, :, c].bitcast(F32R), pl.up_w[:, :, c], ACT.Copy).then_inc(s["w_head"], 1)

            def take_h(t, p):
                eng.wait_ge(s["hturned"], t + 1)
                if not early(t):
                    eng.wait_ge(s["val"], t - 1)
                eng.activation(hT[p][0][:, :, :].bitcast(F32R), ps[:, 0, 0:KC * P].rearrange("p (k n) -> p k n", k=KC), ACT.Copy).then_inc(s["hT"], 1)

            def silu(t, p):
                eng.wait_ge(s["gate"], t + 1)
                if not early(t):
                    eng.wait_ge(s["g"], t - 1)
                eng.activation(sg[p][:, :], ps[:, (1, 4)[p], :], ACT.Silu).then_inc(s["silu"], 1)

            def take_g(t, p):
                eng.wait_ge(s["gturned"], t + 1)
                if not early(t):
                    eng.wait_ge(s["down"], t - 1)
                eng.activation(gT[p][:, :, :], ps[:, 3, 0:2 * P].bitcast(BF16).rearrange("p (k n) -> p k n", k=4), ACT.Copy).then_inc(s["gT"], 1)

            staggered(eng, [(1, silu), (2, take_g), (0, take_h)])

        @block.tensor
        def _(eng):
            eng.wait_ge(s["w_rest"], 2)

            def turn_h(t, p):
                eng.wait_ge(s["hn"], t + 1)
                eng.wait_ge(s["hT_rest"], t)
                for k in range(KC):
                    mm = eng.transpose(ps[:, 0, k * P:(k + 1) * P], hn[p][:, k * P:(k + 1) * P], pl.ident[:, :])
                mm.then_inc(s["hturned"], 1)

            def ups(t, p):
                eng.wait_ge(s["hT_rest"], t + 1)
                for n, (bank, sem, free) in enumerate((((1, 4)[p], s["gate"], s["silu"]), ((2, 5)[p], s["val"], s["g"]))):
                    if not early(t):
                        eng.wait_ge(free, t - 1)
                    for k in range(KC):
                        mm = split_product(eng, ps[:, bank, :], [x[:, k, :] for x in hT[p]], [x[:, k, n * I:(n + 1) * I] for x in up],
                                           k == 0, k == KC - 1)
                    mm.then_inc(sem, 1)

            def turn_g(t, p):
                eng.wait_ge(s["gq"], t + 1)
                eng.wait_ge(s["gT"], t)
                for k in range(4):
                    mm = eng.transpose(ps[:, 3, k * P // 2:(k + 1) * P // 2].bitcast(BF16), gq[p][:, k * P:(k + 1) * P], pl.identb[:, :])
                mm.then_inc(s["gturned"], 1)

            def down(t, p):
                eng.wait_ge(s["gT"], t + 1)
                eng.wait_ge(s["res"], t)
                for k in range(4):
                    mm = eng.matmul(ps[:, 6, 0:D], gT[p][:, k, :], pl.wd[:, k, :], start=(k == 0), stop=(k == 3))
                mm.then_inc(s["down"], 1)

            staggered(eng, [(1, ups), (2, turn_g), (0, turn_h), (2, down)])


def lut_ffn(pl):
    nc, ps = pl.nc, pl.ps
    I = 688
    half = I // 2
    NC = -(-I // P)
    LAST = I - (NC - 1) * P
    pl.end = L_OFF
    w = [pl.at(f"lf_weights_{k}", [P, LUT_COLS], F32, pl.end) for k in ("head", "rest")]
    nu = KC * 2 * I
    wgu = [x[:, 0:nu].rearrange("p (k a n) -> p k a n", k=KC, a=2) for x in w]
    wdn = [x[:, nu:].rearrange("p (c n) -> p c n", c=NC) for x in w]
    two = lambda name, shape, dt=F32: [pl.at(f"lf_{name}{j}", shape, dt, pl.end) for j in range(2)]
    xn = two("xn", [P, D])
    xT, hT = ([[pl.at(f"lf_{name}{j}_{k}", [P, n, P], F32, pl.end) for k in ("head", "rest")] for j in range(2)]
              for name, n in (("xT", KC), ("hT", NC)))
    sg, h = two("sg", [P, I]), two("h", [P, I])
    s = {k: pl.sem(f"lf_{k}") for k in (
        "w_head", "w_rest", "xT_rest", "hT_rest", "rs_in", "rstd", "xn", "xturned", "xT", "gate", "up", "silu", "h", "hturned", "hT", "down", "added", "stored")}

    parts = ((slice(0, 4), P, 4, 0), (slice(4, 5), P, 5, 0), (slice(5, 6), LAST, 5, P))

    with nc.Block() as block:
        @block.sync
        def _(eng):
            def store(t, p):
                eng.wait_ge(s["added"], t + 1)
                eng.dma_start(pl.out[:, t, :], pl.x[:, t, :]).then_inc(s["stored"], 16)
            staggered(eng, [(0, store)])
            eng.wait_ge(s["stored"], 16 * NT)

        @block.gpsimd
        def _(eng):
            pow_of_all(pl, eng, s)

        @block.vector
        def _(eng):
            def weight_rests():
                for n, c in enumerate((slice(0, nu), slice(nu, LUT_COLS))):
                    eng.wait_ge(s["w_head"], n + 1)
                    rest_of(eng, pl.lut_w[:, c], w[0][:, c], w[1][:, c]).then_inc(s["w_rest"], 1)
            rstd_of_all(pl, eng, s, weight_rests)

            def norm(t, p):
                if not early(t):
                    eng.wait_ge(s["xturned"], t - 1)
                eng.tensor_scalar(xn[p][:, :], pl.x[:, t, :], pl.mv[:, t, 0:1], pl.rstd[:, bass.ds(t, 1)],
                                  ALU.subtract, ALU.mult).then_inc(s["xn"], 1)

            def xT_rest(t, p):
                eng.wait_ge(s["xT"], t + 1)
                if not early(t):
                    eng.wait_ge(s["up"], t - 1)
                rest_of(eng, ps[:, 7, 0:KC * P].rearrange("p (k n) -> p k n", k=KC), xT[p][0][:, :, :], xT[p][1][:, :, :]).then_inc(s["xT_rest"], 1)

            def hT_rest(t, p):
                eng.wait_ge(s["hT"], 3 * t + 3)
                if not early(t):
                    eng.wait_ge(s["down"], t - 1)
                for c, m, b, a in parts:
                    src = ps[0:m, b, a:a + (c.stop - c.start) * P].rearrange("p (c n) -> p c n", n=P)
                    rest_of(eng, src, hT[p][0][0:m, c, :], hT[p][1][0:m, c, :]).then_inc(s["hT_rest"], 1)

            def gated(t, p):
                eng.wait_ge(s["silu"], t + 1)
                eng.wait_ge(s["up"], t + 1)
                if not early(t):
                    eng.wait_ge(s["hturned"], 2 * t - 2)
                eng.tensor_tensor(h[p][:, :].rearrange("p (a n) -> p a n", a=2), ps[:, 2:4, 0:half],
                                  sg[p][:, :].rearrange("p (a n) -> p a n", a=2), ALU.mult).then_inc(s["h"], 1)

            def add(t, p):
                eng.wait_ge(s["down"], t + 1)
                eng.tensor_tensor(pl.x[:, t, :], ps[:, 6, 0:D], pl.x[:, t, :], ALU.add).then_inc(s["added"], 1)

            staggered(eng, [(2, gated), (0, norm), (3, add), (2, hT_rest), (0, xT_rest)])

        @block.scalar
        def _(eng):
            eng.preload_act_table(ACT.Silu)
            eng.wait_ge(pl.lut_in, 16)
            for c in (slice(0, nu), slice(nu, LUT_COLS)):
                eng.activation(w[0][:, c].bitcast(F32R), pl.lut_w[:, c], ACT.Copy).then_inc(s["w_head"], 1)

            def take_x(t, p):
                eng.wait_ge(s["xturned"], t + 1)
                if not early(t):
                    eng.wait_ge(s["up"], t - 1)
                eng.activation(xT[p][0][:, :, :].bitcast(F32R), ps[:, 7, 0:KC * P].rearrange("p (k n) -> p k n", k=KC), ACT.Copy).then_inc(s["xT"], 1)

            def silu(t, p):
                eng.wait_ge(s["gate"], t + 1)
                if not early(t):
                    eng.wait_ge(s["h"], t - 1)
                eng.activation(sg[p][:, :].rearrange("p (a n) -> p a n", a=2), ps[:, 0:2, 0:half], ACT.Silu).then_inc(s["silu"], 1)

            def take_h(t, p):
                eng.wait_ge(s["hturned"], 2 * t + 2)
                if not early(t):
                    eng.wait_ge(s["down"], t - 1)
                for c, m, b, a in parts:
                    src = ps[0:m, b, a:a + (c.stop - c.start) * P].rearrange("p (c n) -> p c n", n=P)
                    eng.activation(hT[p][0][0:m, c, :].bitcast(F32R), src, ACT.Copy).then_inc(s["hT"], 1)

            staggered(eng, [(2, take_h), (0, take_x), (1, silu)])

        @block.tensor
        def _(eng):
            eng.wait_ge(s["w_rest"], 2)

            def turn_x(t, p):
                eng.wait_ge(s["xn"], t + 1)
                eng.wait_ge(s["xT_rest"], t)
                for k in range(KC):
                    mm = eng.transpose(ps[:, 7, k * P:(k + 1) * P], xn[p][:, k * P:(k + 1) * P], pl.ident[:, :])
                mm.then_inc(s["xturned"], 1)

            def ups(t, p):
                eng.wait_ge(s["xT_rest"], t + 1)
                for a, (sem, free) in enumerate(((s["gate"], s["silu"]), (s["up"], s["h"]))):
                    eng.wait_ge(free, t)
                    for m in range(2):
                        for k in range(KC):
                            mm = split_product(eng, ps[:, 2 * a + m, 0:half], [x[:, k, :] for x in xT[p]],
                                               [x[:, k, a, m * half:(m + 1) * half] for x in wgu], k == 0, k == KC - 1)
                    mm.then_inc(sem, 1)

            def turn_h(t, p):
                eng.wait_ge(s["h"], t + 1)
                eng.wait_ge(s["hT_rest"], 3 * t)
                for c in range(NC):
                    m = P if c < NC - 1 else LAST
                    mm = eng.transpose(ps[0:m, 4 + c // 4, c % 4 * P:c % 4 * P + P], h[p][:, c * P:c * P + m], pl.ident[:, :])
                    if c in (3, NC - 1):
                        mm.then_inc(s["hturned"], 1)

            def down(t, p):
                eng.wait_ge(s["hT_rest"], 3 * t + 3)
                eng.wait_ge(s["added"], t)
                for c in range(NC):
                    m = P if c < NC - 1 else LAST
                    mm = split_product(eng, ps[:, 6, 0:D], [x[0:m, c, :] for x in hT[p]], [x[0:m, c, :] for x in wdn], c == 0, c == NC - 1)
                mm.then_inc(s["down"], 1)

            staggered(eng, [(2, turn_h), (0, turn_x), (1, ups), (2, down)])


def store(pl, out):
    done = pl.sem("stored")
    with pl.nc.Block() as block:
        @block.sync
        def _(eng):
            eng.dma_start(out.rearrange("(t p) d -> p t d", p=P), pl.x[:, :, :]).then_inc(done, 16)
            eng.wait_ge(done, 16)


def build(nc, ap, out, start=0, stop=6):
    with ExitStack() as ctx:
        pl = Plan(nc, ctx, ap)
        common(pl)
        setup(pl)
        if start < 1 <= stop:
            l0x_queries(pl)
            xattn_batches(pl, "l0x", L_OFF, pl.tmp_off, True)
            xattn_project(pl, "l0xo", pl.Bw, pl.tmp_off, 1)
            pl.clear_layer()
        if start < 2 <= stop:
            self_attention(pl)
        if start < 3 <= stop:
            experts(pl)
            pl.clear_layer()
        if start < 4 <= stop:
            key_norms(pl)
            l1x_queries(pl)
            xattn_batches(pl, "l1x", pl.low1_off, None, False, normed=True)
            xattn_project(pl, "l1xo", pl.Bw1, pl.low1_off, 2, pl.bw1_in, BlockWeights(pl))
            pl.clear_layer()
        if start == 4:
            raise ValueError("the block's weights are made in the layer before")
        if start < 5 <= stop:
            block_attention(pl)
            block_ffn(pl)
        pl.out = out.rearrange("(t p) d -> p t d", p=P)
        if stop >= 6:
            lut_ffn(pl)
        else:
            store(pl, out)


def layout(inputs):
    a = {k: np.asarray(v) for k, v in inputs.items()}
    c = np.ascontiguousarray
    heads = lambda w, n: w.reshape(w.shape[0], n, -1)
    turned = lambda w: w.T.reshape(-1, P, w.shape[0]).transpose(1, 0, 2).reshape(P, -1)
    gu = np.stack([a["L1_ffn_gate_idx"].T, a["L1_ffn_up_idx"].T], 1)
    gu = gu.reshape(KC, P, -1).transpose(1, 0, 2).reshape(P, -1)
    dn = a["L1_ffn_down_idx"].T
    dn = np.concatenate([dn, np.zeros((-dn.shape[0] % P, D), dn.dtype)])
    idx = np.concatenate([gu, dn.reshape(-1, P, D).transpose(1, 0, 2).reshape(P, -1)], 1)
    return {
        **tables(),
        "x": c(a["x"].reshape(NT, P, D).transpose(1, 0, 2)),
        "ctx": c(a["ctx_1024"]),
        "ctxT": c(a["ctx_1024"].reshape(B * CS, CD).T),
        "mask": c(a["mask_BxS2_bf1"]).view(np.uint8),
        "L0_WqT": c(heads(a["L0_xattn_Wq"], NH).transpose(2, 1, 0)),
        "L0_WkT": c(heads(a["L0_xattn_Wk"], 8).transpose(2, 1, 0)),
        "L0_WvT": c(heads(a["L0_xattn_Wv"], 8).transpose(2, 1, 0)),
        "L0_wqkvT": c(a["L0_attn_w_qkv"].T.reshape(KC, P, -1).transpose(1, 0, 2)),
        "L0_woT": c(a["L0_attn_w_o"].T.reshape(NT, P, D).transpose(1, 0, 2)),
        "L1_WqT": c(a["L1_xattn_Wq"].reshape(KC, P, -1).transpose(1, 0, 2)),
        "L1_Wk": c(a["L1_xattn_Wk"]),
        "L1_WkT": c(heads(a["L1_xattn_Wk"], NH).transpose(2, 1, 0)),
        "L1_WvT": c(heads(a["L1_xattn_Wv"], NH).transpose(2, 1, 0)),
        "L1_Wo": c(a["L1_xattn_Wo"].reshape(NH, HD, D).transpose(1, 0, 2)),
        "L1_g": c(np.stack([a["L1_xattn_gq"], a["L1_xattn_gk"]], 1)),
        "L1_qkvT": c(turned(a["L1_attn_qkv_w"])),
        "L1_oT": c(turned(a["L1_attn_o_w"])),
        "L1_downT": c(turned(a["L1_attn_ffn_down_w"])),
        "L1_upT": c(turned(a["L1_attn_ffn_up_w"]).reshape(P, KC, -1)),
        "L1_attn_norm": c(a["L1_attn_attn_norm_w"][None]),
        "L1_ffn_norm": c(a["L1_attn_ffn_norm_w"][None]),
        "L1_lut": c(a["L1_ffn_lut"][None]),
        "L1_idx": c(idx),
        "entries": np.ascontiguousarray(np.broadcast_to(np.arange(NT, dtype=np.float32), (P, NT))),
        "L0_gate": c(a["L0_ffn_gate"].reshape(KC, P, -1).transpose(1, 0, 2)),
        "L0_wg": c(a["L0_ffn_gate_up_proj"][:, :, :96].transpose(1, 0, 2).reshape(KC, P, -1).transpose(1, 0, 2)),
        "L0_wu": c(a["L0_ffn_gate_up_proj"][:, :, 96:].transpose(1, 0, 2).reshape(KC, P, -1).transpose(1, 0, 2)),
        "L0_wd": c(a["L0_ffn_down_proj"].reshape(-1, P, D).transpose(1, 0, 2)),
        "L0_Wo": c(a["L0_xattn_Wo"].reshape(NH, HD, D).transpose(1, 0, 2)),
    }


def kernel(**inputs):
    import concourse.bacc as _bacc
    from concourse import mybir as _mybir
    from concourse.bass_utils import run_bass_kernel_spmd as _run

    nc = _bacc.Bacc("TRN2", target_bir_lowering=False, num_devices=1)
    arrays = layout(inputs)
    ap = {k: nc.dram_tensor(k, a.shape, _mybir.dt.from_np(a.dtype), kind="ExternalInput").ap() for k, a in arrays.items()}
    out = nc.dram_tensor("out", (TOK, D), F32, kind="ExternalOutput").ap()
    build(nc, ap, out)
    r = _run(nc, [arrays], core_ids=[0])
    return r.results[0]["out"].reshape(B, S, D)
```
